# Optimizing a Trainium2 kernel written in Bass

```python
import numpy as np
import jax
import jax.numpy as jnp

def _softmax(x, axis=-1):
    return jax.nn.softmax(x, axis=axis)

def _gelu(x):
    return jax.nn.gelu(x, approximate=True)

def _silu(x):
    return jax.nn.silu(x)

def _sigmoid(x):
    return jax.nn.sigmoid(x)

def _layernorm(x, axis=-1, eps=1e-05):
    m = jnp.mean(x, axis=axis, keepdims=True)
    v = jnp.var(x, axis=axis, keepdims=True)
    return (x - m) / jnp.sqrt(v + eps)

def _scatter_add(tgt, idx, src, axis=0):
    return tgt.at[idx].add(src)

def _segment_sum(src, seg, n):
    return jax.ops.segment_sum(src, seg, n)
kernel_name = 'mk_hybrid_d4_jaxref_r8_3479fc'

def setup_inputs(seed: int=0):
    np.random.seed(seed)
    _w = jnp.asarray

    def _L0_attn_a_setup():
        import jax, jax.numpy as jnp
        import numpy as np
        NUM_HEAD = 16
        D_Q = 64
        D_KV = 64
        ROPE_BASE = 10000.0

        def _cos_sin(seq_len, dim):
            pos = jnp.arange(seq_len, dtype=jnp.float32)[:, None]
            ids = jnp.arange(dim // 2, dtype=jnp.float32)
            theta = ROPE_BASE ** (-2.0 * ids) / (dim // 2)
            r = pos * theta[None, :]
            return (jnp.cos(r), jnp.sin(r))

        def _rope(x, cos, sin):
            b, s, d = x.shape
            xv = x.reshape(b, s, d // 2, 2)
            x0, x1 = (xv[..., 0], xv[..., 1])
            out = jnp.stack([x0 * cos - x1 * sin, x1 * cos + x0 * sin], axis=-1)
            return out.reshape(b, s, d)
        key = jax.random.key(seed)
        ks = jax.random.split(key, 10)
        d_model, d_q, d_kv = (128, D_Q, D_KV)
        b, s = (2, 256)
        w = lambda k, i, o: jax.random.normal(k, (i, o), dtype=jnp.float32) * 0.02
        return {'x': jax.random.normal(ks[0], (b, s, d_model), dtype=jnp.float32), 'Wd_q_w': w(ks[1], d_model, d_q), 'Wd_q_b': jnp.zeros((d_q,), jnp.float32), 'Wu_q_w': w(ks[2], d_q, d_model), 'Wu_q_b': jnp.zeros((d_model,), jnp.float32), 'Wq_r_w': w(ks[3], d_q, d_model), 'Wq_r_b': jnp.zeros((d_model,), jnp.float32), 'Wk_r_w': w(ks[4], d_model, d_model), 'Wk_r_b': jnp.zeros((d_model,), jnp.float32), 'Wd_kv_w': w(ks[5], d_model, d_kv), 'Wd_kv_b': jnp.zeros((d_kv,), jnp.float32), 'Wu_k_w': w(ks[6], d_kv, d_model), 'Wu_k_b': jnp.zeros((d_model,), jnp.float32), 'Wu_v_w': w(ks[7], d_kv, d_model), 'Wu_v_b': jnp.zeros((d_model,), jnp.float32), 'Wo_w': w(ks[8], d_model, d_model), 'Wo_b': jnp.zeros((d_model,), jnp.float32)}
    _L0_attn_a_in = _L0_attn_a_setup()

    def _L0_attn_b_setup():
        import jax, jax.numpy as jnp
        import numpy as np
        B, N, C = (4, 512, 128)
        H = 16
        D = C // H
        key = jax.random.key(seed)
        ks = jax.random.split(key, 4)
        s = 1.0 / np.sqrt(C)
        x = jax.random.normal(ks[0], (B, N, C), dtype=jnp.float32)
        Wqkv = jax.random.normal(ks[1], (C, 3 * C), dtype=jnp.float32) * s
        Wg = jax.random.normal(ks[2], (C, C), dtype=jnp.float32) * s
        bg = jnp.zeros((C,), dtype=jnp.float32)
        Wp = jax.random.normal(ks[3], (C, C), dtype=jnp.float32) * s
        bp = jnp.zeros((C,), dtype=jnp.float32)
        return {'x': x, 'Wqkv': Wqkv, 'Wg': Wg, 'bg': bg, 'Wp': Wp, 'bp': bp}
    _L0_attn_b_in = _L0_attn_b_setup()

    def _L0_ffn_setup():
        import jax, jax.numpy as jnp
        import numpy as np
        B, S, DIM = (4, 512, 128)
        BASE_COUPLING = 0.1
        NUM_CYCLES = 3

        def _gelu(x):
            return jax.nn.gelu(x, approximate=False)

        def _coupling_net(h, w1, b1, w2, b2, w3, b3, w4, b4):
            h = _gelu(h @ w1 + b1)
            h = _gelu(h @ w2 + b2)
            h = _gelu(h @ w3 + b3)
            return jax.nn.sigmoid(h @ w4 + b4)

        def _global_net(h, w1, b1, w2, b2, w3, b3):
            h = _gelu(h @ w1 + b1)
            h = _gelu(h @ w2 + b2)
            return jax.nn.sigmoid(h @ w3 + b3)

        def _twist(x):
            o_r, o_i, p_r, p_i = jnp.split(x, 4, axis=-1)
            return jnp.concatenate([p_r, -p_i, -o_r, o_i], axis=-1)
        key = jax.random.key(seed)
        ks = jax.random.split(key, 9)
        d = DIM

        def w(k, fan_in, fan_out):
            return jax.random.normal(k, (fan_in, fan_out), dtype=jnp.float32) / np.sqrt(fan_in).astype(np.float32)
        inp = {'x': jax.random.normal(ks[0], (B, S, d), dtype=jnp.float32)}
        cn_dims = [(d, d), (d, d // 2), (d // 2, d // 4), (d // 4, 1)]
        for i, (a, b) in enumerate(cn_dims):
            inp[f'cn_w{i + 1}'] = w(ks[1 + i], a, b)
            inp[f'cn_b{i + 1}'] = jnp.zeros((b,), dtype=jnp.float32)
        gc_dims = [(d, d // 2), (d // 2, d // 4), (d // 4, 1)]
        for i, (a, b) in enumerate(gc_dims):
            inp[f'gc_w{i + 1}'] = w(ks[5 + i], a, b)
            inp[f'gc_b{i + 1}'] = jnp.zeros((b,), dtype=jnp.float32)
        inp['adaptive_range'] = jnp.full((1,), 0.2, dtype=jnp.float32)
        return inp
    _L0_ffn_in = _L0_ffn_setup()

    def _L1_attn_a_setup():
        import jax, jax.numpy as jnp
        import numpy as np
        NUM_HEAD = 16
        D_Q = 64
        D_KV = 64
        ROPE_BASE = 10000.0

        def _cos_sin(seq_len, dim):
            pos = jnp.arange(seq_len, dtype=jnp.float32)[:, None]
            ids = jnp.arange(dim // 2, dtype=jnp.float32)
            theta = ROPE_BASE ** (-2.0 * ids) / (dim // 2)
            r = pos * theta[None, :]
            return (jnp.cos(r), jnp.sin(r))

        def _rope(x, cos, sin):
            b, s, d = x.shape
            xv = x.reshape(b, s, d // 2, 2)
            x0, x1 = (xv[..., 0], xv[..., 1])
            out = jnp.stack([x0 * cos - x1 * sin, x1 * cos + x0 * sin], axis=-1)
            return out.reshape(b, s, d)
        key = jax.random.key(seed)
        ks = jax.random.split(key, 10)
        d_model, d_q, d_kv = (128, D_Q, D_KV)
        b, s = (2, 256)
        w = lambda k, i, o: jax.random.normal(k, (i, o), dtype=jnp.float32) * 0.02
        return {'x': jax.random.normal(ks[0], (b, s, d_model), dtype=jnp.float32), 'Wd_q_w': w(ks[1], d_model, d_q), 'Wd_q_b': jnp.zeros((d_q,), jnp.float32), 'Wu_q_w': w(ks[2], d_q, d_model), 'Wu_q_b': jnp.zeros((d_model,), jnp.float32), 'Wq_r_w': w(ks[3], d_q, d_model), 'Wq_r_b': jnp.zeros((d_model,), jnp.float32), 'Wk_r_w': w(ks[4], d_model, d_model), 'Wk_r_b': jnp.zeros((d_model,), jnp.float32), 'Wd_kv_w': w(ks[5], d_model, d_kv), 'Wd_kv_b': jnp.zeros((d_kv,), jnp.float32), 'Wu_k_w': w(ks[6], d_kv, d_model), 'Wu_k_b': jnp.zeros((d_model,), jnp.float32), 'Wu_v_w': w(ks[7], d_kv, d_model), 'Wu_v_b': jnp.zeros((d_model,), jnp.float32), 'Wo_w': w(ks[8], d_model, d_model), 'Wo_b': jnp.zeros((d_model,), jnp.float32)}
    _L1_attn_a_in = _L1_attn_a_setup()

    def _L1_attn_b_setup():
        import jax, jax.numpy as jnp
        import numpy as np
        import math
        D_MODEL = 128
        D_STATE = 16
        DT_RANK = 64
        BATCH = 4
        SEQLEN = 256
        key = jax.random.key(seed)
        ks = jax.random.split(key, 4)
        u = jax.random.normal(ks[0], (BATCH, SEQLEN, D_MODEL), dtype=jnp.float32)
        A = jnp.tile(jnp.arange(1, D_STATE + 1, dtype=jnp.float32)[None, :], (D_MODEL, 1))
        A_log = jnp.log(A)
        D_skip = jnp.ones((D_MODEL,), dtype=jnp.float32)
        dt_init_std = DT_RANK ** (-0.5)
        dt_proj_w = jax.random.uniform(ks[1], (D_MODEL, DT_RANK), dtype=jnp.float32, minval=-dt_init_std, maxval=dt_init_std)
        dt_proj_b = jnp.zeros((D_MODEL,), dtype=jnp.float32)
        x_proj_w = jax.random.normal(ks[2], (DT_RANK + 2 * D_STATE, D_MODEL), dtype=jnp.float32) * D_MODEL ** (-0.5)
        return {'u': u, 'A_log': A_log, 'D_skip': D_skip, 'dt_proj_w': dt_proj_w, 'dt_proj_b': dt_proj_b, 'x_proj_w': x_proj_w}
    _L1_attn_b_in = _L1_attn_b_setup()

    def _L1_ffn_setup():
        import jax, jax.numpy as jnp
        import numpy as np
        E = 16
        F_C = 2.0
        D = 128
        I = 4 * D
        IS = 2 * D
        B, S = (4, 128)
        key = jax.random.key(seed)
        ks = jax.random.split(key, 8)
        w = 0.02
        return {'hidden_states': jax.random.normal(ks[0], (B, S, D), dtype=jnp.float32), 'gate_w': jax.random.normal(ks[1], (E, D), dtype=jnp.float32) * w, 'Wg': jax.random.normal(ks[2], (E, I, D), dtype=jnp.float32) * w, 'Wu': jax.random.normal(ks[3], (E, I, D), dtype=jnp.float32) * w, 'Wd': jax.random.normal(ks[4], (E, D, I), dtype=jnp.float32) * w, 'Sg': jax.random.normal(ks[5], (IS, D), dtype=jnp.float32) * w, 'Su': jax.random.normal(ks[6], (IS, D), dtype=jnp.float32) * w, 'Sd': jax.random.normal(ks[7], (D, IS), dtype=jnp.float32) * w}
    _L1_ffn_in = _L1_ffn_setup()

    def _L2_attn_a_setup():
        import jax, jax.numpy as jnp
        import numpy as np
        B, T, C = (2, 256, 128)
        NH = 16
        HS = C // NH
        BD = max(HS // 4, 16)
        HORIZON = 64
        key = jax.random.key(seed)
        ks = jax.random.split(key, 10)
        s = 0.02
        return {'x': jax.random.normal(ks[0], (B, T, C), dtype=jnp.float32), 'W_disp': jax.random.normal(ks[1], (NH * BD, C), dtype=jnp.float32) * s, 'W_val': jax.random.normal(ks[2], (C, C), dtype=jnp.float32) * s, 'rel_pos_emb': jax.random.normal(ks[3], (HORIZON, BD), dtype=jnp.float32) * s, 'strain_fused_w': jax.random.normal(ks[4], (2 * BD, BD), dtype=jnp.float32) * s, 'strain_fused_b': jnp.zeros((2 * BD,), dtype=jnp.float32), 'pos_proj_w': jax.random.normal(ks[5], (BD, BD), dtype=jnp.float32) * s, 'bond_out_w': jax.random.normal(ks[6], (1, BD), dtype=jnp.float32) * s, 'damage_out_w': jax.random.normal(ks[7], (1, BD), dtype=jnp.float32) * s, 'damage_out_b': jnp.full((1,), -3.0, dtype=jnp.float32), 'c_proj_w': jax.random.normal(ks[8], (C, C), dtype=jnp.float32) * s}
    _L2_attn_a_in = _L2_attn_a_setup()

    def _L2_attn_b_setup():
        import jax, jax.numpy as jnp
        import numpy as np
        B, S, D = (4, 256, 128)
        GAMMA = 1.0
        key = jax.random.key(seed)
        ks = jax.random.split(key, 9)
        scale = 1.0 / np.sqrt(D)
        return {'x': jax.random.normal(ks[0], (B, S, D), dtype=jnp.float32), 'Wq': jax.random.normal(ks[1], (D, D), dtype=jnp.float32) * scale, 'bq': jax.random.normal(ks[2], (D,), dtype=jnp.float32) * 0.01, 'Wk': jax.random.normal(ks[3], (D, D), dtype=jnp.float32) * scale, 'bk': jax.random.normal(ks[4], (D,), dtype=jnp.float32) * 0.01, 'Wv': jax.random.normal(ks[5], (D, D), dtype=jnp.float32) * scale, 'bv': jax.random.normal(ks[6], (D,), dtype=jnp.float32) * 0.01, 'Wo': jax.random.normal(ks[7], (D, D), dtype=jnp.float32) * scale, 'bo': jax.random.normal(ks[8], (D,), dtype=jnp.float32) * 0.01}
    _L2_attn_b_in = _L2_attn_b_setup()

    def _L2_ffn_setup():
        import jax, jax.numpy as jnp
        import numpy as np
        B, S, H, E, K = (4, 256, 128, 8, 2)
        key = jax.random.key(seed)
        k0, k1, k2, k3 = jax.random.split(key, 4)
        x = jax.random.normal(k0, (B, S, H), dtype=jnp.float32)
        router_w = jax.random.normal(k1, (E, H), dtype=jnp.float32) * np.float32(1.0 / np.sqrt(H))
        xav1 = np.float32(np.sqrt(2.0 / (2 * H + H)))
        w1 = jax.random.normal(k2, (E, 2 * H, H), dtype=jnp.float32) * xav1
        w2 = jax.random.normal(k3, (E, H, 2 * H), dtype=jnp.float32) * xav1
        return {'x': x, 'router_w': router_w, 'w1': w1, 'w2': w2}
    _L2_ffn_in = _L2_ffn_setup()

    def _L3_attn_a_setup():
        import jax, jax.numpy as jnp
        import numpy as np
        B, S, E, H, Dh = (2, 256, 128, 16, 64)
        key = jax.random.key(seed)
        ks = jax.random.split(key, 8)
        w = 0.02
        return {'x': jax.random.normal(ks[0], (B, S, E), jnp.float32), 'Wq': jax.random.normal(ks[1], (H, Dh, E), jnp.float32) * w, 'bq': jax.random.normal(ks[2], (H, Dh), jnp.float32) * w, 'Wk': jax.random.normal(ks[3], (H, Dh, E), jnp.float32) * w, 'bk': jax.random.normal(ks[4], (H, Dh), jnp.float32) * w, 'Wv': jax.random.normal(ks[5], (H, Dh, E), jnp.float32) * w, 'bv': jax.random.normal(ks[6], (H, Dh), jnp.float32) * w, 'proj': jax.random.normal(ks[7], (H * Dh, E), jnp.float32) * w}
    _L3_attn_a_in = _L3_attn_a_setup()

    def _L3_attn_b_setup():
        import jax, jax.numpy as jnp
        import numpy as np
        import math
        E, N, K, R = (128, 16, 4, 64)
        B, L = (2, 256)
        key = jax.random.key(seed)
        ks = jax.random.split(key, 8)
        gn = lambda k, sh, sc: jax.random.normal(k, sh, dtype=jnp.float32) * sc
        W_z = gn(ks[0], (E, E), E ** (-0.5))
        W_params = gn(ks[1], (R + 2 * N, E), E ** (-0.5))
        conv_w = gn(ks[2], (E, 1, K), 0.5)
        dt_std = R ** (-0.5) * 0.1
        W_dt = jax.random.uniform(ks[3], (E, R), jnp.float32, -dt_std, dt_std)
        b_dt = jnp.full((E,), math.log(math.expm1(0.001)), dtype=jnp.float32)
        A_log = jnp.tile(jnp.log(jnp.arange(1, N + 1, dtype=jnp.float32))[None, :], (E, 1))
        D = jnp.ones((E,), dtype=jnp.float32)
        W_out = gn(ks[4], (E, E), E ** (-0.5))
        x = jax.random.normal(ks[5], (B, L, E), dtype=jnp.float32)
        return dict(x=x, W_z=W_z, W_params=W_params, conv_w=conv_w, W_dt=W_dt, b_dt=b_dt, A_log=A_log, D=D, W_out=W_out)
    _L3_attn_b_in = _L3_attn_b_setup()

    def _L3_ffn_setup():
        import jax, jax.numpy as jnp
        import numpy as np
        H = 128
        E = 64
        K = 8
        G = 8
        TOPK_GROUP = 4
        I_MOE = 64
        I_SHARED = 256
        SCALE = 2.5

        def relu2(x):
            return jnp.square(jax.nn.relu(x))

        def _route(xf, router_w, correction_bias):
            T = xf.shape[0]
            logits = xf @ router_w.T
            scores = jax.nn.sigmoid(logits)
            sfc = scores + correction_bias[None, :]
            grp = sfc.reshape(T, G, E // G)
            top2, _ = jax.lax.top_k(grp, 2)
            group_scores = top2.sum(-1)
            _, gidx = jax.lax.top_k(group_scores, TOPK_GROUP)
            gmask = jnp.zeros((T, G), sfc.dtype).at[jnp.arange(T)[:, None], gidx].set(1.0)
            emask = jnp.repeat(gmask, E // G, axis=1)
            masked = jnp.where(emask > 0, sfc, 0.0)
            _, tidx = jax.lax.top_k(masked, K)
            tw = jnp.take_along_axis(scores, tidx, axis=1)
            tw = tw / (tw.sum(-1, keepdims=True) + 1e-20)
            return (tidx, tw * SCALE)
        key = jax.random.key(seed)
        ks = jax.random.split(key, 7)
        x = jax.random.normal(ks[0], (2, 128, H), dtype=jnp.float32)
        router_w = jax.random.normal(ks[1], (E, H), dtype=jnp.float32) * 0.02
        correction_bias = jax.random.normal(ks[2], (E,), dtype=jnp.float32) * 0.01
        up_w = jax.random.normal(ks[3], (E, H, I_MOE), dtype=jnp.float32) * 0.02
        down_w = jax.random.normal(ks[4], (E, I_MOE, H), dtype=jnp.float32) * 0.02
        shared_up_w = jax.random.normal(ks[5], (H, I_SHARED), dtype=jnp.float32) * 0.02
        shared_down_w = jax.random.normal(ks[6], (I_SHARED, H), dtype=jnp.float32) * 0.02
        return {'x': x, 'router_w': router_w, 'correction_bias': correction_bias, 'up_w': up_w, 'down_w': down_w, 'shared_up_w': shared_up_w, 'shared_down_w': shared_down_w}
    _L3_ffn_in = _L3_ffn_setup()
    _d = {'L0_attn_a_x': _L0_attn_a_in['x'], 'L0_attn_a_Wd_q_w': _L0_attn_a_in['Wd_q_w'], 'L0_attn_a_Wd_q_b': _L0_attn_a_in['Wd_q_b'], 'L0_attn_a_Wu_q_w': _L0_attn_a_in['Wu_q_w'], 'L0_attn_a_Wu_q_b': _L0_attn_a_in['Wu_q_b'], 'L0_attn_a_Wq_r_w': _L0_attn_a_in['Wq_r_w'], 'L0_attn_a_Wq_r_b': _L0_attn_a_in['Wq_r_b'], 'L0_attn_a_Wk_r_w': _L0_attn_a_in['Wk_r_w'], 'L0_attn_a_Wk_r_b': _L0_attn_a_in['Wk_r_b'], 'L0_attn_a_Wd_kv_w': _L0_attn_a_in['Wd_kv_w'], 'L0_attn_a_Wd_kv_b': _L0_attn_a_in['Wd_kv_b'], 'L0_attn_a_Wu_k_w': _L0_attn_a_in['Wu_k_w'], 'L0_attn_a_Wu_k_b': _L0_attn_a_in['Wu_k_b'], 'L0_attn_a_Wu_v_w': _L0_attn_a_in['Wu_v_w'], 'L0_attn_a_Wu_v_b': _L0_attn_a_in['Wu_v_b'], 'L0_attn_a_Wo_w': _L0_attn_a_in['Wo_w'], 'L0_attn_a_Wo_b': _L0_attn_a_in['Wo_b'], 'L0_attn_b_Wqkv': _L0_attn_b_in['Wqkv'], 'L0_attn_b_Wg': _L0_attn_b_in['Wg'], 'L0_attn_b_bg': _L0_attn_b_in['bg'], 'L0_attn_b_Wp': _L0_attn_b_in['Wp'], 'L0_attn_b_bp': _L0_attn_b_in['bp'], 'L0_ffn_cn_w1': _L0_ffn_in['cn_w1'], 'L0_ffn_cn_b1': _L0_ffn_in['cn_b1'], 'L0_ffn_cn_w2': _L0_ffn_in['cn_w2'], 'L0_ffn_cn_b2': _L0_ffn_in['cn_b2'], 'L0_ffn_cn_w3': _L0_ffn_in['cn_w3'], 'L0_ffn_cn_b3': _L0_ffn_in['cn_b3'], 'L0_ffn_cn_w4': _L0_ffn_in['cn_w4'], 'L0_ffn_cn_b4': _L0_ffn_in['cn_b4'], 'L0_ffn_gc_w1': _L0_ffn_in['gc_w1'], 'L0_ffn_gc_b1': _L0_ffn_in['gc_b1'], 'L0_ffn_gc_w2': _L0_ffn_in['gc_w2'], 'L0_ffn_gc_b2': _L0_ffn_in['gc_b2'], 'L0_ffn_gc_w3': _L0_ffn_in['gc_w3'], 'L0_ffn_gc_b3': _L0_ffn_in['gc_b3'], 'L0_ffn_adaptive_range': _L0_ffn_in['adaptive_range'], 'L1_attn_a_Wd_q_w': _L1_attn_a_in['Wd_q_w'], 'L1_attn_a_Wd_q_b': _L1_attn_a_in['Wd_q_b'], 'L1_attn_a_Wu_q_w': _L1_attn_a_in['Wu_q_w'], 'L1_attn_a_Wu_q_b': _L1_attn_a_in['Wu_q_b'], 'L1_attn_a_Wq_r_w': _L1_attn_a_in['Wq_r_w'], 'L1_attn_a_Wq_r_b': _L1_attn_a_in['Wq_r_b'], 'L1_attn_a_Wk_r_w': _L1_attn_a_in['Wk_r_w'], 'L1_attn_a_Wk_r_b': _L1_attn_a_in['Wk_r_b'], 'L1_attn_a_Wd_kv_w': _L1_attn_a_in['Wd_kv_w'], 'L1_attn_a_Wd_kv_b': _L1_attn_a_in['Wd_kv_b'], 'L1_attn_a_Wu_k_w': _L1_attn_a_in['Wu_k_w'], 'L1_attn_a_Wu_k_b': _L1_attn_a_in['Wu_k_b'], 'L1_attn_a_Wu_v_w': _L1_attn_a_in['Wu_v_w'], 'L1_attn_a_Wu_v_b': _L1_attn_a_in['Wu_v_b'], 'L1_attn_a_Wo_w': _L1_attn_a_in['Wo_w'], 'L1_attn_a_Wo_b': _L1_attn_a_in['Wo_b'], 'L1_attn_b_A_log': _L1_attn_b_in['A_log'], 'L1_attn_b_D_skip': _L1_attn_b_in['D_skip'], 'L1_attn_b_dt_proj_w': _L1_attn_b_in['dt_proj_w'], 'L1_attn_b_dt_proj_b': _L1_attn_b_in['dt_proj_b'], 'L1_attn_b_x_proj_w': _L1_attn_b_in['x_proj_w'], 'L1_ffn_gate_w': _L1_ffn_in['gate_w'], 'L1_ffn_Wg': _L1_ffn_in['Wg'], 'L1_ffn_Wu': _L1_ffn_in['Wu'], 'L1_ffn_Wd': _L1_ffn_in['Wd'], 'L1_ffn_Sg': _L1_ffn_in['Sg'], 'L1_ffn_Su': _L1_ffn_in['Su'], 'L1_ffn_Sd': _L1_ffn_in['Sd'], 'L2_attn_a_W_disp': _L2_attn_a_in['W_disp'], 'L2_attn_a_W_val': _L2_attn_a_in['W_val'], 'L2_attn_a_rel_pos_emb': _L2_attn_a_in['rel_pos_emb'], 'L2_attn_a_strain_fused_w': _L2_attn_a_in['strain_fused_w'], 'L2_attn_a_strain_fused_b': _L2_attn_a_in['strain_fused_b'], 'L2_attn_a_pos_proj_w': _L2_attn_a_in['pos_proj_w'], 'L2_attn_a_bond_out_w': _L2_attn_a_in['bond_out_w'], 'L2_attn_a_damage_out_w': _L2_attn_a_in['damage_out_w'], 'L2_attn_a_damage_out_b': _L2_attn_a_in['damage_out_b'], 'L2_attn_a_c_proj_w': _L2_attn_a_in['c_proj_w'], 'L2_attn_b_Wq': _L2_attn_b_in['Wq'], 'L2_attn_b_bq': _L2_attn_b_in['bq'], 'L2_attn_b_Wk': _L2_attn_b_in['Wk'], 'L2_attn_b_bk': _L2_attn_b_in['bk'], 'L2_attn_b_Wv': _L2_attn_b_in['Wv'], 'L2_attn_b_bv': _L2_attn_b_in['bv'], 'L2_attn_b_Wo': _L2_attn_b_in['Wo'], 'L2_attn_b_bo': _L2_attn_b_in['bo'], 'L2_ffn_router_w': _L2_ffn_in['router_w'], 'L2_ffn_w1': _L2_ffn_in['w1'], 'L2_ffn_w2': _L2_ffn_in['w2'], 'L3_attn_a_Wq': _L3_attn_a_in['Wq'], 'L3_attn_a_bq': _L3_attn_a_in['bq'], 'L3_attn_a_Wk': _L3_attn_a_in['Wk'], 'L3_attn_a_bk': _L3_attn_a_in['bk'], 'L3_attn_a_Wv': _L3_attn_a_in['Wv'], 'L3_attn_a_bv': _L3_attn_a_in['bv'], 'L3_attn_a_proj': _L3_attn_a_in['proj'], 'L3_attn_b_W_z': _L3_attn_b_in['W_z'], 'L3_attn_b_W_params': _L3_attn_b_in['W_params'], 'L3_attn_b_conv_w': _L3_attn_b_in['conv_w'], 'L3_attn_b_W_dt': _L3_attn_b_in['W_dt'], 'L3_attn_b_b_dt': _L3_attn_b_in['b_dt'], 'L3_attn_b_A_log': _L3_attn_b_in['A_log'], 'L3_attn_b_D': _L3_attn_b_in['D'], 'L3_attn_b_W_out': _L3_attn_b_in['W_out'], 'L3_ffn_router_w': _L3_ffn_in['router_w'], 'L3_ffn_correction_bias': _L3_ffn_in['correction_bias'], 'L3_ffn_up_w': _L3_ffn_in['up_w'], 'L3_ffn_down_w': _L3_ffn_in['down_w'], 'L3_ffn_shared_up_w': _L3_ffn_in['shared_up_w'], 'L3_ffn_shared_down_w': _L3_ffn_in['shared_down_w']}
    _x0 = _d['L0_attn_a_x']
    _d['L0_attn_a_x'] = jax.random.normal(jax.random.fold_in(jax.random.key(seed), 1), (16, 256, 128), dtype=_x0.dtype)
    del _x0
    return _d

def reference(L0_attn_a_x, L0_attn_a_Wd_q_w, L0_attn_a_Wd_q_b, L0_attn_a_Wu_q_w, L0_attn_a_Wu_q_b, L0_attn_a_Wq_r_w, L0_attn_a_Wq_r_b, L0_attn_a_Wk_r_w, L0_attn_a_Wk_r_b, L0_attn_a_Wd_kv_w, L0_attn_a_Wd_kv_b, L0_attn_a_Wu_k_w, L0_attn_a_Wu_k_b, L0_attn_a_Wu_v_w, L0_attn_a_Wu_v_b, L0_attn_a_Wo_w, L0_attn_a_Wo_b, L0_attn_b_Wqkv, L0_attn_b_Wg, L0_attn_b_bg, L0_attn_b_Wp, L0_attn_b_bp, L0_ffn_cn_w1, L0_ffn_cn_b1, L0_ffn_cn_w2, L0_ffn_cn_b2, L0_ffn_cn_w3, L0_ffn_cn_b3, L0_ffn_cn_w4, L0_ffn_cn_b4, L0_ffn_gc_w1, L0_ffn_gc_b1, L0_ffn_gc_w2, L0_ffn_gc_b2, L0_ffn_gc_w3, L0_ffn_gc_b3, L0_ffn_adaptive_range, L1_attn_a_Wd_q_w, L1_attn_a_Wd_q_b, L1_attn_a_Wu_q_w, L1_attn_a_Wu_q_b, L1_attn_a_Wq_r_w, L1_attn_a_Wq_r_b, L1_attn_a_Wk_r_w, L1_attn_a_Wk_r_b, L1_attn_a_Wd_kv_w, L1_attn_a_Wd_kv_b, L1_attn_a_Wu_k_w, L1_attn_a_Wu_k_b, L1_attn_a_Wu_v_w, L1_attn_a_Wu_v_b, L1_attn_a_Wo_w, L1_attn_a_Wo_b, L1_attn_b_A_log, L1_attn_b_D_skip, L1_attn_b_dt_proj_w, L1_attn_b_dt_proj_b, L1_attn_b_x_proj_w, L1_ffn_gate_w, L1_ffn_Wg, L1_ffn_Wu, L1_ffn_Wd, L1_ffn_Sg, L1_ffn_Su, L1_ffn_Sd, L2_attn_a_W_disp, L2_attn_a_W_val, L2_attn_a_rel_pos_emb, L2_attn_a_strain_fused_w, L2_attn_a_strain_fused_b, L2_attn_a_pos_proj_w, L2_attn_a_bond_out_w, L2_attn_a_damage_out_w, L2_attn_a_damage_out_b, L2_attn_a_c_proj_w, L2_attn_b_Wq, L2_attn_b_bq, L2_attn_b_Wk, L2_attn_b_bk, L2_attn_b_Wv, L2_attn_b_bv, L2_attn_b_Wo, L2_attn_b_bo, L2_ffn_router_w, L2_ffn_w1, L2_ffn_w2, L3_attn_a_Wq, L3_attn_a_bq, L3_attn_a_Wk, L3_attn_a_bk, L3_attn_a_Wv, L3_attn_a_bv, L3_attn_a_proj, L3_attn_b_W_z, L3_attn_b_W_params, L3_attn_b_conv_w, L3_attn_b_W_dt, L3_attn_b_b_dt, L3_attn_b_A_log, L3_attn_b_D, L3_attn_b_W_out, L3_ffn_router_w, L3_ffn_correction_bias, L3_ffn_up_w, L3_ffn_down_w, L3_ffn_shared_up_w, L3_ffn_shared_down_w):

    def _L0_attn_a_ref(x, Wd_q_w, Wd_q_b, Wu_q_w, Wu_q_b, Wq_r_w, Wq_r_b, Wk_r_w, Wk_r_b, Wd_kv_w, Wd_kv_b, Wu_k_w, Wu_k_b, Wu_v_w, Wu_v_b, Wo_w, Wo_b):
        import jax, jax.numpy as jnp
        import numpy as np
        NUM_HEAD = 16
        D_Q = 64
        D_KV = 64
        ROPE_BASE = 10000.0

        def _cos_sin(seq_len, dim):
            pos = jnp.arange(seq_len, dtype=jnp.float32)[:, None]
            ids = jnp.arange(dim // 2, dtype=jnp.float32)
            theta = ROPE_BASE ** (-2.0 * ids) / (dim // 2)
            r = pos * theta[None, :]
            return (jnp.cos(r), jnp.sin(r))

        def _rope(x, cos, sin):
            b, s, d = x.shape
            xv = x.reshape(b, s, d // 2, 2)
            x0, x1 = (xv[..., 0], xv[..., 1])
            out = jnp.stack([x0 * cos - x1 * sin, x1 * cos + x0 * sin], axis=-1)
            return out.reshape(b, s, d)
        b, s, d_model = x.shape
        h = NUM_HEAD
        hd = d_model // h
        scale = jnp.sqrt(jnp.float32(h + D_KV + D_Q))

        def heads(t):
            return t.reshape(b, s, h, hd).transpose(0, 2, 1, 3)
        cos, sin = _cos_sin(s, d_model)
        ct_q = x @ Wd_q_w + Wd_q_b
        qt_c = heads(ct_q @ Wu_q_w + Wu_q_b)
        qt_r = heads(_rope(ct_q @ Wq_r_w + Wq_r_b, cos, sin))
        query = qt_c + qt_r
        ct_kv = x @ Wd_kv_w + Wd_kv_b
        kt_c = heads(ct_kv @ Wu_k_w + Wu_k_b)
        kt_r = heads(_rope(x @ Wk_r_w + Wk_r_b, cos, sin))
        key = kt_c + kt_r
        value = heads(ct_kv @ Wu_v_w + Wu_v_b)
        attn = jnp.einsum('bhqd,bhkd->bhqk', query, key) / scale
        attn = jax.nn.softmax(attn, axis=-1)
        out = jnp.einsum('bhqk,bhkd->bhqd', attn, value)
        out = out.transpose(0, 2, 1, 3).reshape(b, s, d_model)
        return out @ Wo_w + Wo_b

    def _L0_attn_b_ref(x, Wqkv, Wg, bg, Wp, bp):
        import jax, jax.numpy as jnp
        import numpy as np
        B, N, C = (4, 512, 128)
        H = 16
        D = C // H
        Bb, Nn, Cc = x.shape
        qkv = (x @ Wqkv).reshape(Bb, Nn, 3, H, D).transpose(2, 0, 3, 1, 4)
        q, k, v = (qkv[0], qkv[1], qkv[2])
        gates = jax.nn.sigmoid(x @ Wg + bg).reshape(Bb, Nn, H, D).transpose(0, 2, 1, 3)
        q = jax.nn.elu(q * gates) + 1.0
        k = jax.nn.elu(k * gates) + 1.0
        kv = jnp.einsum('bhnd,bhne->bhde', k, v)
        qkv_out = jnp.einsum('bhnd,bhde->bhne', q, kv)
        k_sum = k.sum(axis=2)
        normalizer = jnp.einsum('bhnd,bhd->bhn', q, k_sum)[..., None]
        out = qkv_out / (normalizer + 1e-08)
        out = out.transpose(0, 2, 1, 3).reshape(Bb, Nn, Cc)
        return out @ Wp + bp

    def _L0_ffn_ref(x, cn_w1, cn_b1, cn_w2, cn_b2, cn_w3, cn_b3, cn_w4, cn_b4, gc_w1, gc_b1, gc_w2, gc_b2, gc_w3, gc_b3, adaptive_range):
        import jax, jax.numpy as jnp
        import numpy as np
        B, S, DIM = (4, 512, 128)
        BASE_COUPLING = 0.1
        NUM_CYCLES = 3

        def _gelu(x):
            return jax.nn.gelu(x, approximate=False)

        def _coupling_net(h, w1, b1, w2, b2, w3, b3, w4, b4):
            h = _gelu(h @ w1 + b1)
            h = _gelu(h @ w2 + b2)
            h = _gelu(h @ w3 + b3)
            return jax.nn.sigmoid(h @ w4 + b4)

        def _global_net(h, w1, b1, w2, b2, w3, b3):
            h = _gelu(h @ w1 + b1)
            h = _gelu(h @ w2 + b2)
            return jax.nn.sigmoid(h @ w3 + b3)

        def _twist(x):
            o_r, o_i, p_r, p_i = jnp.split(x, 4, axis=-1)
            return jnp.concatenate([p_r, -p_i, -o_r, o_i], axis=-1)
        global_context = x.mean(axis=1, keepdims=True)
        gf = _global_net(global_context, gc_w1, gc_b1, gc_w2, gc_b2, gc_w3, gc_b3)
        out = x
        for _ in range(NUM_CYCLES):
            tf = _coupling_net(out, cn_w1, cn_b1, cn_w2, cn_b2, cn_w3, cn_b3, cn_w4, cn_b4)
            combined = 0.7 * gf + 0.3 * tf
            coupling = BASE_COUPLING + adaptive_range * (combined - 0.5) * 2.0
            out = out + coupling * _twist(out)
        return out

    def _L1_attn_a_ref(x, Wd_q_w, Wd_q_b, Wu_q_w, Wu_q_b, Wq_r_w, Wq_r_b, Wk_r_w, Wk_r_b, Wd_kv_w, Wd_kv_b, Wu_k_w, Wu_k_b, Wu_v_w, Wu_v_b, Wo_w, Wo_b):
        import jax, jax.numpy as jnp
        import numpy as np
        NUM_HEAD = 16
        D_Q = 64
        D_KV = 64
        ROPE_BASE = 10000.0

        def _cos_sin(seq_len, dim):
            pos = jnp.arange(seq_len, dtype=jnp.float32)[:, None]
            ids = jnp.arange(dim // 2, dtype=jnp.float32)
            theta = ROPE_BASE ** (-2.0 * ids) / (dim // 2)
            r = pos * theta[None, :]
            return (jnp.cos(r), jnp.sin(r))

        def _rope(x, cos, sin):
            b, s, d = x.shape
            xv = x.reshape(b, s, d // 2, 2)
            x0, x1 = (xv[..., 0], xv[..., 1])
            out = jnp.stack([x0 * cos - x1 * sin, x1 * cos + x0 * sin], axis=-1)
            return out.reshape(b, s, d)
        b, s, d_model = x.shape
        h = NUM_HEAD
        hd = d_model // h
        scale = jnp.sqrt(jnp.float32(h + D_KV + D_Q))

        def heads(t):
            return t.reshape(b, s, h, hd).transpose(0, 2, 1, 3)
        cos, sin = _cos_sin(s, d_model)
        ct_q = x @ Wd_q_w + Wd_q_b
        qt_c = heads(ct_q @ Wu_q_w + Wu_q_b)
        qt_r = heads(_rope(ct_q @ Wq_r_w + Wq_r_b, cos, sin))
        query = qt_c + qt_r
        ct_kv = x @ Wd_kv_w + Wd_kv_b
        kt_c = heads(ct_kv @ Wu_k_w + Wu_k_b)
        kt_r = heads(_rope(x @ Wk_r_w + Wk_r_b, cos, sin))
        key = kt_c + kt_r
        value = heads(ct_kv @ Wu_v_w + Wu_v_b)
        attn = jnp.einsum('bhqd,bhkd->bhqk', query, key) / scale
        attn = jax.nn.softmax(attn, axis=-1)
        out = jnp.einsum('bhqk,bhkd->bhqd', attn, value)
        out = out.transpose(0, 2, 1, 3).reshape(b, s, d_model)
        return out @ Wo_w + Wo_b

    def _L1_attn_b_ref(u, A_log, D_skip, dt_proj_w, dt_proj_b, x_proj_w):
        import jax, jax.numpy as jnp
        import numpy as np
        import math
        D_MODEL = 128
        D_STATE = 16
        DT_RANK = 64
        BATCH = 4
        SEQLEN = 256
        xp = jnp.einsum('bld,kd->blk', u, x_proj_w)
        dlow = xp[..., :DT_RANK]
        Bm = xp[..., DT_RANK:DT_RANK + D_STATE]
        Cm = xp[..., DT_RANK + D_STATE:]
        delta = jax.nn.softplus(jnp.einsum('blr,dr->bld', dlow, dt_proj_w) + dt_proj_b)
        A = -jnp.exp(A_log)

        def step(h, xs):
            dt, b_t, c_t, u_t = xs
            dA = jnp.exp(dt[..., None] * A)
            dB = dt[..., None] * b_t[:, None, :]
            h = dA * h + dB * u_t[..., None]
            y_t = jnp.sum(h * c_t[:, None, :], axis=-1)
            return (h, y_t)
        h0 = jnp.zeros((u.shape[0], D_MODEL, D_STATE), dtype=u.dtype)
        xs = (jnp.moveaxis(delta, 1, 0), jnp.moveaxis(Bm, 1, 0), jnp.moveaxis(Cm, 1, 0), jnp.moveaxis(u, 1, 0))
        _, ys = jax.lax.scan(step, h0, xs)
        y = jnp.moveaxis(ys, 0, 1)
        return y + u * D_skip[None, None, :]

    def _L1_ffn_ref(hidden_states, gate_w, Wg, Wu, Wd, Sg, Su, Sd):
        import jax, jax.numpy as jnp
        import numpy as np
        E = 16
        F_C = 2.0
        D = 128
        I = 4 * D
        IS = 2 * D
        B, S = (4, 128)
        b, s, d = hidden_states.shape
        T = b * s
        C = int(T * F_C / E)
        flat_x = hidden_states.reshape(T, d)
        logits = flat_x @ gate_w.T
        scores = jax.nn.softmax(logits, axis=-1).T
        topk_weight, topk_idx = jax.lax.top_k(scores, C)
        xg = flat_x[topk_idx]
        g = jnp.einsum('ecd,eid->eci', xg, Wg)
        u = jnp.einsum('ecd,eid->eci', xg, Wu)
        h = jax.nn.gelu(g, approximate=False) * u
        eo = jnp.einsum('eci,edi->ecd', h, Wd)
        eo = eo * topk_weight[..., None]
        flat_out = jnp.zeros_like(flat_x).at[topk_idx.reshape(-1)].add(eo.reshape(-1, d))
        out = flat_out.reshape(b, s, d)
        sg = hidden_states @ Sg.T
        su = hidden_states @ Su.T
        shared = jax.nn.gelu(sg, approximate=False) * su @ Sd.T
        return out + shared

    def _L2_attn_a_ref(x, W_disp, W_val, rel_pos_emb, strain_fused_w, strain_fused_b, pos_proj_w, bond_out_w, damage_out_w, damage_out_b, c_proj_w):
        import jax, jax.numpy as jnp
        import numpy as np
        B, T, C = (2, 256, 128)
        NH = 16
        HS = C // NH
        BD = max(HS // 4, 16)
        HORIZON = 64
        Bx, Tx, Cx = x.shape
        delta = min(HORIZON, Tx)
        gelu = lambda t: jax.nn.gelu(t, approximate=False)
        disp = (x @ W_disp.T).reshape(Bx, Tx, NH, BD).transpose(0, 2, 1, 3)
        val = (x @ W_val.T).reshape(Bx, Tx, NH, HS).transpose(0, 2, 1, 3)
        pad = ((0, 0), (0, 0), (delta - 1, 0), (0, 0))
        idx = jnp.arange(Tx)[:, None] + jnp.arange(delta)[None, :]
        disp_win = jnp.pad(disp, pad)[:, :, idx, :]
        strain = disp_win - disp[:, :, :, None, :]
        fused = strain @ strain_fused_w.T + strain_fused_b
        bond_feats, damage_feats = (fused[..., :BD], fused[..., BD:])
        pos_feat = rel_pos_emb[:delta] @ pos_proj_w.T
        bond_logits = (gelu(bond_feats + pos_feat) @ bond_out_w.T)[..., 0]
        damage = jax.nn.sigmoid((gelu(damage_feats) @ damage_out_w.T)[..., 0] + damage_out_b)
        logits = bond_logits - damage * 10.0
        cmask = jnp.arange(Tx)[:, None] - delta + 1 + jnp.arange(delta)[None, :] >= 0
        logits = jnp.where(cmask, logits, -jnp.inf)
        weights = jax.nn.softmax(logits, axis=-1)
        val_win = jnp.pad(val, pad)[:, :, idx, :]
        out = jnp.einsum('bhtw,bhtwd->bhtd', weights, val_win)
        out = out.transpose(0, 2, 1, 3).reshape(Bx, Tx, Cx)
        return out @ c_proj_w.T

    def _L2_attn_b_ref(x, Wq, bq, Wk, bk, Wv, bv, Wo, bo):
        import jax, jax.numpy as jnp
        import numpy as np
        B, S, D = (4, 256, 128)
        GAMMA = 1.0
        q = x @ Wq + bq
        k = x @ Wk + bk
        v = x @ Wv + bv
        q_sq = jnp.sum(q * q, axis=-1)
        k_sq = jnp.sum(k * k, axis=-1)
        qk = jnp.einsum('bqd,bkd->bqk', q, k)
        dist_sq = q_sq[:, :, None] + k_sq[:, None, :] - 2.0 * qk
        scores = jnp.exp(-GAMMA * dist_sq)
        attn = jax.nn.softmax(scores, axis=-1)
        out = jnp.einsum('bqk,bkd->bqd', attn, v)
        return out @ Wo + bo

    def _L2_ffn_ref(x, router_w, w1, w2):
        import jax, jax.numpy as jnp
        import numpy as np
        B, S, H, E, K = (4, 256, 128, 8, 2)
        bsz, seq, hidden = x.shape
        n_experts = w1.shape[0]
        tokens = x.reshape(-1, hidden)
        T = tokens.shape[0]
        logits = tokens @ router_w.T
        topv, topi = jax.lax.top_k(logits, K)
        w = jax.nn.softmax(topv, axis=-1).astype(tokens.dtype)
        gate = jnp.zeros((T, n_experts), tokens.dtype).at[jnp.arange(T)[:, None], topi].add(w)
        out = jnp.zeros_like(tokens)
        for e in range(n_experts):
            h = jax.nn.gelu(tokens @ w1[e].T, approximate=False)
            y = h @ w2[e].T
            out = out + gate[:, e:e + 1] * y
        return out.reshape(bsz, seq, hidden)

    def _L3_attn_a_ref(x, Wq, bq, Wk, bk, Wv, bv, proj):
        import jax, jax.numpy as jnp
        import numpy as np
        B, S, E, H, Dh = (2, 256, 128, 16, 64)
        b, s, e = x.shape
        h, dh, _ = Wq.shape
        scale = jnp.sqrt(jnp.asarray(dh, x.dtype))
        q = jnp.einsum('bse,hde->bhsd', x, Wq) + bq[None, :, None, :]
        k = jnp.einsum('bse,hde->bhsd', x, Wk) + bk[None, :, None, :]
        v = jnp.einsum('bse,hde->bhsd', x, Wv) + bv[None, :, None, :]
        causal = jnp.triu(jnp.ones((s, s), bool), 1)
        scores = jnp.einsum('bhsd,bhtd->bhst', q, k) / scale
        scores = jnp.where(causal[None, None], -jnp.inf, scores)
        att = jax.nn.softmax(scores, axis=-1) / scale
        z = jnp.einsum('bhst,bhtd->bhsd', att, v)
        z = z.reshape(b, s, h * dh)
        return z @ proj

    def _L3_attn_b_ref(x, W_z, W_params, conv_w, W_dt, b_dt, A_log, D, W_out):
        import jax, jax.numpy as jnp
        import numpy as np
        import math
        E, N, K, R = (128, 16, 4, 64)
        B, L = (2, 256)
        b, l, e = x.shape
        n = A_log.shape[1]
        r = W_dt.shape[1]
        k = conv_w.shape[-1]
        z = x @ W_z.T
        params = x @ W_params.T
        dt_unproj = params[..., :r]
        C_proj = params[..., r + n:]
        dt = jax.nn.softplus(dt_unproj @ W_dt.T + b_dt)
        xc = jax.lax.conv_general_dilated(x.transpose(0, 2, 1), conv_w, (1,), [(k - 1, 0)], dimension_numbers=('NCH', 'OIH', 'NCH'), feature_group_count=e)
        u = jax.nn.silu(xc.transpose(0, 2, 1))
        A = -jnp.exp(A_log)
        A_tilde = jnp.exp(dt[..., None] * A[None, None])
        B_tilde = jnp.where(jnp.abs(A)[None, None] < 1e-05, dt[..., None], (A_tilde - 1.0) / (A[None, None] + 1e-10))
        h0 = B_tilde[:, 0] * u[:, 0, :, None]

        def step(h, inp):
            a, bt, uu = inp
            h_new = a * h + bt * uu[..., None]
            return (h_new, h_new)
        xs = (A_tilde[:, :-1].transpose(1, 0, 2, 3), B_tilde[:, :-1].transpose(1, 0, 2, 3), u[:, :-1].transpose(1, 0, 2))
        _, hs = jax.lax.scan(step, h0, xs)
        h = jnp.concatenate([h0[None], hs], axis=0).transpose(1, 0, 2, 3)
        y = jnp.einsum('bln,blen->ble', C_proj, h)
        y_ssm = y + u * D
        y_gated = y_ssm * jax.nn.silu(z)
        return y_gated @ W_out.T

    def _L3_ffn_ref(x, router_w, correction_bias, up_w, down_w, shared_up_w, shared_down_w):
        import jax, jax.numpy as jnp
        import numpy as np
        H = 128
        E = 64
        K = 8
        G = 8
        TOPK_GROUP = 4
        I_MOE = 64
        I_SHARED = 256
        SCALE = 2.5

        def relu2(x):
            return jnp.square(jax.nn.relu(x))

        def _route(xf, router_w, correction_bias):
            T = xf.shape[0]
            logits = xf @ router_w.T
            scores = jax.nn.sigmoid(logits)
            sfc = scores + correction_bias[None, :]
            grp = sfc.reshape(T, G, E // G)
            top2, _ = jax.lax.top_k(grp, 2)
            group_scores = top2.sum(-1)
            _, gidx = jax.lax.top_k(group_scores, TOPK_GROUP)
            gmask = jnp.zeros((T, G), sfc.dtype).at[jnp.arange(T)[:, None], gidx].set(1.0)
            emask = jnp.repeat(gmask, E // G, axis=1)
            masked = jnp.where(emask > 0, sfc, 0.0)
            _, tidx = jax.lax.top_k(masked, K)
            tw = jnp.take_along_axis(scores, tidx, axis=1)
            tw = tw / (tw.sum(-1, keepdims=True) + 1e-20)
            return (tidx, tw * SCALE)
        B, S, Hd = x.shape
        xf = x.reshape(-1, Hd)
        T = xf.shape[0]
        tidx, tw = _route(xf.astype(jnp.float32), router_w, correction_bias)
        combine = jnp.zeros((T, E), xf.dtype).at[jnp.arange(T)[:, None], tidx].add(tw.astype(xf.dtype))

        def body(acc, ew):
            wu, wd, c = ew
            return (acc + c[:, None] * (relu2(xf @ wu) @ wd), None)
        routed, _ = jax.lax.scan(body, jnp.zeros_like(xf), (up_w, down_w, combine.T))
        shared = relu2(xf @ shared_up_w) @ shared_down_w
        return (routed + shared).reshape(B, S, Hd)
    x = L0_attn_a_x
    x = x + _L0_attn_a_ref(_layernorm(x, axis=-1), L0_attn_a_Wd_q_w, L0_attn_a_Wd_q_b, L0_attn_a_Wu_q_w, L0_attn_a_Wu_q_b, L0_attn_a_Wq_r_w, L0_attn_a_Wq_r_b, L0_attn_a_Wk_r_w, L0_attn_a_Wk_r_b, L0_attn_a_Wd_kv_w, L0_attn_a_Wd_kv_b, L0_attn_a_Wu_k_w, L0_attn_a_Wu_k_b, L0_attn_a_Wu_v_w, L0_attn_a_Wu_v_b, L0_attn_a_Wo_w, L0_attn_a_Wo_b)
    x = x + _L0_ffn_ref(_layernorm(x, axis=-1), L0_ffn_cn_w1, L0_ffn_cn_b1, L0_ffn_cn_w2, L0_ffn_cn_b2, L0_ffn_cn_w3, L0_ffn_cn_b3, L0_ffn_cn_w4, L0_ffn_cn_b4, L0_ffn_gc_w1, L0_ffn_gc_b1, L0_ffn_gc_w2, L0_ffn_gc_b2, L0_ffn_gc_w3, L0_ffn_gc_b3, L0_ffn_adaptive_range)
    x = x + _L0_attn_b_ref(_layernorm(x, axis=-1), L0_attn_b_Wqkv, L0_attn_b_Wg, L0_attn_b_bg, L0_attn_b_Wp, L0_attn_b_bp)
    x = x + _L0_ffn_ref(_layernorm(x, axis=-1), L0_ffn_cn_w1, L0_ffn_cn_b1, L0_ffn_cn_w2, L0_ffn_cn_b2, L0_ffn_cn_w3, L0_ffn_cn_b3, L0_ffn_cn_w4, L0_ffn_cn_b4, L0_ffn_gc_w1, L0_ffn_gc_b1, L0_ffn_gc_w2, L0_ffn_gc_b2, L0_ffn_gc_w3, L0_ffn_gc_b3, L0_ffn_adaptive_range)
    x = x + _L1_attn_a_ref(_layernorm(x, axis=-1), L1_attn_a_Wd_q_w, L1_attn_a_Wd_q_b, L1_attn_a_Wu_q_w, L1_attn_a_Wu_q_b, L1_attn_a_Wq_r_w, L1_attn_a_Wq_r_b, L1_attn_a_Wk_r_w, L1_attn_a_Wk_r_b, L1_attn_a_Wd_kv_w, L1_attn_a_Wd_kv_b, L1_attn_a_Wu_k_w, L1_attn_a_Wu_k_b, L1_attn_a_Wu_v_w, L1_attn_a_Wu_v_b, L1_attn_a_Wo_w, L1_attn_a_Wo_b)
    x = x + _L1_ffn_ref(_layernorm(x, axis=-1), L1_ffn_gate_w, L1_ffn_Wg, L1_ffn_Wu, L1_ffn_Wd, L1_ffn_Sg, L1_ffn_Su, L1_ffn_Sd)
    x = x + _L1_attn_b_ref(_layernorm(x, axis=-1), L1_attn_b_A_log, L1_attn_b_D_skip, L1_attn_b_dt_proj_w, L1_attn_b_dt_proj_b, L1_attn_b_x_proj_w)
    x = x + _L1_ffn_ref(_layernorm(x, axis=-1), L1_ffn_gate_w, L1_ffn_Wg, L1_ffn_Wu, L1_ffn_Wd, L1_ffn_Sg, L1_ffn_Su, L1_ffn_Sd)
    x = x + _L2_attn_a_ref(_layernorm(x, axis=-1), L2_attn_a_W_disp, L2_attn_a_W_val, L2_attn_a_rel_pos_emb, L2_attn_a_strain_fused_w, L2_attn_a_strain_fused_b, L2_attn_a_pos_proj_w, L2_attn_a_bond_out_w, L2_attn_a_damage_out_w, L2_attn_a_damage_out_b, L2_attn_a_c_proj_w)
    x = x + _L2_ffn_ref(_layernorm(x, axis=-1), L2_ffn_router_w, L2_ffn_w1, L2_ffn_w2)
    x = x + _L2_attn_b_ref(_layernorm(x, axis=-1), L2_attn_b_Wq, L2_attn_b_bq, L2_attn_b_Wk, L2_attn_b_bk, L2_attn_b_Wv, L2_attn_b_bv, L2_attn_b_Wo, L2_attn_b_bo)
    x = x + _L2_ffn_ref(_layernorm(x, axis=-1), L2_ffn_router_w, L2_ffn_w1, L2_ffn_w2)
    x = x + _L3_attn_a_ref(_layernorm(x, axis=-1), L3_attn_a_Wq, L3_attn_a_bq, L3_attn_a_Wk, L3_attn_a_bk, L3_attn_a_Wv, L3_attn_a_bv, L3_attn_a_proj)
    x = x + _L3_ffn_ref(_layernorm(x, axis=-1), L3_ffn_router_w, L3_ffn_correction_bias, L3_ffn_up_w, L3_ffn_down_w, L3_ffn_shared_up_w, L3_ffn_shared_down_w)
    x = x + _L3_attn_b_ref(_layernorm(x, axis=-1), L3_attn_b_W_z, L3_attn_b_W_params, L3_attn_b_conv_w, L3_attn_b_W_dt, L3_attn_b_b_dt, L3_attn_b_A_log, L3_attn_b_D, L3_attn_b_W_out)
    x = x + _L3_ffn_ref(_layernorm(x, axis=-1), L3_ffn_router_w, L3_ffn_correction_bias, L3_ffn_up_w, L3_ffn_down_w, L3_ffn_shared_up_w, L3_ffn_shared_down_w)
    return x

_drawn_inputs = setup_inputs


def setup_inputs(seed=0):
    import zlib

    import numpy as np

    out = dict(_drawn_inputs(seed))
    spreads = {'L0_attn_a_Wd_q_b': (0.0, 0.8),
     'L0_attn_a_Wu_q_b': (0.0, 0.8),
     'L0_attn_a_Wq_r_b': (0.0, 0.8),
     'L0_attn_a_Wk_r_b': (0.0, 0.8),
     'L0_attn_a_Wd_kv_b': (0.0, 0.74),
     'L0_attn_a_Wu_k_b': (0.0, 2.0),
     'L0_attn_a_Wu_v_b': (0.0, 0.1),
     'L0_attn_a_Wo_b': (0.0, 0.1),
     'L0_attn_b_bg': (0.0, 0.8),
     'L0_attn_b_bp': (0.0, 0.1),
     'L0_ffn_cn_b1': (0.0, 0.8),
     'L0_ffn_cn_b2': (0.0, 0.8),
     'L0_ffn_cn_b3': (0.0, 0.8),
     'L0_ffn_gc_b1': (0.0, 2.0),
     'L0_ffn_gc_b2': (0.0, 2.0),
     'L1_attn_a_Wd_q_b': (0.0, 0.8),
     'L1_attn_a_Wu_q_b': (0.0, 0.8),
     'L1_attn_a_Wq_r_b': (0.0, 0.8),
     'L1_attn_a_Wk_r_b': (0.0, 0.8),
     'L1_attn_a_Wd_kv_b': (0.0, 0.8),
     'L1_attn_a_Wu_k_b': (0.0, 2.0),
     'L1_attn_a_Wu_v_b': (0.0, 0.501),
     'L1_attn_a_Wo_b': (0.0, 0.1),
     'L1_attn_b_D_skip': (1.0, 0.2),
     'L1_attn_b_dt_proj_b': (0.0, 0.1),
     'L2_attn_a_strain_fused_b': (0.0, 0.8),
     'L3_attn_b_b_dt': (-6.907255172729492, 0.6),
     'L3_attn_b_D': (1.0, 0.6)}
    factors = {'L0_attn_a_Wd_q_w': 8.0,
     'L0_attn_a_Wu_q_w': 8.0,
     'L0_attn_a_Wq_r_w': 8.0,
     'L0_attn_a_Wk_r_w': 8.0,
     'L0_attn_a_Wd_kv_w': 8.0,
     'L0_attn_a_Wu_k_w': 8.0,
     'L0_attn_a_Wu_v_w': 5.945,
     'L0_attn_b_Wg': 8.0,
     'L0_ffn_cn_w1': 3.144,
     'L0_ffn_cn_w2': 3.057,
     'L0_ffn_gc_w1': 6.332,
     'L0_ffn_gc_w2': 6.629,
     'L0_ffn_gc_w3': 40.744,
     'L1_attn_a_Wd_q_w': 8.0,
     'L1_attn_a_Wu_q_w': 8.0,
     'L1_attn_a_Wq_r_w': 8.0,
     'L1_attn_a_Wk_r_w': 8.0,
     'L1_attn_a_Wd_kv_w': 8.0,
     'L1_attn_a_Wu_k_w': 8.0,
     'L1_attn_a_Wu_v_w': 8.0,
     'L1_attn_a_Wo_w': 3.733,
     'L1_ffn_gate_w': 8.0,
     'L1_ffn_Wg': 8.0,
     'L1_ffn_Wu': 8.0,
     'L1_ffn_Wd': 8.0,
     'L1_ffn_Sg': 7.078,
     'L1_ffn_Su': 7.548,
     'L1_ffn_Sd': 7.171,
     'L2_attn_a_W_disp': 8.0,
     'L2_attn_a_W_val': 8.0,
     'L2_attn_a_rel_pos_emb': 8.0,
     'L2_attn_a_strain_fused_w': 8.0,
     'L2_attn_a_pos_proj_w': 21.532,
     'L2_attn_a_bond_out_w': 8.0,
     'L2_attn_a_damage_out_w': 8.0,
     'L2_attn_a_c_proj_w': 8.0,
     'L2_attn_b_bv': 8.0,
     'L2_attn_b_bo': 8.0,
     'L3_attn_a_Wq': 8.0,
     'L3_attn_a_bq': 8.0,
     'L3_attn_a_Wk': 8.0,
     'L3_attn_a_bk': 64.0,
     'L3_attn_a_Wv': 8.0,
     'L3_attn_a_bv': 8.0,
     'L3_attn_a_proj': 8.0,
     'L3_attn_b_W_params': 5.023,
     'L3_attn_b_W_dt': 8.0,
     'L3_attn_b_A_log': 8.0,
     'L3_ffn_router_w': 8.0,
     'L3_ffn_correction_bias': 8.0,
     'L3_ffn_up_w': 8.0,
     'L3_ffn_down_w': 8.0,
     'L3_ffn_shared_up_w': 8.0,
     'L3_ffn_shared_down_w': 8.0}
    for name, (base, spread) in spreads.items():
        noise = np.random.default_rng([zlib.crc32(name.encode()), seed]).standard_normal(out[name].shape)
        drawn = base * np.exp(spread * noise) if base else spread * noise
        out[name] = jnp.asarray(drawn.astype(out[name].dtype))
    for name, factor in factors.items():
        out[name] = (out[name] * factor).astype(out[name].dtype)
    return out
```

```python
from contextlib import ExitStack

import numpy as np
import concourse.bass as bass
from concourse import mybir

F32 = mybir.dt.float32
I32 = mybir.dt.int32
U8 = mybir.dt.uint8
ALU = mybir.AluOpType
ACT = mybir.ActivationFunctionType
AX = mybir.AxisListType

P = 128
D = 128
BATCH = 16
SEQ = 256
TOK = BATCH * SEQ
TILES = TOK // P
HEADS = 16
LN_EPS = 1e-5
BANK = 512
NEG = -1.0e30


def bc(ap, at, n):
    x = ap.unsqueeze(at)
    return x.broadcast_to([*x.shape[:at], n, *x.shape[at + 1:]])


class Chain:

    def __init__(self, eng, sem, start=0):
        self.eng, self.sem, self.start, self.n = eng, sem, start, 0

    def link(self, ins):
        self.n += 1
        ins.then_inc(self.sem, 1)
        self.eng.wait_ge(self.sem, self.start + self.n)


class Core:

    def __init__(self, nc, ctx):
        self.nc = nc
        sb = lambda name, shape, dt=F32: ctx.enter_context(nc.sbuf_tensor(name, shape, dt))
        self.x_res = sb("x_res", [P, TILES, D])
        self.xn = sb("xn", [P, TILES, D])
        self.xnT = sb("xnT", [P, TOK])
        self.rstd = sb("rstd", [P, TILES])
        self.ident = sb("ident", [P, P])
        self.ones = sb("ones", [P, P])
        self.n = 0


class Stage:

    def __init__(self, core, name):
        self.core, self.nc = core, core.nc
        core.n += 1
        self.name = f"{name}{core.n}"
        self.ctx = ExitStack()
        self.sems = []

    def __enter__(self):
        self.ctx.__enter__()
        return self

    def __exit__(self, *e):
        self.nc.clear_and_free_semaphores(self.sems)
        self.nc.all_engine_barrier()
        return self.ctx.__exit__(*e)

    def sb(self, name, shape, dt=F32):
        return self.ctx.enter_context(self.nc.sbuf_tensor(f"{self.name}_{name}", shape, dt))

    def ps(self, name, shape, dt=F32):
        return self.ctx.enter_context(self.nc.psum_tensor(f"{self.name}_{name}", shape, dt))

    def sem(self, name):
        s = self.nc.alloc_semaphore(name=f"{self.name}_{name}")
        self.sems.append(s)
        return s

    def weights(self, blob, offsets):
        self.blob = blob
        self.w_sb = self.sb("w", [P, blob.shape[1]])
        return {k: self.w_sb[:, a:b] for k, (a, b) in offsets.items()}


def load_constants(core, ident_dram, x_dram):
    nc = core.nc
    with Stage(core, "init") as st:
        loaded = st.sem("loaded")
        with nc.Block() as block:
            @block.sync
            def _(sp):
                sp.dma_start(core.x_res[:, :, :], x_dram.rearrange("(t p) d -> p t d", p=P)).then_inc(loaded, 16)
                sp.dma_start(core.ident[:, :], ident_dram).then_inc(loaded, 16)
                sp.wait_ge(loaded, 32)

            @block.gpsimd
            def _(pool):
                nc.gpsimd.memset(core.ones[:, :], 1.0)


def store_output(core, out_dram):
    nc = core.nc
    with Stage(core, "store") as st:
        stored = st.sem("stored")
        with nc.Block() as block:
            @block.sync
            def _(sp):
                sp.dma_start(out_dram.rearrange("(t p) d -> p t d", p=P), core.x_res[:, :, :]).then_inc(stored, 16)
                sp.wait_ge(stored, 16)


def layer_norm(core, weights_stage=None):
    nc = core.nc
    GROUPS = TILES // 4
    with Stage(core, "ln") as st:
        sq = st.sb("sq", [P, TILES, D])
        mean = st.sb("mean", [P, TILES])
        var = st.sb("var", [P, TILES])
        rstd = core.rstd
        staged = st.sb("staged", [P, 2, 4, D])
        pT = [st.ps(f"pT{i}", [P, BANK]) for i in range(2)]
        w_loaded = st.sem("w_loaded")
        dve = st.sem("dve")
        centred = st.sem("centred")
        squared = st.sem("squared")
        var_ready = st.sem("var_ready")
        std_ready = st.sem("std_ready")
        norm_ready = st.sem("norm_ready")
        turned = st.sem("turned")
        xnT_ready = st.sem("xnT_ready")
        with nc.Block() as block:
            if weights_stage is not None:
                @block.sync
                def _(sp):
                    sp.dma_start(weights_stage.w_sb[:, :], weights_stage.blob).then_inc(w_loaded, 16)
                    sp.wait_ge(w_loaded, 16)

            @block.vector
            def _(v):
                c = Chain(v, dve)
                c.link(nc.vector.tensor_reduce(mean[:, :], core.x_res[:, :, :], AX.X, ALU.add))
                c.link(nc.vector.tensor_scalar(mean[:, :], mean[:, :], 1.0 / D, None, ALU.mult))
                nc.vector.tensor_tensor(core.xn[:, :, :], core.x_res[:, :, :], bc(mean[:, :], 2, D),
                                        ALU.subtract).then_inc(centred, 1)
                v.wait_ge(squared, 1)
                c.link(nc.vector.tensor_reduce(var[:, :], sq[:, :, :], AX.X, ALU.add))
                nc.vector.tensor_scalar(var[:, :], var[:, :], 1.0 / D, LN_EPS, ALU.mult, ALU.add).then_inc(var_ready, 1)
                v.wait_ge(std_ready, 1)
                c.link(nc.vector.reciprocal(rstd[:, :], rstd[:, :]))
                v.sem_inc(turned, 2)
                with v.Fori(0, GROUPS // 2) as g:
                    for i in range(2):
                        tiles = bass.ds(g * 8 + 4 * i, 4)
                        v.wait_ge(turned, 2 * g + i + 1)
                        nc.vector.tensor_tensor(staged[:, i, :, :], core.xn[:, tiles, :], bc(rstd[:, tiles], 2, D),
                                                ALU.mult).then_inc(norm_ready, 1)

            @block.scalar
            def _(a):
                a.wait_ge(centred, 1)
                nc.scalar.activation(sq[:, :, :], core.xn[:, :, :], ACT.Square).then_inc(squared, 1)
                a.wait_ge(var_ready, 1)
                nc.scalar.activation(rstd[:, :], var[:, :], ACT.Sqrt).then_inc(std_ready, 1)
                with a.Fori(0, GROUPS // 2) as g:
                    for i in range(2):
                        a.wait_ge(turned, 2 * g + i + 3)
                        nc.scalar.copy(core.xnT[:, bass.ds(g * 2 * BANK + i * BANK, BANK)], pT[i][:, :]).then_inc(xnT_ready, 1)

            @block.tensor
            def _(pe):
                pe.sem_inc(xnT_ready, 2)
                with pe.Fori(0, GROUPS // 2) as g:
                    for i in range(2):
                        pe.wait_ge(norm_ready, 2 * g + i + 1)
                        pe.wait_ge(xnT_ready, 2 * g + i + 1)
                        for k in range(4):
                            ins = nc.tensor.transpose(pT[i][:, k * P:(k + 1) * P],
                                                      staged[:, i, k, :], core.ident[:, :])
                        ins.then_inc(turned, 1)


ROPE_BASE = 10000.0
ATTN_A_HD = D // HEADS
LOW = 64
PER = 32 // ATTN_A_HD
QUADS = HEADS // PER
LEAD = 3


def pack(parts):
    offsets, cols, at = {}, [], 0
    for name, a in parts:
        a = np.asarray(a)
        if a.ndim == 1:
            a = a[:, None]
        full = np.zeros((P, a.shape[1]), a.dtype)
        full[:a.shape[0]] = a
        cols.append(full)
        offsets[name] = (at, at + a.shape[1])
        at += a.shape[1]
    return np.concatenate(cols, axis=1), offsets


def rope_tables():
    ids = np.arange(D // 2, dtype=np.float32)
    theta = (np.float32(ROPE_BASE) ** (np.float32(-2.0) * ids) / np.float32(D // 2)).astype(np.float32)
    r = np.arange(SEQ, dtype=np.float32)[:, None] * theta[None, :]
    cos = np.repeat(np.cos(r), 2, axis=1).T
    sin = np.repeat(np.sin(r), 2, axis=1).T.copy()
    sin[0::2] *= -1
    return cos.astype(np.float32), sin.astype(np.float32)


def attn_a_weights(w):
    swap = np.arange(D) ^ 1
    cos, sin = rope_tables()
    low = lambda a: np.concatenate([np.zeros((LOW, a.shape[1]), a.dtype), a], axis=0)
    scale = np.float32(1.0 / np.sqrt(HEADS + LOW + LOW))
    head_of = np.arange(P) // ATTN_A_HD
    quad_in_32 = np.arange(32) // ATTN_A_HD
    own = (quad_in_32[None, :] == np.arange(QUADS)[:, None]).astype(np.float32)
    wo = w["Wo_w"].reshape(QUADS, PER, ATTN_A_HD, D).transpose(1, 0, 2, 3).reshape(D, D)
    return pack([
        ("down", np.concatenate([w["Wd_q_w"], w["Wd_kv_w"]], axis=1)),
        ("down_b", np.concatenate([w["Wd_q_b"], w["Wd_kv_b"]])),
        ("uq", w["Wu_q_w"]), ("qr", w["Wq_r_w"]), ("qr_swap", w["Wq_r_w"][:, swap]),
        ("uk", low(w["Wu_k_w"])), ("uv", low(w["Wu_v_w"])),
        ("kr", w["Wk_r_w"]), ("kr_swap", w["Wk_r_w"][:, swap]),
        ("uq_b", w["Wu_q_b"]), ("qr_b", w["Wq_r_b"]), ("qr_swap_b", w["Wq_r_b"][swap]),
        ("uk_b", w["Wu_k_b"]), ("kr_b", w["Wk_r_b"]), ("kr_swap_b", w["Wk_r_b"][swap]),
        ("uv_b", np.broadcast_to(w["Wu_v_b"], (P, D))),
        ("wo", wo), ("wo_b", w["Wo_b"][None, :]),
        ("cos_q", cos * scale), ("sin_q", sin * scale), ("cos_k", cos), ("sin_k", sin),
        ("head_mask", (head_of[:, None] == np.arange(HEADS)[None, :]).astype(np.float32)),
        ("own", np.broadcast_to(own.reshape(1, -1), (P, QUADS * 32))),
    ])


def attn_a(core, blob, offsets):
    nc = core.nc
    scale = float(np.float32(1.0 / np.sqrt(HEADS + LOW + LOW)))
    with Stage(core, "attn_a") as st:
        w = st.weights(blob, offsets)
        layer_norm(core, st)
        qT = st.sb("qT", [P, TOK])
        kT = st.sb("kT", [P, TOK])
        val = st.sb("val", [P, TILES, D])
        bank = [st.ps(f"bank{i}", [P, BANK]) for i in range(8)]

        ct = st.sb("ct", [P, BANK])
        plain = st.sb("plain", [P, BANK])
        rot = [st.sb(f"rot{i}", [P, BANK]) for i in range(4)]
        down_ready, ct_ready = st.sem("down_ready"), st.sem("ct_ready")
        q_ready, k_ready, v_ready = st.sem("q_ready"), st.sem("k_ready"), st.sem("v_ready")
        plain_ready, plain_used = st.sem("plain_ready"), st.sem("plain_used")
        group_done, dve1 = st.sem("group_done"), st.sem("dve1")
        pd, pq, pqr, pqs, pk, pkr, pks, pv = bank
        GROUPS = TOK // BANK
        with nc.Block() as block:
            @block.tensor
            def _(pe):
                with pe.Fori(0, GROUPS) as g:
                    x = core.xnT[:, bass.ds(g * BANK, BANK)]
                    nc.tensor.matmul(pd[:, :], w["down"], x, start=True, stop=True).then_inc(down_ready, 1)
                    pe.wait_ge(group_done, g)
                    nc.tensor.matmul(pkr[:, :], w["kr"], x, start=True, stop=True)
                    nc.tensor.matmul(pks[:, :], w["kr_swap"], x, start=True, stop=True)
                    pe.wait_ge(ct_ready, g + 1)
                    nc.tensor.matmul(pq[:, :], w["uq"][0:LOW, :], ct[0:LOW, :], start=True, stop=True)
                    nc.tensor.matmul(pqr[:, :], w["qr"][0:LOW, :], ct[0:LOW, :], start=True, stop=True)
                    nc.tensor.matmul(pqs[:, :], w["qr_swap"][0:LOW, :], ct[0:LOW, :], start=True, stop=True).then_inc(q_ready, 1)
                    nc.tensor.matmul(pk[:, :], w["uk"][LOW:P, :], ct[LOW:P, :], start=True, stop=True).then_inc(k_ready, 1)
                    for t in range(4):
                        ins = nc.tensor.matmul(pv[:, t * P:(t + 1) * P], ct[LOW:P, t * P:(t + 1) * P], w["uv"][LOW:P, :],
                                               start=True, stop=True)
                    ins.then_inc(v_ready, 1)

            @block.scalar
            def _(a):
                with a.Fori(0, GROUPS) as g:
                    a.wait_ge(down_ready, g + 1)
                    a.wait_ge(v_ready, g)
                    nc.scalar.activation(ct[:, :], pd[:, :], ACT.Identity, bias=w["down_b"]).then_inc(ct_ready, 1)
                    a.wait_ge(q_ready, g + 1)
                    a.wait_ge(plain_used, 2 * g)
                    nc.scalar.activation(plain[:, :], pq[:, :], ACT.Identity, bias=w["uq_b"]).then_inc(plain_ready, 1)
                    a.wait_ge(k_ready, g + 1)
                    a.wait_ge(plain_used, 2 * g + 1)
                    nc.scalar.activation(plain[:, :], pk[:, :], ACT.Identity, bias=w["uk_b"]).then_inc(plain_ready, 1)

            @block.vector
            def _(v):
                with v.Fori(0, GROUPS) as g:
                    c = Chain(v, dve1, 4 * g)
                    cols = bass.ds(g * BANK, BANK)
                    two = lambda t: t.rearrange("p (b s) -> p b s", b=2)
                    for i, (side, out, direct, swapped, s) in enumerate((("q", qT, pqr, pqs, scale), ("k", kT, pkr, pks, 1.0))):
                        v.wait_ge((q_ready, k_ready)[i], g + 1)
                        rot_a, rot_b = rot[2 * i], rot[2 * i + 1]
                        nc.vector.scalar_tensor_tensor(two(rot_a[:, :]), two(direct[:, :]), w[f"{side}r_b"],
                                                       bc(w[f"cos_{side}"], 1, 2), ALU.add, ALU.mult)
                        c.link(nc.vector.scalar_tensor_tensor(two(rot_b[:, :]), two(swapped[:, :]), w[f"{side}r_swap_b"],
                                                              bc(w[f"sin_{side}"], 1, 2), ALU.add, ALU.mult))
                        c.link(nc.vector.tensor_tensor(rot_a[:, :], rot_a[:, :], rot_b[:, :], ALU.add))
                        v.wait_ge(plain_ready, 2 * g + i + 1)
                        nc.vector.scalar_tensor_tensor(out[:, cols], plain[:, :], s, rot_a[:, :],
                                                       ALU.mult, ALU.add).then_inc(plain_used, 1)
                    v.wait_ge(v_ready, g + 1)
                    nc.vector.tensor_tensor(val[:, bass.ds(g * 4, 4), :], pv[:, :].rearrange("p (t d) -> p t d", t=4),
                                            bc(w["uv_b"], 1, 4), ALU.add).then_inc(group_done, 1)

        q_heads = st.sb("q_heads", [P, 2, HEADS, SEQ])
        k_now = st.sb("k_now", [P, 2, SEQ])
        v_heads = st.sb("v_heads", [P, 2, 2, QUADS, PER, QUADS, ATTN_A_HD])
        prob = st.sb("prob", [P, 4, 2, SEQ])
        probT = st.sb("probT", [P, 2 * PER, 2, SEQ])
        neg_max = st.sb("neg_max", [P, 4, 2])
        row_sum = st.sb("row_sum", [P, 2, 2, HEADS])
        inv_sum = st.sb("inv_sum", [P, 2, HEADS])
        inv_wide = st.sb("inv_wide", [P, 2, PER, QUADS, ATTN_A_HD])
        inv_T = st.sb("inv_T", [P, SEQ])
        outT = st.sb("outT", [P, SEQ])
        pS, pT, pO, pInv, pY = bank[0:4], bank[4:6], bank[6], bank[7][:, 0:SEQ], bank[7][:, SEQ:2 * SEQ]
        names = ("q_heads_ready", "v_heads_ready", "scores_ready", "max_ready", "prob_ready", "probT_psum", "probT_ready", "quad_done",
                 "sums_inverted", "inv_wide_ready", "inv_psum", "inv_T_ready", "outT_ready", "y_ready", "y_added")
        (q_heads_ready, v_heads_ready, scores_ready, max_ready, prob_ready, probT_psum, probT_ready, quad_done,
         sums_inverted, inv_wide_ready, inv_psum, inv_T_ready, outT_ready, y_ready, y_added) = (st.sem(n) for n in names)

        def sequences(eng, step):
            step(0, 0, True, False)
            step(1, 1, False, False)
            with eng.Fori(1, BATCH // 2 - 1) as pair:
                step(pair * 2, 0, False, False)
                step(pair * 2 + 1, 1, False, False)
            step(BATCH - 2, 0, False, False)
            step(BATCH - 1, 1, False, True)

        def known(b, below):
            return isinstance(b, int) and b < below

        with nc.Block() as block:
            @block.gpsimd
            def _(pool):
                def prepare(b, s, first, last):
                    if not known(b, 2):
                        pool.wait_ge(scores_ready, (b - 1) * HEADS)
                    nc.gpsimd.tensor_copy(k_now[:, s, :], kT[:, bass.ds(b * SEQ, SEQ)]).then_inc(q_heads_ready, 1)
                    nc.gpsimd.tensor_tensor(q_heads[:, s, :, :], bc(qT[:, bass.ds(b * SEQ, SEQ)], 1, HEADS),
                                            bc(w["head_mask"], 2, SEQ), ALU.mult).then_inc(q_heads_ready, 1)
                    if not known(b, 2):
                        pool.wait_ge(quad_done, (b - 1) * QUADS)
                    for kt in range(2):
                        for quad in range(QUADS):
                            v = val[:, bass.ds(b * 2 + kt, 1), quad * 32:(quad + 1) * 32].squeeze(1).rearrange("p (j d) -> p j d", j=PER)
                            nc.gpsimd.tensor_tensor(v_heads[:, s, kt, quad, :, :, :], bc(v, 2, QUADS),
                                                    bc(w["own"][:, quad * 32:(quad + 1) * 32].rearrange("p (i d) -> p i d", i=QUADS), 1, PER),
                                                    ALU.mult).then_inc(v_heads_ready, 1)

                sequences(pool, prepare)

            @block.tensor
            def _(pe):
                def scores(b, s, h):
                    if h == 0:
                        pe.wait_ge(q_heads_ready, 2 * b + 2)
                    for qt in range(2):
                        ins = nc.tensor.matmul(pS[h % 4][:, qt * SEQ:(qt + 1) * SEQ], q_heads[:, s, h, qt * P:(qt + 1) * P],
                                               k_now[:, s, :], start=True, stop=True)
                    ins.then_inc(scores_ready, 1)

                def turn(b, h):
                    pe.wait_ge(prob_ready, b * HEADS + h + 1)
                    if not (known(b, 1) and h < 2):
                        pe.wait_ge(probT_ready, b * HEADS + h - 1)
                    for kt in range(2):
                        for qt in range(2):
                            ins = nc.tensor.transpose(pT[h % 2][:, kt * SEQ + qt * P:kt * SEQ + (qt + 1) * P],
                                                      prob[:, h % 4, qt, kt * P:(kt + 1) * P], core.ident[:, :])
                    ins.then_inc(probT_psum, 1)

                def weighted(b, s, quad):
                    if quad == 0:
                        pe.wait_ge(v_heads_ready, 2 * QUADS * (b + 1))
                        if not known(b, 1):
                            pe.wait_ge(outT_ready, b)
                    pe.wait_ge(probT_ready, b * HEADS + (quad + 1) * PER)
                    for kt in range(2):
                        for j in range(PER):
                            ins = nc.tensor.matmul(pO[32 * j:32 * (j + 1), 0:SEQ], v_heads[:, s, kt, quad, j, :, :].rearrange("p i d -> p (i d)"),
                                                   probT[:, (quad * PER + j) % (2 * PER), kt, :], start=(quad == 0 and kt == 0),
                                                   stop=(quad == QUADS - 1 and kt == 1), tile_position=(0, 32 * j))
                    ins.then_inc(quad_done, 1)

                def turn_inverses(b):
                    pe.wait_ge(inv_wide_ready, b + 1)
                    for qt in range(2):
                        ins = nc.tensor.transpose(pInv[:, qt * P:(qt + 1) * P], inv_wide[:, qt, :, :, :].rearrange("p j i d -> p (j i d)"), core.ident[:, :])
                    ins.then_inc(inv_psum, 1)

                def project(b):
                    pe.wait_ge(outT_ready, b + 1)
                    for qt in range(2):
                        y = pY[:, qt * P:(qt + 1) * P]
                        nc.tensor.matmul(y, core.ones[0:1, :], w["wo_b"][0:1, :], start=True, stop=False)
                        ins = nc.tensor.matmul(y, outT[:, qt * P:(qt + 1) * P], w["wo"], start=False, stop=True)
                    ins.then_inc(y_ready, 1)

                def step(b, s, first, last):
                    if first:
                        for h in range(LEAD):
                            scores(b, s, h)
                    for h in range(HEADS):
                        turn(b, h)
                        if h + LEAD < HEADS:
                            scores(b, s, h + LEAD)
                        elif not last:
                            scores(b + 1, 1 - s, h + LEAD - HEADS)
                        if h == 1 and not first:
                            weighted(b - 1, 1 - s, QUADS - 1)
                            turn_inverses(b - 1)
                        if h % PER == 1 and h > PER:
                            weighted(b, s, h // PER - 1)
                        if h == 6 and not first:
                            project(b - 1)
                    if last:
                        weighted(b, s, QUADS - 1)
                        turn_inverses(b)
                        project(b)

                sequences(pe, step)

            @block.scalar
            def _(a):
                def invT(b):
                    a.wait_ge(inv_psum, b + 1)
                    nc.scalar.copy(inv_T[:, :], pInv).then_inc(inv_T_ready, 1)

                def step(b, s, first, last):
                    for h in range(HEADS):
                        if h == 5 and not first:
                            invT(b - 1)
                        a.wait_ge(max_ready, b * HEADS + h + 1)
                        for qt in range(2):
                            ins = nc.scalar.activation(prob[:, h % 4, qt, :], pS[h % 4][:, qt * SEQ:(qt + 1) * SEQ], ACT.Exp,
                                                       bias=neg_max[:, h % 4, qt:qt + 1], accum_out=row_sum[:, s, qt, h:h + 1])
                        ins.then_inc(prob_ready, 1)
                    if last:
                        invT(b)

                sequences(a, step)

            @block.vector
            def _(v):
                def row_max(b, h):
                    v.wait_ge(scores_ready, b * HEADS + h + 1)
                    nc.vector.tensor_reduce(neg_max[:, h % 4, :], pS[h % 4][:, :].rearrange("p (q k) -> p q k", q=2),
                                            AX.X, ALU.max, negate=True).then_inc(max_ready, 1)

                def copy(b, h):
                    v.wait_ge(probT_psum, b * HEADS + h + 1)
                    if h % PER == 0 and not (known(b, 1) and h < 2 * PER):
                        v.wait_ge(quad_done, b * QUADS + h // PER - 1)
                    nc.vector.tensor_copy(probT[:, h % (2 * PER), :, :], pT[h % 2][:, :].rearrange("p (k q) -> p k q", k=2)).then_inc(probT_ready, 1)

                def invert(b, s):
                    v.wait_ge(prob_ready, (b + 1) * HEADS)
                    nc.vector.reciprocal(inv_sum[:, :, :], row_sum[:, s, :, :]).then_inc(sums_inverted, 1)
                    v.wait_ge(sums_inverted, b + 1)
                    for qt in range(2):
                        ins = nc.vector.tensor_copy(inv_wide[:, qt, :, :, :], bc(inv_sum[:, qt, :].rearrange("p (i j) -> p j i", i=QUADS), 3, ATTN_A_HD))
                    ins.then_inc(inv_wide_ready, 1)

                def normalise(b):
                    v.wait_ge(quad_done, (b + 1) * QUADS)
                    v.wait_ge(inv_T_ready, b + 1)
                    nc.vector.tensor_tensor(outT[:, :], pO[:, 0:SEQ], inv_T[:, :], ALU.mult).then_inc(outT_ready, 1)

                def add(b):
                    v.wait_ge(y_ready, b + 1)
                    x = core.x_res[:, bass.ds(b * 2, 2), :]
                    nc.vector.tensor_tensor(x, x, pY.rearrange("p (q d) -> p q d", q=2), ALU.add).then_inc(y_added, 1)

                def step(b, s, first, last):
                    if first:
                        for h in range(LEAD):
                            row_max(b, h)
                    for h in range(HEADS):
                        copy(b, h)
                        if h + LEAD < HEADS:
                            row_max(b, h + LEAD)
                        elif not last:
                            row_max(b + 1, h + LEAD - HEADS)
                        if not first:
                            if h == 0:
                                invert(b - 1, 1 - s)
                            if h == 3:
                                normalise(b - 1)
                            if h == 8:
                                add(b - 1)
                    if last:
                        invert(b, s)
                        normalise(b)
                        add(b)

                sequences(v, step)


def earlier_table(n):
    return np.broadcast_to(np.tril(np.ones((n, n), np.float32), -1).reshape(1, n * n), (P, n * n))


def link_ranks(nc, c, rank, val, above, same, earlier, n):
    vj, vi = bc(val, 2, n), bc(val, 3, n)
    nc.vector.tensor_tensor(above, vj, vi, ALU.is_gt)
    c.link(nc.vector.tensor_tensor(same, vj, vi, ALU.is_equal))
    c.link(nc.vector.tensor_tensor(same, same, bc(earlier.rearrange("p (i j) -> p i j", i=n), 1, val.shape[1]), ALU.mult))
    c.link(nc.vector.tensor_tensor(above, above, same, ALU.add))
    c.link(nc.vector.tensor_reduce(rank, above, AX.X, ALU.add))


def router_logits(core, router, out_bank, experts, st):
    nc = core.nc
    x_now = st.sb("router_x", [P, 2, BANK])
    copied, used = st.sem("router_copied"), st.sem("router_used")
    GROUPS = TOK // BANK
    with nc.Block() as block:
        @block.gpsimd
        def _(pool):
            pool.sem_inc(used, 2)
            with pool.Fori(0, GROUPS // 2) as g:
                for s in range(2):
                    pool.wait_ge(used, 2 * g + s + 1)
                    nc.gpsimd.tensor_copy(x_now[:, s, :], core.xnT[:, bass.ds((2 * g + s) * BANK, BANK)]).then_inc(copied, 1)

        @block.tensor
        def _(pe):
            with pe.Fori(0, GROUPS // 2) as g:
                for s in range(2):
                    pe.wait_ge(copied, 2 * g + s + 1)
                    for t in range(4):
                        ins = nc.tensor.matmul(out_bank(g * 8 + s * 4 + t), x_now[:, s, t * P:(t + 1) * P], router, start=True, stop=True)
                    ins.then_inc(used, 1)


CYCLES = 3
QUARTER = D // 4


def ffn0_weights(w):
    twist = np.zeros((D, D), np.float32)
    for to, (frm, sign) in enumerate(((2, 1.0), (3, -1.0), (0, -1.0), (1, 1.0))):
        for k in range(QUARTER):
            twist[frm * QUARTER + k, to * QUARTER + k] = sign
    wide = lambda a: np.broadcast_to(a.reshape(-1, 1), (a.size, P))
    tall = lambda a: np.broadcast_to(a.reshape(1, 1), (P, 1))
    full = lambda a: np.concatenate([a, np.zeros((a.shape[0], P - a.shape[1]), a.dtype)], axis=1)
    return pack([
        ("cn1", w["cn_w1"]), ("cn2", full(w["cn_w2"])), ("cn3", full(w["cn_w3"])), ("cn4", wide(w["cn_w4"])),
        ("cn1_b", w["cn_b1"]), ("cn2_b", w["cn_b2"]), ("cn3_b", w["cn_b3"]), ("cn4_b", tall(w["cn_b4"])),
        ("gc1", full(w["gc_w1"])), ("gc2", full(w["gc_w2"])), ("gc3", wide(w["gc_w3"])),
        ("gc1_b", w["gc_b1"]), ("gc2_b", w["gc_b2"]), ("gc3_b", tall(w["gc_b3"])),
        ("range", tall(w["adaptive_range"])), ("twist", twist),
    ])


def ffn0(core, blob, offsets):
    nc = core.nc
    base, share_gf, share_tf = 0.1, 0.7, 0.3
    with Stage(core, "ffn0") as st:
        w = st.weights(blob, offsets)
        layer_norm(core, st)
        bank = [st.ps(f"bank{i}", [P, BANK]) for i in range(8)]
        mean = st.sb("mean", [P, BATCH])
        g1, g2 = st.sb("g1", [P, BATCH]), st.sb("g2", [P, BATCH])
        gf = st.sb("gf", [P, BATCH])
        offset = st.sb("offset", [P, BATCH])
        half_b = st.sb("half_b", [P, 2])
        slope = st.sb("slope", [P, 1])
        dve, glob, glob_act, h_ready = st.sem("dve"), st.sem("glob"), st.sem("glob_act"), st.sem("h_ready")
        with nc.Block() as block:
            @block.vector
            def _(v):
                c = Chain(v, dve)
                c.link(nc.vector.tensor_reduce(mean[:, :], core.xnT[:, :].rearrange("p (b s) -> p b s", s=SEQ), AX.X, ALU.add))
                nc.vector.tensor_scalar(half_b[:, 0:1], w["gc3_b"], 0.5, None, ALU.mult)
                nc.vector.tensor_scalar(half_b[:, 1:2], w["cn4_b"], 0.5, None, ALU.mult)
                nc.vector.tensor_scalar(slope[:, :], w["range"], share_tf, None, ALU.mult)
                c.link(nc.vector.tensor_scalar(mean[:, :], mean[:, :], 1.0 / SEQ, None, ALU.mult))
                v.wait_ge(glob_act, 3)
                c.link(nc.vector.tensor_scalar(gf[:, :], gf[:, :], share_gf, share_gf + share_tf - 1.0, ALU.mult, ALU.add))
                c.link(nc.vector.tensor_scalar(offset[:, :], gf[:, :], w["range"], base, ALU.mult, ALU.add))

            @block.tensor
            def _(pe):
                pe.wait_ge(dve, 2)
                nc.tensor.matmul(bank[0][:, 0:BATCH], w["gc1"], mean[:, :], start=True, stop=True).then_inc(glob, 1)
                pe.wait_ge(glob_act, 1)
                nc.tensor.matmul(bank[1][:, 0:BATCH], w["gc2"], g1[:, :], start=True, stop=True).then_inc(glob, 1)
                pe.wait_ge(glob_act, 2)
                nc.tensor.matmul(bank[2][:, 0:BATCH], w["gc3"], g2[:, :], start=True, stop=True).then_inc(glob, 1)

            @block.scalar
            def _(a):
                a.wait_ge(glob, 1)
                nc.scalar.activation(g1[:, :], bank[0][:, 0:BATCH], ACT.Gelu, bias=w["gc1_b"]).then_inc(glob_act, 1)
                a.wait_ge(glob, 2)
                nc.scalar.activation(g2[:, :], bank[1][:, 0:BATCH], ACT.Gelu, bias=w["gc2_b"]).then_inc(glob_act, 1)
                a.wait_ge(glob, 3)
                nc.scalar.activation(gf[:, :], bank[2][:, 0:BATCH], ACT.Tanh, bias=half_b[:, 0:1], scale=0.5).then_inc(glob_act, 1)

        cur = st.sb("cur", [P, 2, 2, BANK])
        h1, h2, h3 = (st.sb(f"h{i}", [P, 2, BANK]) for i in (1, 2, 3))
        tf = st.sb("tf", [P, 2, BANK])
        psum_ready = st.sem("psum_ready")
        hidden_ready = st.sem("hidden_ready")
        twisted, cycled, turned, added, copied, dve2 = (st.sem(n) for n in ("twisted", "cycled", "turned", "added", "copied", "dve2"))
        LAYERS = 4
        GROUPS = TOK // BANK
        with nc.Block() as block:
            @block.tensor
            def _(pe):
                with pe.Fori(0, GROUPS // 2) as g:
                    for cyc in range(CYCLES):
                        step = g * CYCLES * 2 + cyc * 2
                        for layer, name in enumerate(("cn1", "cn2", "cn3", "cn4")):
                            for s in range(2):
                                if layer == 0:
                                    if cyc == 0:
                                        pe.wait_ge(copied, 2 * g + s + 1)
                                    else:
                                        pe.wait_ge(cycled, step + s - 1)
                                    rhs = cur[:, s, cyc % 2, :]
                                    nc.tensor.matmul(bank[4 + s][:, :], w["twist"], rhs, start=True, stop=True).then_inc(twisted, 1)
                                else:
                                    pe.wait_ge(hidden_ready, step * LAYERS + (layer - 1) * 2 + s + 1)
                                    rhs = (h1, h2, h3)[layer - 1][:, s, :]
                                nc.tensor.matmul(bank[2 * (layer % 2) + s][:, :], w[name], rhs, start=True,
                                                 stop=True).then_inc(psum_ready, 1)
                    for s in range(2):
                        pe.wait_ge(cycled, (g + 1) * CYCLES * 2 - 1 + s)
                        for t in range(4):
                            ins = nc.tensor.transpose(bank[6 + s][:, t * P:(t + 1) * P],
                                                      cur[:, s, CYCLES % 2, t * P:(t + 1) * P], core.ident[:, :])
                        ins.then_inc(turned, 1)

            @block.scalar
            def _(a):
                with a.Fori(0, GROUPS // 2) as g:
                    for cyc in range(CYCLES):
                        step = g * CYCLES * 2 + cyc * 2
                        for layer, name in enumerate(("cn1", "cn2", "cn3", "cn4")):
                            for s in range(2):
                                a.wait_ge(psum_ready, step * LAYERS + layer * 2 + s + 1)
                                src = bank[2 * (layer % 2) + s][:, :]
                                if layer < 3:
                                    nc.scalar.activation((h1, h2, h3)[layer][:, s, :], src, ACT.Gelu,
                                                         bias=w[f"{name}_b"]).then_inc(hidden_ready, 1)
                                else:
                                    nc.scalar.activation(tf[:, s, :], src, ACT.Tanh, bias=half_b[:, 1:2],
                                                         scale=0.5).then_inc(hidden_ready, 1)

            @block.vector
            def _(v):
                with v.Fori(0, GROUPS // 2) as g:
                    c = Chain(v, dve2, g * CYCLES * 2 * 2)
                    for s in range(2):
                        nc.vector.tensor_copy(cur[:, s, 0, :], core.xnT[:, bass.ds((2 * g + s) * BANK, BANK)]).then_inc(copied, 1)
                    for cyc in range(CYCLES):
                        step = g * CYCLES * 2 + cyc * 2
                        for s in range(2):
                            v.wait_ge(hidden_ready, step * LAYERS + 6 + s + 1)
                            for b in range(2):
                                ins = nc.vector.tensor_scalar(tf[:, s, b * SEQ:(b + 1) * SEQ], tf[:, s, b * SEQ:(b + 1) * SEQ], slope[:, :],
                                                              offset[:, bass.ds(4 * g + 2 * s + b, 1)], ALU.mult, ALU.add)
                            c.link(ins)
                            v.wait_ge(twisted, step + s + 1)
                            c.link(nc.vector.tensor_tensor(tf[:, s, :], tf[:, s, :], bank[4 + s][:, :], ALU.mult))
                            nc.vector.tensor_tensor(cur[:, s, 1 - cyc % 2, :], cur[:, s, cyc % 2, :], tf[:, s, :], ALU.add).then_inc(cycled, 1)
                    for s in range(2):
                        v.wait_ge(turned, 2 * g + s + 1)
                        x = core.x_res[:, bass.ds((2 * g + s) * 4, 4), :]
                        nc.vector.tensor_tensor(x, x, bank[6 + s][:, :].rearrange("p (t d) -> p t d", t=4), ALU.add).then_inc(added, 1)


ATTN_B0_HD = D // HEADS


def attn_b0_weights(w):
    head = np.arange(D) // ATTN_B0_HD
    return pack([
        ("wq", w["Wqkv"][:, 0:D]), ("wk", w["Wqkv"][:, D:2 * D]), ("wv", w["Wqkv"][:, 2 * D:3 * D]),
        ("wg", w["Wg"]), ("bg", w["bg"]), ("wp", w["Wp"]), ("bp", w["bp"][None, :]),
        ("same_head", (head[:, None] == head[None, :]).astype(np.float32)),
        ("of_head", (head[:, None] == np.arange(HEADS)[None, :]).astype(np.float32)),
    ])


def attn_b0(core, blob, offsets):
    nc = core.nc
    T = BANK // P
    S = BANK // SEQ
    KV = D + 1
    OUT = D + HEADS
    GROUPS = TOK // BANK
    with Stage(core, "attn_b0") as st:
        w = st.weights(blob, offsets)
        layer_norm(core, st)
        bank = [st.ps(f"bank{i}", [P, BANK]) for i in range(8)]
        x_now = st.sb("x_now", [P, BANK])
        half_bg = st.sb("half_bg", [P, 1])
        gate = st.sb("gate", [P, BANK])
        z = st.sb("z", [P, 2, BANK])
        neg_exp = st.sb("neg_exp", [P, 2, BANK])
        feat = st.sb("feat", [P, 2, BANK])
        k_tok = st.sb("k_tok", [P, T, D])
        v_tok = st.sb("v_tok", [P, T, KV])
        kv = st.sb("kv", [P, S, OUT])
        inv = st.sb("inv", [P, T, HEADS])
        o_tok = st.sb("o_tok", [P, T, D])
        oT = st.sb("oT", [P, BANK])
        names = ("x_copied", "qkg_ready", "v_psum", "tanh_ready", "min_ready", "exp_ready", "feat_ready", "v_ready", "k_psum",
                 "k_ready", "kv_psum", "kv_ready", "o_psum", "o_ready", "oT_psum", "oT_ready", "y_ready", "y_added", "dve", "set_up")
        (x_copied, qkg_ready, v_psum, tanh_ready, min_ready, exp_ready, feat_ready, v_ready, k_psum,
         k_ready, kv_psum, kv_ready, o_psum, o_ready, oT_psum, oT_ready, y_ready, y_added, dve, set_up) = (st.sem(n) for n in names)
        by_tile = lambda ap: ap.rearrange("p (t d) -> p t d", t=T)
        with nc.Block() as block:
            @block.gpsimd
            def _(pool):
                nc.gpsimd.memset(v_tok[:, :, D:KV], 1.0).then_inc(set_up, 1)
                with pool.Fori(0, GROUPS) as g:
                    pool.wait_ge(v_psum, g)
                    nc.gpsimd.tensor_copy(x_now[:, :], core.xnT[:, bass.ds(g * BANK, BANK)]).then_inc(x_copied, 1)

            @block.tensor
            def _(pe):
                with pe.Fori(0, GROUPS) as g:
                    x = core.xnT[:, bass.ds(g * BANK, BANK)]
                    nc.tensor.matmul(bank[0][:, :], w["wg"], x, start=True, stop=True)
                    nc.tensor.matmul(bank[1][:, :], w["wq"], x, start=True, stop=True)
                    nc.tensor.matmul(bank[2][:, :], w["wk"], x, start=True, stop=True).then_inc(qkg_ready, 1)
                    pe.wait_ge(x_copied, g + 1)
                    pe.wait_ge(y_added, g)
                    for t in range(T):
                        ins = nc.tensor.matmul(bank[3][:, t * P:(t + 1) * P], x_now[:, t * P:(t + 1) * P], w["wv"], start=True, stop=True)
                    ins.then_inc(v_psum, 1)
                    pe.wait_ge(feat_ready, g + 1)
                    for t in range(T):
                        ins = nc.tensor.transpose(bank[4][:, t * P:(t + 1) * P], feat[:, 1, t * P:(t + 1) * P], core.ident[:, :])
                    ins.then_inc(k_psum, 1)
                    pe.wait_ge(k_ready, g + 1)
                    pe.wait_ge(v_ready, g + 1)
                    for s in range(S):
                        for t in range(2):
                            ins = nc.tensor.matmul(bank[5][:, s * KV:(s + 1) * KV], k_tok[:, 2 * s + t, :], v_tok[:, 2 * s + t, :],
                                                   start=(t == 0), stop=(t == 1))
                    ins.then_inc(kv_psum, 1)
                    pe.wait_ge(kv_ready, g + 1)
                    for t in range(T):
                        at = (t % 2) * OUT
                        ins = nc.tensor.matmul(bank[6 + t // 2][:, at:at + OUT], feat[:, 0, t * P:(t + 1) * P], kv[:, t // 2, :],
                                               start=True, stop=True)
                    ins.then_inc(o_psum, 1)
                    pe.wait_ge(o_ready, g + 1)
                    for t in range(T):
                        ins = nc.tensor.transpose(bank[4][:, t * P:(t + 1) * P], o_tok[:, t, :], core.ident[:, :])
                    ins.then_inc(oT_psum, 1)
                    pe.wait_ge(oT_ready, g + 1)
                    for t in range(T):
                        y = bank[3][:, t * P:(t + 1) * P]
                        nc.tensor.matmul(y, core.ones[0:1, :], w["bp"][0:1, :], start=True, stop=False)
                        ins = nc.tensor.matmul(y, oT[:, t * P:(t + 1) * P], w["wp"], start=False, stop=True)
                    ins.then_inc(y_ready, 1)

            @block.scalar
            def _(a):
                a.wait_ge(set_up, 2)
                with a.Fori(0, GROUPS) as g:
                    a.wait_ge(qkg_ready, g + 1)
                    nc.scalar.activation(gate[:, :], bank[0][:, :], ACT.Tanh, bias=half_bg[:, :], scale=0.5).then_inc(tanh_ready, 1)
                    a.wait_ge(min_ready, g + 1)
                    nc.scalar.activation(neg_exp[:, :, :], neg_exp[:, :, :], ACT.Exp).then_inc(exp_ready, 1)
                    a.wait_ge(k_psum, g + 1)
                    nc.scalar.copy(k_tok[:, :, :], by_tile(bank[4][:, :])).then_inc(k_ready, 1)
                    a.wait_ge(oT_psum, g + 1)
                    nc.scalar.copy(oT[:, :], bank[4][:, :]).then_inc(oT_ready, 1)

            @block.vector
            def _(v):
                nc.vector.tensor_scalar(half_bg[:, :], w["bg"], 0.5, None, ALU.mult).then_inc(set_up, 1)
                with v.Fori(0, GROUPS) as g:
                    c = Chain(v, dve, g * 4)
                    v.wait_ge(tanh_ready, g + 1)
                    c.link(nc.vector.tensor_scalar(gate[:, :], gate[:, :], 0.5, 0.5, ALU.mult, ALU.add))
                    nc.vector.tensor_tensor(z[:, 0, :], gate[:, :], bank[1][:, :], ALU.mult)
                    c.link(nc.vector.tensor_tensor(z[:, 1, :], gate[:, :], bank[2][:, :], ALU.mult))
                    nc.vector.tensor_scalar(neg_exp[:, :, :], z[:, :, :], 0.0, None, ALU.min).then_inc(min_ready, 1)
                    v.wait_ge(exp_ready, g + 1)
                    nc.vector.scalar_tensor_tensor(feat[:, :, :], z[:, :, :], 0.0, neg_exp[:, :, :], ALU.max,
                                                   ALU.add).then_inc(feat_ready, 1)
                    v.wait_ge(v_psum, g + 1)
                    nc.vector.tensor_copy(v_tok[:, :, 0:D], by_tile(bank[3][:, :])).then_inc(v_ready, 1)
                    v.wait_ge(kv_psum, g + 1)
                    for s in range(S):
                        nc.vector.tensor_tensor(kv[:, s, 0:D], bank[5][:, s * KV:s * KV + D], w["same_head"], ALU.mult)
                        ins = nc.vector.tensor_tensor(kv[:, s, D:OUT], w["of_head"],
                                                      bank[5][:, s * KV + D:(s + 1) * KV].broadcast_to([P, HEADS]), ALU.mult)
                    ins.then_inc(kv_ready, 1)
                    v.wait_ge(o_psum, g + 1)
                    pair = [bank[6 + i][:, 0:2 * OUT].rearrange("p (t o) -> p t o", t=2) for i in range(2)]
                    for i in range(2):
                        ins = nc.vector.tensor_scalar(inv[:, 2 * i:2 * i + 2, :], pair[i][:, :, D:OUT], 1e-8, None, ALU.add)
                    c.link(ins)
                    c.link(nc.vector.reciprocal(inv[:, :, :], inv[:, :, :]))
                    for i in range(2):
                        for t in range(2):
                            ins = nc.vector.tensor_tensor(o_tok[:, 2 * i + t, :].rearrange("p (h d) -> p h d", h=HEADS),
                                                          pair[i][:, t, 0:D].rearrange("p (h d) -> p h d", h=HEADS),
                                                          bc(inv[:, 2 * i + t, :], 2, ATTN_B0_HD), ALU.mult)
                    ins.then_inc(o_ready, 1)
                    v.wait_ge(y_ready, g + 1)
                    xr = core.x_res[:, bass.ds(g * T, T), :]
                    nc.vector.tensor_tensor(xr, xr, by_tile(bank[3][:, :]), ALU.add).then_inc(y_added, 1)


FFN1_EXPERTS = 16
FFN1_HID = 4 * D
FFN1_SHARED = 2 * D
CAPACITY = 2 * TOK // FFN1_EXPERTS
SLICES = P // FFN1_EXPERTS
RUNS = TILES // SLICES
RANKS = CAPACITY // P
LO = 32
HI = CAPACITY // LO
ROW = D + FFN1_EXPERTS
BITS = 30


def ffn1_weights(w):
    p = np.arange(P)
    same = (p[:, None] % FFN1_EXPERTS) == (p[None, :] % FFN1_EXPERTS)
    before = same & (p[:, None] < p[None, :])
    chunked = lambda a: a.reshape(-1, P, D).transpose(1, 0, 2).reshape(P, -1)
    in_half = p // HI
    return pack([
        ("router", w["gate_w"].T),
        ("token", (np.arange(TILES)[None, :] * P + p[:, None]).astype(np.float32)),
        ("iota", np.broadcast_to(np.arange(LO, dtype=np.float32), (P, LO))),
        ("own", (in_half[:, None] == np.arange(FFN1_EXPERTS // 2)[None, :]).astype(np.float32)),
        ("wg", w["Wg"].reshape(FFN1_EXPERTS * FFN1_HID, D).T), ("wu", w["Wu"].reshape(FFN1_EXPERTS * FFN1_HID, D).T),
        ("wd", chunked(w["Wd"].transpose(0, 2, 1).reshape(FFN1_EXPERTS * FFN1_HID, D))),
        ("sg", w["Sg"].T), ("su", w["Su"].T), ("sd", chunked(w["Sd"].T)),
        ("same", same.astype(np.float32)), ("before", before.astype(np.float32)),
        ("powers", np.broadcast_to((2.0 ** np.arange(BITS - 1, -1, -1)).astype(np.float32), (P, BITS))),
    ])


def ffn1(core, blob, offsets):
    nc = core.nc
    GROUPS = TOK // BANK
    with Stage(core, "ffn1") as st:
        w = st.weights(blob, offsets)
        layer_norm(core, st)
        bank = [st.ps(f"bank{i}", [P, BANK]) for i in range(8)]
        tok_major = bank[0][:, :].rearrange("p (t e) -> p t e", t=TILES)
        router_logits(core, w["router"], lambda t: tok_major[:, bass.ds(t, 1), :].squeeze(1), FFN1_EXPERTS, st)

        score = st.sb("score", [P, TILES, FFN1_EXPERTS])
        best, total = st.sb("best", [P, TILES]), st.sb("total", [P, TILES])
        score_e, above, ties, rank, restart = (st.sb(n, [P, BANK]) for n in ("score_e", "above", "ties", "rank", "restart"))
        power_bits, threshold, trial, kept = st.sb("power_bits", [P, BITS], I32), st.sb("threshold", [P, 1], I32), st.sb("trial", [P, 1], I32), st.sb("kept", [P, 1], I32)
        count = st.sb("count", [P, 1])
        wanted = st.sb("wanted", [P, 1])
        tie_count, base, run_total = (st.sb(n, [P, RUNS]) for n in ("tie_count", "base", "run_total"))
        names = ("dve", "centred", "exp_ready", "score_ready", "score_psum", "counted", "summed", "bit_chain", "tie_chain", "place_e_ready", "place_psum", "consts", "normed", "table_stored")
        (dve, centred, exp_ready, score_ready, score_psum, counted, summed, bit_chain, tie_chain, place_e_ready, place_psum, consts, normed, table_stored) = (st.sem(n) for n in names)
        table = nc.dram_tensor(f"{st.name}_table", (TOK, ROW), F32, kind="Internal").ap()
        with nc.Block() as block:
            @block.sync
            def _(sp):
                by_tile = table.rearrange("(t p) d -> p t d", p=P)
                sp.wait_ge(normed, 1)
                sp.dma_start(by_tile[:, :, 0:D], core.xn[:, :, :]).then_inc(table_stored, 16)
                sp.wait_ge(score_ready, 1)
                sp.dma_start(by_tile[:, :, D:ROW], score[:, :, :]).then_inc(table_stored, 16)
                sp.wait_ge(table_stored, 32)

            @block.gpsimd
            def _(pool):
                nc.gpsimd.memset(restart[:, :], 1.0).then_inc(consts, 1)
                nc.gpsimd.memset(threshold[:, :], 0).then_inc(consts, 1)
                nc.gpsimd.tensor_copy(power_bits[:, :], w["powers"]).then_inc(consts, 1)
                pool.wait_ge(consts, 3)
                nc.gpsimd.memset(restart[:, 0:BANK:P], 0.0).then_inc(consts, 1)
                nc.gpsimd.tensor_tensor(core.xn[:, :, :], core.xn[:, :, :], bc(core.rstd[:, :], 2, D), ALU.mult).then_inc(normed, 1)

            @block.tensor
            def _(pe):
                pe.wait_ge(score_ready, 1)
                for r in range(RUNS):
                    ins = nc.tensor.transpose(bank[1][:, r * P:(r + 1) * P], score[:, r * SLICES:(r + 1) * SLICES, :].rearrange("p t e -> p (t e)"), core.ident[:, :])
                ins.then_inc(score_psum, 1)
                with pe.Fori(0, BITS) as i:
                    pe.wait_ge(counted, i + 1)
                    nc.tensor.matmul(bank[2][:, 0:1], w["same"], count[:, :], start=True, stop=True).then_inc(summed, 1)
                pe.wait_ge(counted, BITS + 1)
                nc.tensor.matmul(bank[2][:, 1:2], w["same"], count[:, :], start=True, stop=True)
                nc.tensor.matmul(bank[2][:, 4:4 + RUNS], w["same"], tie_count[:, :], start=True, stop=True)
                nc.tensor.matmul(bank[2][:, 8:8 + RUNS], w["before"], tie_count[:, :], start=True, stop=True).then_inc(summed, 1)
                pe.wait_ge(counted, BITS + 2)
                nc.tensor.matmul(bank[2][:, 16:16 + RUNS], w["same"], tie_count[:, :], start=True, stop=True)
                nc.tensor.matmul(bank[2][:, 20:20 + RUNS], w["before"], tie_count[:, :], start=True, stop=True).then_inc(summed, 1)
                pe.wait_ge(place_e_ready, 1)
                for r in range(RUNS):
                    ins = nc.tensor.transpose(bank[3][:, r * P:(r + 1) * P], rank[:, r * P:(r + 1) * P], core.ident[:, :])
                ins.then_inc(place_psum, 1)

            @block.scalar
            def _(a):
                a.wait_ge(centred, 1)
                nc.scalar.activation(score[:, :, :], score[:, :, :], ACT.Exp).then_inc(exp_ready, 1)

            @block.vector
            def _(v):
                c = Chain(v, dve)
                c.link(nc.vector.tensor_reduce(best[:, :], tok_major, AX.X, ALU.max))
                nc.vector.tensor_tensor(score[:, :, :], tok_major, bc(best[:, :], 2, FFN1_EXPERTS), ALU.subtract).then_inc(centred, 1)
                v.wait_ge(exp_ready, 1)
                c.link(nc.vector.tensor_reduce(total[:, :], score[:, :, :], AX.X, ALU.add))
                c.link(nc.vector.reciprocal(total[:, :], total[:, :]))
                nc.vector.tensor_tensor(score[:, :, :], score[:, :, :], bc(total[:, :], 2, FFN1_EXPERTS), ALU.mult).then_inc(score_ready, 1)
                v.wait_ge(score_psum, 1)
                c.link(nc.vector.tensor_copy(score_e[:, :], bank[1][:, :]))
                v.wait_ge(consts, 4)
                with v.Fori(0, BITS) as i:
                    b = Chain(v, bit_chain, i * 3)
                    b.link(nc.vector.tensor_tensor(trial[:, :], threshold[:, :], power_bits[:, bass.ds(i, 1)], ALU.bitwise_or))
                    nc.vector.tensor_scalar(above[:, :], score_e[:, :], trial[:, :].bitcast(F32), 0.0, ALU.is_ge, ALU.add,
                                            accum_out=count[:, :]).then_inc(counted, 1)
                    v.wait_ge(summed, i + 1)
                    b.link(nc.vector.tensor_scalar(kept[:, :], bank[2][:, 0:1], float(CAPACITY), w["powers"][:, bass.ds(i, 1)], ALU.is_ge, ALU.mult))
                    b.link(nc.vector.tensor_tensor(threshold[:, :], threshold[:, :], kept[:, :], ALU.bitwise_or))
                e = Chain(v, tie_chain)
                limit = threshold[:, :].bitcast(F32)
                e.link(nc.vector.tensor_scalar(above[:, :], score_e[:, :], limit, 0.0, ALU.is_gt, ALU.add, accum_out=count[:, :]))
                e.link(nc.vector.tensor_scalar(ties[:, :], score_e[:, :], limit, None, ALU.is_equal))
                by_run = lambda t: t[:, :].rearrange("p (r s) -> p r s", r=RUNS)

                def places(marks, at, nth):
                    e.link(nc.vector.tensor_tensor_scan(rank[:, :], restart[:, :], marks[:, :], 0.0, ALU.mult, ALU.add))
                    nc.vector.tensor_copy(tie_count[:, :], rank[:, P - 1:BANK:P]).then_inc(counted, 1)
                    v.wait_ge(summed, BITS + nth)
                    e.link(nc.vector.tensor_copy(run_total[:, :], bank[2][:, at:at + RUNS]))
                    e.link(nc.vector.tensor_copy(base[:, :], bank[2][:, at + RUNS:at + 2 * RUNS]))
                    for r in range(1, RUNS):
                        e.link(nc.vector.tensor_scalar(base[:, r:RUNS], base[:, r:RUNS], run_total[:, r - 1:r], None, ALU.add))
                    e.link(nc.vector.tensor_tensor(rank[:, :], rank[:, :], marks[:, :], ALU.subtract))
                    e.link(nc.vector.tensor_tensor(by_run(rank), by_run(rank), bc(base[:, :], 2, P), ALU.add))

                places(ties, 4, 1)
                e.link(nc.vector.tensor_scalar(wanted[:, :], bank[2][:, 1:2], -1.0, float(CAPACITY), ALU.mult, ALU.add))
                e.link(nc.vector.tensor_scalar(rank[:, :], rank[:, :], wanted[:, :], None, ALU.is_lt))
                e.link(nc.vector.tensor_tensor(ties[:, :], ties[:, :], rank[:, :], ALU.mult))
                e.link(nc.vector.tensor_tensor(above[:, :], above[:, :], ties[:, :], ALU.add))
                places(above, 16, 2)
                e.link(nc.vector.scalar_tensor_tensor(rank[:, :], rank[:, :], 1.0, above[:, :], ALU.add, ALU.mult))
                e.link(nc.vector.tensor_scalar(rank[:, :], rank[:, :], -1.0, None, ALU.add))
                e.eng.sem_inc(place_e_ready, 1)
                v.wait_ge(place_psum, 1)
                place = ties[:, :].bitcast(I32)
                e.link(nc.vector.tensor_copy(place, bank[3][:, :]))
                split = above[:, :].bitcast(I32), restart[:, :].bitcast(I32)
                e.link(nc.vector.tensor_scalar(split[0], place, LO.bit_length() - 1, None, ALU.arith_shift_right))
                e.link(nc.vector.tensor_scalar(split[1], place, LO - 1, None, ALU.bitwise_and))
                e.link(nc.vector.tensor_copy(score_e[:, :], split[0]))
                e.link(nc.vector.tensor_copy(rank[:, :], split[1]))

        gelu = st.sb("gelu", [P, 2, BANK])
        hid = st.sb("hid", [P, 2, FFN1_HID // P, BANK])
        index = st.sb("index", [P, FFN1_EXPERTS * RANKS], I32)
        lists = nc.dram_tensor(f"{st.name}_lists", (FFN1_EXPERTS * CAPACITY,), F32, kind="Internal").ap()
        hi = score_e[:, :].rearrange("p (t e) -> p t e", t=TILES)
        lo = rank[:, :].rearrange("p (t e) -> p t e", t=TILES)
        STEP = 2
        hid_flat = hid[:, :, :, :].rearrange("p i k s -> p i (k s)")
        is_hi = [hid_flat[:, i, 0:STEP * FFN1_EXPERTS * HI].rearrange("p (t e h) -> p t e h", t=STEP, e=FFN1_EXPERTS) for i in range(2)]
        is_lo = [hid_flat[:, i, STEP * FFN1_EXPERTS * HI:STEP * FFN1_EXPERTS * (HI + LO)].rearrange("p (t e l) -> p t e l", t=STEP, e=FFN1_EXPERTS) for i in range(2)]
        own_idx, rows_64 = gelu[:, 0, 0:2 * LO], gelu[0:FFN1_EXPERTS * RANKS, 1, 0:P]
        hot_chain, hot_ready, hot_used, list_psum, list_chain, list_ready, list_moved, index_psum = (st.sem(n) for n in (
            "hot_chain", "hot_ready", "hot_used", "list_psum", "list_chain", "list_ready", "list_moved", "index_psum"))
        with nc.Block() as block:
            @block.vector
            def _(v):
                for n in range(TILES // STEP):
                    tiles = slice(n * STEP, (n + 1) * STEP)
                    i = n % 2
                    if n >= 2:
                        v.wait_ge(hot_used, n - 1)
                    nc.vector.tensor_tensor(is_hi[i], bc(hi[:, tiles, :], 3, HI), bc(bc(w["iota"][:, 0:HI], 1, FFN1_EXPERTS), 1, STEP), ALU.is_equal).then_inc(hot_chain, 1)
                    nc.vector.tensor_tensor(is_lo[i], bc(lo[:, tiles, :], 3, LO), bc(bc(w["iota"], 1, FFN1_EXPERTS), 1, STEP), ALU.is_equal).then_inc(hot_ready, 1)
                    v.wait_ge(hot_chain, n + 1)
                    nc.vector.tensor_tensor(is_hi[i].rearrange("p t e h -> p t (e h)"), is_hi[i].rearrange("p t e h -> p t (e h)"),
                                            bc(w["token"][:, tiles], 2, FFN1_EXPERTS * HI), ALU.mult).then_inc(hot_ready, 1)
                v.wait_ge(list_psum, 1)
                c = Chain(v, list_chain)
                own = hid_flat[:, 0, 0:BANK].rearrange("p (h e l) -> p h e l", h=2, e=FFN1_EXPERTS // 2)
                for half in range(2):
                    found = bank[4 + half][:, 0:FFN1_EXPERTS // 2 * LO].rearrange("p (e l) -> p e l", e=FFN1_EXPERTS // 2)
                    c.link(nc.vector.tensor_tensor(own[:, half], found, bc(w["own"], 2, LO), ALU.mult))
                nc.vector.tensor_reduce(own_idx.rearrange("p (h l) -> p h l", h=2), own.rearrange("p h e l -> p h l e"), AX.X, ALU.add).then_inc(list_ready, 1)
                v.wait_ge(index_psum, 1)
                nc.vector.tensor_copy(index[:, :], bank[6][:, 0:FFN1_EXPERTS * RANKS])

            @block.sync
            def _(sp):
                sp.wait_ge(list_ready, 1)
                sp.dma_start(lists.rearrange("(h p l) -> p h l", h=2, p=P), own_idx.rearrange("p (h l) -> p h l", h=2)).then_inc(list_moved, 16)
                sp.wait_ge(list_moved, 16)
                sp.dma_start(rows_64, lists.rearrange("(r p) -> r p", p=P)).then_inc(list_moved, 16)

            @block.tensor
            def _(pe):
                E2 = FFN1_EXPERTS // 2
                for n in range(TILES // STEP):
                    pe.wait_ge(hot_ready, 2 * (n + 1))
                    for t in range(STEP):
                        for half in range(2):
                            es = slice(half * E2, (half + 1) * E2)
                            ins = nc.tensor.matmul(bank[4 + half][:, 0:E2 * LO], is_hi[n % 2][:, t, es, :].rearrange("p e h -> p (e h)"),
                                                   is_lo[n % 2][:, t, es, :].rearrange("p e l -> p (e l)"),
                                                   start=(n == 0 and t == 0), stop=(n == TILES // STEP - 1 and t == STEP - 1))
                    ins.then_inc(hot_used, 1)
                pe.wait_ge(hot_used, TILES // STEP)
                pe.sem_inc(list_psum, 1)
                pe.wait_ge(list_moved, 32)
                nc.tensor.transpose(bank[6][:, 0:FFN1_EXPERTS * RANKS], rows_64, core.ident[0:FFN1_EXPERTS * RANKS, 0:FFN1_EXPERTS * RANKS]).then_inc(index_psum, 1)

        names = ("up_ready", "gelu_ready", "hid_ready", "y_ready", "added")
        up_ready, gelu_ready, hid_ready, y_ready, added = (st.sem("shared_" + n) for n in names)
        N = FFN1_SHARED // P
        with nc.Block() as block:
            @block.tensor
            def _(pe):
                with pe.Fori(0, GROUPS) as g:
                    x = core.xnT[:, bass.ds(g * BANK, BANK)]
                    for k in range(N):
                        pe.wait_ge(hid_ready, g * N)
                        nc.tensor.matmul(bank[2 * k][:, :], w["sg"][:, k * P:(k + 1) * P], x, start=True, stop=True)
                        nc.tensor.matmul(bank[2 * k + 1][:, :], w["su"][:, k * P:(k + 1) * P], x, start=True, stop=True).then_inc(up_ready, 1)
                    pe.wait_ge(hid_ready, (g + 1) * N)
                    pe.wait_ge(added, g)
                    for t in range(4):
                        for k in range(N):
                            ins = nc.tensor.matmul(bank[4][:, t * P:(t + 1) * P], hid[:, 0, k, t * P:(t + 1) * P], w["sd"][:, k * D:(k + 1) * D],
                                                   start=(k == 0), stop=(k == N - 1))
                    ins.then_inc(y_ready, 1)

            @block.scalar
            def _(a):
                with a.Fori(0, GROUPS) as g:
                    for k in range(N):
                        a.wait_ge(up_ready, g * N + k + 1)
                        nc.scalar.activation(gelu[:, k, :], bank[2 * k][:, :], ACT.Gelu).then_inc(gelu_ready, 1)

            @block.vector
            def _(v):
                with v.Fori(0, GROUPS) as g:
                    for k in range(N):
                        v.wait_ge(gelu_ready, g * N + k + 1)
                        v.wait_ge(y_ready, g)
                        nc.vector.tensor_tensor(hid[:, 0, k, :], gelu[:, k, :], bank[2 * k + 1][:, :], ALU.mult).then_inc(hid_ready, 1)
                    v.wait_ge(y_ready, g + 1)
                    x = core.x_res[:, bass.ds(g * 4, 4), :]
                    nc.vector.tensor_tensor(x, x, bank[4][:, :].rearrange("p (t d) -> p t d", t=4), ALU.add).then_inc(added, 1)

        stream = nc.dram_tensor(f"{st.name}_stream", (TOK, D), F32, kind="Internal").ap()
        XS = 3
        rows = st.sb("rows", [P, XS, RANKS, ROW])
        rowsT = st.sb("rowsT", [P, 2, BANK])
        y = st.sb("y", [P, 2, RANKS, D])
        gathered = [st.sem(f"gathered{i}") for i in range(XS)]
        names = ("turned", "rowsT_ready", "up_ready", "gelu_ready", "hid_ready", "y_psum", "y_ready", "scattered", "stream_stored", "stream_loaded")
        (turned, rowsT_ready, up_ready, gelu_ready, hid_ready, y_psum, y_ready, scattered, stream_stored, stream_loaded) = (st.sem(n) for n in names)
        KS = FFN1_HID // P
        with nc.Block() as block:
            @block.sync
            def _(sp):
                sp.dma_start(stream.rearrange("(t p) d -> p t d", p=P), core.x_res[:, :, :]).then_inc(stream_stored, 16)
                sp.wait_ge(stream_stored, 16)
                sp.wait_ge(scattered, FFN1_EXPERTS * RANKS * 16)
                sp.dma_start(core.x_res[:, :, :], stream.rearrange("(t p) d -> p t d", p=P)).then_inc(stream_loaded, 16)
                sp.wait_ge(stream_loaded, 16)

            @block.gpsimd
            def _(pool):
                def gather(e):
                    for r in range(RANKS):
                        at = e * RANKS + r
                        nc.gpsimd.indirect_dma_start(rows[:, e % XS, r, :], None, table, bass.IndirectOffsetOnAxis(index[:, at:at + 1], 0)).then_inc(gathered[e % XS], 16)

                def scatter(e):
                    if e == 0:
                        pool.wait_ge(stream_stored, 16)
                    else:
                        pool.wait_ge(scattered, e * RANKS * 16)
                    for r in range(RANKS):
                        at = e * RANKS + r
                        nc.gpsimd.indirect_dma_start(stream, bass.IndirectOffsetOnAxis(index[:, at:at + 1], 0), y[:, e % 2, r, :], None,
                                                     compute_op=ALU.add).then_inc(scattered, 16)

                gather(0)
                gather(1)
                for e in range(FFN1_EXPERTS):
                    if e > 0:
                        pool.wait_ge(y_ready, e)
                    if e + 2 < FFN1_EXPERTS:
                        gather(e + 2)
                    if e > 0:
                        scatter(e - 1)
                pool.wait_ge(y_ready, FFN1_EXPERTS)
                scatter(FFN1_EXPERTS - 1)

            @block.tensor
            def _(pe):
                def turn(e):
                    pe.wait_ge(gathered[e % XS], (e // XS + 1) * RANKS * 16)
                    if e >= 2:
                        pe.wait_ge(rowsT_ready, e - 1)
                    for r in range(RANKS):
                        ins = nc.tensor.transpose(bank[6 + e % 2][:, r * P:(r + 1) * P], rows[:, e % XS, r, 0:D], core.ident[:, :])
                    ins.then_inc(turned, 1)

                def down(e):
                    pe.wait_ge(hid_ready, (e + 1) * KS)
                    if e >= 2:
                        pe.wait_ge(y_ready, e - 1)
                    for r in range(RANKS):
                        for k in range(KS):
                            at = e * KS + k
                            ins = nc.tensor.matmul(bank[4 + e % 2][:, r * P:(r + 1) * P], hid[:, e % 2, k, r * P:(r + 1) * P], w["wd"][:, at * D:(at + 1) * D],
                                                   start=(k == 0), stop=(k == KS - 1))
                    ins.then_inc(y_psum, 1)

                turn(0)
                for e in range(FFN1_EXPERTS):
                    pe.wait_ge(rowsT_ready, e + 1)
                    for k in range(KS):
                        i = e * KS + k
                        if i >= 2:
                            pe.wait_ge(hid_ready, i - 1)
                        nc.tensor.matmul(bank[2 * (i % 2)][:, :], w["wg"][:, i * P:(i + 1) * P], rowsT[:, e % 2, :], start=True, stop=True)
                        nc.tensor.matmul(bank[2 * (i % 2) + 1][:, :], w["wu"][:, i * P:(i + 1) * P], rowsT[:, e % 2, :], start=True, stop=True).then_inc(up_ready, 1)
                        if k == 1 and e > 0:
                            down(e - 1)
                        if k == 2 and e + 1 < FFN1_EXPERTS:
                            turn(e + 1)
                down(FFN1_EXPERTS - 1)

            @block.scalar
            def _(a):
                def rows_turned(e):
                    a.wait_ge(turned, e + 1)
                    if e >= 2:
                        a.wait_ge(up_ready, (e - 1) * KS)
                    nc.scalar.copy(rowsT[:, e % 2, :], bank[6 + e % 2][:, :]).then_inc(rowsT_ready, 1)

                rows_turned(0)
                for e in range(FFN1_EXPERTS):
                    for k in range(KS):
                        i = e * KS + k
                        a.wait_ge(up_ready, i + 1)
                        if i >= 2:
                            a.wait_ge(hid_ready, i - 1)
                        nc.scalar.activation(gelu[:, i % 2, :], bank[2 * (i % 2)][:, :], ACT.Gelu).then_inc(gelu_ready, 1)
                        if k == 3 and e + 1 < FFN1_EXPERTS:
                            rows_turned(e + 1)

            @block.vector
            def _(v):
                def weigh(e):
                    v.wait_ge(y_psum, e + 1)
                    if e >= 2:
                        v.wait_ge(scattered, (e - 1) * RANKS * 16)
                    nc.vector.tensor_tensor(y[:, e % 2, :, :], bank[4 + e % 2][:, :].rearrange("p (r d) -> p r d", r=RANKS),
                                            bc(rows[:, e % XS, :, D + e:D + e + 1].squeeze(2), 2, D), ALU.mult).then_inc(y_ready, 1)

                for e in range(FFN1_EXPERTS):
                    for k in range(KS):
                        i = e * KS + k
                        v.wait_ge(gelu_ready, i + 1)
                        if e >= 2:
                            v.wait_ge(y_psum, e - 1)
                        nc.vector.tensor_tensor(hid[:, e % 2, k, :], gelu[:, i % 2, :], bank[2 * (i % 2) + 1][:, :], ALU.mult).then_inc(hid_ready, 1)
                        if k == 2 and e > 0:
                            weigh(e - 1)
                weigh(FFN1_EXPERTS - 1)


STATES = 16
RANK = 64
CHN = 4
SCAN_CHUNKS = STATES // CHN


def two_slots(eng, front, back):
    front(0, 0)
    with eng.Fori(0, BATCH // 2 - 1) as i:
        front(2 * i + 1, 1)
        back(2 * i, 0)
        front(2 * i + 2, 0)
        back(2 * i + 1, 1)
    front(BATCH - 1, 1)
    back(BATCH - 2, 0)
    back(BATCH - 1, 1)


def full(a):
    return np.concatenate([a, np.zeros((a.shape[0], P - a.shape[1]), a.dtype)], axis=1)


def scan1_weights(w):
    xp = w["x_proj_w"].T
    return pack([
        ("low", full(xp[:, 0:RANK])), ("b", xp[:, RANK:RANK + STATES]), ("c", xp[:, RANK + STATES:]),
        ("dt", w["dt_proj_w"].T), ("dt_b", w["dt_proj_b"]), ("a_log", w["A_log"]), ("skip", w["D_skip"]),
    ])


def scan3_weights(w):
    wp = w["W_params"].T
    return pack([
        ("low", full(wp[:, 0:RANK])), ("c", wp[:, RANK + STATES:]),
        ("dt", w["W_dt"].T), ("dt_b", w["b_dt"]), ("a_log", w["A_log"]), ("skip", w["D"]),
        ("conv", w["conv_w"][:, 0, :]), ("wz", w["W_z"].T), ("wo", w["W_out"].T),
    ])


def step_sizes(core, st, w, bank, delta, extra_pe=None, extra_act=None, extra_dve=None):
    nc = core.nc
    GROUPS = TOK // BANK
    low, y, e = (st.sb(n, [P, BANK]) for n in ("dt_low", "dt_y", "dt_e"))
    names = ("low_psum", "low_ready", "y_psum", "y_shifted", "abs_ready", "ln_ready", "delta_done", "act_chain")
    low_psum, low_ready, y_psum, y_shifted, abs_ready, ln_ready, delta_done, act_chain = (st.sem(n) for n in names)
    with nc.Block() as block:
        @block.tensor
        def _(pe):
            with pe.Fori(0, GROUPS) as g:
                nc.tensor.matmul(bank[0][:, :], w["low"], core.xnT[:, bass.ds(g * BANK, BANK)], start=True, stop=True).then_inc(low_psum, 1)
                if extra_pe:
                    extra_pe(pe, g)
                pe.wait_ge(low_ready, g + 1)
                nc.tensor.matmul(bank[1][:, :], w["dt"], low[:, :], start=True, stop=True).then_inc(y_psum, 1)

        @block.scalar
        def _(a):
            with a.Fori(0, GROUPS) as g:
                c = Chain(a, act_chain, 3 * g)
                a.wait_ge(low_psum, g + 1)
                nc.scalar.copy(low[:, :], bank[0][:, :]).then_inc(low_ready, 1)
                a.wait_ge(y_psum, g + 1)
                a.wait_ge(delta_done, g)
                c.link(nc.scalar.activation(y[:, :], bank[1][:, :], ACT.Identity, bias=w["dt_b"]))
                c.link(nc.scalar.activation(e[:, :], y[:, :], ACT.Abs))
                c.link(nc.scalar.activation(e[:, :], e[:, :], ACT.Exp, scale=-1.0))
                nc.scalar.activation(e[:, :], e[:, :], ACT.Ln, bias=1.0).then_inc(ln_ready, 1)

        @block.vector
        def _(v):
            with v.Fori(0, GROUPS) as g:
                v.wait_ge(ln_ready, g + 1)
                nc.vector.scalar_tensor_tensor(delta[:, bass.ds(g * BANK, BANK)], y[:, :], 0.0, e[:, :], ALU.max, ALU.add).then_inc(delta_done, 1)


def scan1(core, blob, offsets):
    nc = core.nc
    with Stage(core, "scan1") as st:
        w = st.weights(blob, offsets)
        layer_norm(core, st)
        pB = [st.ps(f"pB{i}", [P, CHN, SEQ]) for i in range(2)]
        pC = [st.ps(f"pC{i}", [P, 2, SEQ]) for i in range(2)]
        pX = [st.ps(f"pX{i}", [P, BANK]) for i in range(2)]
        delta = st.sb("delta", [P, TOK])
        step_sizes(core, st, w, pX, delta)
        decay = [st.sb(f"decay{i}", [P, STATES, SEQ]) for i in range(2)]
        h = [st.sb(f"h{i}", [P, STATES, SEQ]) for i in range(2)]
        c_all = st.sb("c_all", [P, STATES, SEQ])
        du = st.sb("du", [P, 2, SEQ])
        y = st.sb("y", [P, 2, SEQ])
        pos_a, neg_a = st.sb("pos_a", [P, STATES]), st.sb("neg_a", [P, STATES])
        names = ("set_up", "du_ready", "b_psum", "b_used", "c_psum", "c_ready", "decay_ready", "scanned", "times_c", "y_ready", "summed",
                 "skip_added", "yT_ready", "added")
        (set_up, du_ready, b_psum, b_used, c_psum, c_ready, decay_ready, scanned, times_c, y_ready, summed,
         skip_added, yT_ready, added) = (st.sem(n) for n in names)
        with nc.Block() as block:
            @block.gpsimd
            def _(pool):
                for s in range(2):
                    nc.gpsimd.memset(decay[s][:, :, 0:1], 0.0).then_inc(set_up, 1)

                def front(b, s):
                    cols = bass.ds(b * SEQ, SEQ)
                    nc.gpsimd.tensor_tensor(du[:, s, :], delta[:, cols], core.xnT[:, cols], ALU.mult).then_inc(du_ready, 1)

                def back(b, s):
                    for j in range(SCAN_CHUNKS):
                        part = slice(j * CHN, (j + 1) * CHN)
                        pool.wait_ge(scanned, b * SCAN_CHUNKS + j + 1)
                        pool.wait_ge(c_ready, (b * SCAN_CHUNKS + j) * 2 + 4)
                        nc.gpsimd.tensor_tensor(h[s][:, part, :], h[s][:, part, :], c_all[:, part, :], ALU.mult).then_inc(times_c, 1)

                two_slots(pool, front, back)

            @block.tensor
            def _(pe):
                pe.sem_inc(b_used, 2)
                pe.sem_inc(c_ready, 2)
                x_of = lambda b: core.xnT[:, bass.ds(b * SEQ, SEQ)]

                def front(b, s):
                    for j in range(SCAN_CHUNKS):
                        pe.wait_ge(b_used, b * SCAN_CHUNKS + j + 1)
                        for n in range(CHN):
                            at = j * CHN + n
                            ins = nc.tensor.matmul(pB[j % 2][:, n, :], w["b"][:, at:at + 1].broadcast_to([P, P]), x_of(b), start=True, stop=True)
                        ins.then_inc(b_psum, 1)

                def back(b, s):
                    for i in range(2 * SCAN_CHUNKS):
                        pe.wait_ge(c_ready, b * 2 * SCAN_CHUNKS + i + 1)
                        for n in range(2):
                            at = i * 2 + n
                            ins = nc.tensor.matmul(pC[i % 2][:, n, :], w["c"][:, at:at + 1].broadcast_to([P, P]), x_of(b), start=True, stop=True)
                        ins.then_inc(c_psum, 1)
                    pe.wait_ge(y_ready, b + 1)
                    for t in range(2):
                        ins = nc.tensor.transpose(pX[s][:, t * P:(t + 1) * P], y[:, s, t * P:(t + 1) * P], core.ident[:, :])
                    ins.then_inc(yT_ready, 1)

                two_slots(pe, front, back)

            @block.scalar
            def _(a):
                nc.scalar.activation(pos_a[:, :], w["a_log"], ACT.Exp).then_inc(set_up, 1)
                a.wait_ge(set_up, 4)

                def front(b, s):
                    for n in range(STATES):
                        ins = nc.scalar.activation(decay[s][:, n, 1:SEQ], delta[:, bass.ds(b * SEQ + 1, SEQ - 1)], ACT.Exp, scale=neg_a[:, n:n + 1])
                        if n % CHN == CHN - 1:
                            ins.then_inc(decay_ready, 1)

                def back(b, s):
                    for i in range(2 * SCAN_CHUNKS):
                        a.wait_ge(c_psum, b * 2 * SCAN_CHUNKS + i + 1)
                        if i % 2 == 0:
                            a.wait_ge(times_c, b * SCAN_CHUNKS)
                        nc.scalar.copy(c_all[:, 2 * i:2 * i + 2, :], pC[i % 2][:, :, :]).then_inc(c_ready, 1)

                two_slots(a, front, back)

            @block.vector
            def _(v):
                v.wait_ge(set_up, 3)
                nc.vector.tensor_scalar(neg_a[:, :], pos_a[:, :], -1.0, None, ALU.mult).then_inc(set_up, 1)

                def front(b, s):
                    def enter(j):
                        v.wait_ge(b_psum, b * SCAN_CHUNKS + j + 1)
                        nc.vector.tensor_tensor(h[s][:, j * CHN:(j + 1) * CHN, :], pB[j % 2][:, :, :], bc(du[:, s, :], 1, CHN), ALU.mult).then_inc(b_used, 1)

                    v.wait_ge(du_ready, b + 1)
                    enter(0)
                    for j in range(SCAN_CHUNKS):
                        if j + 1 < SCAN_CHUNKS:
                            enter(j + 1)
                        v.wait_ge(b_used, b * SCAN_CHUNKS + j + 3)
                        v.wait_ge(decay_ready, b * SCAN_CHUNKS + j + 1)
                        flat = lambda t: t[:, j * CHN:(j + 1) * CHN, :].rearrange("p n s -> p (n s)")
                        nc.vector.tensor_tensor_scan(flat(h[s]), flat(decay[s]), flat(h[s]), 0.0, ALU.mult, ALU.add).then_inc(scanned, 1)

                def back(b, s):
                    v.wait_ge(times_c, (b + 1) * SCAN_CHUNKS)
                    nc.vector.tensor_reduce(y[:, s, :], h[s][:, :, :].rearrange("p n s -> p s n"), AX.X, ALU.add).then_inc(summed, 1)
                    v.wait_ge(summed, b + 1)
                    nc.vector.scalar_tensor_tensor(y[:, s, :], core.xnT[:, bass.ds(b * SEQ, SEQ)], w["skip"], y[:, s, :], ALU.mult, ALU.add).then_inc(y_ready, 1)
                    v.wait_ge(yT_ready, b + 1)
                    x = core.x_res[:, bass.ds(b * 2, 2), :]
                    nc.vector.tensor_tensor(x, x, pX[s][:, 0:2 * D].rearrange("p (t d) -> p t d", t=2), ALU.add).then_inc(added, 1)

                two_slots(v, front, back)


def scan3(core, blob, offsets):
    nc = core.nc
    TAPS = 4
    GROUPS = TOK // BANK
    with Stage(core, "scan3") as st:
        w = st.weights(blob, offsets)
        layer_norm(core, st)
        bank = [st.ps(f"bank{i}", [P, BANK]) for i in range(8)]
        delta = st.sb("delta", [P, TOK])
        u = st.sb("u", [P, TOK])
        gate = st.sb("gate", [P, TOK])

        conv = st.sb("conv", [P, 2, 2, SEQ])
        z_psum, gate_ready, conv_chain, conv_ready, u_ready = (st.sem(n) for n in ("z_psum", "gate_ready", "conv_chain", "conv_ready", "u_ready"))
        with nc.Block() as block:
            @block.tensor
            def _(pe):
                pe.sem_inc(gate_ready, 2)
                with pe.Fori(0, GROUPS // 2) as g:
                    for s in range(2):
                        pe.wait_ge(gate_ready, 2 * g + s + 1)
                        nc.tensor.matmul(bank[s][:, :], w["wz"], core.xnT[:, bass.ds((2 * g + s) * BANK, BANK)], start=True, stop=True).then_inc(z_psum, 1)

            @block.scalar
            def _(a):
                with a.Fori(0, GROUPS // 2) as g:
                    for s in range(2):
                        cols = bass.ds((2 * g + s) * BANK, BANK)
                        a.wait_ge(z_psum, 2 * g + s + 1)
                        nc.scalar.activation(gate[:, cols], bank[s][:, :], ACT.Silu).then_inc(gate_ready, 1)
                        a.wait_ge(conv_ready, 2 * g + s + 1)
                        nc.scalar.activation(u[:, cols], conv[:, s, :, :].rearrange("p b s -> p (b s)"), ACT.Silu).then_inc(u_ready, 1)

            @block.vector
            def _(v):
                v.sem_inc(u_ready, 2)
                with v.Fori(0, GROUPS // 2) as g:
                    c = Chain(v, conv_chain, g * 2 * (TAPS - 1))
                    for s in range(2):
                        x = core.xnT[:, bass.ds((2 * g + s) * BANK, BANK)].rearrange("p (b s) -> p b s", b=2)
                        out = conv[:, s, :, :]
                        v.wait_ge(u_ready, 2 * g + s + 1)
                        ins = nc.vector.tensor_scalar(out, x, w["conv"][:, TAPS - 1:TAPS], None, ALU.mult)
                        for back in range(1, TAPS):
                            c.link(ins)
                            ins = nc.vector.scalar_tensor_tensor(out[:, :, back:SEQ], x[:, :, 0:SEQ - back], w["conv"][:, TAPS - 1 - back:TAPS - back],
                                                                 out[:, :, back:SEQ], ALU.mult, ALU.add)
                        ins.then_inc(conv_ready, 1)

        step_sizes(core, st, w, bank, delta)

        pC, pSum, pY = bank[0:2], bank[2], bank[3]
        decay = st.sb("decay", [P, STATES, SEQ])
        h = [st.sb(f"h{i}", [P, STATES, SEQ]) for i in range(2)]
        c_all = st.sb("c_all", [P, STATES, SEQ])
        prev = st.sb("prev", [P, 2, 2, SEQ])
        du = st.sb("du", [P, 2, SEQ])
        du_small = st.sb("du_small", [P, STATES, SEQ])
        yT = st.sb("yT", [P, SEQ])
        pos_a, neg_a, small, inv_a, den = (st.sb(n, [P, STATES]) for n in ("pos_a", "neg_a", "small", "inv_a", "den"))
        names = ("set_up", "setup_chain", "du_made", "prev_ready", "du_ready", "decay_ready", "entered", "shrunk", "scanned", "zeroed", "c_psum", "c_ready", "times_c",
                 "sum_psum", "skip_added", "y_ready", "out_psum", "added")
        (set_up, setup_chain, du_made, prev_ready, du_ready, decay_ready, entered, shrunk, scanned, zeroed, c_psum, c_ready, times_c,
         sum_psum, skip_added, y_ready, out_psum, added) = (st.sem(n) for n in names)
        with nc.Block() as block:
            @block.gpsimd
            def _(pool):
                pool.wait_ge(set_up, 2)

                def front(b, s):
                    for i, src in enumerate((delta, u)):
                        nc.gpsimd.tensor_copy(prev[:, s, i, 1:SEQ], src[:, bass.ds(b * SEQ, SEQ - 1)])
                        ins = nc.gpsimd.tensor_copy(prev[:, s, i, 0:1], src[:, bass.ds(b * SEQ, 1)])
                    ins.then_inc(prev_ready, 1)
                    pool.wait_ge(prev_ready, b + 1)
                    nc.gpsimd.tensor_tensor(du[:, s, :], prev[:, s, 0, :], prev[:, s, 1, :], ALU.mult).then_inc(du_made, 1)
                    pool.wait_ge(du_made, b + 1)
                    if not isinstance(b, int) or b > 0:
                        pool.wait_ge(shrunk, b * SCAN_CHUNKS)
                    nc.gpsimd.tensor_tensor(du_small[:, :, :], bc(du[:, s, :], 1, STATES), bc(small[:, :], 2, SEQ), ALU.mult).then_inc(du_ready, 1)

                def back(b, s):
                    for j in range(SCAN_CHUNKS):
                        part = slice(j * CHN, (j + 1) * CHN)
                        pool.wait_ge(scanned, b * SCAN_CHUNKS + j + 1)
                        pool.wait_ge(c_ready, (b * SCAN_CHUNKS + j) * 2 + 4)
                        nc.gpsimd.tensor_tensor(h[s][:, part, :], h[s][:, part, :], c_all[:, part, :], ALU.mult).then_inc(times_c, 1)

                two_slots(pool, front, back)

            @block.tensor
            def _(pe):
                pe.sem_inc(c_ready, 2)

                def front(b, s):
                    for i in range(2 * SCAN_CHUNKS):
                        pe.wait_ge(c_ready, b * 2 * SCAN_CHUNKS + i + 1)
                        for n in range(2):
                            at = i * 2 + n
                            ins = nc.tensor.matmul(pC[i % 2][:, n * SEQ:(n + 1) * SEQ], w["c"][:, at:at + 1].broadcast_to([P, P]),
                                                   core.xnT[:, bass.ds(b * SEQ, SEQ)], start=True, stop=True)
                        ins.then_inc(c_psum, 1)

                def back(b, s):
                    for n in range(STATES):
                        if n % CHN == 0:
                            pe.wait_ge(times_c, b * SCAN_CHUNKS + n // CHN + 1)
                        ins = nc.tensor.matmul(pSum[:, 0:SEQ], core.ident[:, :], h[s][:, n, :], start=(n == 0), stop=(n == STATES - 1))
                    ins.then_inc(sum_psum, 1)
                    pe.wait_ge(y_ready, b + 1)
                    for t in range(2):
                        ins = nc.tensor.matmul(pY[:, t * P:(t + 1) * P], yT[:, t * P:(t + 1) * P], w["wo"], start=True, stop=True)
                    ins.then_inc(out_psum, 1)

                two_slots(pe, front, back)

            @block.scalar
            def _(a):
                nc.scalar.activation(pos_a[:, :], w["a_log"], ACT.Exp).then_inc(set_up, 1)
                a.wait_ge(set_up, 2)

                def front(b, s):
                    a.wait_ge(prev_ready, b + 1)
                    for j in range(SCAN_CHUNKS):
                        if not isinstance(b, int) or b > 0:
                            a.wait_ge(scanned, (b - 1) * SCAN_CHUNKS + j + 1)
                        for n in range(j * CHN, (j + 1) * CHN):
                            ins = nc.scalar.activation(decay[:, n, :], prev[:, s, 0, :], ACT.Exp, scale=neg_a[:, n:n + 1])
                        ins.then_inc(decay_ready, 1)
                    for i in range(2 * SCAN_CHUNKS):
                        a.wait_ge(c_psum, b * 2 * SCAN_CHUNKS + i + 1)
                        if i == 0:
                            a.wait_ge(times_c, b * SCAN_CHUNKS)
                        nc.scalar.copy(c_all[:, 2 * i:2 * i + 2, :], pC[i % 2][:, :].rearrange("p (n s) -> p n s", n=2)).then_inc(c_ready, 1)

                def back(b, s):
                    pass

                two_slots(a, front, back)

            @block.vector
            def _(v):
                c = Chain(v, setup_chain)
                v.wait_ge(set_up, 1)
                c.link(nc.vector.tensor_scalar(neg_a[:, :], pos_a[:, :], -1.0, None, ALU.mult))
                c.link(nc.vector.tensor_scalar(small[:, :], pos_a[:, :], 1e-5, None, ALU.is_lt))
                c.link(nc.vector.tensor_scalar(den[:, :], neg_a[:, :], 1e-10, None, ALU.add))
                c.link(nc.vector.tensor_tensor(den[:, :], den[:, :], small[:, :], ALU.add))
                c.link(nc.vector.reciprocal(den[:, :], den[:, :]))
                c.link(nc.vector.tensor_scalar(inv_a[:, :], small[:, :], -1.0, 1.0, ALU.mult, ALU.add))
                nc.vector.tensor_tensor(inv_a[:, :], inv_a[:, :], den[:, :], ALU.mult).then_inc(set_up, 1)
                v.wait_ge(set_up, 2)

                def front(b, s):
                    v.wait_ge(du_ready, b + 1)
                    for j in range(SCAN_CHUNKS):
                        part = slice(j * CHN, (j + 1) * CHN)
                        v.wait_ge(decay_ready, b * SCAN_CHUNKS + j + 1)
                        nc.vector.scalar_tensor_tensor(h[s][:, part, :], decay[:, part, :], -1.0, bc(prev[:, s, 1, :], 1, CHN), ALU.add,
                                                       ALU.mult).then_inc(entered, 1)
                        v.wait_ge(entered, b * SCAN_CHUNKS + j + 1)
                        nc.vector.memset(decay[:, part, 0:1], 0.0).then_inc(zeroed, 1)
                        for n in range(j * CHN, (j + 1) * CHN):
                            ins = nc.vector.scalar_tensor_tensor(h[s][:, n, :], h[s][:, n, :], inv_a[:, n:n + 1], du_small[:, n, :], ALU.mult, ALU.add)
                        ins.then_inc(shrunk, 1)
                        v.wait_ge(shrunk, b * SCAN_CHUNKS + j + 1)
                        v.wait_ge(zeroed, b * SCAN_CHUNKS + j + 1)
                        flat = lambda t: t[:, part, :].rearrange("p n s -> p (n s)")
                        nc.vector.tensor_tensor_scan(flat(h[s]), flat(decay), flat(h[s]), 0.0, ALU.mult, ALU.add).then_inc(scanned, 1)

                def back(b, s):
                    cols = bass.ds(b * SEQ, SEQ)
                    v.wait_ge(sum_psum, b + 1)
                    nc.vector.scalar_tensor_tensor(yT[:, :], u[:, cols], w["skip"], pSum[:, 0:SEQ], ALU.mult, ALU.add).then_inc(skip_added, 1)
                    v.wait_ge(skip_added, b + 1)
                    nc.vector.tensor_tensor(yT[:, :], yT[:, :], gate[:, cols], ALU.mult).then_inc(y_ready, 1)
                    v.wait_ge(out_psum, b + 1)
                    x = core.x_res[:, bass.ds(b * 2, 2), :]
                    nc.vector.tensor_tensor(x, x, pY[:, 0:2 * D].rearrange("p (t d) -> p t d", t=2), ALU.add).then_inc(added, 1)

                two_slots(v, front, back)


ATTN_A2_HD = D // HEADS
BD = 16
WINDOW = 64
PAD = WINDOW - 1
HALF = P // BD
SLOTS = P // HEADS
ROWS = WINDOW // SLOTS
KINDS = 2


def attn_a2_weights(w):
    def place(out_w):
        a = np.zeros((HALF, BD, 2, 2, 2, HEADS), np.float32)
        for slot in range(2):
            for half in range(2):
                for h in range(HALF):
                    a[h, :, slot, half, slot, half * HALF + h] = out_w.reshape(BD)
        return a.reshape(P, -1)

    def diag(m):
        a = np.zeros((HALF, BD, HALF, BD), np.float32)
        for h in range(HALF):
            a[h, :, h, :] = m
        return a.reshape(P, P)

    slot, head = np.arange(P) // HEADS, np.arange(P) % HEADS
    to_head = np.arange(D) // ATTN_A2_HD
    spread = [((slot[:, None] == s) & (head[:, None] == to_head[None, :])).astype(np.float32) for s in range(SLOTS)]
    seen = np.where(np.arange(SLOTS)[None, :] >= slot[:, None], np.float32(0.0), np.float32(NEG))
    strain, b = w["strain_fused_w"], w["strain_fused_b"]
    tall = lambda a: np.broadcast_to(a.reshape(1, 1), (P, 1))
    return pack([
        ("disp", w["W_disp"].T), ("val", w["W_val"].T), ("out", w["c_proj_w"].T),
        ("strain", np.concatenate([diag(strain[0:BD].T), diag(strain[BD:].T)], axis=1)),
        ("bond_b", np.tile(b[0:BD], HALF)), ("damage_b", np.tile(b[BD:], HALF)), ("damage_out_b", tall(w["damage_out_b"])),
        ("pos_proj", np.tile(w["pos_proj_w"].T, (1, HALF))), ("pos_emb", w["rel_pos_emb"][::-1].T),
        ("place", np.concatenate([place(w["bond_out_w"]), place(w["damage_out_w"])], axis=1)),
        ("spread", np.concatenate(spread + [sum(spread)], axis=1)),
        ("seen", seen),
    ])


def attn_a2(core, blob, offsets):
    nc = core.nc
    GROUPS = TOK // BANK
    with Stage(core, "attn_a2") as st:
        w = st.weights(blob, offsets)
        layer_norm(core, st)
        bank = [st.ps(f"bank{i}", [P, BANK]) for i in range(8)]
        feat = st.sb("feat", [P, KINDS, 2, BATCH, PAD + SEQ])
        val = st.sb("val", [P, BATCH, PAD + SEQ])
        lag_b = st.sb("lag_b", [P, WINDOW])
        half_out_b = st.sb("half_out_b", [P, 1])
        two = lambda ap: ap.rearrange("p (b s) -> p b s", b=2)

        disp = st.sb("disp", [P, 2, BANK])
        names = ("padded", "disp_psum", "disp_ready", "feat_psum", "feat_ready", "val_psum", "val_ready", "pos_psum", "misc")
        padded, disp_psum, disp_ready, feat_psum, feat_ready, val_psum, val_ready, pos_psum, misc = (st.sem(n) for n in names)
        with nc.Block() as block:
            @block.gpsimd
            def _(pool):
                nc.gpsimd.memset(feat[:, :, :, :, 0:PAD].rearrange("p k h b s -> p (k h b) s"), 0.0).then_inc(padded, 1)
                nc.gpsimd.memset(val[:, :, 0:PAD], 0.0).then_inc(padded, 1)

            @block.tensor
            def _(pe):
                nc.tensor.matmul(bank[7][:, 0:WINDOW], w["pos_proj"], w["pos_emb"], start=True, stop=True).then_inc(pos_psum, 1)
                with pe.Fori(0, GROUPS) as g:
                    x = core.xnT[:, bass.ds(g * BANK, BANK)]
                    for half in range(2):
                        nc.tensor.matmul(bank[half][:, :], w["disp"][:, half * P:(half + 1) * P], x, start=True, stop=True).then_inc(disp_psum, 1)
                    pe.wait_ge(val_ready, g)
                    nc.tensor.matmul(bank[2][:, :], w["val"], x, start=True, stop=True).then_inc(val_psum, 1)
                    for half in range(2):
                        pe.wait_ge(disp_ready, 2 * g + half + 1)
                        pe.wait_ge(feat_ready, 2 * g)
                        for kind in range(KINDS):
                            ins = nc.tensor.matmul(bank[3 + 2 * half + kind][:, :], w["strain"][:, kind * P:(kind + 1) * P], disp[:, half, :], start=True, stop=True)
                        ins.then_inc(feat_psum, 1)

            @block.scalar
            def _(a):
                with a.Fori(0, GROUPS) as g:
                    for half in range(2):
                        a.wait_ge(disp_psum, 2 * g + half + 1)
                        a.wait_ge(feat_psum, 2 * g)
                        nc.scalar.copy(disp[:, half, :], bank[half][:, :]).then_inc(disp_ready, 1)
                    a.wait_ge(val_psum, g + 1)
                    nc.scalar.copy(val[:, bass.ds(2 * g, 2), PAD:], two(bank[2][:, :])).then_inc(val_ready, 1)

            @block.vector
            def _(v):
                nc.vector.tensor_scalar(half_out_b[:, :], w["damage_out_b"], 0.5, None, ALU.mult)
                v.wait_ge(pos_psum, 1)
                nc.vector.tensor_scalar(lag_b[:, :], bank[7][:, 0:WINDOW], w["bond_b"], None, ALU.add)
                with v.Fori(0, GROUPS) as g:
                    for half in range(2):
                        v.wait_ge(feat_psum, 2 * g + half + 1)
                        for kind in range(KINDS):
                            ins = nc.vector.tensor_copy(feat[:, kind, half, bass.ds(2 * g, 2), PAD:], two(bank[3 + 2 * half + kind][:, :]))
                        ins.then_inc(feat_ready, 1)

        logit = core.xn[:, :, :].rearrange("p t d -> p (t d)").rearrange("p (r s) -> p r s", r=ROWS)
        RING = 8
        more = st.sb("more", [P, 4, 2, 2, SEQ])
        first_half = core.xnT[:, :].rearrange("p (i h b s) -> p i h b s", i=4, h=2, b=2)
        ring = lambda i, n=1: (first_half if i % RING < 4 else more)[:, i % 4:i % 4 + n]
        scratch = disp
        feat_now = st.sb("feat_now", [P, KINDS, 2, 2, PAD + SEQ])
        val_now = st.sb("val_now", [P, 2, PAD + SEQ])
        slot_max, acc_even, acc_odd = (st.sb(n, [P, BANK]) for n in ("slot_max", "acc_even", "acc_odd"))
        neg_max = st.sb("neg_max", [P, 4, HEADS])
        neg_max_wide = st.sb("neg_max_wide", [P, 4, SLOTS, HEADS])
        p_bond, p_damage, p_wide, p_max, p_x = bank[0:2], bank[2:4], bank[4:6], bank[6], bank[7]
        names = ("cleared", "feat_copied", "val_copied", "diff_v", "diff_p", "gelu_ready", "placed", "tanh_ready", "combined", "masked", "slot_max_ready", "max_psum", "neg_max_done", "neg_max_ready",
                 "neg_max_psum", "shifted", "prob_ready", "den_psum", "wide_even", "wide_odd", "weighted_even", "weighted_odd", "even_added", "odd_added", "inv_ready", "oT_ready",
                 "y_ready", "added", "dve2")
        (cleared, feat_copied, val_copied, diff_v, diff_p, gelu_ready, placed, tanh_ready, combined, masked, slot_max_ready, max_psum, neg_max_done, neg_max_ready,
         neg_max_psum, shifted, prob_ready, den_psum, wide_even, wide_odd, weighted_even, weighted_odd, even_added, odd_added, inv_ready, oT_ready,
         y_ready, added, dve2) = (st.sem(n) for n in names)
        pairs = [(row, slot, slot + 2) for row in range(ROWS) for slot in range(SLOTS) if slot % 4 < 2]
        units = [(row, slots, kind) for row, *slots in pairs for kind in range(KINDS)]
        UNITS = len(units)
        PER_ROW = UNITS // ROWS
        RING_UNITS = RING // 2
        reach = lambda row: slice(row * SLOTS, SEQ)
        N_DIFF_V, N_DIFF_P = 3 * len(pairs), len(pairs)

        def difference(eng, u, n, row, slot, kind):
            both = feat_now[:, kind].rearrange("p h b s -> p (h b) s")
            lag, at = row * SLOTS + slot, PAD + row * SLOTS
            return eng.tensor_tensor(ring(2 * u + n)[:, 0].rearrange("p h b s -> p (h b) s")[:, :, reach(row)],
                                     both[:, :, at - lag:PAD - lag + SEQ], both[:, :, at:PAD + SEQ], ALU.subtract)

        wide_psum, weighted = (wide_even, wide_odd), (weighted_even, weighted_odd)
        LAGS = WINDOW // 2
        PARTS = 4
        with nc.Block() as block:
            @block.tensor
            def _(pe):
                pe.sem_inc(placed, RING_UNITS)
                with pe.Fori(0, GROUPS) as g:
                    for u, (row, slots, kind) in enumerate(units):
                        if u % PER_ROW == 0:
                            pe.wait_ge(combined, g * ROWS + row + 1)
                        pe.wait_ge(gelu_ready, g * UNITS + u + 1)
                        for half in range(2):
                            for n, slot in enumerate(slots):
                                at = ((kind * 2 + slot % 2) * 2 + half) * 32
                                part = slice(slot // 2 * 32, (slot // 2 + 1) * 32)
                                ins = nc.tensor.matmul(two((p_bond, p_damage)[kind][row % 2][part, :])[:, :, reach(row)], w["place"][:, at:at + 32],
                                                       ring(2 * u + n)[:, 0, half, :, reach(row)],
                                                       start=(slot % 2 == 0 and half == 0), stop=(slot % 2 == 1 and half == 1),
                                                       tile_position=(0, part.start))
                        ins.then_inc(placed, 1)
                    pe.wait_ge(slot_max_ready, g + 1)
                    for t in range(4):
                        ins = nc.tensor.transpose(p_max[:, t * P:(t + 1) * P], slot_max[:, t * P:(t + 1) * P], core.ident[:, :])
                    ins.then_inc(max_psum, 1)
                    pe.wait_ge(neg_max_ready, g + 1)
                    for t in range(4):
                        ins = nc.tensor.matmul(p_x[:, t * P:(t + 1) * P], neg_max_wide[:, t, :, :].rearrange("p s h -> p (s h)"), core.ident[:, :],
                                               start=True, stop=True)
                    ins.then_inc(neg_max_psum, 1)
                    for row in range(ROWS):
                        pe.wait_ge(prob_ready, g * PARTS + row * PARTS // ROWS + 1)
                        ins = nc.tensor.matmul(two(p_max[:, :])[:, :, reach(row)], w["spread"][:, SLOTS * D:(SLOTS + 1) * D], two(logit[:, row, :])[:, :, reach(row)],
                                               start=(row == 0), stop=(row == ROWS - 1))
                    ins.then_inc(den_psum, 1)
                    for lag in range(WINDOW):
                        slot = lag % SLOTS
                        pe.wait_ge(weighted[lag % 2], g * LAGS + lag // 2 + 1)
                        row = lag // SLOTS
                        nc.tensor.matmul(two(p_wide[lag % 2][:, :])[:, :, reach(row)], w["spread"][:, slot * D:(slot + 1) * D], two(logit[:, row, :])[:, :, reach(row)],
                                         start=True, stop=True).then_inc(wide_psum[lag % 2], 1)
                    pe.wait_ge(oT_ready, g + 1)
                    for t in range(4):
                        ins = nc.tensor.matmul(p_x[:, t * P:(t + 1) * P], slot_max[:, t * P:(t + 1) * P], w["out"], start=True, stop=True)
                    ins.then_inc(y_ready, 1)

            @block.scalar
            def _(a):
                with a.Fori(0, GROUPS) as g:
                    def tanh(row):
                        a.wait_ge(placed, g * UNITS + (row + 1) * PER_ROW + RING_UNITS)
                        a.wait_ge(combined, g * ROWS + row + 1)
                        nc.scalar.activation(two(scratch[:, row % 2, :])[:, :, reach(row)], two(p_damage[row % 2][:, :])[:, :, reach(row)],
                                             ACT.Tanh, bias=half_out_b[:, :], scale=0.5).then_inc(tanh_ready, 1)

                    for u, (row, slots, kind) in enumerate(units):
                        pair = u // 2
                        a.wait_ge(diff_v, g * N_DIFF_V + 3 * pair + (2, 3)[kind])
                        if kind == 0:
                            for n, slot in enumerate(slots):
                                x = ring(2 * u + n)[:, 0].rearrange("p h b s -> p (h b) s")[:, :, reach(row)]
                                lag = row * SLOTS + slot
                                ins = nc.scalar.activation(x, x, ACT.Gelu, bias=lag_b[:, lag:lag + 1])
                        else:
                            a.wait_ge(diff_p, g * N_DIFF_P + pair + 1)
                            x = ring(2 * u, 2).rearrange("p i h b s -> p (i h b) s")[:, :, reach(row)]
                            ins = nc.scalar.activation(x, x, ACT.Gelu, bias=w["damage_b"])
                        ins.then_inc(gelu_ready, 1)
                        if row > 0 and u % PER_ROW == 1:
                            tanh(row - 1)
                    tanh(ROWS - 1)
                    for j in range(PARTS):
                        rows = slice(j * ROWS // PARTS, (j + 1) * ROWS // PARTS)
                        a.wait_ge(shifted, g * PARTS + j + 1)
                        nc.scalar.activation(logit[:, rows, :], logit[:, rows, :], ACT.Exp).then_inc(prob_ready, 1)

            @block.gpsimd
            def _(pool):
                with pool.Fori(0, GROUPS) as g:
                    now = bass.ds(2 * g, 2)
                    pool.wait_ge(diff_v, g * N_DIFF_V)
                    pool.wait_ge(diff_p, g * N_DIFF_P)
                    for kind in range(KINDS):
                        for half in range(2):
                            ins = nc.gpsimd.tensor_copy(feat_now[:, kind, half, :, :], feat[:, kind, half, now, :])
                    ins.then_inc(feat_copied, 1)
                    for parity in range(2):
                        pool.wait_ge(weighted[parity], g * LAGS + 1)
                    nc.gpsimd.tensor_copy(val_now[:, :, :], val[:, now, :]).then_inc(val_copied, 1)
                    for row in range(1, ROWS):
                        ins = nc.gpsimd.memset(two(logit[:, row, :])[:, :, 0:row * SLOTS], NEG)
                    ins.then_inc(masked, 1)

                    def mask(row):
                        pool.wait_ge(combined, g * ROWS + row + 3)
                        x = two(logit[:, row, :])[:, :, row * SLOTS:(row + 1) * SLOTS]
                        nc.gpsimd.tensor_tensor(x, x, bc(w["seen"], 1, 2), ALU.add).then_inc(masked, 1)

                    pool.wait_ge(feat_copied, g + 1)
                    for u, (row, slots, kind) in enumerate(units):
                        if kind == 1:
                            pool.wait_ge(placed, g * UNITS + u + 1)
                            difference(nc.gpsimd, u, 1, row, slots[1], kind).then_inc(diff_p, 1)
                        if row > 0 and u % PER_ROW == 5:
                            mask(row - 1)
                    mask(ROWS - 1)
                    nc.gpsimd.memset(acc_even[:, :], 0.0).then_inc(cleared, 1)
                    for lag in range(0, WINDOW, 2):
                        pool.wait_ge(weighted_even, g * LAGS + lag // 2 + 2)
                        if lag == 0:
                            pool.wait_ge(cleared, g + 1)
                        else:
                            pool.wait_ge(even_added, g * LAGS + lag // 2)
                        part = lambda x: two(x)[:, :, reach(lag // SLOTS)]
                        nc.gpsimd.tensor_tensor(part(acc_even[:, :]), part(acc_even[:, :]), part(scratch[:, 0, :]), ALU.add).then_inc(even_added, 1)

            @block.vector
            def _(v):
                v.sem_inc(combined, 2)
                v.sem_inc(weighted_even, 1)
                v.sem_inc(weighted_odd, 1)
                with v.Fori(0, GROUPS) as g:
                    v.wait_ge(feat_copied, g + 1)

                    def combine(row):
                        v.wait_ge(tanh_ready, g * ROWS + row + 1)
                        part = lambda x: two(x)[:, :, reach(row)]
                        nc.vector.scalar_tensor_tensor(part(logit[:, row, :]), part(scratch[:, row % 2, :]), -5.0, part(p_bond[row % 2][:, :]), ALU.mult, ALU.add).then_inc(combined, 1)

                    for u, (row, slots, kind) in enumerate(units):
                        v.wait_ge(placed, g * UNITS + u + 1)
                        for n, slot in enumerate(slots):
                            if kind == 0 or n == 0:
                                difference(nc.vector, u, n, row, slot, kind).then_inc(diff_v, 1)
                        if row > 0 and u % PER_ROW == 3:
                            combine(row - 1)
                    combine(ROWS - 1)
                    v.wait_ge(masked, (g + 1) * (ROWS + 1))
                    nc.vector.tensor_reduce(slot_max[:, :], logit.rearrange("p r s -> p s r"), AX.X, ALU.max).then_inc(slot_max_ready, 1)
                    v.wait_ge(max_psum, g + 1)
                    by_head = p_max[:, :].rearrange("p (t s h) -> p t h s", t=4, s=SLOTS)
                    nc.vector.tensor_reduce(neg_max[:, :, :], by_head, AX.X, ALU.max, negate=True).then_inc(neg_max_done, 1)
                    v.wait_ge(neg_max_done, g + 1)
                    nc.vector.tensor_copy(neg_max_wide[:, :, :, :], bc(neg_max[:, :, :], 2, SLOTS)).then_inc(neg_max_ready, 1)
                    v.wait_ge(neg_max_psum, g + 1)
                    for j in range(PARTS):
                        rows = slice(j * ROWS // PARTS, (j + 1) * ROWS // PARTS)
                        nc.vector.tensor_tensor(logit[:, rows, :], logit[:, rows, :], bc(p_x[:, :], 1, ROWS // PARTS), ALU.add).then_inc(shifted, 1)
                    v.wait_ge(val_copied, g + 1)
                    for lag in range(WINDOW):
                        v.wait_ge(wide_psum[lag % 2], g * LAGS + lag // 2 + 1)
                        if lag % 2 == 0 and lag >= 2:
                            v.wait_ge(even_added, g * LAGS + lag // 2)
                        start = lag // SLOTS * SLOTS
                        part = lambda x: two(x)[:, :, start:]
                        nc.vector.tensor_tensor(part(scratch[:, lag % 2, :]), part(p_wide[lag % 2][:, :]), val_now[:, :, PAD - lag + start:PAD - lag + SEQ],
                                                ALU.mult).then_inc(weighted[lag % 2], 1)
                        if lag % 2 == 1:
                            v.wait_ge(weighted_odd, g * LAGS + lag // 2 + 2)
                            n = g * LAGS + lag // 2
                            if lag == 1:
                                nc.vector.tensor_copy(acc_odd[:, :], scratch[:, 1, :]).then_inc(odd_added, 1)
                            else:
                                nc.vector.tensor_tensor(part(acc_odd[:, :]), part(acc_odd[:, :]), part(scratch[:, 1, :]), ALU.add).then_inc(odd_added, 1)
                            v.wait_ge(odd_added, n + 1)
                    v.wait_ge(even_added, (g + 1) * LAGS)
                    c = Chain(v, dve2, g)
                    c.link(nc.vector.tensor_tensor(acc_odd[:, :], acc_odd[:, :], acc_even[:, :], ALU.add))
                    v.wait_ge(den_psum, g + 1)
                    nc.vector.reciprocal(slot_max[:, :], p_max[:, :]).then_inc(inv_ready, 1)
                    v.wait_ge(inv_ready, g + 1)
                    nc.vector.tensor_tensor(slot_max[:, :], acc_odd[:, :], slot_max[:, :], ALU.mult).then_inc(oT_ready, 1)
                    v.wait_ge(y_ready, g + 1)
                    x = core.x_res[:, bass.ds(4 * g, 4), :]
                    nc.vector.tensor_tensor(x, x, p_x[:, :].rearrange("p (t d) -> p t d", t=4), ALU.add).then_inc(added, 1)


FFN2_EXPERTS = 8
FFN2_TOP = 2
FFN2_HID = 2 * D
CH = FFN2_HID // P


def ffn2_weights(w):
    return pack([
        ("router", w["router_w"].T), ("earlier", earlier_table(FFN2_EXPERTS)),
        ("w1", w["w1"].transpose(2, 0, 1).reshape(D, FFN2_EXPERTS * FFN2_HID)),
        ("w2", w["w2"].transpose(2, 0, 1).reshape(CH, P, FFN2_EXPERTS, D).transpose(1, 2, 0, 3).reshape(P, FFN2_EXPERTS * FFN2_HID)),
    ])


def ffn2(core, blob, offsets):
    nc = core.nc
    GROUPS = TOK // BANK
    with Stage(core, "ffn2") as st:
        w = st.weights(blob, offsets)
        layer_norm(core, st)
        w1 = w["w1"].rearrange("p (e c h) -> p e c h", e=FFN2_EXPERTS, c=CH)
        w2 = w["w2"].rearrange("p (e c d) -> p e c d", e=FFN2_EXPERTS, c=CH)
        bank = [st.ps(f"bank{i}", [P, BANK]) for i in range(8)]
        logit_psum = bank[0][:, 0:TILES * FFN2_EXPERTS].rearrange("p (t e) -> p t e", t=TILES)
        router_logits(core, w["router"], lambda t: logit_psum[:, bass.ds(t, 1), :].squeeze(1), FFN2_EXPERTS, st)

        gate = st.sb("gate", [P, TILES, FFN2_EXPERTS])
        logit, sel, rank = (st.sb(n, [P, TILES, FFN2_EXPERTS]) for n in ("logit", "sel", "rank"))
        above, same = (st.sb(n, [P, TILES, FFN2_EXPERTS, FFN2_EXPERTS]) for n in ("above", "same"))
        best, total = st.sb("best", [P, TILES]), st.sb("total", [P, TILES])
        dve, centred, exp_ready = st.sem("dve"), st.sem("centred"), st.sem("exp_ready")
        with nc.Block() as block:
            @block.vector
            def _(v):
                c = Chain(v, dve)
                c.link(nc.vector.tensor_copy(logit[:, :, :], logit_psum))
                c.link(nc.vector.tensor_reduce(best[:, :], logit[:, :, :], AX.X, ALU.max))
                nc.vector.tensor_tensor(gate[:, :, :], logit[:, :, :], bc(best[:, :], 2, FFN2_EXPERTS), ALU.subtract).then_inc(centred, 1)
                link_ranks(nc, c, rank[:, :, :], logit[:, :, :], above[:, :, :, :], same[:, :, :, :], w["earlier"], FFN2_EXPERTS)
                c.link(nc.vector.tensor_scalar(sel[:, :, :], rank[:, :, :], float(FFN2_TOP), None, ALU.is_lt))
                v.wait_ge(exp_ready, 1)
                c.link(nc.vector.tensor_tensor(gate[:, :, :], gate[:, :, :], sel[:, :, :], ALU.mult))
                c.link(nc.vector.tensor_reduce(total[:, :], gate[:, :, :], AX.X, ALU.add))
                c.link(nc.vector.reciprocal(total[:, :], total[:, :]))
                nc.vector.tensor_tensor(gate[:, :, :], gate[:, :, :], bc(total[:, :], 2, FFN2_EXPERTS), ALU.mult)

            @block.scalar
            def _(a):
                a.wait_ge(centred, 1)
                nc.scalar.activation(gate[:, :, :], gate[:, :, :], ACT.Exp).then_inc(exp_ready, 1)

        hid = st.sb("hid", [P, 2, CH, BANK])
        up_ready, hid_ready, y_ready, added, up_free, y_free = (st.sem(n) for n in ("up_ready", "hid_ready", "y_ready", "added", "up_free", "y_free"))
        with nc.Block() as block:
            @block.tensor
            def _(pe):
                with pe.Fori(0, GROUPS) as g:
                    n0 = g * FFN2_EXPERTS
                    x = core.xnT[:, bass.ds(g * BANK, BANK)]

                    def up(e):
                        for k in range(CH):
                            ins = nc.tensor.matmul(bank[2 * (e % 2) + k][:, :], w1[:, e, k, :], x, start=True, stop=True)
                        ins.then_inc(up_ready, 1)

                    def down(e):
                        pe.wait_ge(hid_ready, n0 + e + 1)
                        pe.wait_ge(y_free, n0 + e + 1)
                        for t in range(4):
                            for k in range(CH):
                                ins = nc.tensor.matmul(bank[4 + e % 2][:, t * P:(t + 1) * P], hid[:, e % 2, k, t * P:(t + 1) * P], w2[:, e, k, :],
                                                       start=(k == 0), stop=(k == CH - 1))
                        ins.then_inc(y_ready, 1)

                    up(0)
                    up(1)
                    for e in range(FFN2_EXPERTS):
                        down(e)
                        if e + 2 < FFN2_EXPERTS:
                            up(e + 2)

            @block.scalar
            def _(a):
                with a.Fori(0, GROUPS) as g:
                    for e in range(FFN2_EXPERTS):
                        a.wait_ge(up_ready, g * FFN2_EXPERTS + e + 1)
                        for k in range(CH):
                            ins = nc.scalar.activation(hid[:, e % 2, k, :], bank[2 * (e % 2) + k][:, :], ACT.Gelu)
                        ins.then_inc(hid_ready, 1)

            @block.vector
            def _(v):
                v.sem_inc(y_free, 2)
                with v.Fori(0, GROUPS) as g:
                    for e in range(FFN2_EXPERTS):
                        v.wait_ge(y_ready, g * FFN2_EXPERTS + e + 1)
                        if e > 0:
                            v.wait_ge(y_free, g * FFN2_EXPERTS + e + 2)
                        for t in range(4):
                            x = core.x_res[:, bass.ds(g * 4 + t, 1), :].squeeze(1)
                            ins = nc.vector.scalar_tensor_tensor(x, bank[4 + e % 2][:, t * P:(t + 1) * P],
                                                                 gate[:, bass.ds(g * 4 + t, 1), e:e + 1].squeeze(1), x, ALU.mult, ALU.add)
                        ins.then_inc(y_free, 1)


def attn_b2_weights(w):
    return pack([
        ("wq", w["Wq"]), ("wk", w["Wk"]), ("wv", w["Wv"]), ("wo", w["Wo"]),
        ("bq", w["bq"]), ("bk", w["bk"]), ("bv", np.broadcast_to(w["bv"], (P, D))), ("bo", w["bo"][None, :]),
    ])


def attn_b2(core, blob, offsets):
    nc = core.nc
    T = SEQ // P
    with Stage(core, "attn_b2") as st:
        w = st.weights(blob, offsets)
        layer_norm(core, st)
        bank = [st.ps(f"bank{i}", [P, BANK]) for i in range(8)]
        x_now = st.sb("x_now", [P, SEQ])
        q, k2 = st.sb("q", [P, SEQ]), st.sb("k2", [P, SEQ])
        qk_sq = st.sb("qk_sq", [P, 2, SEQ])
        val = st.sb("val", [P, T, D])
        neg_ones = st.sb("neg_ones", [P, P])
        zero = st.sb("zero", [P, 1])
        score = st.sb("score", [P, T, SEQ])
        neg_max = st.sb("neg_max", [P, T])
        prob = st.sb("prob", [P, T, SEQ])
        row_sum, inv = st.sb("row_sum", [P, T]), st.sb("inv", [P, T])
        probT = st.sb("probT", [P, T, SEQ])
        o_tok = st.sb("o_tok", [P, T, D])
        oT = st.sb("oT", [P, SEQ])
        names = ("x_copied", "qk_psum", "v_psum", "qk_ready", "sq_ready", "v_ready", "dist_ready", "score_ready", "max_ready", "prob_ready",
                 "probT_psum", "probT_ready", "o_psum", "inv_ready", "o_ready", "oT_psum", "oT_ready", "y_ready", "y_added", "set_up")
        (x_copied, qk_psum, v_psum, qk_ready, sq_ready, v_ready, dist_ready, score_ready, max_ready, prob_ready,
         probT_psum, probT_ready, o_psum, inv_ready, o_ready, oT_psum, oT_ready, y_ready, y_added, set_up) = (st.sem(n) for n in names)
        tiled = lambda ap: ap.rearrange("p (t d) -> p t d", t=T)
        with nc.Block() as block:
            @block.gpsimd
            def _(pool):
                nc.gpsimd.memset(neg_ones[:, :], -1.0).then_inc(set_up, 1)
                with pool.Fori(0, BATCH) as b:
                    pool.wait_ge(v_psum, b)
                    nc.gpsimd.tensor_copy(x_now[:, :], core.xnT[:, bass.ds(b * SEQ, SEQ)]).then_inc(x_copied, 1)

            @block.tensor
            def _(pe):
                pe.wait_ge(set_up, 1)
                with pe.Fori(0, BATCH) as b:
                    pe.wait_ge(x_copied, b + 1)
                    nc.tensor.matmul(bank[0][:, 0:SEQ], w["wq"], x_now[:, :], start=True, stop=True)
                    nc.tensor.matmul(bank[0][:, SEQ:2 * SEQ], w["wk"], x_now[:, :], start=True, stop=True).then_inc(qk_psum, 1)
                    for t in range(T):
                        ins = nc.tensor.matmul(bank[1][:, t * D:(t + 1) * D], x_now[:, t * P:(t + 1) * P], w["wv"], start=True, stop=True)
                    ins.then_inc(v_psum, 1)
                    pe.wait_ge(sq_ready, b + 1)
                    for t in range(T):
                        out = bank[2][:, t * SEQ:(t + 1) * SEQ]
                        nc.tensor.matmul(out, q[:, t * P:(t + 1) * P], k2[:, :], start=True, stop=False)
                        nc.tensor.matmul(out, qk_sq[:, 0, t * P:(t + 1) * P], neg_ones[:, 0:1].broadcast_to([P, SEQ]), start=False, stop=False)
                        ins = nc.tensor.matmul(out, neg_ones[:, :], qk_sq[:, 1, :], start=False, stop=True)
                    ins.then_inc(dist_ready, 1)
                    pe.wait_ge(prob_ready, b + 1)
                    for kt in range(T):
                        for qt in range(T):
                            ins = nc.tensor.transpose(bank[3][:, kt * SEQ + qt * P:kt * SEQ + (qt + 1) * P],
                                                      prob[:, qt, kt * P:(kt + 1) * P], core.ident[:, :])
                    ins.then_inc(probT_psum, 1)
                    pe.wait_ge(probT_ready, b + 1)
                    for qt in range(T):
                        for kt in range(T):
                            ins = nc.tensor.matmul(bank[4][:, qt * D:(qt + 1) * D], probT[:, kt, qt * P:(qt + 1) * P], val[:, kt, :],
                                                   start=(kt == 0), stop=(kt == T - 1))
                    ins.then_inc(o_psum, 1)
                    pe.wait_ge(o_ready, b + 1)
                    for t in range(T):
                        ins = nc.tensor.transpose(bank[5][:, t * P:(t + 1) * P], o_tok[:, t, :], core.ident[:, :])
                    ins.then_inc(oT_psum, 1)
                    pe.wait_ge(oT_ready, b + 1)
                    for t in range(T):
                        y = bank[6][:, t * P:(t + 1) * P]
                        nc.tensor.matmul(y, core.ones[0:1, :], w["bo"][0:1, :], start=True, stop=False)
                        ins = nc.tensor.matmul(y, oT[:, t * P:(t + 1) * P], w["wo"], start=False, stop=True)
                    ins.then_inc(y_ready, 1)

            @block.scalar
            def _(a):
                with a.Fori(0, BATCH) as b:
                    a.wait_ge(qk_ready, b + 1)
                    nc.scalar.activation(qk_sq[:, 0, :], q[:, :], ACT.Square)
                    nc.scalar.activation(qk_sq[:, 1, :], k2[:, :], ACT.Square, scale=0.5).then_inc(sq_ready, 1)
                    a.wait_ge(dist_ready, b + 1)
                    nc.scalar.activation(score[:, :, :], tiled(bank[2][:, :]), ACT.Exp).then_inc(score_ready, 1)
                    a.wait_ge(max_ready, b + 1)
                    for t in range(T):
                        ins = nc.scalar.activation(prob[:, t, :], score[:, t, :], ACT.Exp, bias=neg_max[:, t:t + 1],
                                                   accum_out=row_sum[:, t:t + 1])
                    ins.then_inc(prob_ready, 1)
                    a.wait_ge(oT_psum, b + 1)
                    nc.scalar.copy(oT[:, :], bank[5][:, 0:SEQ]).then_inc(oT_ready, 1)

            @block.vector
            def _(v):
                with v.Fori(0, BATCH) as b:
                    v.wait_ge(qk_psum, b + 1)
                    nc.vector.tensor_scalar(q[:, :], bank[0][:, 0:SEQ], w["bq"], None, ALU.add)
                    nc.vector.tensor_scalar(k2[:, :], bank[0][:, SEQ:2 * SEQ], w["bk"], 2.0, ALU.add, ALU.mult).then_inc(qk_ready, 1)
                    v.wait_ge(v_psum, b + 1)
                    nc.vector.tensor_tensor(val[:, :, :], tiled(bank[1][:, 0:T * D]), bc(w["bv"], 1, T), ALU.add).then_inc(v_ready, 1)
                    v.wait_ge(score_ready, b + 1)
                    nc.vector.tensor_reduce(neg_max[:, :], score[:, :, :], AX.X, ALU.max, negate=True).then_inc(max_ready, 1)
                    v.wait_ge(probT_psum, b + 1)
                    nc.vector.tensor_copy(probT[:, :, :], tiled(bank[3][:, :])).then_inc(probT_ready, 1)
                    nc.vector.reciprocal(inv[:, :], row_sum[:, :]).then_inc(inv_ready, 1)
                    v.wait_ge(inv_ready, b + 1)
                    v.wait_ge(o_psum, b + 1)
                    nc.vector.tensor_tensor(o_tok[:, :, :], tiled(bank[4][:, 0:T * D]), bc(inv[:, :], 2, D), ALU.mult).then_inc(o_ready, 1)
                    v.wait_ge(y_ready, b + 1)
                    x = core.x_res[:, bass.ds(b * T, T), :]
                    nc.vector.tensor_tensor(x, x, tiled(bank[6][:, 0:T * D]), ALU.add).then_inc(y_added, 1)


ATTN_A3_HD = 64
ATTN_A3_CHUNKS = HEADS * ATTN_A3_HD // P
PER_OUT = 4


def attn_a3_weights(w):
    flat = lambda a: a.reshape(HEADS * ATTN_A3_HD, D).T
    col = lambda a: a.reshape(ATTN_A3_CHUNKS, P).T
    query, key = np.arange(P)[:, None], np.arange(P)[None, :]
    return pack([
        ("wq", flat(w["Wq"])), ("wk", flat(w["Wk"])), ("wv", flat(w["Wv"])),
        ("bq", col(w["bq"])), ("bk", col(w["bk"])), ("bv", np.broadcast_to(w["bv"].reshape(1, HEADS * ATTN_A3_HD), (P, HEADS * ATTN_A3_HD))),
        ("proj", w["proj"].reshape(ATTN_A3_CHUNKS, P, D).transpose(1, 0, 2).reshape(P, ATTN_A3_CHUNKS * D)),
        ("causal", np.where(key > query, np.float32(NEG), np.float32(0))),
    ])


def attn_a3(core, blob, offsets):
    nc = core.nc
    T = SEQ // P
    inv_scale = 1.0 / np.sqrt(float(ATTN_A3_HD))
    with Stage(core, "attn_a3") as st:
        w = st.weights(blob, offsets)
        layer_norm(core, st)
        bank = [st.ps(f"bank{i}", [P, BANK]) for i in range(8)]
        pS, pT, pO, pP, pY = bank[0:2], bank[2:4], bank[4], bank[5:7], bank[7]
        x_now = st.sb("x_now", [P, SEQ])
        q = st.sb("q", [P, 2, ATTN_A3_CHUNKS, 2, SEQ])
        k = st.sb("k", [P, 2, ATTN_A3_CHUNKS, SEQ])
        val = st.sb("val", [P, 2, T, HEADS * ATTN_A3_HD])
        small_b = st.sb("small_b", [P, ATTN_A3_CHUNKS])
        prob = st.sb("prob", [P, 2, 3, P])
        probT = st.sb("probT", [P, 4, 3, P])
        neg_max, row_sum, inv = (st.sb(n, [P, 2, T]) for n in ("neg_max", "row_sum", "inv"))
        oT = st.sb("oT", [P, HEADS, SEQ // 2])
        names = ("set_up", "zeroed", "x_copied", "proj_psum", "proj_by_act", "proj_by_dve", "scores_ready", "masked", "max_ready", "exp_ready",
                 "inverted", "prob_ready", "probT_psum", "probT_ready", "pair_done", "oT_ready", "y_ready", "y_added")
        (set_up, zeroed, x_copied, proj_psum, proj_by_act, proj_by_dve, scores_ready, masked, max_ready, exp_ready,
         inverted, prob_ready, probT_psum, probT_ready, pair_done, oT_ready, y_ready, y_added) = (st.sem(n) for n in names)
        by_act = lambda i: i < 8 and i % 2 == 0
        reader = lambda i: (proj_by_act, i // 2 + 1) if by_act(i) else (proj_by_dve, i // 2 + 1 if i < 8 else i - 3)
        ACT_FILLS, DVE_FILLS = 4, 8
        FILLS = 12
        GROUPS = HEADS // PER_OUT
        PAIRS = HEADS // 2
        HALF = HEADS // T * SEQ // 2
        oT_flat = oT[:, :, :].rearrange("p h s -> p (h s)")

        def known(b, below):
            return isinstance(b, int) and b < below

        def sequences(eng, step):
            step(0, 0, True, False)
            step(1, 1, False, False)
            with eng.Fori(1, BATCH // 2 - 1) as pair:
                step(pair * 2, 0, False, False)
                step(pair * 2 + 1, 1, False, False)
            step(BATCH - 2, 0, False, False)
            step(BATCH - 1, 1, False, True)

        with nc.Block() as block:
            @block.gpsimd
            def _(pool):
                def x_copy(b):
                    if not known(b, 1):
                        pool.wait_ge(proj_psum, b * FILLS)
                    nc.gpsimd.tensor_copy(x_now[:, :], core.xnT[:, bass.ds(b * SEQ, SEQ)]).then_inc(x_copied, 1)

                def step(b, s, first, last):
                    if first:
                        x_copy(b)
                        pool.wait_ge(x_copied, 1)
                        for s_zero in range(2):
                            for head in range(2):
                                other = slice(ATTN_A3_HD * (1 - head), ATTN_A3_HD * (2 - head))
                                nc.gpsimd.memset(q[other, s_zero, :, head, :], 0.0).then_inc(zeroed, 1)
                                pool.wait_ge(zeroed, 2 * s_zero + head + 1)
                        x_copy(b + 1)
                    for h in range(HEADS):
                        pool.wait_ge(inverted, b * HEADS + h + 1)
                        for t, blocks in enumerate((slice(0, 1), slice(1, 3))):
                            x = prob[:, h % 2, blocks, :]
                            ins = nc.gpsimd.tensor_tensor(x, x, bc(bc(inv[:, h % 2, t:t + 1].squeeze(1), 1, P), 1, blocks.stop - blocks.start), ALU.mult)
                        ins.then_inc(prob_ready, 1)
                        if h == 13 and not last:
                            if not known(b, BATCH) or b + 2 < BATCH:
                                x_copy(b + 2)

                sequences(pool, step)

            @block.tensor
            def _(pe):
                def fill(b, i):
                    if i == 0:
                        pe.wait_ge(x_copied, b + 1)
                    if i >= 2 or not known(b, 1):
                        j, c = (i - 2, b) if i >= 2 else (i - 2 + FILLS, b - 1)
                        done, count = reader(j)
                        pe.wait_ge(done, c * (ACT_FILLS if by_act(j) else DVE_FILLS) + count)
                    if i < 8:
                        for c in range(2):
                            ch = 2 * (i % 4) + c
                            ins = nc.tensor.matmul(pP[i % 2][:, c * SEQ:(c + 1) * SEQ], w["wq" if i < 4 else "wk"][:, ch * P:(ch + 1) * P],
                                                   x_now[:, :], start=True, stop=True)
                    else:
                        t, half = (i - 8) // 2, (i - 8) % 2
                        ins = nc.tensor.matmul(pP[i % 2][:, :], x_now[:, t * P:(t + 1) * P], w["wv"][:, half * BANK:(half + 1) * BANK],
                                               start=True, stop=True)
                    ins.then_inc(proj_psum, 1)

                def scores(b, s, h):
                    if h == 0:
                        pe.wait_ge(zeroed, 4)
                        pe.wait_ge(proj_by_act, (b + 1) * ACT_FILLS)
                        pe.wait_ge(proj_by_dve, (b + 1) * DVE_FILLS)
                    qh = q[:, s, h // 2, h % 2, :]
                    nc.tensor.matmul(pS[h % 2][:, 0:P], qh[:, 0:P], k[:, s, h // 2, 0:P], start=True, stop=True)
                    nc.tensor.matmul(pS[h % 2][:, SEQ:2 * SEQ], qh[:, P:2 * P], k[:, s, h // 2, :], start=True, stop=True).then_inc(scores_ready, 1)

                def turn(b, h):
                    pe.wait_ge(prob_ready, b * HEADS + h + 1)
                    if not (known(b, 1) and h < 2):
                        pe.wait_ge(probT_ready, b * HEADS + h - 1)
                    for j in range(3):
                        ins = nc.tensor.transpose(pT[h % 2][:, j * P:(j + 1) * P], prob[:, h % 2, j, :], core.ident[:, :])
                    ins.then_inc(probT_psum, 1)

                def weighted(b, s, pair):
                    pe.wait_ge(probT_ready, b * HEADS + 2 * pair + 2)
                    if pair % 2 == 0 and not (known(b, 1) and pair == 0):
                        pe.wait_ge(oT_ready, b * GROUPS + pair // 2)
                    at = pair % 2 * SEQ
                    for t in range(T):
                        for odd in range(2):
                            h = 2 * pair + odd
                            rows = slice(odd * ATTN_A3_HD, (odd + 1) * ATTN_A3_HD)
                            moving = probT[:, h % 4, 0:2, :] if t == 0 else probT[:, h % 4, 2, :]
                            out = pO[rows, at:at + SEQ].rearrange("p (j q) -> p j q", j=2) if t == 0 else pO[rows, at + P:at + SEQ]
                            ins = nc.tensor.matmul(out, val[:, s, t, h * ATTN_A3_HD:(h + 1) * ATTN_A3_HD], moving, start=(t == 0), stop=(t == 1),
                                                   tile_position=(0, rows.start))
                    ins.then_inc(pair_done, 1)

                def project(b):
                    pe.wait_ge(oT_ready, (b + 1) * GROUPS)
                    if not known(b, 1):
                        pe.wait_ge(y_added, b)
                    for t in range(T):
                        for c in range(ATTN_A3_CHUNKS):
                            ins = nc.tensor.matmul(pY[:, t * P:(t + 1) * P], oT_flat[:, t * HALF + c:(t + 1) * HALF:ATTN_A3_CHUNKS], w["proj"][:, c * D:(c + 1) * D],
                                                   start=(c == 0), stop=(c == ATTN_A3_CHUNKS - 1))
                    ins.then_inc(y_ready, 1)

                def step(b, s, first, last):
                    if first:
                        for i in range(FILLS):
                            fill(b, i)
                        scores(b, s, 0)
                        scores(b, s, 1)
                    for h in range(HEADS):
                        turn(b, h)
                        if h + 2 < HEADS:
                            scores(b, s, h + 2)
                        elif not last:
                            scores(b + 1, 1 - s, h + 2 - HEADS)
                        if h < FILLS and not last:
                            fill(b + 1, h)
                        if h == 0 and not first:
                            weighted(b - 1, 1 - s, PAIRS - 1)
                        if h == 3 and not first:
                            project(b - 1)
                        if h >= 2 and h % 2 == 0:
                            weighted(b, s, h // 2 - 1)
                    if last:
                        weighted(b, s, PAIRS - 1)
                        project(b)

                sequences(pe, step)

            def evacuate(eng, act, b, s, i):
                done = proj_by_act if act else proj_by_dve
                src = pP[i % 2]
                eng.wait_ge(proj_psum, b * FILLS + i + 1)
                if i >= 8:
                    t, half = (i - 8) // 2, (i - 8) % 2
                    if i == 8 and not known(b, 2):
                        eng.wait_ge(pair_done, (b - 1) * PAIRS)
                    nc.vector.tensor_tensor(val[:, s, t, half * BANK:(half + 1) * BANK], src[:, :], w["bv"][:, half * BANK:(half + 1) * BANK],
                                            ALU.add).then_inc(done, 1)
                    return
                for c in range(2):
                    ch, part = 2 * (i % 4) + c, src[:, c * SEQ:(c + 1) * SEQ]
                    if i >= 4:
                        if act:
                            ins = nc.scalar.activation(k[:, s, ch, :], part, ACT.Identity, bias=w["bk"][:, ch:ch + 1])
                        else:
                            ins = nc.vector.tensor_scalar(k[:, s, ch, :], part, w["bk"][:, ch:ch + 1], None, ALU.add)
                        continue
                    for head in range(2):
                        rows = slice(head * ATTN_A3_HD, (head + 1) * ATTN_A3_HD)
                        if act:
                            ins = nc.scalar.activation(q[rows, s, ch, head, :], part[rows], ACT.Identity, bias=small_b[rows, ch:ch + 1], scale=inv_scale)
                        else:
                            ins = nc.vector.tensor_scalar(q[rows, s, ch, head, :], part[rows], w["bq"][rows, ch:ch + 1], inv_scale, ALU.add, ALU.mult)
                ins.then_inc(done, 1)

            @block.scalar
            def _(a):
                a.wait_ge(set_up, 1)

                def out_copy(b, g):
                    a.wait_ge(pair_done, b * PAIRS + 2 * g + 2)
                    if g == 0 and not known(b, 1):
                        a.wait_ge(y_ready, b)
                    for odd_head in range(2):
                        for odd_u in range(2):
                            src = pO[odd_head * ATTN_A3_HD:(odd_head + 1) * ATTN_A3_HD, :].rearrange("p (c s u) -> p c s u", c=2, u=2)[:, :, :, odd_u]
                            dst = oT[odd_u * ATTN_A3_HD:(odd_u + 1) * ATTN_A3_HD, 4 * g + odd_head:4 * g + odd_head + 3:2, :]
                            ins = nc.scalar.activation(dst, src, ACT.Copy, scale=inv_scale)
                    ins.then_inc(oT_ready, 1)

                def step(b, s, first, last):
                    if first:
                        for i in filter(by_act, range(FILLS)):
                            evacuate(a, True, b, s, i)
                    for h in range(HEADS):
                        a.wait_ge(max_ready, b * HEADS + h + 1)
                        nc.scalar.activation(prob[:, h % 2, 0, :], pS[h % 2][:, 0:P], ACT.Exp, bias=neg_max[:, h % 2, 0:1],
                                             accum_out=row_sum[:, h % 2, 0:1])
                        nc.scalar.activation(prob[:, h % 2, 1:3, :], pS[h % 2][:, SEQ:2 * SEQ].rearrange("p (j k) -> p j k", j=2), ACT.Exp,
                                             bias=neg_max[:, h % 2, 1:2], accum_out=row_sum[:, h % 2, 1:2]).then_inc(exp_ready, 1)
                        if h == 2 and not first:
                            out_copy(b - 1, GROUPS - 1)
                        if h >= 1 and by_act(h - 1) and not last:
                            evacuate(a, True, b + 1, 1 - s, h - 1)
                        if h % PER_OUT == 2 and h > 2:
                            out_copy(b, h // PER_OUT - 1)
                    if last:
                        out_copy(b, GROUPS - 1)

                sequences(a, step)

            @block.vector
            def _(v):
                nc.vector.tensor_scalar(small_b[:, :], w["bq"], inv_scale, None, ALU.mult).then_inc(set_up, 1)

                def row_max(b, h):
                    n = b * HEADS + h + 1
                    v.wait_ge(scores_ready, n)
                    blocks = pS[h % 2][:, :].rearrange("p (j k) -> p j k", k=P)[:, 0:4:3, :]
                    nc.vector.tensor_tensor(blocks, blocks, bc(w["causal"], 1, 2), ALU.add).then_inc(masked, 1)
                    v.wait_ge(masked, n)
                    nc.vector.tensor_reduce(neg_max[:, h % 2, 0:1], pS[h % 2][:, 0:P], AX.X, ALU.max, negate=True)
                    nc.vector.tensor_reduce(neg_max[:, h % 2, 1:2], pS[h % 2][:, SEQ:2 * SEQ], AX.X, ALU.max, negate=True).then_inc(max_ready, 1)

                def invert(b, h):
                    v.wait_ge(exp_ready, b * HEADS + h + 1)
                    nc.vector.reciprocal(inv[:, h % 2, :], row_sum[:, h % 2, :]).then_inc(inverted, 1)

                def step(b, s, first, last):
                    if first:
                        for i in (i for i in range(FILLS) if not by_act(i)):
                            evacuate(v, False, b, s, i)
                        row_max(b, 0)
                        invert(b, 0)
                        row_max(b, 1)
                    for h in range(HEADS):
                        if h + 1 < HEADS:
                            invert(b, h + 1)
                        elif not last:
                            invert(b + 1, 0)
                        v.wait_ge(probT_psum, b * HEADS + h + 1)
                        if h % 2 == 0 and not (known(b, 1) and h < 4):
                            v.wait_ge(pair_done, b * PAIRS + h // 2 - 1)
                        nc.vector.tensor_copy(probT[:, h % 4, :, :], pT[h % 2][:, 0:3 * P].rearrange("p (j q) -> p j q", j=3)).then_inc(probT_ready, 1)
                        if h + 2 < HEADS:
                            row_max(b, h + 2)
                        elif not last:
                            row_max(b + 1, h + 2 - HEADS)
                        if 1 <= h <= FILLS and not by_act(h - 1) and not last:
                            evacuate(v, False, b + 1, 1 - s, h - 1)
                        if h == 5 and not first:
                            add(b - 1)
                    if last:
                        add(b)

                def add(b):
                    v.wait_ge(y_ready, b + 1)
                    x = core.x_res[:, bass.ds(b * T, T), :]
                    nc.vector.tensor_tensor(x, x, pY[:, 0:T * D].rearrange("p (t d) -> p t d", t=T), ALU.add).then_inc(y_added, 1)

                sequences(v, step)


FFN3_EXPERTS = 64
FFN3_TOP = 8
ROUTE_GROUPS = 8
TOP_GROUPS = 4
IN_GROUP = FFN3_EXPERTS // ROUTE_GROUPS
FFN3_HID = 64
FFN3_SHARED = 256
PAIRS = FFN3_EXPERTS // 2
SCALE = 2.5


def ffn3_weights(w):
    return pack([
        ("router", w["router_w"].T), ("earlier", earlier_table(ROUTE_GROUPS)),
        ("correction", np.broadcast_to(w["correction_bias"], (P, FFN3_EXPERTS))),
        ("up", w["up_w"].transpose(1, 0, 2).reshape(D, FFN3_EXPERTS * FFN3_HID)),
        ("down", w["down_w"].reshape(PAIRS, P, D).transpose(1, 0, 2).reshape(P, PAIRS * D)),
        ("shared_up", w["shared_up_w"]),
        ("shared_down", w["shared_down_w"].reshape(FFN3_SHARED // P, P, D).transpose(1, 0, 2).reshape(P, FFN3_SHARED // P * D)),
    ])


def ffn3(core, blob, offsets):
    nc = core.nc
    GROUPS = TOK // BANK
    with Stage(core, "ffn3") as st:
        w = st.weights(blob, offsets)
        layer_norm(core, st)
        bank = [st.ps(f"bank{i}", [P, BANK]) for i in range(8)]
        per_bank = BANK // FFN3_EXPERTS
        sfc = st.sb("sfc", [P, TILES, FFN3_EXPERTS])
        score = st.sb("score", [P, TILES, FFN3_EXPERTS])
        x_now = st.sb("x_now", [P, 2, BANK])
        copied, logits_ready, scores_ready = st.sem("copied"), st.sem("logits_ready"), st.sem("scores_ready")
        with nc.Block() as block:
            @block.gpsimd
            def _(pool):
                pool.sem_inc(scores_ready, 2)
                with pool.Fori(0, GROUPS // 2) as g:
                    for s in range(2):
                        pool.wait_ge(scores_ready, 2 * g + s + 1)
                        nc.gpsimd.tensor_copy(x_now[:, s, :], core.xnT[:, bass.ds((2 * g + s) * BANK, BANK)]).then_inc(copied, 1)

            @block.tensor
            def _(pe):
                with pe.Fori(0, GROUPS // 2) as g:
                    for s in range(2):
                        pe.wait_ge(copied, 2 * g + s + 1)
                        for t in range(4):
                            ins = nc.tensor.matmul(bank[s][:, t * FFN3_EXPERTS:(t + 1) * FFN3_EXPERTS], x_now[:, s, t * P:(t + 1) * P], w["router"],
                                                   start=True, stop=True)
                        ins.then_inc(logits_ready, 1)

            @block.scalar
            def _(a):
                with a.Fori(0, GROUPS // 2) as g:
                    for s in range(2):
                        a.wait_ge(logits_ready, 2 * g + s + 1)
                        nc.scalar.activation(score[:, bass.ds(8 * g + 4 * s, 4), :], bank[s][:, 0:4 * FFN3_EXPERTS].rearrange("p (t e) -> p t e", t=4),
                                             ACT.Sigmoid).then_inc(scores_ready, 1)

        comb = st.sb("comb", [P, TILES, FFN3_EXPERTS])
        work = st.sb("work", [P, TILES, FFN3_EXPERTS])
        repl = st.sb("repl", [P, TILES, FFN3_EXPERTS])
        first, second, ties, gscore, gsel = (st.sb(n, [P, TILES, ROUTE_GROUPS]) for n in ("first", "second", "ties", "gscore", "gsel"))
        above, same = (st.sb(n, [P, TILES, ROUTE_GROUPS, ROUTE_GROUPS]) for n in ("above", "same"))
        top8 = st.sb("top8", [P, TILES, FFN3_TOP])
        total = st.sb("total", [P, TILES])
        spread = st.sb("spread", [FFN3_EXPERTS, FFN3_EXPERTS, FFN3_HID])
        dve = st.sem("dve")
        grouped = lambda t: t[:, :, :].rearrange("p t (g e) -> p (t g) e", g=ROUTE_GROUPS)
        flat = lambda t: t[:, :, :].rearrange("p t g -> p (t g)")
        with nc.Block() as block:
            @block.gpsimd
            def _(pool):
                nc.gpsimd.tensor_copy(spread[:, :, :], bc(core.ident[0:FFN3_EXPERTS, 0:FFN3_EXPERTS], 2, FFN3_HID))

            @block.vector
            def _(v):
                c = Chain(v, dve)
                c.link(nc.vector.tensor_tensor(sfc[:, :, :], score[:, :, :], bc(w["correction"], 1, TILES), ALU.add))
                c.link(nc.vector.tensor_reduce(flat(first), grouped(sfc), AX.X, ALU.max))
                c.link(nc.vector.tensor_tensor(grouped(work), grouped(sfc), bc(flat(first), 2, IN_GROUP), ALU.is_equal))
                c.link(nc.vector.tensor_reduce(flat(ties), grouped(work), AX.X, ALU.add))
                c.link(nc.vector.scalar_tensor_tensor(work[:, :, :], work[:, :, :], NEG, sfc[:, :, :], ALU.mult, ALU.add))
                c.link(nc.vector.tensor_reduce(flat(second), grouped(work), AX.X, ALU.max))
                c.link(nc.vector.tensor_scalar(ties[:, :, :], ties[:, :, :], 2.0, None, ALU.is_ge))
                c.link(nc.vector.tensor_tensor(gscore[:, :, :], first[:, :, :], ties[:, :, :], ALU.mult))
                c.link(nc.vector.tensor_scalar(ties[:, :, :], ties[:, :, :], -1.0, 1.0, ALU.mult, ALU.add))
                c.link(nc.vector.tensor_tensor(second[:, :, :], second[:, :, :], ties[:, :, :], ALU.mult))
                c.link(nc.vector.tensor_tensor(second[:, :, :], second[:, :, :], gscore[:, :, :], ALU.add))
                c.link(nc.vector.tensor_tensor(gscore[:, :, :], second[:, :, :], first[:, :, :], ALU.add))
                link_ranks(nc, c, gsel[:, :, :], gscore[:, :, :], above[:, :, :, :], same[:, :, :, :], w["earlier"], ROUTE_GROUPS)
                c.link(nc.vector.tensor_scalar(gsel[:, :, :], gsel[:, :, :], float(TOP_GROUPS), None, ALU.is_lt))
                c.link(nc.vector.tensor_tensor(grouped(work), grouped(sfc), bc(flat(gsel), 2, IN_GROUP), ALU.mult))
                for t in range(TILES):
                    ins = nc.vector.max(top8[:, t, :], work[:, t, :])
                c.link(ins)
                for t in range(TILES):
                    ins = nc.vector.match_replace(repl[:, t, :], top8[:, t, :], work[:, t, :], NEG)
                c.link(ins)
                c.link(nc.vector.tensor_tensor(work[:, :, :], work[:, :, :], repl[:, :, :], ALU.not_equal))
                c.link(nc.vector.tensor_tensor(comb[:, :, :], score[:, :, :], work[:, :, :], ALU.mult))
                c.link(nc.vector.tensor_reduce(total[:, :], comb[:, :, :], AX.X, ALU.add))
                c.link(nc.vector.tensor_scalar(total[:, :], total[:, :], 1e-20, None, ALU.add))
                c.link(nc.vector.reciprocal(total[:, :], total[:, :]))
                c.link(nc.vector.tensor_scalar(total[:, :], total[:, :], SCALE, None, ALU.mult))
                nc.vector.tensor_tensor(comb[:, :, :], comb[:, :, :], bc(total[:, :], 2, FFN3_EXPERTS), ALU.mult)

        CHUNKS = PAIRS + FFN3_SHARED // P
        c_now = st.sb("c_now", [P, 4, FFN3_EXPERTS])
        combT = st.sb("combT", [FFN3_EXPERTS, BANK])
        relu = st.sb("relu", [P, 2, BANK])
        part = st.sb("part", [P, 2, BANK])
        hid = st.sb("hid", [P, 2, BANK])
        yT = st.sb("yT", [P, BANK])
        names = ("c_copied", "combT_psum", "combT_ready", "up_ready", "relu_ready", "part_ready", "hid_ready", "yT_psum", "yT_ready", "y_ready", "added")
        (c_copied, combT_psum, combT_ready, up_ready, relu_ready, part_ready, hid_ready, yT_psum, yT_ready, y_ready, added) = (st.sem(n) for n in names)
        with nc.Block() as block:
            @block.tensor
            def _(pe):
                with pe.Fori(0, GROUPS) as g:
                    x = core.xnT[:, bass.ds(g * BANK, BANK)]
                    n0 = g * CHUNKS

                    def up(k):
                        if k < PAIRS:
                            nc.tensor.matmul(bank[2 + k % 2][:, :], spread[:, 2 * k:2 * k + 2, :].rearrange("e a h -> e (a h)"), combT[:, :],
                                             start=True, stop=True)
                            lhs = w["up"][:, k * P:(k + 1) * P]
                        else:
                            lhs = w["shared_up"][:, (k - PAIRS) * P:(k - PAIRS + 1) * P]
                        nc.tensor.matmul(bank[k % 2][:, :], lhs, x, start=True, stop=True).then_inc(up_ready, 1)

                    def down(k):
                        pe.wait_ge(hid_ready, n0 + k + 1)
                        lhs = w["down"][:, k * D:(k + 1) * D] if k < PAIRS else w["shared_down"][:, (k - PAIRS) * D:(k - PAIRS + 1) * D]
                        return nc.tensor.matmul(bank[4][:, :], lhs, hid[:, k % 2, :], start=(k == 0), stop=(k == CHUNKS - 1))

                    pe.wait_ge(c_copied, g + 1)
                    for t in range(4):
                        ins = nc.tensor.matmul(bank[5][0:FFN3_EXPERTS, t * P:(t + 1) * P], c_now[:, t, :], core.ident[:, :], start=True, stop=True)
                    ins.then_inc(combT_psum, 1)
                    pe.wait_ge(combT_ready, g + 1)
                    up(0)
                    up(1)
                    for k in range(CHUNKS):
                        ins = down(k)
                        if k + 2 < CHUNKS:
                            up(k + 2)
                    ins.then_inc(yT_psum, 1)
                    pe.wait_ge(yT_ready, g + 1)
                    for t in range(4):
                        ins = nc.tensor.transpose(bank[6][:, t * P:(t + 1) * P], yT[:, t * P:(t + 1) * P], core.ident[:, :])
                    ins.then_inc(y_ready, 1)

            @block.scalar
            def _(a):
                with a.Fori(0, GROUPS) as g:
                    a.wait_ge(combT_psum, g + 1)
                    nc.scalar.copy(combT[:, :], bank[5][0:FFN3_EXPERTS, :]).then_inc(combT_ready, 1)
                    for k in range(CHUNKS):
                        a.wait_ge(up_ready, g * CHUNKS + k + 1)
                        nc.scalar.activation(relu[:, k % 2, :], bank[k % 2][:, :], ACT.Relu).then_inc(relu_ready, 1)

            @block.vector
            def _(v):
                with v.Fori(0, GROUPS) as g:
                    for k in range(PAIRS):
                        v.wait_ge(relu_ready, g * CHUNKS + k + 1)
                        nc.vector.tensor_tensor(part[:, k % 2, :], relu[:, k % 2, :], bank[2 + k % 2][:, :], ALU.mult).then_inc(part_ready, 1)
                    v.wait_ge(yT_psum, g + 1)
                    nc.vector.tensor_copy(yT[:, :], bank[4][:, :]).then_inc(yT_ready, 1)
                    v.wait_ge(y_ready, g + 1)
                    xr = core.x_res[:, bass.ds(g * 4, 4), :]
                    nc.vector.tensor_tensor(xr, xr, bank[6][:, :].rearrange("p (t d) -> p t d", t=4), ALU.add).then_inc(added, 1)

            @block.gpsimd
            def _(pool):
                with pool.Fori(0, GROUPS) as g:
                    pool.wait_ge(combT_psum, g)
                    nc.gpsimd.tensor_copy(c_now[:, :, :], comb[:, bass.ds(g * 4, 4), :]).then_inc(c_copied, 1)
                    for k in range(CHUNKS):
                        if k < PAIRS:
                            pool.wait_ge(part_ready, g * PAIRS + k + 1)
                            nc.gpsimd.tensor_tensor(hid[:, k % 2, :], part[:, k % 2, :], relu[:, k % 2, :], ALU.mult).then_inc(hid_ready, 1)
                        else:
                            pool.wait_ge(relu_ready, g * CHUNKS + k + 1)
                            nc.gpsimd.tensor_tensor(hid[:, k % 2, :], relu[:, k % 2, :], relu[:, k % 2, :], ALU.mult).then_inc(hid_ready, 1)


def build_program(nc, x, ident, blobs, out):
    with ExitStack() as ctx:
        core = Core(nc, ctx)
        load_constants(core, ident, x)
        attn_a(core, *blobs["L0_attn_a"])
        ffn0(core, *blobs["L0_ffn"])
        attn_b0(core, *blobs["L0_attn_b"])
        ffn0(core, *blobs["L0_ffn"])
        attn_a(core, *blobs["L1_attn_a"])
        ffn1(core, *blobs["L1_ffn"])
        scan1(core, *blobs["L1_attn_b"])
        ffn1(core, *blobs["L1_ffn"])
        attn_a2(core, *blobs["L2_attn_a"])
        ffn2(core, *blobs["L2_ffn"])
        attn_b2(core, *blobs["L2_attn_b"])
        ffn2(core, *blobs["L2_ffn"])
        attn_a3(core, *blobs["L3_attn_a"])
        ffn3(core, *blobs["L3_ffn"])
        scan3(core, *blobs["L3_attn_b"])
        ffn3(core, *blobs["L3_ffn"])
        store_output(core, out)


_LAYOUTS = {"L0_attn_a": attn_a_weights, "L0_ffn": ffn0_weights, "L0_attn_b": attn_b0_weights, "L1_attn_a": attn_a_weights,
            "L1_ffn": ffn1_weights, "L1_attn_b": scan1_weights, "L2_attn_a": attn_a2_weights, "L2_ffn": ffn2_weights,
            "L2_attn_b": attn_b2_weights, "L3_attn_a": attn_a3_weights, "L3_ffn": ffn3_weights, "L3_attn_b": scan3_weights}


def kernel(**inputs):
    import concourse.bacc as bacc
    from concourse.bass_utils import run_bass_kernel_spmd

    arrays = {"x": np.ascontiguousarray(np.asarray(inputs["L0_attn_a_x"]).reshape(TOK, D)), "ident": np.eye(P, dtype=np.float32)}
    offsets = {}
    for stage, layout in _LAYOUTS.items():
        own = {k[len(stage) + 1:]: np.asarray(v) for k, v in inputs.items() if k.startswith(stage + "_")}
        arrays[stage], offsets[stage] = layout(own)
    nc = bacc.Bacc("TRN2", target_bir_lowering=False, num_devices=1)
    dram = {k: nc.dram_tensor(f"in_{k}", a.shape, mybir.dt.from_np(a.dtype), kind="ExternalInput").ap() for k, a in arrays.items()}
    out = nc.dram_tensor("out", (TOK, D), F32, kind="ExternalOutput").ap()
    build_program(nc, dram["x"], dram["ident"], {k: (dram[k], offsets[k]) for k in _LAYOUTS}, out)
    r = run_bass_kernel_spmd(nc, [{f"in_{k}": a for k, a in arrays.items()}], core_ids=[0])
    return r.results[0]["out"].reshape(BATCH, SEQ, D)
```

```python
from contextlib import ExitStack

import numpy as np
import concourse.bass as bass
from concourse import mybir

F32 = mybir.dt.float32
I32 = mybir.dt.int32
U8 = mybir.dt.uint8
ALU = mybir.AluOpType
ACT = mybir.ActivationFunctionType
AX = mybir.AxisListType

P = 128
D = 128
BATCH = 16
SEQ = 256
TOK = BATCH * SEQ
TILES = TOK // P
HEADS = 16
LN_EPS = 1e-5
BANK = 512
NEG = -1.0e30


def bc(ap, at, n):
    x = ap.unsqueeze(at)
    return x.broadcast_to([*x.shape[:at], n, *x.shape[at + 1:]])


def known(b, below):
    return isinstance(b, int) and b < below


def sequences(eng, step):
    step(0, 0, True, False)
    step(1, 1, False, False)
    with eng.Fori(1, BATCH // 2 - 1) as pair:
        step(pair * 2, 0, False, False)
        step(pair * 2 + 1, 1, False, False)
    step(BATCH - 2, 0, False, False)
    step(BATCH - 1, 1, False, True)


class Chain:

    def __init__(self, eng, sem, start=0):
        self.eng, self.sem, self.start, self.n = eng, sem, start, 0

    def link(self, ins):
        self.n += 1
        ins.then_inc(self.sem, 1)
        self.eng.wait_ge(self.sem, self.start + self.n)


class Core:

    def __init__(self, nc, ctx):
        self.nc = nc
        sb = lambda name, shape, dt=F32: ctx.enter_context(nc.sbuf_tensor(name, shape, dt))
        self.x_res = sb("x_res", [P, TILES, D])
        self.xn = sb("xn", [P, TILES, D])
        self.xnT = sb("xnT", [P, TOK])
        self.rstd = sb("rstd", [P, TILES])
        self.ident = sb("ident", [P, P])
        self.ones = sb("ones", [P, P])
        self.n = 0


class Stage:

    def __init__(self, core, name):
        self.core, self.nc = core, core.nc
        core.n += 1
        self.name = f"{name}{core.n}"
        self.ctx = ExitStack()
        self.sems = []

    def __enter__(self):
        self.ctx.__enter__()
        return self

    def __exit__(self, *e):
        self.nc.clear_and_free_semaphores(self.sems)
        self.nc.all_engine_barrier()
        return self.ctx.__exit__(*e)

    def sb(self, name, shape, dt=F32):
        return self.ctx.enter_context(self.nc.sbuf_tensor(f"{self.name}_{name}", shape, dt))

    def ps(self, name, shape, dt=F32):
        return self.ctx.enter_context(self.nc.psum_tensor(f"{self.name}_{name}", shape, dt))

    def sem(self, name):
        s = self.nc.alloc_semaphore(name=f"{self.name}_{name}")
        self.sems.append(s)
        return s

    def weights(self, blob, offsets):
        self.blob = blob
        self.w_sb = self.sb("w", [P, blob.shape[1]])
        return {k: self.w_sb[:, a:b] for k, (a, b) in offsets.items()}


def load_constants(core, ident_dram, x_dram):
    nc = core.nc
    with Stage(core, "init") as st:
        loaded = st.sem("loaded")
        with nc.Block() as block:
            @block.sync
            def _(sp):
                sp.dma_start(core.x_res[:, :, :], x_dram.rearrange("(t p) d -> p t d", p=P)).then_inc(loaded, 16)
                sp.dma_start(core.ident[:, :], ident_dram).then_inc(loaded, 16)
                sp.wait_ge(loaded, 32)

            @block.gpsimd
            def _(pool):
                nc.gpsimd.memset(core.ones[:, :], 1.0)


def store_output(core, out_dram):
    nc = core.nc
    with Stage(core, "store") as st:
        stored = st.sem("stored")
        with nc.Block() as block:
            @block.sync
            def _(sp):
                sp.dma_start(out_dram.rearrange("(t p) d -> p t d", p=P), core.x_res[:, :, :]).then_inc(stored, 16)
                sp.wait_ge(stored, 16)


def layer_norm(core, weights_stage=None):
    nc = core.nc
    GROUPS = TILES // 4
    PARTS = 2
    IN_PART = GROUPS // PARTS
    with Stage(core, "ln") as st:
        sq = st.sb("sq", [P, TILES, D])
        mean = st.sb("mean", [P, TILES])
        var = st.sb("var", [P, TILES])
        rstd = core.rstd
        staged = st.sb("staged", [P, 2, 4, D])
        pT = [st.ps(f"pT{i}", [P, BANK]) for i in range(2)]
        names = ("w_loaded", "summed", "mean_ready", "centred", "squared", "squares_summed", "var_ready", "std_ready", "rstd_ready", "norm_ready", "turned", "xnT_ready")
        (w_loaded, summed, mean_ready, centred, squared, squares_summed, var_ready, std_ready, rstd_ready, norm_ready, turned, xnT_ready) = (st.sem(n) for n in names)
        tiles = lambda part: slice(part * TILES // PARTS, (part + 1) * TILES // PARTS)
        with nc.Block() as block:
            if weights_stage is not None:
                @block.sync
                def _(sp):
                    sp.dma_start(weights_stage.w_sb[:, :], weights_stage.blob).then_inc(w_loaded, 16)
                    sp.wait_ge(w_loaded, 16)

            @block.vector
            def _(v):
                def mean_of(part):
                    ts = tiles(part)
                    nc.vector.tensor_reduce(mean[:, ts], core.x_res[:, ts, :], AX.X, ALU.add).then_inc(summed, 1)
                    v.wait_ge(summed, part + 1)
                    nc.vector.tensor_scalar(mean[:, ts], mean[:, ts], 1.0 / D, None, ALU.mult).then_inc(mean_ready, 1)

                def centre(part):
                    ts = tiles(part)
                    v.wait_ge(mean_ready, part + 1)
                    nc.vector.tensor_tensor(core.xn[:, ts, :], core.x_res[:, ts, :], bc(mean[:, ts], 2, D), ALU.subtract).then_inc(centred, 1)

                def variance(part):
                    ts = tiles(part)
                    v.wait_ge(squared, part + 1)
                    nc.vector.tensor_reduce(var[:, ts], sq[:, ts, :], AX.X, ALU.add).then_inc(squares_summed, 1)
                    v.wait_ge(squares_summed, part + 1)
                    nc.vector.tensor_scalar(var[:, ts], var[:, ts], 1.0 / D, LN_EPS, ALU.mult, ALU.add).then_inc(var_ready, 1)

                def normalise(part):
                    ts = tiles(part)
                    v.wait_ge(std_ready, part + 1)
                    nc.vector.reciprocal(rstd[:, ts], rstd[:, ts]).then_inc(rstd_ready, 1)
                    v.wait_ge(rstd_ready, part + 1)
                    with v.Fori(part * IN_PART // 2, (part + 1) * IN_PART // 2) as g:
                        for i in range(2):
                            four = bass.ds(g * 8 + 4 * i, 4)
                            v.wait_ge(turned, 2 * g + i + 1)
                            nc.vector.tensor_tensor(staged[:, i, :, :], core.xn[:, four, :], bc(rstd[:, four], 2, D),
                                                    ALU.mult).then_inc(norm_ready, 1)

                v.sem_inc(turned, 2)
                mean_of(0)
                centre(0)
                mean_of(1)
                variance(0)
                centre(1)
                normalise(0)
                variance(1)
                normalise(1)

            @block.scalar
            def _(a):
                def square(part):
                    ts = tiles(part)
                    a.wait_ge(centred, part + 1)
                    nc.scalar.activation(sq[:, ts, :], core.xn[:, ts, :], ACT.Square).then_inc(squared, 1)

                def root(part):
                    ts = tiles(part)
                    a.wait_ge(var_ready, part + 1)
                    nc.scalar.activation(rstd[:, ts], var[:, ts], ACT.Sqrt).then_inc(std_ready, 1)

                def take(part):
                    with a.Fori(part * IN_PART // 2, (part + 1) * IN_PART // 2) as g:
                        for i in range(2):
                            a.wait_ge(turned, 2 * g + i + 3)
                            nc.scalar.copy(core.xnT[:, bass.ds(g * 2 * BANK + i * BANK, BANK)], pT[i][:, :]).then_inc(xnT_ready, 1)

                square(0)
                root(0)
                square(1)
                take(0)
                root(1)
                take(1)

            @block.tensor
            def _(pe):
                pe.sem_inc(xnT_ready, 2)
                with pe.Fori(0, GROUPS // 2) as g:
                    for i in range(2):
                        pe.wait_ge(norm_ready, 2 * g + i + 1)
                        pe.wait_ge(xnT_ready, 2 * g + i + 1)
                        for k in range(4):
                            ins = nc.tensor.transpose(pT[i][:, k * P:(k + 1) * P],
                                                      staged[:, i, k, :], core.ident[:, :])
                        ins.then_inc(turned, 1)


ROPE_BASE = 10000.0
ATTN_A_HD = D // HEADS
LOW = 64
PER = 32 // ATTN_A_HD
QUADS = HEADS // PER
LEAD = 3


def pack(parts):
    offsets, cols, at = {}, [], 0
    for name, a in parts:
        a = np.asarray(a)
        if a.ndim == 1:
            a = a[:, None]
        full = np.zeros((P, a.shape[1]), a.dtype)
        full[:a.shape[0]] = a
        cols.append(full)
        offsets[name] = (at, at + a.shape[1])
        at += a.shape[1]
    return np.concatenate(cols, axis=1), offsets


def rope_tables():
    ids = np.arange(D // 2, dtype=np.float32)
    theta = (np.float32(ROPE_BASE) ** (np.float32(-2.0) * ids) / np.float32(D // 2)).astype(np.float32)
    r = np.arange(SEQ, dtype=np.float32)[:, None] * theta[None, :]
    cos = np.repeat(np.cos(r), 2, axis=1).T
    sin = np.repeat(np.sin(r), 2, axis=1).T.copy()
    sin[0::2] *= -1
    return cos.astype(np.float32), sin.astype(np.float32)


def attn_a_weights(w):
    swap = np.arange(D) ^ 1
    cos, sin = rope_tables()
    low = lambda a: np.concatenate([np.zeros((LOW, a.shape[1]), a.dtype), a], axis=0)
    scale = np.float32(1.0 / np.sqrt(HEADS + LOW + LOW))
    head_of = np.arange(P) // ATTN_A_HD
    quad_in_32 = np.arange(32) // ATTN_A_HD
    own = (quad_in_32[None, :] == np.arange(QUADS)[:, None]).astype(np.float32)
    wo = w["Wo_w"].reshape(QUADS, PER, ATTN_A_HD, D).transpose(1, 0, 2, 3).reshape(D, D)
    return pack([
        ("down", np.concatenate([w["Wd_q_w"], w["Wd_kv_w"]], axis=1)),
        ("down_b", np.concatenate([w["Wd_q_b"], w["Wd_kv_b"]])),
        ("uq", w["Wu_q_w"]), ("qr", w["Wq_r_w"]), ("qr_swap", w["Wq_r_w"][:, swap]),
        ("uk", low(w["Wu_k_w"])), ("uv", low(w["Wu_v_w"])),
        ("kr", w["Wk_r_w"]), ("kr_swap", w["Wk_r_w"][:, swap]),
        ("uq_b", w["Wu_q_b"]), ("qr_b", w["Wq_r_b"]), ("qr_swap_b", w["Wq_r_b"][swap]),
        ("uk_b", w["Wu_k_b"]), ("kr_b", w["Wk_r_b"]), ("kr_swap_b", w["Wk_r_b"][swap]),
        ("uv_b", np.broadcast_to(w["Wu_v_b"], (P, D))),
        ("wo", wo), ("wo_b", w["Wo_b"][None, :]),
        ("cos_q", cos * scale), ("sin_q", sin * scale), ("cos_k", cos), ("sin_k", sin),
        ("head_mask", (head_of[:, None] == np.arange(HEADS)[None, :]).astype(np.float32)),
        ("own", np.broadcast_to(own.reshape(1, -1), (P, QUADS * 32))),
    ])


def attn_a(core, blob, offsets):
    nc = core.nc
    scale = float(np.float32(1.0 / np.sqrt(HEADS + LOW + LOW)))
    with Stage(core, "attn_a") as st:
        w = st.weights(blob, offsets)
        layer_norm(core, st)
        qT = st.sb("qT", [P, TOK])
        kT = st.sb("kT", [P, TOK])
        val = st.sb("val", [P, TILES, D])
        bank = [st.ps(f"bank{i}", [P, BANK]) for i in range(8)]

        ct = st.sb("ct", [P, BANK])
        plain = st.sb("plain", [P, BANK])
        rot = [st.sb(f"rot{i}", [P, BANK]) for i in range(4)]
        down_ready, ct_ready = st.sem("down_ready"), st.sem("ct_ready")
        q_ready, k_ready, v_ready = st.sem("q_ready"), st.sem("k_ready"), st.sem("v_ready")
        plain_ready, plain_used = st.sem("plain_ready"), st.sem("plain_used")
        group_done, dve1 = st.sem("group_done"), st.sem("dve1")
        pd, pq, pqr, pqs, pk, pkr, pks, pv = bank
        GROUPS = TOK // BANK
        with nc.Block() as block:
            @block.tensor
            def _(pe):
                with pe.Fori(0, GROUPS) as g:
                    x = core.xnT[:, bass.ds(g * BANK, BANK)]
                    nc.tensor.matmul(pd[:, :], w["down"], x, start=True, stop=True).then_inc(down_ready, 1)
                    pe.wait_ge(group_done, g)
                    nc.tensor.matmul(pkr[:, :], w["kr"], x, start=True, stop=True)
                    nc.tensor.matmul(pks[:, :], w["kr_swap"], x, start=True, stop=True)
                    pe.wait_ge(ct_ready, g + 1)
                    nc.tensor.matmul(pq[:, :], w["uq"][0:LOW, :], ct[0:LOW, :], start=True, stop=True)
                    nc.tensor.matmul(pqr[:, :], w["qr"][0:LOW, :], ct[0:LOW, :], start=True, stop=True)
                    nc.tensor.matmul(pqs[:, :], w["qr_swap"][0:LOW, :], ct[0:LOW, :], start=True, stop=True).then_inc(q_ready, 1)
                    nc.tensor.matmul(pk[:, :], w["uk"][LOW:P, :], ct[LOW:P, :], start=True, stop=True).then_inc(k_ready, 1)
                    for t in range(4):
                        ins = nc.tensor.matmul(pv[:, t * P:(t + 1) * P], ct[LOW:P, t * P:(t + 1) * P], w["uv"][LOW:P, :],
                                               start=True, stop=True)
                    ins.then_inc(v_ready, 1)

            @block.scalar
            def _(a):
                with a.Fori(0, GROUPS) as g:
                    a.wait_ge(down_ready, g + 1)
                    a.wait_ge(v_ready, g)
                    nc.scalar.activation(ct[:, :], pd[:, :], ACT.Identity, bias=w["down_b"]).then_inc(ct_ready, 1)
                    a.wait_ge(q_ready, g + 1)
                    a.wait_ge(plain_used, 2 * g)
                    nc.scalar.activation(plain[:, :], pq[:, :], ACT.Identity, bias=w["uq_b"]).then_inc(plain_ready, 1)
                    a.wait_ge(k_ready, g + 1)
                    a.wait_ge(plain_used, 2 * g + 1)
                    nc.scalar.activation(plain[:, :], pk[:, :], ACT.Identity, bias=w["uk_b"]).then_inc(plain_ready, 1)

            @block.vector
            def _(v):
                with v.Fori(0, GROUPS) as g:
                    c = Chain(v, dve1, 4 * g)
                    cols = bass.ds(g * BANK, BANK)
                    two = lambda t: t.rearrange("p (b s) -> p b s", b=2)
                    for i, (side, out, direct, swapped, s) in enumerate((("q", qT, pqr, pqs, scale), ("k", kT, pkr, pks, 1.0))):
                        v.wait_ge((q_ready, k_ready)[i], g + 1)
                        rot_a, rot_b = rot[2 * i], rot[2 * i + 1]
                        nc.vector.scalar_tensor_tensor(two(rot_a[:, :]), two(direct[:, :]), w[f"{side}r_b"],
                                                       bc(w[f"cos_{side}"], 1, 2), ALU.add, ALU.mult)
                        c.link(nc.vector.scalar_tensor_tensor(two(rot_b[:, :]), two(swapped[:, :]), w[f"{side}r_swap_b"],
                                                              bc(w[f"sin_{side}"], 1, 2), ALU.add, ALU.mult))
                        c.link(nc.vector.tensor_tensor(rot_a[:, :], rot_a[:, :], rot_b[:, :], ALU.add))
                        v.wait_ge(plain_ready, 2 * g + i + 1)
                        nc.vector.scalar_tensor_tensor(out[:, cols], plain[:, :], s, rot_a[:, :],
                                                       ALU.mult, ALU.add).then_inc(plain_used, 1)
                    v.wait_ge(v_ready, g + 1)
                    nc.vector.tensor_tensor(val[:, bass.ds(g * 4, 4), :], pv[:, :].rearrange("p (t d) -> p t d", t=4),
                                            bc(w["uv_b"], 1, 4), ALU.add).then_inc(group_done, 1)

        q_heads = st.sb("q_heads", [P, 2, HEADS, SEQ])
        k_now = st.sb("k_now", [P, 2, SEQ])
        v_heads = st.sb("v_heads", [P, 2, 2, QUADS, PER, QUADS, ATTN_A_HD])
        prob = st.sb("prob", [P, 4, 2, SEQ])
        probT = st.sb("probT", [P, 2 * PER, 2, SEQ])
        neg_max = st.sb("neg_max", [P, 4, 2])
        row_sum = st.sb("row_sum", [P, 2, 2, HEADS])
        inv_sum = st.sb("inv_sum", [P, 2, HEADS])
        inv_wide = st.sb("inv_wide", [P, 2, PER, QUADS, ATTN_A_HD])
        inv_T = st.sb("inv_T", [P, SEQ])
        outT = st.sb("outT", [P, SEQ])
        pS, pT, pO, pInv, pY = bank[0:4], bank[4:6], bank[6], bank[7][:, 0:SEQ], bank[7][:, SEQ:2 * SEQ]
        names = ("q_heads_ready", "v_heads_ready", "scores_ready", "max_ready", "prob_ready", "probT_psum", "probT_ready", "quad_done",
                 "sums_inverted", "inv_wide_ready", "inv_psum", "inv_T_ready", "outT_ready", "y_ready", "y_added")
        (q_heads_ready, v_heads_ready, scores_ready, max_ready, prob_ready, probT_psum, probT_ready, quad_done,
         sums_inverted, inv_wide_ready, inv_psum, inv_T_ready, outT_ready, y_ready, y_added) = (st.sem(n) for n in names)

        with nc.Block() as block:
            @block.gpsimd
            def _(pool):
                def prepare(b, s, first, last):
                    if not known(b, 2):
                        pool.wait_ge(scores_ready, (b - 1) * HEADS)
                    nc.gpsimd.tensor_copy(k_now[:, s, :], kT[:, bass.ds(b * SEQ, SEQ)]).then_inc(q_heads_ready, 1)
                    nc.gpsimd.tensor_tensor(q_heads[:, s, :, :], bc(qT[:, bass.ds(b * SEQ, SEQ)], 1, HEADS),
                                            bc(w["head_mask"], 2, SEQ), ALU.mult).then_inc(q_heads_ready, 1)
                    if not known(b, 2):
                        pool.wait_ge(quad_done, (b - 1) * QUADS)
                    for kt in range(2):
                        for quad in range(QUADS):
                            v = val[:, bass.ds(b * 2 + kt, 1), quad * 32:(quad + 1) * 32].squeeze(1).rearrange("p (j d) -> p j d", j=PER)
                            nc.gpsimd.tensor_tensor(v_heads[:, s, kt, quad, :, :, :], bc(v, 2, QUADS),
                                                    bc(w["own"][:, quad * 32:(quad + 1) * 32].rearrange("p (i d) -> p i d", i=QUADS), 1, PER),
                                                    ALU.mult).then_inc(v_heads_ready, 1)

                sequences(pool, prepare)

            @block.tensor
            def _(pe):
                def scores(b, s, h):
                    if h == 0:
                        pe.wait_ge(q_heads_ready, 2 * b + 2)
                    for qt in range(2):
                        ins = nc.tensor.matmul(pS[h % 4][:, qt * SEQ:(qt + 1) * SEQ], q_heads[:, s, h, qt * P:(qt + 1) * P],
                                               k_now[:, s, :], start=True, stop=True)
                    ins.then_inc(scores_ready, 1)

                def turn(b, h):
                    pe.wait_ge(prob_ready, b * HEADS + h + 1)
                    if not (known(b, 1) and h < 2):
                        pe.wait_ge(probT_ready, b * HEADS + h - 1)
                    for kt in range(2):
                        for qt in range(2):
                            ins = nc.tensor.transpose(pT[h % 2][:, kt * SEQ + qt * P:kt * SEQ + (qt + 1) * P],
                                                      prob[:, h % 4, qt, kt * P:(kt + 1) * P], core.ident[:, :])
                    ins.then_inc(probT_psum, 1)

                def weighted(b, s, quad):
                    if quad == 0:
                        pe.wait_ge(v_heads_ready, 2 * QUADS * (b + 1))
                        if not known(b, 1):
                            pe.wait_ge(outT_ready, b)
                    pe.wait_ge(probT_ready, b * HEADS + (quad + 1) * PER)
                    for kt in range(2):
                        for j in range(PER):
                            ins = nc.tensor.matmul(pO[32 * j:32 * (j + 1), 0:SEQ], v_heads[:, s, kt, quad, j, :, :].rearrange("p i d -> p (i d)"),
                                                   probT[:, (quad * PER + j) % (2 * PER), kt, :], start=(quad == 0 and kt == 0),
                                                   stop=(quad == QUADS - 1 and kt == 1), tile_position=(0, 32 * j))
                    ins.then_inc(quad_done, 1)

                def turn_inverses(b):
                    pe.wait_ge(inv_wide_ready, b + 1)
                    for qt in range(2):
                        ins = nc.tensor.transpose(pInv[:, qt * P:(qt + 1) * P], inv_wide[:, qt, :, :, :].rearrange("p j i d -> p (j i d)"), core.ident[:, :])
                    ins.then_inc(inv_psum, 1)

                def project(b):
                    pe.wait_ge(outT_ready, b + 1)
                    for qt in range(2):
                        y = pY[:, qt * P:(qt + 1) * P]
                        nc.tensor.matmul(y, core.ones[0:1, :], w["wo_b"][0:1, :], start=True, stop=False)
                        ins = nc.tensor.matmul(y, outT[:, qt * P:(qt + 1) * P], w["wo"], start=False, stop=True)
                    ins.then_inc(y_ready, 1)

                def step(b, s, first, last):
                    if first:
                        for h in range(LEAD):
                            scores(b, s, h)
                    for h in range(HEADS):
                        turn(b, h)
                        if h + LEAD < HEADS:
                            scores(b, s, h + LEAD)
                        elif not last:
                            scores(b + 1, 1 - s, h + LEAD - HEADS)
                        if h == 1 and not first:
                            weighted(b - 1, 1 - s, QUADS - 1)
                            turn_inverses(b - 1)
                        if h % PER == 1 and h > PER:
                            weighted(b, s, h // PER - 1)
                        if h == 6 and not first:
                            project(b - 1)
                    if last:
                        weighted(b, s, QUADS - 1)
                        turn_inverses(b)
                        project(b)

                sequences(pe, step)

            @block.scalar
            def _(a):
                def invT(b):
                    a.wait_ge(inv_psum, b + 1)
                    nc.scalar.copy(inv_T[:, :], pInv).then_inc(inv_T_ready, 1)

                def step(b, s, first, last):
                    for h in range(HEADS):
                        if h == 5 and not first:
                            invT(b - 1)
                        a.wait_ge(max_ready, b * HEADS + h + 1)
                        for qt in range(2):
                            ins = nc.scalar.activation(prob[:, h % 4, qt, :], pS[h % 4][:, qt * SEQ:(qt + 1) * SEQ], ACT.Exp,
                                                       bias=neg_max[:, h % 4, qt:qt + 1], accum_out=row_sum[:, s, qt, h:h + 1])
                        ins.then_inc(prob_ready, 1)
                    if last:
                        invT(b)

                sequences(a, step)

            @block.vector
            def _(v):
                def row_max(b, h):
                    v.wait_ge(scores_ready, b * HEADS + h + 1)
                    nc.vector.tensor_reduce(neg_max[:, h % 4, :], pS[h % 4][:, :].rearrange("p (q k) -> p q k", q=2),
                                            AX.X, ALU.max, negate=True).then_inc(max_ready, 1)

                def copy(b, h):
                    v.wait_ge(probT_psum, b * HEADS + h + 1)
                    if h % PER == 0 and not (known(b, 1) and h < 2 * PER):
                        v.wait_ge(quad_done, b * QUADS + h // PER - 1)
                    nc.vector.tensor_copy(probT[:, h % (2 * PER), :, :], pT[h % 2][:, :].rearrange("p (k q) -> p k q", k=2)).then_inc(probT_ready, 1)

                def invert(b, s):
                    v.wait_ge(prob_ready, (b + 1) * HEADS)
                    nc.vector.reciprocal(inv_sum[:, :, :], row_sum[:, s, :, :]).then_inc(sums_inverted, 1)
                    v.wait_ge(sums_inverted, b + 1)
                    for qt in range(2):
                        ins = nc.vector.tensor_copy(inv_wide[:, qt, :, :, :], bc(inv_sum[:, qt, :].rearrange("p (i j) -> p j i", i=QUADS), 3, ATTN_A_HD))
                    ins.then_inc(inv_wide_ready, 1)

                def normalise(b):
                    v.wait_ge(quad_done, (b + 1) * QUADS)
                    v.wait_ge(inv_T_ready, b + 1)
                    nc.vector.tensor_tensor(outT[:, :], pO[:, 0:SEQ], inv_T[:, :], ALU.mult).then_inc(outT_ready, 1)

                def add(b):
                    v.wait_ge(y_ready, b + 1)
                    x = core.x_res[:, bass.ds(b * 2, 2), :]
                    nc.vector.tensor_tensor(x, x, pY.rearrange("p (q d) -> p q d", q=2), ALU.add).then_inc(y_added, 1)

                def step(b, s, first, last):
                    if first:
                        for h in range(LEAD):
                            row_max(b, h)
                    for h in range(HEADS):
                        copy(b, h)
                        if h + LEAD < HEADS:
                            row_max(b, h + LEAD)
                        elif not last:
                            row_max(b + 1, h + LEAD - HEADS)
                        if not first:
                            if h == 0:
                                invert(b - 1, 1 - s)
                            if h == 3:
                                normalise(b - 1)
                            if h == 8:
                                add(b - 1)
                    if last:
                        invert(b, s)
                        normalise(b)
                        add(b)

                sequences(v, step)


def earlier_table(n):
    return np.broadcast_to(np.tril(np.ones((n, n), np.float32), -1).reshape(1, n * n), (P, n * n))


def link_ranks(nc, c, rank, val, above, same, earlier, n):
    vj, vi = bc(val, 2, n), bc(val, 3, n)
    nc.vector.tensor_tensor(above, vj, vi, ALU.is_gt)
    c.link(nc.vector.tensor_tensor(same, vj, vi, ALU.is_equal))
    c.link(nc.vector.tensor_tensor(same, same, bc(earlier.rearrange("p (i j) -> p i j", i=n), 1, val.shape[1]), ALU.mult))
    c.link(nc.vector.tensor_tensor(above, above, same, ALU.add))
    c.link(nc.vector.tensor_reduce(rank, above, AX.X, ALU.add))


def router_logits(core, router, out_bank, experts, st):
    nc = core.nc
    x_now = st.sb("router_x", [P, 2, BANK])
    copied, used = st.sem("router_copied"), st.sem("router_used")
    GROUPS = TOK // BANK
    with nc.Block() as block:
        @block.gpsimd
        def _(pool):
            pool.sem_inc(used, 2)
            with pool.Fori(0, GROUPS // 2) as g:
                for s in range(2):
                    pool.wait_ge(used, 2 * g + s + 1)
                    nc.gpsimd.tensor_copy(x_now[:, s, :], core.xnT[:, bass.ds((2 * g + s) * BANK, BANK)]).then_inc(copied, 1)

        @block.tensor
        def _(pe):
            with pe.Fori(0, GROUPS // 2) as g:
                for s in range(2):
                    pe.wait_ge(copied, 2 * g + s + 1)
                    for t in range(4):
                        ins = nc.tensor.matmul(out_bank(g * 8 + s * 4 + t), x_now[:, s, t * P:(t + 1) * P], router, start=True, stop=True)
                    ins.then_inc(used, 1)


CYCLES = 3
QUARTER = D // 4


def ffn0_weights(w):
    twist = np.zeros((D, D), np.float32)
    for to, (frm, sign) in enumerate(((2, 1.0), (3, -1.0), (0, -1.0), (1, 1.0))):
        for k in range(QUARTER):
            twist[frm * QUARTER + k, to * QUARTER + k] = sign
    wide = lambda a: np.broadcast_to(a.reshape(-1, 1), (a.size, P))
    tall = lambda a: np.broadcast_to(a.reshape(1, 1), (P, 1))
    full = lambda a: np.concatenate([a, np.zeros((a.shape[0], P - a.shape[1]), a.dtype)], axis=1)
    return pack([
        ("cn1", w["cn_w1"]), ("cn2", full(w["cn_w2"])), ("cn3", full(w["cn_w3"])), ("cn4", wide(w["cn_w4"])),
        ("cn1_b", w["cn_b1"]), ("cn2_b", w["cn_b2"]), ("cn3_b", w["cn_b3"]), ("cn4_b", tall(w["cn_b4"])),
        ("gc1", full(w["gc_w1"])), ("gc2", full(w["gc_w2"])), ("gc3", wide(w["gc_w3"])),
        ("gc1_b", w["gc_b1"]), ("gc2_b", w["gc_b2"]), ("gc3_b", tall(w["gc_b3"])),
        ("range", tall(w["adaptive_range"])), ("twist", twist),
    ])


def ffn0(core, blob, offsets):
    nc = core.nc
    base, share_gf, share_tf = 0.1, 0.7, 0.3
    with Stage(core, "ffn0") as st:
        w = st.weights(blob, offsets)
        layer_norm(core, st)
        bank = [st.ps(f"bank{i}", [P, BANK]) for i in range(8)]
        mean = st.sb("mean", [P, BATCH])
        g1, g2 = st.sb("g1", [P, BATCH]), st.sb("g2", [P, BATCH])
        gf = st.sb("gf", [P, BATCH])
        offset = st.sb("offset", [P, BATCH])
        half_b = st.sb("half_b", [P, 2])
        slope = st.sb("slope", [P, 1])
        dve, glob, glob_act, h_ready = st.sem("dve"), st.sem("glob"), st.sem("glob_act"), st.sem("h_ready")
        with nc.Block() as block:
            @block.vector
            def _(v):
                c = Chain(v, dve)
                c.link(nc.vector.tensor_reduce(mean[:, :], core.xnT[:, :].rearrange("p (b s) -> p b s", s=SEQ), AX.X, ALU.add))
                nc.vector.tensor_scalar(half_b[:, 0:1], w["gc3_b"], 0.5, None, ALU.mult)
                nc.vector.tensor_scalar(half_b[:, 1:2], w["cn4_b"], 0.5, None, ALU.mult)
                nc.vector.tensor_scalar(slope[:, :], w["range"], share_tf, None, ALU.mult)
                c.link(nc.vector.tensor_scalar(mean[:, :], mean[:, :], 1.0 / SEQ, None, ALU.mult))
                v.wait_ge(glob_act, 3)
                c.link(nc.vector.tensor_scalar(gf[:, :], gf[:, :], share_gf, share_gf + share_tf - 1.0, ALU.mult, ALU.add))
                c.link(nc.vector.tensor_scalar(offset[:, :], gf[:, :], w["range"], base, ALU.mult, ALU.add))

            @block.tensor
            def _(pe):
                pe.wait_ge(dve, 2)
                nc.tensor.matmul(bank[0][:, 0:BATCH], w["gc1"], mean[:, :], start=True, stop=True).then_inc(glob, 1)
                pe.wait_ge(glob_act, 1)
                nc.tensor.matmul(bank[1][:, 0:BATCH], w["gc2"], g1[:, :], start=True, stop=True).then_inc(glob, 1)
                pe.wait_ge(glob_act, 2)
                nc.tensor.matmul(bank[2][:, 0:BATCH], w["gc3"], g2[:, :], start=True, stop=True).then_inc(glob, 1)

            @block.scalar
            def _(a):
                a.wait_ge(glob, 1)
                nc.scalar.activation(g1[:, :], bank[0][:, 0:BATCH], ACT.Gelu, bias=w["gc1_b"]).then_inc(glob_act, 1)
                a.wait_ge(glob, 2)
                nc.scalar.activation(g2[:, :], bank[1][:, 0:BATCH], ACT.Gelu, bias=w["gc2_b"]).then_inc(glob_act, 1)
                a.wait_ge(glob, 3)
                nc.scalar.activation(gf[:, :], bank[2][:, 0:BATCH], ACT.Tanh, bias=half_b[:, 0:1], scale=0.5).then_inc(glob_act, 1)

        cur = st.sb("cur", [P, 2, 2, BANK])
        h1, h2, h3 = (st.sb(f"h{i}", [P, 2, BANK]) for i in (1, 2, 3))
        tf = st.sb("tf", [P, 2, BANK])
        psum_ready = st.sem("psum_ready")
        hidden_ready = st.sem("hidden_ready")
        twisted, cycled, turned, added, copied, dve2 = (st.sem(n) for n in ("twisted", "cycled", "turned", "added", "copied", "dve2"))
        LAYERS = 4
        GROUPS = TOK // BANK
        with nc.Block() as block:
            @block.tensor
            def _(pe):
                with pe.Fori(0, GROUPS // 2) as g:
                    for cyc in range(CYCLES):
                        step = g * CYCLES * 2 + cyc * 2
                        for layer, name in enumerate(("cn1", "cn2", "cn3", "cn4")):
                            for s in range(2):
                                if layer == 0:
                                    if cyc == 0:
                                        pe.wait_ge(copied, 2 * g + s + 1)
                                    else:
                                        pe.wait_ge(cycled, step + s - 1)
                                    rhs = cur[:, s, cyc % 2, :]
                                    nc.tensor.matmul(bank[4 + s][:, :], w["twist"], rhs, start=True, stop=True).then_inc(twisted, 1)
                                else:
                                    pe.wait_ge(hidden_ready, step * LAYERS + (layer - 1) * 2 + s + 1)
                                    rhs = (h1, h2, h3)[layer - 1][:, s, :]
                                nc.tensor.matmul(bank[2 * (layer % 2) + s][:, :], w[name], rhs, start=True,
                                                 stop=True).then_inc(psum_ready, 1)
                    for s in range(2):
                        pe.wait_ge(cycled, (g + 1) * CYCLES * 2 - 1 + s)
                        for t in range(4):
                            ins = nc.tensor.transpose(bank[6 + s][:, t * P:(t + 1) * P],
                                                      cur[:, s, CYCLES % 2, t * P:(t + 1) * P], core.ident[:, :])
                        ins.then_inc(turned, 1)

            @block.scalar
            def _(a):
                with a.Fori(0, GROUPS // 2) as g:
                    for cyc in range(CYCLES):
                        step = g * CYCLES * 2 + cyc * 2
                        for layer, name in enumerate(("cn1", "cn2", "cn3", "cn4")):
                            for s in range(2):
                                a.wait_ge(psum_ready, step * LAYERS + layer * 2 + s + 1)
                                src = bank[2 * (layer % 2) + s][:, :]
                                if layer < 3:
                                    nc.scalar.activation((h1, h2, h3)[layer][:, s, :], src, ACT.Gelu,
                                                         bias=w[f"{name}_b"]).then_inc(hidden_ready, 1)
                                else:
                                    nc.scalar.activation(tf[:, s, :], src, ACT.Tanh, bias=half_b[:, 1:2],
                                                         scale=0.5).then_inc(hidden_ready, 1)

            @block.vector
            def _(v):
                with v.Fori(0, GROUPS // 2) as g:
                    c = Chain(v, dve2, g * CYCLES * 2 * 2)
                    for s in range(2):
                        nc.vector.tensor_copy(cur[:, s, 0, :], core.xnT[:, bass.ds((2 * g + s) * BANK, BANK)]).then_inc(copied, 1)
                    for cyc in range(CYCLES):
                        step = g * CYCLES * 2 + cyc * 2
                        for s in range(2):
                            v.wait_ge(hidden_ready, step * LAYERS + 6 + s + 1)
                            for b in range(2):
                                ins = nc.vector.tensor_scalar(tf[:, s, b * SEQ:(b + 1) * SEQ], tf[:, s, b * SEQ:(b + 1) * SEQ], slope[:, :],
                                                              offset[:, bass.ds(4 * g + 2 * s + b, 1)], ALU.mult, ALU.add)
                            c.link(ins)
                            v.wait_ge(twisted, step + s + 1)
                            c.link(nc.vector.tensor_tensor(tf[:, s, :], tf[:, s, :], bank[4 + s][:, :], ALU.mult))
                            nc.vector.tensor_tensor(cur[:, s, 1 - cyc % 2, :], cur[:, s, cyc % 2, :], tf[:, s, :], ALU.add).then_inc(cycled, 1)
                    for s in range(2):
                        v.wait_ge(turned, 2 * g + s + 1)
                        x = core.x_res[:, bass.ds((2 * g + s) * 4, 4), :]
                        nc.vector.tensor_tensor(x, x, bank[6 + s][:, :].rearrange("p (t d) -> p t d", t=4), ALU.add).then_inc(added, 1)


ATTN_B0_HD = D // HEADS


def attn_b0_weights(w):
    head = np.arange(D) // ATTN_B0_HD
    return pack([
        ("wq", w["Wqkv"][:, 0:D]), ("wk", w["Wqkv"][:, D:2 * D]), ("wv", w["Wqkv"][:, 2 * D:3 * D]),
        ("wg", w["Wg"]), ("bg", w["bg"]), ("wp", w["Wp"]), ("bp", w["bp"][None, :]),
        ("same_head", (head[:, None] == head[None, :]).astype(np.float32)),
        ("of_head", (head[:, None] == np.arange(HEADS)[None, :]).astype(np.float32)),
    ])


def attn_b0(core, blob, offsets):
    nc = core.nc
    T = BANK // P
    S = BANK // SEQ
    KV = D + 1
    OUT = D + HEADS
    GROUPS = TOK // BANK
    with Stage(core, "attn_b0") as st:
        w = st.weights(blob, offsets)
        layer_norm(core, st)
        bank = [st.ps(f"bank{i}", [P, BANK]) for i in range(8)]
        x_now = st.sb("x_now", [P, BANK])
        half_bg = st.sb("half_bg", [P, 1])
        gate = st.sb("gate", [P, BANK])
        z = st.sb("z", [P, 2, BANK])
        neg_exp = st.sb("neg_exp", [P, 2, BANK])
        feat = st.sb("feat", [P, 2, BANK])
        k_tok = st.sb("k_tok", [P, T, D])
        v_tok = st.sb("v_tok", [P, T, KV])
        kv = st.sb("kv", [P, S, OUT])
        inv = st.sb("inv", [P, T, HEADS])
        o_tok = st.sb("o_tok", [P, T, D])
        oT = st.sb("oT", [P, BANK])
        names = ("x_copied", "qkg_ready", "v_psum", "tanh_ready", "min_ready", "exp_ready", "feat_ready", "v_ready", "k_psum",
                 "k_ready", "kv_psum", "kv_ready", "o_psum", "o_ready", "oT_psum", "oT_ready", "y_ready", "y_added", "dve", "set_up")
        (x_copied, qkg_ready, v_psum, tanh_ready, min_ready, exp_ready, feat_ready, v_ready, k_psum,
         k_ready, kv_psum, kv_ready, o_psum, o_ready, oT_psum, oT_ready, y_ready, y_added, dve, set_up) = (st.sem(n) for n in names)
        by_tile = lambda ap: ap.rearrange("p (t d) -> p t d", t=T)
        with nc.Block() as block:
            @block.gpsimd
            def _(pool):
                nc.gpsimd.memset(v_tok[:, :, D:KV], 1.0).then_inc(set_up, 1)
                with pool.Fori(0, GROUPS) as g:
                    pool.wait_ge(v_psum, g)
                    nc.gpsimd.tensor_copy(x_now[:, :], core.xnT[:, bass.ds(g * BANK, BANK)]).then_inc(x_copied, 1)

            @block.tensor
            def _(pe):
                with pe.Fori(0, GROUPS) as g:
                    x = core.xnT[:, bass.ds(g * BANK, BANK)]
                    nc.tensor.matmul(bank[0][:, :], w["wg"], x, start=True, stop=True)
                    nc.tensor.matmul(bank[1][:, :], w["wq"], x, start=True, stop=True)
                    nc.tensor.matmul(bank[2][:, :], w["wk"], x, start=True, stop=True).then_inc(qkg_ready, 1)
                    pe.wait_ge(x_copied, g + 1)
                    pe.wait_ge(y_added, g)
                    for t in range(T):
                        ins = nc.tensor.matmul(bank[3][:, t * P:(t + 1) * P], x_now[:, t * P:(t + 1) * P], w["wv"], start=True, stop=True)
                    ins.then_inc(v_psum, 1)
                    pe.wait_ge(feat_ready, g + 1)
                    for t in range(T):
                        ins = nc.tensor.transpose(bank[4][:, t * P:(t + 1) * P], feat[:, 1, t * P:(t + 1) * P], core.ident[:, :])
                    ins.then_inc(k_psum, 1)
                    pe.wait_ge(k_ready, g + 1)
                    pe.wait_ge(v_ready, g + 1)
                    for s in range(S):
                        for t in range(2):
                            ins = nc.tensor.matmul(bank[5][:, s * KV:(s + 1) * KV], k_tok[:, 2 * s + t, :], v_tok[:, 2 * s + t, :],
                                                   start=(t == 0), stop=(t == 1))
                    ins.then_inc(kv_psum, 1)
                    pe.wait_ge(kv_ready, g + 1)
                    for t in range(T):
                        at = (t % 2) * OUT
                        ins = nc.tensor.matmul(bank[6 + t // 2][:, at:at + OUT], feat[:, 0, t * P:(t + 1) * P], kv[:, t // 2, :],
                                               start=True, stop=True)
                    ins.then_inc(o_psum, 1)
                    pe.wait_ge(o_ready, g + 1)
                    for t in range(T):
                        ins = nc.tensor.transpose(bank[4][:, t * P:(t + 1) * P], o_tok[:, t, :], core.ident[:, :])
                    ins.then_inc(oT_psum, 1)
                    pe.wait_ge(oT_ready, g + 1)
                    for t in range(T):
                        y = bank[3][:, t * P:(t + 1) * P]
                        nc.tensor.matmul(y, core.ones[0:1, :], w["bp"][0:1, :], start=True, stop=False)
                        ins = nc.tensor.matmul(y, oT[:, t * P:(t + 1) * P], w["wp"], start=False, stop=True)
                    ins.then_inc(y_ready, 1)

            @block.scalar
            def _(a):
                a.wait_ge(set_up, 2)
                with a.Fori(0, GROUPS) as g:
                    a.wait_ge(qkg_ready, g + 1)
                    nc.scalar.activation(gate[:, :], bank[0][:, :], ACT.Tanh, bias=half_bg[:, :], scale=0.5).then_inc(tanh_ready, 1)
                    a.wait_ge(min_ready, g + 1)
                    nc.scalar.activation(neg_exp[:, :, :], neg_exp[:, :, :], ACT.Exp).then_inc(exp_ready, 1)
                    a.wait_ge(k_psum, g + 1)
                    nc.scalar.copy(k_tok[:, :, :], by_tile(bank[4][:, :])).then_inc(k_ready, 1)
                    a.wait_ge(oT_psum, g + 1)
                    nc.scalar.copy(oT[:, :], bank[4][:, :]).then_inc(oT_ready, 1)

            @block.vector
            def _(v):
                nc.vector.tensor_scalar(half_bg[:, :], w["bg"], 0.5, None, ALU.mult).then_inc(set_up, 1)
                with v.Fori(0, GROUPS) as g:
                    c = Chain(v, dve, g * 4)
                    v.wait_ge(tanh_ready, g + 1)
                    c.link(nc.vector.tensor_scalar(gate[:, :], gate[:, :], 0.5, 0.5, ALU.mult, ALU.add))
                    nc.vector.tensor_tensor(z[:, 0, :], gate[:, :], bank[1][:, :], ALU.mult)
                    c.link(nc.vector.tensor_tensor(z[:, 1, :], gate[:, :], bank[2][:, :], ALU.mult))
                    nc.vector.tensor_scalar(neg_exp[:, :, :], z[:, :, :], 0.0, None, ALU.min).then_inc(min_ready, 1)
                    v.wait_ge(exp_ready, g + 1)
                    nc.vector.scalar_tensor_tensor(feat[:, :, :], z[:, :, :], 0.0, neg_exp[:, :, :], ALU.max,
                                                   ALU.add).then_inc(feat_ready, 1)
                    v.wait_ge(v_psum, g + 1)
                    nc.vector.tensor_copy(v_tok[:, :, 0:D], by_tile(bank[3][:, :])).then_inc(v_ready, 1)
                    v.wait_ge(kv_psum, g + 1)
                    for s in range(S):
                        nc.vector.tensor_tensor(kv[:, s, 0:D], bank[5][:, s * KV:s * KV + D], w["same_head"], ALU.mult)
                        ins = nc.vector.tensor_tensor(kv[:, s, D:OUT], w["of_head"],
                                                      bank[5][:, s * KV + D:(s + 1) * KV].broadcast_to([P, HEADS]), ALU.mult)
                    ins.then_inc(kv_ready, 1)
                    v.wait_ge(o_psum, g + 1)
                    pair = [bank[6 + i][:, 0:2 * OUT].rearrange("p (t o) -> p t o", t=2) for i in range(2)]
                    for i in range(2):
                        ins = nc.vector.tensor_scalar(inv[:, 2 * i:2 * i + 2, :], pair[i][:, :, D:OUT], 1e-8, None, ALU.add)
                    c.link(ins)
                    c.link(nc.vector.reciprocal(inv[:, :, :], inv[:, :, :]))
                    for i in range(2):
                        for t in range(2):
                            ins = nc.vector.tensor_tensor(o_tok[:, 2 * i + t, :].rearrange("p (h d) -> p h d", h=HEADS),
                                                          pair[i][:, t, 0:D].rearrange("p (h d) -> p h d", h=HEADS),
                                                          bc(inv[:, 2 * i + t, :], 2, ATTN_B0_HD), ALU.mult)
                    ins.then_inc(o_ready, 1)
                    v.wait_ge(y_ready, g + 1)
                    xr = core.x_res[:, bass.ds(g * T, T), :]
                    nc.vector.tensor_tensor(xr, xr, by_tile(bank[3][:, :]), ALU.add).then_inc(y_added, 1)


FFN1_EXPERTS = 16
FFN1_HID = 4 * D
FFN1_SHARED = 2 * D
CAPACITY = 2 * TOK // FFN1_EXPERTS
SLICES = P // FFN1_EXPERTS
RUNS = TILES // SLICES
RANKS = CAPACITY // P
LO = 32
HI = CAPACITY // LO
ROW = D + FFN1_EXPERTS
BITS = 30


def ffn1_weights(w):
    p = np.arange(P)
    same = (p[:, None] % FFN1_EXPERTS) == (p[None, :] % FFN1_EXPERTS)
    before = same & (p[:, None] < p[None, :])
    chunked = lambda a: a.reshape(-1, P, D).transpose(1, 0, 2).reshape(P, -1)
    in_half = p // HI
    return pack([
        ("router", w["gate_w"].T),
        ("token", (np.arange(TILES)[None, :] * P + p[:, None]).astype(np.float32)),
        ("iota", np.broadcast_to(np.arange(LO, dtype=np.float32), (P, LO))),
        ("own", (in_half[:, None] == np.arange(FFN1_EXPERTS // 2)[None, :]).astype(np.float32)),
        ("wg", w["Wg"].reshape(FFN1_EXPERTS * FFN1_HID, D).T), ("wu", w["Wu"].reshape(FFN1_EXPERTS * FFN1_HID, D).T),
        ("wd", chunked(w["Wd"].transpose(0, 2, 1).reshape(FFN1_EXPERTS * FFN1_HID, D))),
        ("sg", w["Sg"].T), ("su", w["Su"].T), ("sd", chunked(w["Sd"].T)),
        ("same", same.astype(np.float32)), ("before", before.astype(np.float32)),
        ("powers", np.broadcast_to((2.0 ** np.arange(BITS - 1, -1, -1)).astype(np.float32), (P, BITS))),
    ])


def ffn1(core, blob, offsets):
    nc = core.nc
    GROUPS = TOK // BANK
    with Stage(core, "ffn1") as st:
        w = st.weights(blob, offsets)
        layer_norm(core, st)
        bank = [st.ps(f"bank{i}", [P, BANK]) for i in range(8)]
        tok_major = bank[0][:, :].rearrange("p (t e) -> p t e", t=TILES)
        router_logits(core, w["router"], lambda t: tok_major[:, bass.ds(t, 1), :].squeeze(1), FFN1_EXPERTS, st)

        score = st.sb("score", [P, TILES, FFN1_EXPERTS])
        best, total = st.sb("best", [P, TILES]), st.sb("total", [P, TILES])
        score_e, above, ties, rank, restart = (st.sb(n, [P, BANK]) for n in ("score_e", "above", "ties", "rank", "restart"))
        power_bits, threshold, trial, kept = st.sb("power_bits", [P, BITS], I32), st.sb("threshold", [P, 1], I32), st.sb("trial", [P, 1], I32), st.sb("kept", [P, 1], I32)
        count = st.sb("count", [P, 1])
        wanted = st.sb("wanted", [P, 1])
        tie_count, base, run_total = (st.sb(n, [P, RUNS]) for n in ("tie_count", "base", "run_total"))
        names = ("dve", "centred", "exp_ready", "score_ready", "score_psum", "counted", "summed", "bit_chain", "tie_chain", "place_e_ready", "place_psum", "consts", "normed", "table_stored")
        (dve, centred, exp_ready, score_ready, score_psum, counted, summed, bit_chain, tie_chain, place_e_ready, place_psum, consts, normed, table_stored) = (st.sem(n) for n in names)
        table = nc.dram_tensor(f"{st.name}_table", (TOK, ROW), F32, kind="Internal").ap()
        with nc.Block() as block:
            @block.sync
            def _(sp):
                by_tile = table.rearrange("(t p) d -> p t d", p=P)
                sp.wait_ge(normed, 1)
                sp.dma_start(by_tile[:, :, 0:D], core.xn[:, :, :]).then_inc(table_stored, 16)
                sp.wait_ge(score_ready, 1)
                sp.dma_start(by_tile[:, :, D:ROW], score[:, :, :]).then_inc(table_stored, 16)
                sp.wait_ge(table_stored, 32)

            @block.gpsimd
            def _(pool):
                nc.gpsimd.memset(restart[:, :], 1.0).then_inc(consts, 1)
                nc.gpsimd.memset(threshold[:, :], 0).then_inc(consts, 1)
                nc.gpsimd.tensor_copy(power_bits[:, :], w["powers"]).then_inc(consts, 1)
                pool.wait_ge(consts, 3)
                nc.gpsimd.memset(restart[:, 0:BANK:P], 0.0).then_inc(consts, 1)
                nc.gpsimd.tensor_tensor(core.xn[:, :, :], core.xn[:, :, :], bc(core.rstd[:, :], 2, D), ALU.mult).then_inc(normed, 1)

            @block.tensor
            def _(pe):
                pe.wait_ge(score_ready, 1)
                for r in range(RUNS):
                    ins = nc.tensor.transpose(bank[1][:, r * P:(r + 1) * P], score[:, r * SLICES:(r + 1) * SLICES, :].rearrange("p t e -> p (t e)"), core.ident[:, :])
                ins.then_inc(score_psum, 1)
                with pe.Fori(0, BITS) as i:
                    pe.wait_ge(counted, i + 1)
                    nc.tensor.matmul(bank[2][:, 0:1], w["same"], count[:, :], start=True, stop=True).then_inc(summed, 1)
                pe.wait_ge(counted, BITS + 1)
                nc.tensor.matmul(bank[2][:, 1:2], w["same"], count[:, :], start=True, stop=True)
                nc.tensor.matmul(bank[2][:, 4:4 + RUNS], w["same"], tie_count[:, :], start=True, stop=True)
                nc.tensor.matmul(bank[2][:, 8:8 + RUNS], w["before"], tie_count[:, :], start=True, stop=True).then_inc(summed, 1)
                pe.wait_ge(counted, BITS + 2)
                nc.tensor.matmul(bank[2][:, 16:16 + RUNS], w["same"], tie_count[:, :], start=True, stop=True)
                nc.tensor.matmul(bank[2][:, 20:20 + RUNS], w["before"], tie_count[:, :], start=True, stop=True).then_inc(summed, 1)
                pe.wait_ge(place_e_ready, 1)
                for r in range(RUNS):
                    ins = nc.tensor.transpose(bank[3][:, r * P:(r + 1) * P], rank[:, r * P:(r + 1) * P], core.ident[:, :])
                ins.then_inc(place_psum, 1)

            @block.scalar
            def _(a):
                a.wait_ge(centred, 1)
                nc.scalar.activation(score[:, :, :], score[:, :, :], ACT.Exp).then_inc(exp_ready, 1)

            @block.vector
            def _(v):
                c = Chain(v, dve)
                c.link(nc.vector.tensor_reduce(best[:, :], tok_major, AX.X, ALU.max))
                nc.vector.tensor_tensor(score[:, :, :], tok_major, bc(best[:, :], 2, FFN1_EXPERTS), ALU.subtract).then_inc(centred, 1)
                v.wait_ge(exp_ready, 1)
                c.link(nc.vector.tensor_reduce(total[:, :], score[:, :, :], AX.X, ALU.add))
                c.link(nc.vector.reciprocal(total[:, :], total[:, :]))
                nc.vector.tensor_tensor(score[:, :, :], score[:, :, :], bc(total[:, :], 2, FFN1_EXPERTS), ALU.mult).then_inc(score_ready, 1)
                v.wait_ge(score_psum, 1)
                c.link(nc.vector.tensor_copy(score_e[:, :], bank[1][:, :]))
                v.wait_ge(consts, 4)
                with v.Fori(0, BITS) as i:
                    b = Chain(v, bit_chain, i * 3)
                    b.link(nc.vector.tensor_tensor(trial[:, :], threshold[:, :], power_bits[:, bass.ds(i, 1)], ALU.bitwise_or))
                    nc.vector.tensor_scalar(above[:, :], score_e[:, :], trial[:, :].bitcast(F32), 0.0, ALU.is_ge, ALU.add,
                                            accum_out=count[:, :]).then_inc(counted, 1)
                    v.wait_ge(summed, i + 1)
                    b.link(nc.vector.tensor_scalar(kept[:, :], bank[2][:, 0:1], float(CAPACITY), w["powers"][:, bass.ds(i, 1)], ALU.is_ge, ALU.mult))
                    b.link(nc.vector.tensor_tensor(threshold[:, :], threshold[:, :], kept[:, :], ALU.bitwise_or))
                e = Chain(v, tie_chain)
                limit = threshold[:, :].bitcast(F32)
                e.link(nc.vector.tensor_scalar(above[:, :], score_e[:, :], limit, 0.0, ALU.is_gt, ALU.add, accum_out=count[:, :]))
                e.link(nc.vector.tensor_scalar(ties[:, :], score_e[:, :], limit, None, ALU.is_equal))
                by_run = lambda t: t[:, :].rearrange("p (r s) -> p r s", r=RUNS)

                def places(marks, at, nth):
                    e.link(nc.vector.tensor_tensor_scan(rank[:, :], restart[:, :], marks[:, :], 0.0, ALU.mult, ALU.add))
                    nc.vector.tensor_copy(tie_count[:, :], rank[:, P - 1:BANK:P]).then_inc(counted, 1)
                    v.wait_ge(summed, BITS + nth)
                    e.link(nc.vector.tensor_copy(run_total[:, :], bank[2][:, at:at + RUNS]))
                    e.link(nc.vector.tensor_copy(base[:, :], bank[2][:, at + RUNS:at + 2 * RUNS]))
                    for r in range(1, RUNS):
                        e.link(nc.vector.tensor_scalar(base[:, r:RUNS], base[:, r:RUNS], run_total[:, r - 1:r], None, ALU.add))
                    e.link(nc.vector.tensor_tensor(rank[:, :], rank[:, :], marks[:, :], ALU.subtract))
                    e.link(nc.vector.tensor_tensor(by_run(rank), by_run(rank), bc(base[:, :], 2, P), ALU.add))

                places(ties, 4, 1)
                e.link(nc.vector.tensor_scalar(wanted[:, :], bank[2][:, 1:2], -1.0, float(CAPACITY), ALU.mult, ALU.add))
                e.link(nc.vector.tensor_scalar(rank[:, :], rank[:, :], wanted[:, :], None, ALU.is_lt))
                e.link(nc.vector.tensor_tensor(ties[:, :], ties[:, :], rank[:, :], ALU.mult))
                e.link(nc.vector.tensor_tensor(above[:, :], above[:, :], ties[:, :], ALU.add))
                places(above, 16, 2)
                e.link(nc.vector.scalar_tensor_tensor(rank[:, :], rank[:, :], 1.0, above[:, :], ALU.add, ALU.mult))
                e.link(nc.vector.tensor_scalar(rank[:, :], rank[:, :], -1.0, None, ALU.add))
                e.eng.sem_inc(place_e_ready, 1)
                v.wait_ge(place_psum, 1)
                place = ties[:, :].bitcast(I32)
                e.link(nc.vector.tensor_copy(place, bank[3][:, :]))
                split = above[:, :].bitcast(I32), restart[:, :].bitcast(I32)
                e.link(nc.vector.tensor_scalar(split[0], place, LO.bit_length() - 1, None, ALU.arith_shift_right))
                e.link(nc.vector.tensor_scalar(split[1], place, LO - 1, None, ALU.bitwise_and))
                e.link(nc.vector.tensor_copy(score_e[:, :], split[0]))
                e.link(nc.vector.tensor_copy(rank[:, :], split[1]))

        gelu = st.sb("gelu", [P, 2, BANK])
        hid = st.sb("hid", [P, 2, FFN1_HID // P, BANK])
        index = st.sb("index", [P, FFN1_EXPERTS * RANKS], I32)
        lists = nc.dram_tensor(f"{st.name}_lists", (FFN1_EXPERTS * CAPACITY,), F32, kind="Internal").ap()
        hi = score_e[:, :].rearrange("p (t e) -> p t e", t=TILES)
        lo = rank[:, :].rearrange("p (t e) -> p t e", t=TILES)
        STEP = 2
        hid_flat = hid[:, :, :, :].rearrange("p i k s -> p i (k s)")
        is_hi = [hid_flat[:, i, 0:STEP * FFN1_EXPERTS * HI].rearrange("p (t e h) -> p t e h", t=STEP, e=FFN1_EXPERTS) for i in range(2)]
        is_lo = [hid_flat[:, i, STEP * FFN1_EXPERTS * HI:STEP * FFN1_EXPERTS * (HI + LO)].rearrange("p (t e l) -> p t e l", t=STEP, e=FFN1_EXPERTS) for i in range(2)]
        own_idx, rows_64 = gelu[:, 0, 0:2 * LO], gelu[0:FFN1_EXPERTS * RANKS, 1, 0:P]
        hot_chain, hot_ready, hot_used, list_psum, list_chain, list_ready, list_moved, index_psum = (st.sem(n) for n in (
            "hot_chain", "hot_ready", "hot_used", "list_psum", "list_chain", "list_ready", "list_moved", "index_psum"))
        with nc.Block() as block:
            @block.vector
            def _(v):
                for n in range(TILES // STEP):
                    tiles = slice(n * STEP, (n + 1) * STEP)
                    i = n % 2
                    if n >= 2:
                        v.wait_ge(hot_used, n - 1)
                    nc.vector.tensor_tensor(is_hi[i], bc(hi[:, tiles, :], 3, HI), bc(bc(w["iota"][:, 0:HI], 1, FFN1_EXPERTS), 1, STEP), ALU.is_equal).then_inc(hot_chain, 1)
                    nc.vector.tensor_tensor(is_lo[i], bc(lo[:, tiles, :], 3, LO), bc(bc(w["iota"], 1, FFN1_EXPERTS), 1, STEP), ALU.is_equal).then_inc(hot_ready, 1)
                    v.wait_ge(hot_chain, n + 1)
                    nc.vector.tensor_tensor(is_hi[i].rearrange("p t e h -> p t (e h)"), is_hi[i].rearrange("p t e h -> p t (e h)"),
                                            bc(w["token"][:, tiles], 2, FFN1_EXPERTS * HI), ALU.mult).then_inc(hot_ready, 1)
                v.wait_ge(list_psum, 1)
                c = Chain(v, list_chain)
                own = hid_flat[:, 0, 0:BANK].rearrange("p (h e l) -> p h e l", h=2, e=FFN1_EXPERTS // 2)
                for half in range(2):
                    found = bank[4 + half][:, 0:FFN1_EXPERTS // 2 * LO].rearrange("p (e l) -> p e l", e=FFN1_EXPERTS // 2)
                    c.link(nc.vector.tensor_tensor(own[:, half], found, bc(w["own"], 2, LO), ALU.mult))
                nc.vector.tensor_reduce(own_idx.rearrange("p (h l) -> p h l", h=2), own.rearrange("p h e l -> p h l e"), AX.X, ALU.add).then_inc(list_ready, 1)
                v.wait_ge(index_psum, 1)
                nc.vector.tensor_copy(index[:, :], bank[6][:, 0:FFN1_EXPERTS * RANKS])

            @block.sync
            def _(sp):
                sp.wait_ge(list_ready, 1)
                sp.dma_start(lists.rearrange("(h p l) -> p h l", h=2, p=P), own_idx.rearrange("p (h l) -> p h l", h=2)).then_inc(list_moved, 16)
                sp.wait_ge(list_moved, 16)
                sp.dma_start(rows_64, lists.rearrange("(r p) -> r p", p=P)).then_inc(list_moved, 16)

            @block.tensor
            def _(pe):
                E2 = FFN1_EXPERTS // 2
                for n in range(TILES // STEP):
                    pe.wait_ge(hot_ready, 2 * (n + 1))
                    for t in range(STEP):
                        for half in range(2):
                            es = slice(half * E2, (half + 1) * E2)
                            ins = nc.tensor.matmul(bank[4 + half][:, 0:E2 * LO], is_hi[n % 2][:, t, es, :].rearrange("p e h -> p (e h)"),
                                                   is_lo[n % 2][:, t, es, :].rearrange("p e l -> p (e l)"),
                                                   start=(n == 0 and t == 0), stop=(n == TILES // STEP - 1 and t == STEP - 1))
                    ins.then_inc(hot_used, 1)
                pe.wait_ge(hot_used, TILES // STEP)
                pe.sem_inc(list_psum, 1)
                pe.wait_ge(list_moved, 32)
                nc.tensor.transpose(bank[6][:, 0:FFN1_EXPERTS * RANKS], rows_64, core.ident[0:FFN1_EXPERTS * RANKS, 0:FFN1_EXPERTS * RANKS]).then_inc(index_psum, 1)

        names = ("up_ready", "gelu_ready", "hid_ready", "y_ready", "added")
        up_ready, gelu_ready, hid_ready, y_ready, added = (st.sem("shared_" + n) for n in names)
        N = FFN1_SHARED // P
        with nc.Block() as block:
            @block.tensor
            def _(pe):
                with pe.Fori(0, GROUPS) as g:
                    x = core.xnT[:, bass.ds(g * BANK, BANK)]
                    for k in range(N):
                        pe.wait_ge(hid_ready, g * N)
                        nc.tensor.matmul(bank[2 * k][:, :], w["sg"][:, k * P:(k + 1) * P], x, start=True, stop=True)
                        nc.tensor.matmul(bank[2 * k + 1][:, :], w["su"][:, k * P:(k + 1) * P], x, start=True, stop=True).then_inc(up_ready, 1)
                    pe.wait_ge(hid_ready, (g + 1) * N)
                    pe.wait_ge(added, g)
                    for t in range(4):
                        for k in range(N):
                            ins = nc.tensor.matmul(bank[4][:, t * P:(t + 1) * P], hid[:, 0, k, t * P:(t + 1) * P], w["sd"][:, k * D:(k + 1) * D],
                                                   start=(k == 0), stop=(k == N - 1))
                    ins.then_inc(y_ready, 1)

            @block.scalar
            def _(a):
                with a.Fori(0, GROUPS) as g:
                    for k in range(N):
                        a.wait_ge(up_ready, g * N + k + 1)
                        nc.scalar.activation(gelu[:, k, :], bank[2 * k][:, :], ACT.Gelu).then_inc(gelu_ready, 1)

            @block.vector
            def _(v):
                with v.Fori(0, GROUPS) as g:
                    for k in range(N):
                        v.wait_ge(gelu_ready, g * N + k + 1)
                        v.wait_ge(y_ready, g)
                        nc.vector.tensor_tensor(hid[:, 0, k, :], gelu[:, k, :], bank[2 * k + 1][:, :], ALU.mult).then_inc(hid_ready, 1)
                    v.wait_ge(y_ready, g + 1)
                    x = core.x_res[:, bass.ds(g * 4, 4), :]
                    nc.vector.tensor_tensor(x, x, bank[4][:, :].rearrange("p (t d) -> p t d", t=4), ALU.add).then_inc(added, 1)

        stream = nc.dram_tensor(f"{st.name}_stream", (TOK, D), F32, kind="Internal").ap()
        XS = 3
        rows = st.sb("rows", [P, XS, RANKS, ROW])
        rowsT = st.sb("rowsT", [P, 2, BANK])
        y = st.sb("y", [P, 2, RANKS, D])
        gathered = [st.sem(f"gathered{i}") for i in range(XS)]
        names = ("turned", "rowsT_ready", "up_ready", "gelu_ready", "hid_ready", "y_psum", "y_ready", "scattered", "stream_stored", "stream_loaded")
        (turned, rowsT_ready, up_ready, gelu_ready, hid_ready, y_psum, y_ready, scattered, stream_stored, stream_loaded) = (st.sem(n) for n in names)
        KS = FFN1_HID // P
        with nc.Block() as block:
            @block.sync
            def _(sp):
                sp.dma_start(stream.rearrange("(t p) d -> p t d", p=P), core.x_res[:, :, :]).then_inc(stream_stored, 16)
                sp.wait_ge(stream_stored, 16)
                sp.wait_ge(scattered, FFN1_EXPERTS * RANKS * 16)
                sp.dma_start(core.x_res[:, :, :], stream.rearrange("(t p) d -> p t d", p=P)).then_inc(stream_loaded, 16)
                sp.wait_ge(stream_loaded, 16)

            @block.gpsimd
            def _(pool):
                def gather(e):
                    for r in range(RANKS):
                        at = e * RANKS + r
                        nc.gpsimd.indirect_dma_start(rows[:, e % XS, r, :], None, table, bass.IndirectOffsetOnAxis(index[:, at:at + 1], 0)).then_inc(gathered[e % XS], 16)

                def scatter(e):
                    if e == 0:
                        pool.wait_ge(stream_stored, 16)
                    else:
                        pool.wait_ge(scattered, e * RANKS * 16)
                    for r in range(RANKS):
                        at = e * RANKS + r
                        nc.gpsimd.indirect_dma_start(stream, bass.IndirectOffsetOnAxis(index[:, at:at + 1], 0), y[:, e % 2, r, :], None,
                                                     compute_op=ALU.add).then_inc(scattered, 16)

                gather(0)
                gather(1)
                for e in range(FFN1_EXPERTS):
                    if e > 0:
                        pool.wait_ge(y_ready, e)
                    if e + 2 < FFN1_EXPERTS:
                        gather(e + 2)
                    if e > 0:
                        scatter(e - 1)
                pool.wait_ge(y_ready, FFN1_EXPERTS)
                scatter(FFN1_EXPERTS - 1)

            @block.tensor
            def _(pe):
                def turn(e):
                    pe.wait_ge(gathered[e % XS], (e // XS + 1) * RANKS * 16)
                    if e >= 2:
                        pe.wait_ge(rowsT_ready, e - 1)
                    for r in range(RANKS):
                        ins = nc.tensor.transpose(bank[6 + e % 2][:, r * P:(r + 1) * P], rows[:, e % XS, r, 0:D], core.ident[:, :])
                    ins.then_inc(turned, 1)

                def down(e):
                    pe.wait_ge(hid_ready, (e + 1) * KS)
                    if e >= 2:
                        pe.wait_ge(y_ready, e - 1)
                    for r in range(RANKS):
                        for k in range(KS):
                            at = e * KS + k
                            ins = nc.tensor.matmul(bank[4 + e % 2][:, r * P:(r + 1) * P], hid[:, e % 2, k, r * P:(r + 1) * P], w["wd"][:, at * D:(at + 1) * D],
                                                   start=(k == 0), stop=(k == KS - 1))
                    ins.then_inc(y_psum, 1)

                turn(0)
                for e in range(FFN1_EXPERTS):
                    pe.wait_ge(rowsT_ready, e + 1)
                    for k in range(KS):
                        i = e * KS + k
                        if i >= 2:
                            pe.wait_ge(hid_ready, i - 1)
                        nc.tensor.matmul(bank[2 * (i % 2)][:, :], w["wg"][:, i * P:(i + 1) * P], rowsT[:, e % 2, :], start=True, stop=True)
                        nc.tensor.matmul(bank[2 * (i % 2) + 1][:, :], w["wu"][:, i * P:(i + 1) * P], rowsT[:, e % 2, :], start=True, stop=True).then_inc(up_ready, 1)
                        if k == 1 and e > 0:
                            down(e - 1)
                        if k == 2 and e + 1 < FFN1_EXPERTS:
                            turn(e + 1)
                down(FFN1_EXPERTS - 1)

            @block.scalar
            def _(a):
                def rows_turned(e):
                    a.wait_ge(turned, e + 1)
                    if e >= 2:
                        a.wait_ge(up_ready, (e - 1) * KS)
                    nc.scalar.copy(rowsT[:, e % 2, :], bank[6 + e % 2][:, :]).then_inc(rowsT_ready, 1)

                rows_turned(0)
                for e in range(FFN1_EXPERTS):
                    for k in range(KS):
                        i = e * KS + k
                        a.wait_ge(up_ready, i + 1)
                        if i >= 2:
                            a.wait_ge(hid_ready, i - 1)
                        nc.scalar.activation(gelu[:, i % 2, :], bank[2 * (i % 2)][:, :], ACT.Gelu).then_inc(gelu_ready, 1)
                        if k == 3 and e + 1 < FFN1_EXPERTS:
                            rows_turned(e + 1)

            @block.vector
            def _(v):
                def weigh(e):
                    v.wait_ge(y_psum, e + 1)
                    if e >= 2:
                        v.wait_ge(scattered, (e - 1) * RANKS * 16)
                    nc.vector.tensor_tensor(y[:, e % 2, :, :], bank[4 + e % 2][:, :].rearrange("p (r d) -> p r d", r=RANKS),
                                            bc(rows[:, e % XS, :, D + e:D + e + 1].squeeze(2), 2, D), ALU.mult).then_inc(y_ready, 1)

                for e in range(FFN1_EXPERTS):
                    for k in range(KS):
                        i = e * KS + k
                        v.wait_ge(gelu_ready, i + 1)
                        if e >= 2:
                            v.wait_ge(y_psum, e - 1)
                        nc.vector.tensor_tensor(hid[:, e % 2, k, :], gelu[:, i % 2, :], bank[2 * (i % 2) + 1][:, :], ALU.mult).then_inc(hid_ready, 1)
                        if k == 2 and e > 0:
                            weigh(e - 1)
                weigh(FFN1_EXPERTS - 1)


STATES = 16
RANK = 64
CHN = 4
SCAN_CHUNKS = STATES // CHN


SCAN_PIECES = 3
SCAN_BF16 = mybir.dt.bfloat16


def full(a):
    return np.concatenate([a, np.zeros((a.shape[0], P - a.shape[1]), a.dtype)], axis=1)


def pick(n):
    return np.tile(np.eye(n, dtype=np.float32), (SCAN_PIECES, 1))


def scan1_weights(w):
    xp = w["x_proj_w"].T
    return pack([
        ("low", full(xp[:, 0:RANK])), ("states", np.tile(xp[:, RANK:], (1, SCAN_PIECES))), ("pick", pick(2 * STATES)),
        ("dt", w["dt_proj_w"].T), ("dt_b", w["dt_proj_b"]), ("a_log", w["A_log"]), ("skip", w["D_skip"]),
    ])


def scan3_weights(w):
    wp = w["W_params"].T
    return pack([
        ("low", full(wp[:, 0:RANK])), ("states", np.tile(full(wp[:, RANK + STATES:])[:, 0:2 * STATES], (1, SCAN_PIECES))), ("pick", pick(2 * STATES)),
        ("dt", w["W_dt"].T), ("dt_b", w["b_dt"]), ("a_log", w["A_log"]), ("skip", w["D"]),
        ("conv", w["conv_w"][:, 0, :]), ("wz", w["W_z"].T), ("wo", w["W_out"].T),
    ])


def step_sizes(core, st, w, bank, delta):
    nc = core.nc
    GROUPS = TOK // BANK
    ROWS = 2 * STATES
    KP = SCAN_PIECES * ROWS
    low = st.sb("dt_low", [P, 2, BANK])
    e = core.xn[:, :, :].rearrange("p t d -> p (t d)")
    pieces = st.sb("pieces", [KP, TOK], SCAN_BF16)
    pick_bf = st.sb("pick_bf", [KP, ROWS], SCAN_BF16)
    rounded = st.sb("rounded", [KP, 2, BANK], SCAN_BF16)
    rest = st.sb("rest", [KP, 2, BANK])
    names = ("low_psum", "low_ready", "y_psum", "y_ready", "ln_ready", "delta_done", "act_chain", "picks_ready", "rows_psum", "rounded_1", "rest_1", "rounded_2",
             "rest_2", "pieces_ready")
    (low_psum, low_ready, y_psum, y_ready, ln_ready, delta_done, act_chain, picks_ready, rows_psum, rounded_1, rest_1, rounded_2,
     rest_2, pieces_ready) = (st.sem("dt_" + n) for n in names)
    HALVES = 2
    with nc.Block() as block:
        @block.tensor
        def _(pe):
            pe.sem_inc(y_ready, 2)
            pe.sem_inc(pieces_ready, 2)
            with pe.Fori(0, GROUPS // 2) as g2:
                for i in range(2):
                    g = g2 * 2 + i
                    x = core.xnT[:, bass.ds(g * BANK, BANK)]
                    pe.wait_ge(y_ready, g + 1)
                    nc.tensor.matmul(bank[i][:, :], w["low"], x, start=True, stop=True).then_inc(low_psum, 1)
                    pe.wait_ge(pieces_ready, g + 1)
                    nc.tensor.matmul(bank[4 + i][0:KP, :], w["states"], x, start=True, stop=True).then_inc(rows_psum, 1)
                    pe.wait_ge(low_ready, g + 1)
                    nc.tensor.matmul(bank[2 + i][:, :], w["dt"], low[:, i, :], start=True, stop=True).then_inc(y_psum, 1)

        @block.scalar
        def _(a):
            with a.Fori(0, GROUPS // 2) as g2:
                for i in range(2):
                    g = g2 * 2 + i
                    a.wait_ge(low_psum, g + 1)
                    nc.scalar.copy(low[:, i, :], bank[i][:, :]).then_inc(low_ready, 1)
            a.wait_ge(y_ready, GROUPS + 2)
            c = Chain(a, act_chain)
            for half in range(HALVES):
                part = slice(half * TOK // HALVES, (half + 1) * TOK // HALVES)
                c.link(nc.scalar.activation(e[:, part], delta[:, part], ACT.Abs))
                c.link(nc.scalar.activation(e[:, part], e[:, part], ACT.Exp, scale=-1.0))
                nc.scalar.activation(e[:, part], e[:, part], ACT.Ln, bias=1.0).then_inc(ln_ready, 1)

        @block.vector
        def _(v):
            with v.Fori(0, GROUPS // 2) as g2:
                for i in range(2):
                    g = g2 * 2 + i
                    cols = bass.ds(g * BANK, BANK)
                    rows, src = rounded[:, i, :], bank[4 + i][0:KP, :]
                    v.wait_ge(y_psum, g + 1)
                    nc.vector.tensor_scalar(delta[:, cols], bank[2 + i][:, :], w["dt_b"], None, ALU.add).then_inc(y_ready, 1)
                    v.wait_ge(rows_psum, g + 1)
                    nc.vector.tensor_copy(pieces[0:ROWS, cols], src[0:ROWS])
                    nc.vector.tensor_copy(rows, src).then_inc(rounded_1, 1)
                    v.wait_ge(rounded_1, g + 1)
                    nc.vector.tensor_tensor(rest[:, i, :], src, rows, ALU.subtract).then_inc(rest_1, 1)
                    v.wait_ge(rest_1, g + 1)
                    nc.vector.tensor_copy(pieces[ROWS:2 * ROWS, cols], rest[ROWS:2 * ROWS, i, :])
                    nc.vector.tensor_copy(rounded[2 * ROWS:KP, i, :], rest[2 * ROWS:KP, i, :]).then_inc(rounded_2, 1)
                    v.wait_ge(rounded_2, g + 1)
                    nc.vector.tensor_tensor(rest[2 * ROWS:KP, i, :], rest[2 * ROWS:KP, i, :], rounded[2 * ROWS:KP, i, :], ALU.subtract).then_inc(rest_2, 1)
                    v.wait_ge(rest_2, g + 1)
                    nc.vector.tensor_copy(pieces[2 * ROWS:KP, cols], rest[2 * ROWS:KP, i, :]).then_inc(pieces_ready, 1)
            for half in range(HALVES):
                part = slice(half * TOK // HALVES, (half + 1) * TOK // HALVES)
                v.wait_ge(ln_ready, half + 1)
                nc.vector.scalar_tensor_tensor(delta[:, part], delta[:, part], 0.0, e[:, part], ALU.max, ALU.add).then_inc(delta_done, 1)

        @block.gpsimd
        def _(pool):
            nc.gpsimd.tensor_copy(pick_bf[:, :], w["pick"][0:KP, :]).then_inc(picks_ready, 1)
    return pieces, pick_bf


def scan1(core, blob, offsets):
    nc = core.nc
    with Stage(core, "scan1") as st:
        w = st.weights(blob, offsets)
        layer_norm(core, st)
        bank = [st.ps(f"bank{i}", [P, BANK]) for i in range(8)]
        delta = st.sb("delta", [P, TOK])
        pieces, pick_bf = step_sizes(core, st, w, bank, delta)
        spread = lambda n: pick_bf[:, n:n + 1].broadcast_to([SCAN_PIECES * 2 * STATES, P])
        pB = lambda j: [bank[2 * (j % 2) + i] for i in range(2)]
        pC, pSum = bank[4:6], bank[6:8]
        decay = [st.sb(f"decay{i}", [P, STATES, SEQ]) for i in range(2)]
        h = [st.sb(f"h{i}", [P, STATES, SEQ]) for i in range(2)]
        c_all = st.sb("c_all", [P, STATES, SEQ])
        du = st.sb("du", [P, 2, SEQ])
        y = st.sb("y", [P, 2, SEQ])
        pos_a, neg_a = st.sb("pos_a", [P, STATES]), st.sb("neg_a", [P, STATES])
        names = ("set_up", "du_ready", "b_psum", "b_used", "c_psum", "c_ready", "decay_ready", "scanned", "times_c", "sum_psum", "y_ready", "yT_ready", "added")
        (set_up, du_ready, b_psum, b_used, c_psum, c_ready, decay_ready, scanned, times_c, sum_psum, y_ready, yT_ready, added) = (st.sem(n) for n in names)
        with nc.Block() as block:
            @block.gpsimd
            def _(pool):
                for s in range(2):
                    nc.gpsimd.memset(decay[s][:, :, 0:1], 0.0).then_inc(set_up, 1)

                def enter(b, s):
                    cols = bass.ds(b * SEQ, SEQ)
                    if not known(b, 2):
                        pool.wait_ge(b_used, (b - 1) * SCAN_CHUNKS + 2)
                    nc.gpsimd.tensor_tensor(du[:, s, :], delta[:, cols], core.xnT[:, cols], ALU.mult).then_inc(du_ready, 1)

                def step(b, s, first, last):
                    if first:
                        enter(b, s)
                    if not last:
                        enter(b + 1, 1 - s)
                    for j in range(SCAN_CHUNKS):
                        part = slice(j * CHN, (j + 1) * CHN)
                        pool.wait_ge(scanned, b * SCAN_CHUNKS + j + 1)
                        pool.wait_ge(c_ready, (b * SCAN_CHUNKS + j) * 2 + 4)
                        nc.gpsimd.tensor_tensor(h[s][:, part, :], h[s][:, part, :], c_all[:, part, :], ALU.mult).then_inc(times_c, 1)

                sequences(pool, step)

            @block.tensor
            def _(pe):
                pe.sem_inc(b_used, 2)
                pe.sem_inc(c_ready, 2)
                at = lambda b: pieces[:, bass.ds(b * SEQ, SEQ)]

                def b_rows(b, j):
                    pe.wait_ge(b_used, b * SCAN_CHUNKS + j + 1)
                    for n in range(CHN):
                        ins = nc.tensor.matmul(pB(j)[n // 2][:, n % 2 * SEQ:(n % 2 + 1) * SEQ], spread(j * CHN + n), at(b), start=True, stop=True)
                    ins.then_inc(b_psum, 1)

                def c_rows(b, j):
                    for i in range(2 * j, 2 * j + 2):
                        pe.wait_ge(c_ready, b * 2 * SCAN_CHUNKS + i + 1)
                        for n in range(2):
                            ins = nc.tensor.matmul(pC[i % 2][:, n * SEQ:(n + 1) * SEQ], spread(STATES + i * 2 + n), at(b), start=True, stop=True)
                        ins.then_inc(c_psum, 1)

                def add_up(b, s, j):
                    pe.wait_ge(times_c, b * SCAN_CHUNKS + j + 1)
                    for n in range(j * CHN, (j + 1) * CHN):
                        ins = nc.tensor.matmul(pSum[s][:, 0:SEQ], core.ident[:, :], h[s][:, n, :], start=(n == 0), stop=(n == STATES - 1))
                    if j == SCAN_CHUNKS - 1:
                        ins.then_inc(sum_psum, 1)

                def put_out(b, s):
                    pe.wait_ge(y_ready, b + 1)
                    for t in range(2):
                        ins = nc.tensor.transpose(pSum[s][:, SEQ + t * P:SEQ + (t + 1) * P], y[:, s, t * P:(t + 1) * P], core.ident[:, :])
                    ins.then_inc(yT_ready, 1)

                def step(b, s, first, last):
                    if first:
                        b_rows(b, 0)
                    for j in range(SCAN_CHUNKS):
                        if j + 1 < SCAN_CHUNKS:
                            b_rows(b, j + 1)
                        elif not last:
                            b_rows(b + 1, 0)
                        c_rows(b, j)
                        if j >= 2:
                            if j == 2 and not known(b, 2):
                                pe.wait_ge(added, b - 1)
                            add_up(b, s, j - 2)
                        elif not first:
                            add_up(b - 1, 1 - s, SCAN_CHUNKS - 2 + j)
                        if j == 3 and not first:
                            put_out(b - 1, 1 - s)
                    if last:
                        add_up(b, s, SCAN_CHUNKS - 2)
                        add_up(b, s, SCAN_CHUNKS - 1)
                        put_out(b, s)

                sequences(pe, step)

            @block.scalar
            def _(a):
                nc.scalar.activation(pos_a[:, :], w["a_log"], ACT.Exp).then_inc(set_up, 1)
                a.wait_ge(set_up, 4)

                def decays(b, s, j):
                    for n in range(j * CHN, (j + 1) * CHN):
                        ins = nc.scalar.activation(decay[s][:, n, 1:SEQ], delta[:, bass.ds(b * SEQ + 1, SEQ - 1)], ACT.Exp, scale=neg_a[:, n:n + 1])
                    ins.then_inc(decay_ready, 1)

                def step(b, s, first, last):
                    if first:
                        for j in range(SCAN_CHUNKS):
                            decays(b, s, j)
                    for j in range(SCAN_CHUNKS):
                        for i in range(2 * j, 2 * j + 2):
                            a.wait_ge(c_psum, b * 2 * SCAN_CHUNKS + i + 1)
                            if i % 2 == 0 and not first:
                                a.wait_ge(times_c, (b - 1) * SCAN_CHUNKS + j + 1)
                            nc.scalar.copy(c_all[:, 2 * i:2 * i + 2, :], pC[i % 2][:, :].rearrange("p (n s) -> p n s", n=2)).then_inc(c_ready, 1)
                        if not last:
                            decays(b + 1, 1 - s, j)

                sequences(a, step)

            @block.vector
            def _(v):
                v.wait_ge(set_up, 3)
                nc.vector.tensor_scalar(neg_a[:, :], pos_a[:, :], -1.0, None, ALU.mult).then_inc(set_up, 1)

                def enter(b, s, j):
                    v.wait_ge(b_psum, b * SCAN_CHUNKS + j + 1)
                    for i in range(2):
                        rows = slice(j * CHN + 2 * i, j * CHN + 2 * i + 2)
                        ins = nc.vector.tensor_tensor(h[s][:, rows, :], pB(j)[i][:, :].rearrange("p (n s) -> p n s", n=2), bc(du[:, s, :], 1, 2), ALU.mult)
                    ins.then_inc(b_used, 1)

                def skip(b, s):
                    v.wait_ge(sum_psum, b + 1)
                    nc.vector.scalar_tensor_tensor(y[:, s, :], core.xnT[:, bass.ds(b * SEQ, SEQ)], w["skip"], pSum[s][:, 0:SEQ], ALU.mult, ALU.add).then_inc(y_ready, 1)

                def add(b, s):
                    v.wait_ge(yT_ready, b + 1)
                    x = core.x_res[:, bass.ds(b * 2, 2), :]
                    nc.vector.tensor_tensor(x, x, pSum[s][:, SEQ:2 * SEQ].rearrange("p (t d) -> p t d", t=2), ALU.add).then_inc(added, 1)

                def step(b, s, first, last):
                    v.wait_ge(du_ready, b + 1)
                    enter(b, s, 0)
                    if not known(b, 2):
                        add(b - 2, s)
                    for j in range(SCAN_CHUNKS):
                        if j + 1 < SCAN_CHUNKS:
                            enter(b, s, j + 1)
                        v.wait_ge(b_used, b * SCAN_CHUNKS + j + 3)
                        v.wait_ge(decay_ready, b * SCAN_CHUNKS + j + 1)
                        flat = lambda t: t[:, j * CHN:(j + 1) * CHN, :].rearrange("p n s -> p (n s)")
                        nc.vector.tensor_tensor_scan(flat(h[s]), flat(decay[s]), flat(h[s]), 0.0, ALU.mult, ALU.add).then_inc(scanned, 1)
                        if j == 2 and not first:
                            skip(b - 1, 1 - s)
                    if last:
                        add(b - 1, 1 - s)
                        skip(b, s)
                        add(b, s)

                sequences(v, step)


def scan3(core, blob, offsets):
    nc = core.nc
    TAPS = 4
    GROUPS = TOK // BANK
    with Stage(core, "scan3") as st:
        w = st.weights(blob, offsets)
        layer_norm(core, st)
        bank = [st.ps(f"bank{i}", [P, BANK]) for i in range(8)]
        delta = st.sb("delta", [P, TOK])
        u = st.sb("u", [P, TOK])
        gate = st.sb("gate", [P, TOK])

        conv = st.sb("conv", [P, 2, 2, SEQ])
        z_psum, gate_ready, conv_chain, conv_ready, u_ready = (st.sem(n) for n in ("z_psum", "gate_ready", "conv_chain", "conv_ready", "u_ready"))
        with nc.Block() as block:
            @block.tensor
            def _(pe):
                pe.sem_inc(gate_ready, 2)
                with pe.Fori(0, GROUPS // 2) as g:
                    for s in range(2):
                        pe.wait_ge(gate_ready, 2 * g + s + 1)
                        nc.tensor.matmul(bank[s][:, :], w["wz"], core.xnT[:, bass.ds((2 * g + s) * BANK, BANK)], start=True, stop=True).then_inc(z_psum, 1)

            @block.scalar
            def _(a):
                with a.Fori(0, GROUPS // 2) as g:
                    for s in range(2):
                        cols = bass.ds((2 * g + s) * BANK, BANK)
                        a.wait_ge(z_psum, 2 * g + s + 1)
                        nc.scalar.activation(gate[:, cols], bank[s][:, :], ACT.Silu).then_inc(gate_ready, 1)
                        a.wait_ge(conv_ready, 2 * g + s + 1)
                        nc.scalar.activation(u[:, cols], conv[:, s, :, :].rearrange("p b s -> p (b s)"), ACT.Silu).then_inc(u_ready, 1)

            @block.vector
            def _(v):
                v.sem_inc(u_ready, 2)
                with v.Fori(0, GROUPS // 2) as g:
                    c = Chain(v, conv_chain, g * 2 * (TAPS - 1))
                    for s in range(2):
                        x = core.xnT[:, bass.ds((2 * g + s) * BANK, BANK)].rearrange("p (b s) -> p b s", b=2)
                        out = conv[:, s, :, :]
                        v.wait_ge(u_ready, 2 * g + s + 1)
                        ins = nc.vector.tensor_scalar(out, x, w["conv"][:, TAPS - 1:TAPS], None, ALU.mult)
                        for back in range(1, TAPS):
                            c.link(ins)
                            ins = nc.vector.scalar_tensor_tensor(out[:, :, back:SEQ], x[:, :, 0:SEQ - back], w["conv"][:, TAPS - 1 - back:TAPS - back],
                                                                 out[:, :, back:SEQ], ALU.mult, ALU.add)
                        ins.then_inc(conv_ready, 1)

        pieces, pick_bf = step_sizes(core, st, w, bank, delta)
        spread = lambda n: pick_bf[:, n:n + 1].broadcast_to([SCAN_PIECES * 2 * STATES, P])

        pC, pSum = bank[4:6], bank[6:8]
        decay = st.sb("decay", [P, STATES, SEQ])
        h = [st.sb(f"h{i}", [P, STATES, SEQ]) for i in range(2)]
        c_all = core.xn[:, :, :].rearrange("p t d -> p (t d)").rearrange("p (n s) -> p n s", n=STATES)
        prev = st.sb("prev", [P, 2, 2, SEQ])
        du = st.sb("du", [P, 2, SEQ])
        du_small = st.sb("du_small", [P, STATES, SEQ])
        yT = st.sb("yT", [P, SEQ])
        pos_a, neg_a, small, inv_a, den = (st.sb(n, [P, STATES]) for n in ("pos_a", "neg_a", "small", "inv_a", "den"))
        names = ("set_up", "setup_chain", "du_made", "prev_ready", "small_by_pool", "small_by_act", "decay_ready", "entered", "shrunk", "scanned", "zeroed", "c_psum",
                 "c_ready", "times_c", "sum_psum", "skip_added", "y_ready", "out_psum", "added")
        (set_up, setup_chain, du_made, prev_ready, small_by_pool, small_by_act, decay_ready, entered, shrunk, scanned, zeroed, c_psum,
         c_ready, times_c, sum_psum, skip_added, y_ready, out_psum, added) = (st.sem(n) for n in names)
        BY_POOL = 1
        BY_ACT = SCAN_CHUNKS - BY_POOL
        with nc.Block() as block:
            @block.gpsimd
            def _(pool):
                pool.wait_ge(set_up, 2)

                def before(b, s):
                    for i, src in enumerate((delta, u)):
                        nc.gpsimd.tensor_copy(prev[:, s, i, 1:SEQ], src[:, bass.ds(b * SEQ, SEQ - 1)])
                        ins = nc.gpsimd.tensor_copy(prev[:, s, i, 0:1], src[:, bass.ds(b * SEQ, 1)])
                    ins.then_inc(prev_ready, 1)
                    pool.wait_ge(prev_ready, b + 1)
                    nc.gpsimd.tensor_tensor(du[:, s, :], prev[:, s, 0, :], prev[:, s, 1, :], ALU.mult).then_inc(du_made, 1)

                def small_part(b, s):
                    pool.wait_ge(du_made, b + 1)
                    if not known(b, 1):
                        pool.wait_ge(shrunk, b * SCAN_CHUNKS)
                    part = slice(BY_ACT * CHN, STATES)
                    nc.gpsimd.tensor_tensor(du_small[:, part, :], bc(du[:, s, :], 1, BY_POOL * CHN), bc(small[:, part], 2, SEQ), ALU.mult).then_inc(small_by_pool, 1)

                def step(b, s, first, last):
                    if first:
                        before(b, s)
                        small_part(b, s)
                    if not last:
                        before(b + 1, 1 - s)
                    for j in range(SCAN_CHUNKS):
                        part = slice(j * CHN, (j + 1) * CHN)
                        pool.wait_ge(scanned, b * SCAN_CHUNKS + j + 1)
                        pool.wait_ge(c_ready, (b * SCAN_CHUNKS + j) * 2 + 4)
                        nc.gpsimd.tensor_tensor(h[s][:, part, :], h[s][:, part, :], c_all[:, part, :], ALU.mult).then_inc(times_c, 1)
                    if not last:
                        small_part(b + 1, 1 - s)

                sequences(pool, step)

            @block.tensor
            def _(pe):
                pe.sem_inc(c_ready, 2)

                def c_rows(b, j):
                    for i in range(2 * j, 2 * j + 2):
                        pe.wait_ge(c_ready, b * 2 * SCAN_CHUNKS + i + 1)
                        for n in range(2):
                            ins = nc.tensor.matmul(pC[i % 2][:, n * SEQ:(n + 1) * SEQ], spread(i * 2 + n), pieces[:, bass.ds(b * SEQ, SEQ)], start=True, stop=True)
                        ins.then_inc(c_psum, 1)

                def add_up(b, s, j):
                    pe.wait_ge(times_c, b * SCAN_CHUNKS + j + 1)
                    for n in range(j * CHN, (j + 1) * CHN):
                        ins = nc.tensor.matmul(pSum[s][:, 0:SEQ], core.ident[:, :], h[s][:, n, :], start=(n == 0), stop=(n == STATES - 1))
                    if j == SCAN_CHUNKS - 1:
                        ins.then_inc(sum_psum, 1)

                def put_out(b, s):
                    pe.wait_ge(y_ready, b + 1)
                    for t in range(2):
                        ins = nc.tensor.matmul(pSum[s][:, SEQ + t * P:SEQ + (t + 1) * P], yT[:, t * P:(t + 1) * P], w["wo"], start=True, stop=True)
                    ins.then_inc(out_psum, 1)

                def step(b, s, first, last):
                    for j in range(SCAN_CHUNKS):
                        c_rows(b, j)
                        if j >= 2:
                            if j == 2 and not known(b, 2):
                                pe.wait_ge(added, b - 1)
                            add_up(b, s, j - 2)
                        elif not first:
                            add_up(b - 1, 1 - s, SCAN_CHUNKS - 2 + j)
                        if j == 3 and not first:
                            put_out(b - 1, 1 - s)
                    if last:
                        add_up(b, s, SCAN_CHUNKS - 2)
                        add_up(b, s, SCAN_CHUNKS - 1)
                        put_out(b, s)

                sequences(pe, step)

            @block.scalar
            def _(a):
                nc.scalar.activation(pos_a[:, :], w["a_log"], ACT.Exp).then_inc(set_up, 1)
                a.wait_ge(set_up, 2)

                def decays(b, s, j):
                    a.wait_ge(prev_ready, b + 1)
                    if not known(b, 1):
                        a.wait_ge(scanned, (b - 1) * SCAN_CHUNKS + j + 1)
                    for n in range(j * CHN, (j + 1) * CHN):
                        ins = nc.scalar.activation(decay[:, n, :], prev[:, s, 0, :], ACT.Exp, scale=neg_a[:, n:n + 1])
                    ins.then_inc(decay_ready, 1)
                    if j < BY_ACT:
                        a.wait_ge(du_made, b + 1)
                        for n in range(j * CHN, (j + 1) * CHN):
                            ins = nc.scalar.activation(du_small[:, n, :], du[:, s, :], ACT.Copy, scale=small[:, n:n + 1])
                        ins.then_inc(small_by_act, 1)

                def step(b, s, first, last):
                    if first:
                        for j in range(SCAN_CHUNKS):
                            decays(b, s, j)
                    for j in range(SCAN_CHUNKS):
                        for i in range(2 * j, 2 * j + 2):
                            a.wait_ge(c_psum, b * 2 * SCAN_CHUNKS + i + 1)
                            if i % 2 == 0 and not first:
                                a.wait_ge(times_c, (b - 1) * SCAN_CHUNKS + j + 1)
                            nc.scalar.copy(c_all[:, 2 * i:2 * i + 2, :], pC[i % 2][:, :].rearrange("p (n s) -> p n s", n=2)).then_inc(c_ready, 1)
                        if not last:
                            decays(b + 1, 1 - s, j)

                sequences(a, step)

            @block.vector
            def _(v):
                c = Chain(v, setup_chain)
                v.wait_ge(set_up, 1)
                c.link(nc.vector.tensor_scalar(neg_a[:, :], pos_a[:, :], -1.0, None, ALU.mult))
                c.link(nc.vector.tensor_scalar(small[:, :], pos_a[:, :], 1e-5, None, ALU.is_lt))
                c.link(nc.vector.tensor_scalar(den[:, :], neg_a[:, :], 1e-10, None, ALU.add))
                c.link(nc.vector.tensor_tensor(den[:, :], den[:, :], small[:, :], ALU.add))
                c.link(nc.vector.reciprocal(den[:, :], den[:, :]))
                c.link(nc.vector.tensor_scalar(inv_a[:, :], small[:, :], -1.0, 1.0, ALU.mult, ALU.add))
                nc.vector.tensor_tensor(inv_a[:, :], inv_a[:, :], den[:, :], ALU.mult).then_inc(set_up, 1)
                v.wait_ge(set_up, 2)

                def enter(b, s, j):
                    part = slice(j * CHN, (j + 1) * CHN)
                    v.wait_ge(decay_ready, b * SCAN_CHUNKS + j + 1)
                    nc.vector.scalar_tensor_tensor(h[s][:, part, :], decay[:, part, :], -1.0, bc(prev[:, s, 1, :], 1, CHN), ALU.add,
                                                   ALU.mult).then_inc(entered, 1)
                    v.wait_ge(entered, b * SCAN_CHUNKS + j + 1)
                    nc.vector.memset(decay[:, part, 0:1], 0.0).then_inc(zeroed, 1)
                    if j < BY_ACT:
                        v.wait_ge(small_by_act, b * BY_ACT + j + 1)
                    else:
                        v.wait_ge(small_by_pool, b + 1)
                    for n in range(j * CHN, (j + 1) * CHN):
                        ins = nc.vector.scalar_tensor_tensor(h[s][:, n, :], h[s][:, n, :], inv_a[:, n:n + 1], du_small[:, n, :], ALU.mult, ALU.add)
                    ins.then_inc(shrunk, 1)

                def scan(b, s, j):
                    v.wait_ge(shrunk, b * SCAN_CHUNKS + j + 1)
                    v.wait_ge(zeroed, b * SCAN_CHUNKS + j + 1)
                    flat = lambda t: t[:, j * CHN:(j + 1) * CHN, :].rearrange("p n s -> p (n s)")
                    nc.vector.tensor_tensor_scan(flat(h[s]), flat(decay), flat(h[s]), 0.0, ALU.mult, ALU.add).then_inc(scanned, 1)

                def gated(b, s):
                    cols = bass.ds(b * SEQ, SEQ)
                    v.wait_ge(sum_psum, b + 1)
                    nc.vector.scalar_tensor_tensor(yT[:, :], u[:, cols], w["skip"], pSum[s][:, 0:SEQ], ALU.mult, ALU.add).then_inc(skip_added, 1)
                    v.wait_ge(skip_added, b + 1)
                    nc.vector.tensor_tensor(yT[:, :], yT[:, :], gate[:, cols], ALU.mult).then_inc(y_ready, 1)

                def add(b, s):
                    v.wait_ge(out_psum, b + 1)
                    x = core.x_res[:, bass.ds(b * 2, 2), :]
                    nc.vector.tensor_tensor(x, x, pSum[s][:, SEQ:2 * SEQ].rearrange("p (t d) -> p t d", t=2), ALU.add).then_inc(added, 1)

                def step(b, s, first, last):
                    for j in range(SCAN_CHUNKS):
                        enter(b, s, j)
                        scan(b, s, j)
                        if j == 0 and not known(b, 2):
                            add(b - 2, s)
                        if j == 2 and not first:
                            gated(b - 1, 1 - s)
                    if last:
                        add(b - 1, 1 - s)
                        gated(b, s)
                        add(b, s)

                sequences(v, step)


ATTN_A2_HD = D // HEADS
BD = 16
WINDOW = 64
PAD = WINDOW - 1
HALF = P // BD
SLOTS = P // HEADS
ROWS = WINDOW // SLOTS
KINDS = 2


def attn_a2_weights(w):
    def place(out_w):
        a = np.zeros((HALF, BD, 2, 2, 2, HEADS), np.float32)
        for slot in range(2):
            for half in range(2):
                for h in range(HALF):
                    a[h, :, slot, half, slot, half * HALF + h] = out_w.reshape(BD)
        return a.reshape(P, -1)

    def diag(m):
        a = np.zeros((HALF, BD, HALF, BD), np.float32)
        for h in range(HALF):
            a[h, :, h, :] = m
        return a.reshape(P, P)

    slot, head = np.arange(P) // HEADS, np.arange(P) % HEADS
    to_head = np.arange(D) // ATTN_A2_HD
    spread = [((slot[:, None] == s) & (head[:, None] == to_head[None, :])).astype(np.float32) for s in range(SLOTS)]
    seen = np.where(np.arange(SLOTS)[None, :] >= slot[:, None], np.float32(0.0), np.float32(NEG))
    strain, b = w["strain_fused_w"], w["strain_fused_b"]
    tall = lambda a: np.broadcast_to(a.reshape(1, 1), (P, 1))
    return pack([
        ("disp", w["W_disp"].T), ("val", w["W_val"].T), ("out", w["c_proj_w"].T),
        ("strain", np.concatenate([diag(strain[0:BD].T), diag(strain[BD:].T)], axis=1)),
        ("bond_b", np.tile(b[0:BD], HALF)), ("damage_b", np.tile(b[BD:], HALF)), ("damage_out_b", tall(w["damage_out_b"])),
        ("pos_proj", np.tile(w["pos_proj_w"].T, (1, HALF))), ("pos_emb", w["rel_pos_emb"][::-1].T),
        ("place", np.concatenate([place(w["bond_out_w"]), place(w["damage_out_w"])], axis=1)),
        ("spread", np.concatenate(spread + [sum(spread)], axis=1)),
        ("seen", seen),
    ])


def attn_a2(core, blob, offsets):
    nc = core.nc
    GROUPS = TOK // BANK
    with Stage(core, "attn_a2") as st:
        w = st.weights(blob, offsets)
        layer_norm(core, st)
        bank = [st.ps(f"bank{i}", [P, BANK]) for i in range(8)]
        feat = st.sb("feat", [P, KINDS, 2, BATCH, SEQ])
        val = st.sb("val", [P, BATCH, SEQ])
        lag_b = st.sb("lag_b", [P, WINDOW])
        half_out_b = st.sb("half_out_b", [P, 1])
        two = lambda ap: ap.rearrange("p (b s) -> p b s", b=2)

        disp = st.sb("disp", [P, 2, BANK])
        names = ("disp_psum", "disp_ready", "feat_psum", "feat_ready", "val_psum", "val_ready", "pos_psum", "misc")
        disp_psum, disp_ready, feat_psum, feat_ready, val_psum, val_ready, pos_psum, misc = (st.sem(n) for n in names)
        with nc.Block() as block:
            @block.tensor
            def _(pe):
                nc.tensor.matmul(bank[7][:, 0:WINDOW], w["pos_proj"], w["pos_emb"], start=True, stop=True).then_inc(pos_psum, 1)
                with pe.Fori(0, GROUPS) as g:
                    x = core.xnT[:, bass.ds(g * BANK, BANK)]
                    for half in range(2):
                        nc.tensor.matmul(bank[half][:, :], w["disp"][:, half * P:(half + 1) * P], x, start=True, stop=True).then_inc(disp_psum, 1)
                    pe.wait_ge(val_ready, g)
                    nc.tensor.matmul(bank[2][:, :], w["val"], x, start=True, stop=True).then_inc(val_psum, 1)
                    for half in range(2):
                        pe.wait_ge(disp_ready, 2 * g + half + 1)
                        pe.wait_ge(feat_ready, 2 * g)
                        for kind in range(KINDS):
                            ins = nc.tensor.matmul(bank[3 + 2 * half + kind][:, :], w["strain"][:, kind * P:(kind + 1) * P], disp[:, half, :], start=True, stop=True)
                        ins.then_inc(feat_psum, 1)

            @block.scalar
            def _(a):
                with a.Fori(0, GROUPS) as g:
                    for half in range(2):
                        a.wait_ge(disp_psum, 2 * g + half + 1)
                        a.wait_ge(feat_psum, 2 * g)
                        nc.scalar.copy(disp[:, half, :], bank[half][:, :]).then_inc(disp_ready, 1)
                    a.wait_ge(val_psum, g + 1)
                    nc.scalar.copy(val[:, bass.ds(2 * g, 2), :], two(bank[2][:, :])).then_inc(val_ready, 1)

            @block.vector
            def _(v):
                nc.vector.tensor_scalar(half_out_b[:, :], w["damage_out_b"], 0.5, None, ALU.mult)
                v.wait_ge(pos_psum, 1)
                nc.vector.tensor_scalar(lag_b[:, :], bank[7][:, 0:WINDOW], w["bond_b"], None, ALU.add)
                with v.Fori(0, GROUPS) as g:
                    for half in range(2):
                        v.wait_ge(feat_psum, 2 * g + half + 1)
                        for kind in range(KINDS):
                            ins = nc.vector.tensor_copy(feat[:, kind, half, bass.ds(2 * g, 2), :], two(bank[3 + 2 * half + kind][:, :]))
                        ins.then_inc(feat_ready, 1)

        logit = core.xn[:, :, :].rearrange("p t d -> p (t d)").rearrange("p (r s) -> p r s", r=ROWS)
        RING = 8
        more = st.sb("more", [P, 4, 2, 2, SEQ])
        first_half = core.xnT[:, :].rearrange("p (i h b s) -> p i h b s", i=4, h=2, b=2)
        ring = lambda i, n=1: (first_half if i % RING < 4 else more)[:, i % 4:i % 4 + n]
        tanh_out = disp
        feat_now = st.sb("feat_now", [P, KINDS, 2, 2, PAD + SEQ])
        val_now = st.sb("val_now", [P, 2, PAD + SEQ])
        prob = st.sb("prob", [P, ROWS, BANK])
        product = st.sb("product", [P, 4, BANK])
        slot_max, acc, inv, oT = (st.sb(n, [P, BANK]) for n in ("slot_max", "acc", "inv", "oT"))
        neg_max = st.sb("neg_max", [P, 4, HEADS])
        neg_max_wide = st.sb("neg_max_wide", [P, 4, SLOTS, HEADS])
        p_bond, p_damage, p_wide, p_max, p_x = bank[0:2], bank[2:4], bank[4:6], bank[6], bank[7]
        names = ("padded", "feat_by_act", "feat_by_dve", "val_copied", "diff_v", "diff_p", "gelu_ready", "placed", "tanh_ready", "combined", "masked",
                 "slot_max_ready", "max_psum", "neg_max_done", "neg_max_ready", "neg_max_psum", "shifted", "prob_ready", "den_psum", "wide_even", "wide_odd",
                 "weighted_even", "weighted_odd", "summed", "inv_ready", "oT_ready", "y_ready", "added")
        (padded, feat_by_act, feat_by_dve, val_copied, diff_v, diff_p, gelu_ready, placed, tanh_ready, combined, masked,
         slot_max_ready, max_psum, neg_max_done, neg_max_ready, neg_max_psum, shifted, prob_ready, den_psum, wide_even, wide_odd,
         weighted_even, weighted_odd, summed, inv_ready, oT_ready, y_ready, added) = (st.sem(n) for n in names)
        pairs = [(row, slot, slot + 2) for row in range(ROWS) for slot in range(SLOTS) if slot % 4 < 2]
        units = [(row, slots, kind) for row, *slots in pairs for kind in range(KINDS)]
        UNITS = len(units)
        PER_ROW = UNITS // ROWS
        RING_UNITS = RING // 2
        reach = lambda row: slice(row * SLOTS, SEQ)
        N_DIFF_V, N_DIFF_P = 3 * len(pairs), len(pairs)
        wide_psum, weighted = (wide_even, wide_odd), (weighted_even, weighted_odd)
        LAGS = WINDOW // 2
        PARTS = 4
        BEHIND = 3

        def difference(eng, u, n, row, slot, kind):
            both = feat_now[:, kind].rearrange("p h b s -> p (h b) s")
            lag, at = row * SLOTS + slot, PAD + row * SLOTS
            return eng.tensor_tensor(ring(2 * u + n)[:, 0].rearrange("p h b s -> p (h b) s")[:, :, reach(row)],
                                     both[:, :, at - lag:PAD - lag + SEQ], both[:, :, at:PAD + SEQ], ALU.subtract)

        def groups(eng, logits, lag, finish, before_last=lambda: None):
            logits(0, lambda l: None, lambda: None)
            with eng.Fori(1, GROUPS) as g:
                logits(g, lambda l: lag(g - 1, l), lambda: finish(g - 1))
            before_last()
            for l in range(WINDOW):
                lag(GROUPS - 1, l)
            finish(GROUPS - 1)

        def later(g):
            return not isinstance(g, int) or g > 0

        with nc.Block() as block:
            @block.tensor
            def _(pe):
                pe.sem_inc(placed, RING_UNITS)

                def logits(g, lag, finish):
                    for u, (row, slots, kind) in enumerate(units):
                        if u % PER_ROW == 0:
                            pe.wait_ge(combined, g * ROWS + row + 1)
                        pe.wait_ge(gelu_ready, g * UNITS + u + 1)
                        for half in range(2):
                            for n, slot in enumerate(slots):
                                at = ((kind * 2 + slot % 2) * 2 + half) * 32
                                part = slice(slot // 2 * 32, (slot // 2 + 1) * 32)
                                ins = nc.tensor.matmul(two((p_bond, p_damage)[kind][row % 2][part, :])[:, :, reach(row)], w["place"][:, at:at + 32],
                                                       ring(2 * u + n)[:, 0, half, :, reach(row)],
                                                       start=(slot % 2 == 0 and half == 0), stop=(slot % 2 == 1 and half == 1),
                                                       tile_position=(0, part.start))
                        ins.then_inc(placed, 1)
                        lag(u)
                    finish()
                    pe.wait_ge(slot_max_ready, g + 1)
                    if later(g):
                        pe.wait_ge(inv_ready, g)
                    for t in range(4):
                        ins = nc.tensor.transpose(p_max[:, t * P:(t + 1) * P], slot_max[:, t * P:(t + 1) * P], core.ident[:, :])
                    ins.then_inc(max_psum, 1)
                    pe.wait_ge(neg_max_ready, g + 1)
                    if later(g):
                        pe.wait_ge(added, g)
                    for t in range(4):
                        ins = nc.tensor.matmul(p_x[:, t * P:(t + 1) * P], neg_max_wide[:, t, :, :].rearrange("p s h -> p (s h)"), core.ident[:, :],
                                               start=True, stop=True)
                    ins.then_inc(neg_max_psum, 1)
                    for row in range(ROWS):
                        pe.wait_ge(prob_ready, g * PARTS + row * PARTS // ROWS + 1)
                        ins = nc.tensor.matmul(two(p_max[:, :])[:, :, reach(row)], w["spread"][:, SLOTS * D:(SLOTS + 1) * D], two(prob[:, row, :])[:, :, reach(row)],
                                               start=(row == 0), stop=(row == ROWS - 1))
                    ins.then_inc(den_psum, 1)

                def lag(g, l):
                    slot, row = l % SLOTS, l // SLOTS
                    pe.wait_ge(weighted[l % 2], g * LAGS + l // 2 + 1)
                    nc.tensor.matmul(two(p_wide[l % 2][:, :])[:, :, reach(row)], w["spread"][:, slot * D:(slot + 1) * D], two(prob[:, row, :])[:, :, reach(row)],
                                     start=True, stop=True).then_inc(wide_psum[l % 2], 1)

                def finish(g):
                    pe.wait_ge(oT_ready, g + 1)
                    for t in range(4):
                        ins = nc.tensor.matmul(p_x[:, t * P:(t + 1) * P], oT[:, t * P:(t + 1) * P], w["out"], start=True, stop=True)
                    ins.then_inc(y_ready, 1)

                groups(pe, logits, lag, finish)

            @block.scalar
            def _(a):
                def logits(g, lag, finish):
                    if later(g):
                        a.wait_ge(diff_v, g * N_DIFF_V)
                        a.wait_ge(diff_p, g * N_DIFF_P)
                    a.wait_ge(padded, 2)
                    nc.scalar.copy(feat_now[:, 1, :, :, PAD:].rearrange("p h b s -> p (h b) s"),
                                   feat[:, 1, :, bass.ds(2 * g, 2), :]).then_inc(feat_by_act, 1)

                    def tanh(row):
                        a.wait_ge(placed, g * UNITS + (row + 1) * PER_ROW + RING_UNITS)
                        a.wait_ge(combined, g * ROWS + row + 1)
                        nc.scalar.activation(two(tanh_out[:, row % 2, :])[:, :, reach(row)], two(p_damage[row % 2][:, :])[:, :, reach(row)],
                                             ACT.Tanh, bias=half_out_b[:, :], scale=0.5).then_inc(tanh_ready, 1)

                    for u, (row, slots, kind) in enumerate(units):
                        pair = u // 2
                        a.wait_ge(diff_v, g * N_DIFF_V + 3 * pair + (2, 3)[kind])
                        if kind == 0:
                            for n, slot in enumerate(slots):
                                x = ring(2 * u + n)[:, 0].rearrange("p h b s -> p (h b) s")[:, :, reach(row)]
                                shift = row * SLOTS + slot
                                ins = nc.scalar.activation(x, x, ACT.Gelu, bias=lag_b[:, shift:shift + 1])
                        else:
                            a.wait_ge(diff_p, g * N_DIFF_P + pair + 1)
                            x = ring(2 * u, 2).rearrange("p i h b s -> p (i h b) s")[:, :, reach(row)]
                            ins = nc.scalar.activation(x, x, ACT.Gelu, bias=w["damage_b"])
                        ins.then_inc(gelu_ready, 1)
                        if row > 0 and u % PER_ROW == 1:
                            tanh(row - 1)
                    tanh(ROWS - 1)
                    if later(g):
                        for parity in range(2):
                            a.wait_ge(wide_psum[parity], g * LAGS)
                    for j in range(PARTS):
                        rows = slice(j * ROWS // PARTS, (j + 1) * ROWS // PARTS)
                        a.wait_ge(shifted, g * PARTS + j + 1)
                        nc.scalar.activation(prob[:, rows, :], logit[:, rows, :], ACT.Exp).then_inc(prob_ready, 1)

                groups(a, logits, lambda g, l: None, lambda g: None)

            @block.gpsimd
            def _(pool):
                nc.gpsimd.memset(feat_now[:, :, :, :, 0:PAD].rearrange("p k h b s -> p (k h b) s"), 0.0).then_inc(padded, 1)
                nc.gpsimd.memset(val_now[:, :, 0:PAD], 0.0).then_inc(padded, 1)
                for row in range(1, ROWS):
                    ins = nc.gpsimd.memset(two(logit[:, row, :])[:, :, 0:row * SLOTS], NEG)
                ins.then_inc(masked, 1)

                def logits(g, lag, finish):
                    def mask(row):
                        pool.wait_ge(combined, g * ROWS + row + 3)
                        x = two(logit[:, row, :])[:, :, row * SLOTS:(row + 1) * SLOTS]
                        nc.gpsimd.tensor_tensor(x, x, bc(w["seen"], 1, 2), ALU.add).then_inc(masked, 1)

                    pool.wait_ge(feat_by_act, g + 1)
                    for u, (row, slots, kind) in enumerate(units):
                        if kind == 1:
                            pool.wait_ge(placed, g * UNITS + u + 1)
                            difference(nc.gpsimd, u, 1, row, slots[1], kind).then_inc(diff_p, 1)
                        if row > 0 and u % PER_ROW == 5:
                            mask(row - 1)
                        if u >= BEHIND + 2:
                            lag(u - BEHIND - 2)
                    for l in range(UNITS - BEHIND - 2, WINDOW):
                        lag(l)
                    mask(ROWS - 1)

                def lag(g, l):
                    part = lambda x: two(x)[:, :, reach(l // SLOTS)]
                    pool.wait_ge(weighted[l % 2], g * LAGS + l // 2 + 2)
                    if l == 0:
                        if later(g):
                            pool.wait_ge(oT_ready, g)
                        by_p = lambda x: x.rearrange("p (t q) -> p t q", q=P)
                        nc.gpsimd.tensor_tensor(by_p(acc[:, :]), by_p(product[:, 0, :]), bc(core.ones[:, :], 1, BANK // P), ALU.mult).then_inc(summed, 1)
                        return
                    pool.wait_ge(summed, g * WINDOW + l)
                    nc.gpsimd.tensor_tensor(part(acc[:, :]), part(acc[:, :]), part(product[:, l % 4, :]), ALU.add).then_inc(summed, 1)

                groups(pool, logits, lag, lambda g: None)

            @block.vector
            def _(v):
                v.sem_inc(combined, 2)
                v.sem_inc(weighted_even, 1)
                v.sem_inc(weighted_odd, 1)
                v.wait_ge(padded, 2)

                def logits(g, lag, finish):
                    if later(g):
                        v.wait_ge(diff_p, g * N_DIFF_P)
                        v.wait_ge(diff_v, g * N_DIFF_V)
                    nc.vector.tensor_copy(feat_now[:, 0, :, :, PAD:].rearrange("p h b s -> p (h b) s"),
                                          feat[:, 0, :, bass.ds(2 * g, 2), :]).then_inc(feat_by_dve, 1)
                    if later(g):
                        nc.vector.tensor_copy(val_now[:, :, PAD:], val[:, bass.ds(2 * g - 2, 2), :]).then_inc(val_copied, 1)
                    v.wait_ge(feat_by_dve, g + 1)
                    v.wait_ge(feat_by_act, g + 1)
                    if later(g):
                        v.wait_ge(val_copied, g)

                    def combine(row):
                        v.wait_ge(tanh_ready, g * ROWS + row + 1)
                        part = lambda x: two(x)[:, :, reach(row)]
                        nc.vector.scalar_tensor_tensor(part(logit[:, row, :]), part(tanh_out[:, row % 2, :]), -5.0, part(p_bond[row % 2][:, :]), ALU.mult, ALU.add).then_inc(combined, 1)

                    for u, (row, slots, kind) in enumerate(units):
                        v.wait_ge(placed, g * UNITS + u + 1)
                        for n, slot in enumerate(slots):
                            if kind == 0 or n == 0:
                                difference(nc.vector, u, n, row, slot, kind).then_inc(diff_v, 1)
                        if row > 0 and u % PER_ROW == 3:
                            combine(row - 1)
                        if u >= BEHIND:
                            lag(u - BEHIND)
                    for l in range(UNITS - BEHIND, WINDOW):
                        lag(l)
                    combine(ROWS - 1)
                    finish()
                    v.wait_ge(masked, (g + 1) * ROWS + 1)
                    nc.vector.tensor_reduce(slot_max[:, :], logit.rearrange("p r s -> p s r"), AX.X, ALU.max).then_inc(slot_max_ready, 1)
                    v.wait_ge(max_psum, g + 1)
                    by_head = p_max[:, :].rearrange("p (t s h) -> p t h s", t=4, s=SLOTS)
                    nc.vector.tensor_reduce(neg_max[:, :, :], by_head, AX.X, ALU.max, negate=True).then_inc(neg_max_done, 1)
                    v.wait_ge(neg_max_done, g + 1)
                    nc.vector.tensor_copy(neg_max_wide[:, :, :, :], bc(neg_max[:, :, :], 2, SLOTS)).then_inc(neg_max_ready, 1)
                    v.wait_ge(neg_max_psum, g + 1)
                    for j in range(PARTS):
                        rows = slice(j * ROWS // PARTS, (j + 1) * ROWS // PARTS)
                        nc.vector.tensor_tensor(logit[:, rows, :], logit[:, rows, :], bc(p_x[:, :], 1, ROWS // PARTS), ALU.add).then_inc(shifted, 1)
                    v.wait_ge(den_psum, g + 1)
                    nc.vector.reciprocal(inv[:, :], p_max[:, :]).then_inc(inv_ready, 1)

                def lag(g, l):
                    v.wait_ge(wide_psum[l % 2], g * LAGS + l // 2 + 1)
                    if l >= 4:
                        v.wait_ge(summed, g * WINDOW + l - 3)
                    start = l // SLOTS * SLOTS
                    part = lambda x: two(x)[:, :, start:]
                    nc.vector.tensor_tensor(part(product[:, l % 4, :]), part(p_wide[l % 2][:, :]), val_now[:, :, PAD - l + start:PAD - l + SEQ],
                                            ALU.mult).then_inc(weighted[l % 2], 1)

                def finish(g):
                    v.wait_ge(summed, (g + 1) * WINDOW)
                    v.wait_ge(inv_ready, g + 1)
                    nc.vector.tensor_tensor(oT[:, :], acc[:, :], inv[:, :], ALU.mult).then_inc(oT_ready, 1)
                    v.wait_ge(y_ready, g + 1)
                    x = core.x_res[:, bass.ds(4 * g, 4), :]
                    nc.vector.tensor_tensor(x, x, p_x[:, :].rearrange("p (t d) -> p t d", t=4), ALU.add).then_inc(added, 1)

                def last_values():
                    for parity in range(2):
                        v.wait_ge(weighted[parity], (GROUPS - 1) * LAGS + 1)
                    nc.vector.tensor_copy(val_now[:, :, PAD:], val[:, BATCH - 2:BATCH, :]).then_inc(val_copied, 1)
                    v.wait_ge(val_copied, GROUPS)

                groups(v, logits, lag, finish, last_values)


FFN2_EXPERTS = 8
FFN2_TOP = 2
FFN2_HID = 2 * D
CH = FFN2_HID // P


def ffn2_weights(w):
    return pack([
        ("router", w["router_w"].T), ("earlier", earlier_table(FFN2_EXPERTS)),
        ("w1", w["w1"].transpose(2, 0, 1).reshape(D, FFN2_EXPERTS * FFN2_HID)),
        ("w2", w["w2"].transpose(2, 0, 1).reshape(CH, P, FFN2_EXPERTS, D).transpose(1, 2, 0, 3).reshape(P, FFN2_EXPERTS * FFN2_HID)),
    ])


def ffn2(core, blob, offsets):
    nc = core.nc
    GROUPS = TOK // BANK
    with Stage(core, "ffn2") as st:
        w = st.weights(blob, offsets)
        layer_norm(core, st)
        w1 = w["w1"].rearrange("p (e c h) -> p e c h", e=FFN2_EXPERTS, c=CH)
        w2 = w["w2"].rearrange("p (e c d) -> p e c d", e=FFN2_EXPERTS, c=CH)
        bank = [st.ps(f"bank{i}", [P, BANK]) for i in range(8)]
        logit_psum = bank[0][:, 0:TILES * FFN2_EXPERTS].rearrange("p (t e) -> p t e", t=TILES)
        router_logits(core, w["router"], lambda t: logit_psum[:, bass.ds(t, 1), :].squeeze(1), FFN2_EXPERTS, st)

        gate = st.sb("gate", [P, TILES, FFN2_EXPERTS])
        logit, sel, rank = (st.sb(n, [P, TILES, FFN2_EXPERTS]) for n in ("logit", "sel", "rank"))
        above, same = (st.sb(n, [P, TILES, FFN2_EXPERTS, FFN2_EXPERTS]) for n in ("above", "same"))
        best, total = st.sb("best", [P, TILES]), st.sb("total", [P, TILES])
        dve, centred, exp_ready = st.sem("dve"), st.sem("centred"), st.sem("exp_ready")
        with nc.Block() as block:
            @block.vector
            def _(v):
                c = Chain(v, dve)
                c.link(nc.vector.tensor_copy(logit[:, :, :], logit_psum))
                c.link(nc.vector.tensor_reduce(best[:, :], logit[:, :, :], AX.X, ALU.max))
                nc.vector.tensor_tensor(gate[:, :, :], logit[:, :, :], bc(best[:, :], 2, FFN2_EXPERTS), ALU.subtract).then_inc(centred, 1)
                link_ranks(nc, c, rank[:, :, :], logit[:, :, :], above[:, :, :, :], same[:, :, :, :], w["earlier"], FFN2_EXPERTS)
                c.link(nc.vector.tensor_scalar(sel[:, :, :], rank[:, :, :], float(FFN2_TOP), None, ALU.is_lt))
                v.wait_ge(exp_ready, 1)
                c.link(nc.vector.tensor_tensor(gate[:, :, :], gate[:, :, :], sel[:, :, :], ALU.mult))
                c.link(nc.vector.tensor_reduce(total[:, :], gate[:, :, :], AX.X, ALU.add))
                c.link(nc.vector.reciprocal(total[:, :], total[:, :]))
                nc.vector.tensor_tensor(gate[:, :, :], gate[:, :, :], bc(total[:, :], 2, FFN2_EXPERTS), ALU.mult)

            @block.scalar
            def _(a):
                a.wait_ge(centred, 1)
                nc.scalar.activation(gate[:, :, :], gate[:, :, :], ACT.Exp).then_inc(exp_ready, 1)

        hid = st.sb("hid", [P, 2, CH, BANK])
        up_ready, hid_ready, y_ready, added, up_free, y_free = (st.sem(n) for n in ("up_ready", "hid_ready", "y_ready", "added", "up_free", "y_free"))
        with nc.Block() as block:
            @block.tensor
            def _(pe):
                with pe.Fori(0, GROUPS) as g:
                    n0 = g * FFN2_EXPERTS
                    x = core.xnT[:, bass.ds(g * BANK, BANK)]

                    def up(e):
                        for k in range(CH):
                            ins = nc.tensor.matmul(bank[2 * (e % 2) + k][:, :], w1[:, e, k, :], x, start=True, stop=True)
                        ins.then_inc(up_ready, 1)

                    def down(e):
                        pe.wait_ge(hid_ready, n0 + e + 1)
                        pe.wait_ge(y_free, n0 + e + 1)
                        for t in range(4):
                            for k in range(CH):
                                ins = nc.tensor.matmul(bank[4 + e % 2][:, t * P:(t + 1) * P], hid[:, e % 2, k, t * P:(t + 1) * P], w2[:, e, k, :],
                                                       start=(k == 0), stop=(k == CH - 1))
                        ins.then_inc(y_ready, 1)

                    up(0)
                    up(1)
                    for e in range(FFN2_EXPERTS):
                        down(e)
                        if e + 2 < FFN2_EXPERTS:
                            up(e + 2)

            @block.scalar
            def _(a):
                with a.Fori(0, GROUPS) as g:
                    for e in range(FFN2_EXPERTS):
                        a.wait_ge(up_ready, g * FFN2_EXPERTS + e + 1)
                        for k in range(CH):
                            ins = nc.scalar.activation(hid[:, e % 2, k, :], bank[2 * (e % 2) + k][:, :], ACT.Gelu)
                        ins.then_inc(hid_ready, 1)

            @block.vector
            def _(v):
                v.sem_inc(y_free, 2)
                with v.Fori(0, GROUPS) as g:
                    for e in range(FFN2_EXPERTS):
                        v.wait_ge(y_ready, g * FFN2_EXPERTS + e + 1)
                        if e > 0:
                            v.wait_ge(y_free, g * FFN2_EXPERTS + e + 2)
                        for t in range(4):
                            x = core.x_res[:, bass.ds(g * 4 + t, 1), :].squeeze(1)
                            ins = nc.vector.scalar_tensor_tensor(x, bank[4 + e % 2][:, t * P:(t + 1) * P],
                                                                 gate[:, bass.ds(g * 4 + t, 1), e:e + 1].squeeze(1), x, ALU.mult, ALU.add)
                        ins.then_inc(y_free, 1)


def attn_b2_weights(w):
    return pack([
        ("wq", w["Wq"]), ("wk", w["Wk"]), ("wv", w["Wv"]), ("wo", w["Wo"]),
        ("bq", w["bq"]), ("bk", w["bk"]), ("bv", np.broadcast_to(w["bv"], (P, D))), ("bo", w["bo"][None, :]),
    ])


def attn_b2(core, blob, offsets):
    nc = core.nc
    T = SEQ // P
    with Stage(core, "attn_b2") as st:
        w = st.weights(blob, offsets)
        layer_norm(core, st)
        bank = [st.ps(f"bank{i}", [P, BANK]) for i in range(8)]
        x_now = st.sb("x_now", [P, SEQ])
        q, k2 = st.sb("q", [P, SEQ]), st.sb("k2", [P, SEQ])
        qk_sq = st.sb("qk_sq", [P, 2, SEQ])
        val = st.sb("val", [P, T, D])
        neg_ones = st.sb("neg_ones", [P, P])
        zero = st.sb("zero", [P, 1])
        score = st.sb("score", [P, T, SEQ])
        neg_max = st.sb("neg_max", [P, T])
        prob = st.sb("prob", [P, T, SEQ])
        row_sum, inv = st.sb("row_sum", [P, T]), st.sb("inv", [P, T])
        probT = st.sb("probT", [P, T, SEQ])
        o_tok = st.sb("o_tok", [P, T, D])
        oT = st.sb("oT", [P, SEQ])
        names = ("x_copied", "qk_psum", "v_psum", "qk_ready", "sq_ready", "v_ready", "dist_ready", "score_ready", "max_ready", "prob_ready",
                 "probT_psum", "probT_ready", "o_psum", "inv_ready", "o_ready", "oT_psum", "oT_ready", "y_ready", "y_added", "set_up")
        (x_copied, qk_psum, v_psum, qk_ready, sq_ready, v_ready, dist_ready, score_ready, max_ready, prob_ready,
         probT_psum, probT_ready, o_psum, inv_ready, o_ready, oT_psum, oT_ready, y_ready, y_added, set_up) = (st.sem(n) for n in names)
        tiled = lambda ap: ap.rearrange("p (t d) -> p t d", t=T)
        with nc.Block() as block:
            @block.gpsimd
            def _(pool):
                nc.gpsimd.memset(neg_ones[:, :], -1.0).then_inc(set_up, 1)
                with pool.Fori(0, BATCH) as b:
                    pool.wait_ge(v_psum, b)
                    nc.gpsimd.tensor_copy(x_now[:, :], core.xnT[:, bass.ds(b * SEQ, SEQ)]).then_inc(x_copied, 1)

            @block.tensor
            def _(pe):
                pe.wait_ge(set_up, 1)
                with pe.Fori(0, BATCH) as b:
                    pe.wait_ge(x_copied, b + 1)
                    nc.tensor.matmul(bank[0][:, 0:SEQ], w["wq"], x_now[:, :], start=True, stop=True)
                    nc.tensor.matmul(bank[0][:, SEQ:2 * SEQ], w["wk"], x_now[:, :], start=True, stop=True).then_inc(qk_psum, 1)
                    for t in range(T):
                        ins = nc.tensor.matmul(bank[1][:, t * D:(t + 1) * D], x_now[:, t * P:(t + 1) * P], w["wv"], start=True, stop=True)
                    ins.then_inc(v_psum, 1)
                    pe.wait_ge(sq_ready, b + 1)
                    for t in range(T):
                        out = bank[2][:, t * SEQ:(t + 1) * SEQ]
                        nc.tensor.matmul(out, q[:, t * P:(t + 1) * P], k2[:, :], start=True, stop=False)
                        nc.tensor.matmul(out, qk_sq[:, 0, t * P:(t + 1) * P], neg_ones[:, 0:1].broadcast_to([P, SEQ]), start=False, stop=False)
                        ins = nc.tensor.matmul(out, neg_ones[:, :], qk_sq[:, 1, :], start=False, stop=True)
                    ins.then_inc(dist_ready, 1)
                    pe.wait_ge(prob_ready, b + 1)
                    for kt in range(T):
                        for qt in range(T):
                            ins = nc.tensor.transpose(bank[3][:, kt * SEQ + qt * P:kt * SEQ + (qt + 1) * P],
                                                      prob[:, qt, kt * P:(kt + 1) * P], core.ident[:, :])
                    ins.then_inc(probT_psum, 1)
                    pe.wait_ge(probT_ready, b + 1)
                    for qt in range(T):
                        for kt in range(T):
                            ins = nc.tensor.matmul(bank[4][:, qt * D:(qt + 1) * D], probT[:, kt, qt * P:(qt + 1) * P], val[:, kt, :],
                                                   start=(kt == 0), stop=(kt == T - 1))
                    ins.then_inc(o_psum, 1)
                    pe.wait_ge(o_ready, b + 1)
                    for t in range(T):
                        ins = nc.tensor.transpose(bank[5][:, t * P:(t + 1) * P], o_tok[:, t, :], core.ident[:, :])
                    ins.then_inc(oT_psum, 1)
                    pe.wait_ge(oT_ready, b + 1)
                    for t in range(T):
                        y = bank[6][:, t * P:(t + 1) * P]
                        nc.tensor.matmul(y, core.ones[0:1, :], w["bo"][0:1, :], start=True, stop=False)
                        ins = nc.tensor.matmul(y, oT[:, t * P:(t + 1) * P], w["wo"], start=False, stop=True)
                    ins.then_inc(y_ready, 1)

            @block.scalar
            def _(a):
                with a.Fori(0, BATCH) as b:
                    a.wait_ge(qk_ready, b + 1)
                    nc.scalar.activation(qk_sq[:, 0, :], q[:, :], ACT.Square)
                    nc.scalar.activation(qk_sq[:, 1, :], k2[:, :], ACT.Square, scale=0.5).then_inc(sq_ready, 1)
                    a.wait_ge(dist_ready, b + 1)
                    nc.scalar.activation(score[:, :, :], tiled(bank[2][:, :]), ACT.Exp).then_inc(score_ready, 1)
                    a.wait_ge(max_ready, b + 1)
                    for t in range(T):
                        ins = nc.scalar.activation(prob[:, t, :], score[:, t, :], ACT.Exp, bias=neg_max[:, t:t + 1],
                                                   accum_out=row_sum[:, t:t + 1])
                    ins.then_inc(prob_ready, 1)
                    a.wait_ge(oT_psum, b + 1)
                    nc.scalar.copy(oT[:, :], bank[5][:, 0:SEQ]).then_inc(oT_ready, 1)

            @block.vector
            def _(v):
                with v.Fori(0, BATCH) as b:
                    v.wait_ge(qk_psum, b + 1)
                    nc.vector.tensor_scalar(q[:, :], bank[0][:, 0:SEQ], w["bq"], None, ALU.add)
                    nc.vector.tensor_scalar(k2[:, :], bank[0][:, SEQ:2 * SEQ], w["bk"], 2.0, ALU.add, ALU.mult).then_inc(qk_ready, 1)
                    v.wait_ge(v_psum, b + 1)
                    nc.vector.tensor_tensor(val[:, :, :], tiled(bank[1][:, 0:T * D]), bc(w["bv"], 1, T), ALU.add).then_inc(v_ready, 1)
                    v.wait_ge(score_ready, b + 1)
                    nc.vector.tensor_reduce(neg_max[:, :], score[:, :, :], AX.X, ALU.max, negate=True).then_inc(max_ready, 1)
                    v.wait_ge(probT_psum, b + 1)
                    nc.vector.tensor_copy(probT[:, :, :], tiled(bank[3][:, :])).then_inc(probT_ready, 1)
                    nc.vector.reciprocal(inv[:, :], row_sum[:, :]).then_inc(inv_ready, 1)
                    v.wait_ge(inv_ready, b + 1)
                    v.wait_ge(o_psum, b + 1)
                    nc.vector.tensor_tensor(o_tok[:, :, :], tiled(bank[4][:, 0:T * D]), bc(inv[:, :], 2, D), ALU.mult).then_inc(o_ready, 1)
                    v.wait_ge(y_ready, b + 1)
                    x = core.x_res[:, bass.ds(b * T, T), :]
                    nc.vector.tensor_tensor(x, x, tiled(bank[6][:, 0:T * D]), ALU.add).then_inc(y_added, 1)


ATTN_A3_HD = 64
ATTN_A3_CHUNKS = HEADS * ATTN_A3_HD // P
PER_OUT = 4


def attn_a3_weights(w):
    flat = lambda a: a.reshape(HEADS * ATTN_A3_HD, D).T
    col = lambda a: a.reshape(ATTN_A3_CHUNKS, P).T
    query, key = np.arange(P)[:, None], np.arange(P)[None, :]
    return pack([
        ("wq", flat(w["Wq"])), ("wk", flat(w["Wk"])), ("wv", flat(w["Wv"])),
        ("bq", col(w["bq"])), ("bk", col(w["bk"])), ("bv", np.broadcast_to(w["bv"].reshape(1, HEADS * ATTN_A3_HD), (P, HEADS * ATTN_A3_HD))),
        ("proj", w["proj"].reshape(ATTN_A3_CHUNKS, P, D).transpose(1, 0, 2).reshape(P, ATTN_A3_CHUNKS * D)),
        ("causal", np.where(key > query, np.float32(NEG), np.float32(0))),
    ])


def attn_a3(core, blob, offsets):
    nc = core.nc
    T = SEQ // P
    inv_scale = 1.0 / np.sqrt(float(ATTN_A3_HD))
    with Stage(core, "attn_a3") as st:
        w = st.weights(blob, offsets)
        layer_norm(core, st)
        bank = [st.ps(f"bank{i}", [P, BANK]) for i in range(8)]
        pS, pT, pO, pP, pY = bank[0:2], bank[2:4], bank[4], bank[5:7], bank[7]
        x_now = st.sb("x_now", [P, SEQ])
        q = st.sb("q", [P, 2, ATTN_A3_CHUNKS, 2, SEQ])
        k = st.sb("k", [P, 2, ATTN_A3_CHUNKS, SEQ])
        val = st.sb("val", [P, 2, T, HEADS * ATTN_A3_HD])
        small_b = st.sb("small_b", [P, ATTN_A3_CHUNKS])
        prob = st.sb("prob", [P, 2, 3, P])
        probT = st.sb("probT", [P, 4, 3, P])
        neg_max, row_sum, inv = (st.sb(n, [P, 2, T]) for n in ("neg_max", "row_sum", "inv"))
        oT = st.sb("oT", [P, HEADS, SEQ // 2])
        names = ("set_up", "zeroed", "x_copied", "proj_psum", "proj_by_act", "proj_by_dve", "scores_ready", "masked", "max_ready", "exp_ready",
                 "inverted", "prob_ready", "probT_psum", "probT_ready", "pair_done", "oT_ready", "y_ready", "y_added")
        (set_up, zeroed, x_copied, proj_psum, proj_by_act, proj_by_dve, scores_ready, masked, max_ready, exp_ready,
         inverted, prob_ready, probT_psum, probT_ready, pair_done, oT_ready, y_ready, y_added) = (st.sem(n) for n in names)
        by_act = lambda i: i < 8 and i % 2 == 0
        reader = lambda i: (proj_by_act, i // 2 + 1) if by_act(i) else (proj_by_dve, i // 2 + 1 if i < 8 else i - 3)
        ACT_FILLS, DVE_FILLS = 4, 8
        FILLS = 12
        GROUPS = HEADS // PER_OUT
        PAIRS = HEADS // 2
        HALF = HEADS // T * SEQ // 2
        oT_flat = oT[:, :, :].rearrange("p h s -> p (h s)")

        with nc.Block() as block:
            @block.gpsimd
            def _(pool):
                def x_copy(b):
                    if not known(b, 1):
                        pool.wait_ge(proj_psum, b * FILLS)
                    nc.gpsimd.tensor_copy(x_now[:, :], core.xnT[:, bass.ds(b * SEQ, SEQ)]).then_inc(x_copied, 1)

                def step(b, s, first, last):
                    if first:
                        x_copy(b)
                        pool.wait_ge(x_copied, 1)
                        for s_zero in range(2):
                            for head in range(2):
                                other = slice(ATTN_A3_HD * (1 - head), ATTN_A3_HD * (2 - head))
                                nc.gpsimd.memset(q[other, s_zero, :, head, :], 0.0).then_inc(zeroed, 1)
                                pool.wait_ge(zeroed, 2 * s_zero + head + 1)
                        x_copy(b + 1)
                    for h in range(HEADS):
                        pool.wait_ge(inverted, b * HEADS + h + 1)
                        for t, blocks in enumerate((slice(0, 1), slice(1, 3))):
                            x = prob[:, h % 2, blocks, :]
                            ins = nc.gpsimd.tensor_tensor(x, x, bc(bc(inv[:, h % 2, t:t + 1].squeeze(1), 1, P), 1, blocks.stop - blocks.start), ALU.mult)
                        ins.then_inc(prob_ready, 1)
                        if h == 13 and not last:
                            if not known(b, BATCH) or b + 2 < BATCH:
                                x_copy(b + 2)

                sequences(pool, step)

            @block.tensor
            def _(pe):
                def fill(b, i):
                    if i == 0:
                        pe.wait_ge(x_copied, b + 1)
                    if i >= 2 or not known(b, 1):
                        j, c = (i - 2, b) if i >= 2 else (i - 2 + FILLS, b - 1)
                        done, count = reader(j)
                        pe.wait_ge(done, c * (ACT_FILLS if by_act(j) else DVE_FILLS) + count)
                    if i < 8:
                        for c in range(2):
                            ch = 2 * (i % 4) + c
                            ins = nc.tensor.matmul(pP[i % 2][:, c * SEQ:(c + 1) * SEQ], w["wq" if i < 4 else "wk"][:, ch * P:(ch + 1) * P],
                                                   x_now[:, :], start=True, stop=True)
                    else:
                        t, half = (i - 8) // 2, (i - 8) % 2
                        ins = nc.tensor.matmul(pP[i % 2][:, :], x_now[:, t * P:(t + 1) * P], w["wv"][:, half * BANK:(half + 1) * BANK],
                                               start=True, stop=True)
                    ins.then_inc(proj_psum, 1)

                def scores(b, s, h):
                    if h == 0:
                        pe.wait_ge(zeroed, 4)
                        pe.wait_ge(proj_by_act, (b + 1) * ACT_FILLS)
                        pe.wait_ge(proj_by_dve, (b + 1) * DVE_FILLS)
                    qh = q[:, s, h // 2, h % 2, :]
                    nc.tensor.matmul(pS[h % 2][:, 0:P], qh[:, 0:P], k[:, s, h // 2, 0:P], start=True, stop=True)
                    nc.tensor.matmul(pS[h % 2][:, SEQ:2 * SEQ], qh[:, P:2 * P], k[:, s, h // 2, :], start=True, stop=True).then_inc(scores_ready, 1)

                def turn(b, h):
                    pe.wait_ge(prob_ready, b * HEADS + h + 1)
                    if not (known(b, 1) and h < 2):
                        pe.wait_ge(probT_ready, b * HEADS + h - 1)
                    for j in range(3):
                        ins = nc.tensor.transpose(pT[h % 2][:, j * P:(j + 1) * P], prob[:, h % 2, j, :], core.ident[:, :])
                    ins.then_inc(probT_psum, 1)

                def weighted(b, s, pair):
                    pe.wait_ge(probT_ready, b * HEADS + 2 * pair + 2)
                    if pair % 2 == 0 and not (known(b, 1) and pair == 0):
                        pe.wait_ge(oT_ready, b * GROUPS + pair // 2)
                    at = pair % 2 * SEQ
                    for t in range(T):
                        for odd in range(2):
                            h = 2 * pair + odd
                            rows = slice(odd * ATTN_A3_HD, (odd + 1) * ATTN_A3_HD)
                            moving = probT[:, h % 4, 0:2, :] if t == 0 else probT[:, h % 4, 2, :]
                            out = pO[rows, at:at + SEQ].rearrange("p (j q) -> p j q", j=2) if t == 0 else pO[rows, at + P:at + SEQ]
                            ins = nc.tensor.matmul(out, val[:, s, t, h * ATTN_A3_HD:(h + 1) * ATTN_A3_HD], moving, start=(t == 0), stop=(t == 1),
                                                   tile_position=(0, rows.start))
                    ins.then_inc(pair_done, 1)

                def project(b):
                    pe.wait_ge(oT_ready, (b + 1) * GROUPS)
                    if not known(b, 1):
                        pe.wait_ge(y_added, b)
                    for t in range(T):
                        for c in range(ATTN_A3_CHUNKS):
                            ins = nc.tensor.matmul(pY[:, t * P:(t + 1) * P], oT_flat[:, t * HALF + c:(t + 1) * HALF:ATTN_A3_CHUNKS], w["proj"][:, c * D:(c + 1) * D],
                                                   start=(c == 0), stop=(c == ATTN_A3_CHUNKS - 1))
                    ins.then_inc(y_ready, 1)

                def step(b, s, first, last):
                    if first:
                        for i in range(FILLS):
                            fill(b, i)
                        scores(b, s, 0)
                        scores(b, s, 1)
                    for h in range(HEADS):
                        turn(b, h)
                        if h + 2 < HEADS:
                            scores(b, s, h + 2)
                        elif not last:
                            scores(b + 1, 1 - s, h + 2 - HEADS)
                        if h < FILLS and not last:
                            fill(b + 1, h)
                        if h == 0 and not first:
                            weighted(b - 1, 1 - s, PAIRS - 1)
                        if h == 3 and not first:
                            project(b - 1)
                        if h >= 2 and h % 2 == 0:
                            weighted(b, s, h // 2 - 1)
                    if last:
                        weighted(b, s, PAIRS - 1)
                        project(b)

                sequences(pe, step)

            def evacuate(eng, act, b, s, i):
                done = proj_by_act if act else proj_by_dve
                src = pP[i % 2]
                eng.wait_ge(proj_psum, b * FILLS + i + 1)
                if i >= 8:
                    t, half = (i - 8) // 2, (i - 8) % 2
                    if i == 8 and not known(b, 2):
                        eng.wait_ge(pair_done, (b - 1) * PAIRS)
                    nc.vector.tensor_tensor(val[:, s, t, half * BANK:(half + 1) * BANK], src[:, :], w["bv"][:, half * BANK:(half + 1) * BANK],
                                            ALU.add).then_inc(done, 1)
                    return
                for c in range(2):
                    ch, part = 2 * (i % 4) + c, src[:, c * SEQ:(c + 1) * SEQ]
                    if i >= 4:
                        if act:
                            ins = nc.scalar.activation(k[:, s, ch, :], part, ACT.Identity, bias=w["bk"][:, ch:ch + 1])
                        else:
                            ins = nc.vector.tensor_scalar(k[:, s, ch, :], part, w["bk"][:, ch:ch + 1], None, ALU.add)
                        continue
                    for head in range(2):
                        rows = slice(head * ATTN_A3_HD, (head + 1) * ATTN_A3_HD)
                        if act:
                            ins = nc.scalar.activation(q[rows, s, ch, head, :], part[rows], ACT.Identity, bias=small_b[rows, ch:ch + 1], scale=inv_scale)
                        else:
                            ins = nc.vector.tensor_scalar(q[rows, s, ch, head, :], part[rows], w["bq"][rows, ch:ch + 1], inv_scale, ALU.add, ALU.mult)
                ins.then_inc(done, 1)

            @block.scalar
            def _(a):
                a.wait_ge(set_up, 1)

                def out_copy(b, g):
                    a.wait_ge(pair_done, b * PAIRS + 2 * g + 2)
                    if g == 0 and not known(b, 1):
                        a.wait_ge(y_ready, b)
                    for odd_head in range(2):
                        for odd_u in range(2):
                            src = pO[odd_head * ATTN_A3_HD:(odd_head + 1) * ATTN_A3_HD, :].rearrange("p (c s u) -> p c s u", c=2, u=2)[:, :, :, odd_u]
                            dst = oT[odd_u * ATTN_A3_HD:(odd_u + 1) * ATTN_A3_HD, 4 * g + odd_head:4 * g + odd_head + 3:2, :]
                            ins = nc.scalar.activation(dst, src, ACT.Copy, scale=inv_scale)
                    ins.then_inc(oT_ready, 1)

                def step(b, s, first, last):
                    if first:
                        for i in filter(by_act, range(FILLS)):
                            evacuate(a, True, b, s, i)
                    for h in range(HEADS):
                        a.wait_ge(max_ready, b * HEADS + h + 1)
                        nc.scalar.activation(prob[:, h % 2, 0, :], pS[h % 2][:, 0:P], ACT.Exp, bias=neg_max[:, h % 2, 0:1],
                                             accum_out=row_sum[:, h % 2, 0:1])
                        nc.scalar.activation(prob[:, h % 2, 1:3, :], pS[h % 2][:, SEQ:2 * SEQ].rearrange("p (j k) -> p j k", j=2), ACT.Exp,
                                             bias=neg_max[:, h % 2, 1:2], accum_out=row_sum[:, h % 2, 1:2]).then_inc(exp_ready, 1)
                        if h == 2 and not first:
                            out_copy(b - 1, GROUPS - 1)
                        if h >= 1 and by_act(h - 1) and not last:
                            evacuate(a, True, b + 1, 1 - s, h - 1)
                        if h % PER_OUT == 2 and h > 2:
                            out_copy(b, h // PER_OUT - 1)
                    if last:
                        out_copy(b, GROUPS - 1)

                sequences(a, step)

            @block.vector
            def _(v):
                nc.vector.tensor_scalar(small_b[:, :], w["bq"], inv_scale, None, ALU.mult).then_inc(set_up, 1)

                def row_max(b, h):
                    n = b * HEADS + h + 1
                    v.wait_ge(scores_ready, n)
                    blocks = pS[h % 2][:, :].rearrange("p (j k) -> p j k", k=P)[:, 0:4:3, :]
                    nc.vector.tensor_tensor(blocks, blocks, bc(w["causal"], 1, 2), ALU.add).then_inc(masked, 1)
                    v.wait_ge(masked, n)
                    nc.vector.tensor_reduce(neg_max[:, h % 2, 0:1], pS[h % 2][:, 0:P], AX.X, ALU.max, negate=True)
                    nc.vector.tensor_reduce(neg_max[:, h % 2, 1:2], pS[h % 2][:, SEQ:2 * SEQ], AX.X, ALU.max, negate=True).then_inc(max_ready, 1)

                def invert(b, h):
                    v.wait_ge(exp_ready, b * HEADS + h + 1)
                    nc.vector.reciprocal(inv[:, h % 2, :], row_sum[:, h % 2, :]).then_inc(inverted, 1)

                def step(b, s, first, last):
                    if first:
                        for i in (i for i in range(FILLS) if not by_act(i)):
                            evacuate(v, False, b, s, i)
                        row_max(b, 0)
                        invert(b, 0)
                        row_max(b, 1)
                    for h in range(HEADS):
                        if h + 1 < HEADS:
                            invert(b, h + 1)
                        elif not last:
                            invert(b + 1, 0)
                        v.wait_ge(probT_psum, b * HEADS + h + 1)
                        if h % 2 == 0 and not (known(b, 1) and h < 4):
                            v.wait_ge(pair_done, b * PAIRS + h // 2 - 1)
                        nc.vector.tensor_copy(probT[:, h % 4, :, :], pT[h % 2][:, 0:3 * P].rearrange("p (j q) -> p j q", j=3)).then_inc(probT_ready, 1)
                        if h + 2 < HEADS:
                            row_max(b, h + 2)
                        elif not last:
                            row_max(b + 1, h + 2 - HEADS)
                        if 1 <= h <= FILLS and not by_act(h - 1) and not last:
                            evacuate(v, False, b + 1, 1 - s, h - 1)
                        if h == 5 and not first:
                            add(b - 1)
                    if last:
                        add(b)

                def add(b):
                    v.wait_ge(y_ready, b + 1)
                    x = core.x_res[:, bass.ds(b * T, T), :]
                    nc.vector.tensor_tensor(x, x, pY[:, 0:T * D].rearrange("p (t d) -> p t d", t=T), ALU.add).then_inc(y_added, 1)

                sequences(v, step)


FFN3_EXPERTS = 64
FFN3_TOP = 8
ROUTE_GROUPS = 8
TOP_GROUPS = 4
IN_GROUP = FFN3_EXPERTS // ROUTE_GROUPS
FFN3_HID = 64
FFN3_SHARED = 256
PAIRS = FFN3_EXPERTS // 2
SCALE = 2.5
FFN3_PIECES = 3
SIDE = FFN3_EXPERTS // 2
FFN3_BF16 = mybir.dt.bfloat16


def ffn3_weights(w):
    expert_of_row = np.tile(np.arange(SIDE), FFN3_PIECES)
    spread = np.repeat(expert_of_row[:, None] == np.arange(SIDE)[None, :], FFN3_HID, axis=1).astype(np.float32)
    return pack([
        ("spread", spread),
        ("router", w["router_w"].T), ("earlier", earlier_table(ROUTE_GROUPS)),
        ("correction", np.broadcast_to(w["correction_bias"], (P, FFN3_EXPERTS))),
        ("up", w["up_w"].transpose(1, 0, 2).reshape(D, FFN3_EXPERTS * FFN3_HID)),
        ("down", w["down_w"].reshape(PAIRS, P, D).transpose(1, 0, 2).reshape(P, PAIRS * D)),
        ("shared_up", w["shared_up_w"]),
        ("shared_down", w["shared_down_w"].reshape(FFN3_SHARED // P, P, D).transpose(1, 0, 2).reshape(P, FFN3_SHARED // P * D)),
    ])


def ffn3(core, blob, offsets):
    nc = core.nc
    GROUPS = TOK // BANK
    with Stage(core, "ffn3") as st:
        w = st.weights(blob, offsets)
        layer_norm(core, st)
        bank = [st.ps(f"bank{i}", [P, BANK]) for i in range(8)]
        per_bank = BANK // FFN3_EXPERTS
        sfc = st.sb("sfc", [P, TILES, FFN3_EXPERTS])
        score = st.sb("score", [P, TILES, FFN3_EXPERTS])
        x_now = st.sb("x_now", [P, 2, BANK])
        copied, logits_ready, scores_ready = st.sem("copied"), st.sem("logits_ready"), st.sem("scores_ready")
        with nc.Block() as block:
            @block.gpsimd
            def _(pool):
                pool.sem_inc(scores_ready, 2)
                with pool.Fori(0, GROUPS // 2) as g:
                    for s in range(2):
                        pool.wait_ge(scores_ready, 2 * g + s + 1)
                        nc.gpsimd.tensor_copy(x_now[:, s, :], core.xnT[:, bass.ds((2 * g + s) * BANK, BANK)]).then_inc(copied, 1)

            @block.tensor
            def _(pe):
                with pe.Fori(0, GROUPS // 2) as g:
                    for s in range(2):
                        pe.wait_ge(copied, 2 * g + s + 1)
                        for t in range(4):
                            ins = nc.tensor.matmul(bank[s][:, t * FFN3_EXPERTS:(t + 1) * FFN3_EXPERTS], x_now[:, s, t * P:(t + 1) * P], w["router"],
                                                   start=True, stop=True)
                        ins.then_inc(logits_ready, 1)

            @block.scalar
            def _(a):
                with a.Fori(0, GROUPS // 2) as g:
                    for s in range(2):
                        a.wait_ge(logits_ready, 2 * g + s + 1)
                        nc.scalar.activation(score[:, bass.ds(8 * g + 4 * s, 4), :], bank[s][:, 0:4 * FFN3_EXPERTS].rearrange("p (t e) -> p t e", t=4),
                                             ACT.Sigmoid).then_inc(scores_ready, 1)

        comb = st.sb("comb", [P, TILES, FFN3_EXPERTS])
        work = st.sb("work", [P, TILES, FFN3_EXPERTS])
        repl = st.sb("repl", [P, TILES, FFN3_EXPERTS])
        first, second, ties, gscore, gsel = (st.sb(n, [P, TILES, ROUTE_GROUPS]) for n in ("first", "second", "ties", "gscore", "gsel"))
        above, same = (st.sb(n, [P, TILES, ROUTE_GROUPS, ROUTE_GROUPS]) for n in ("above", "same"))
        top8 = st.sb("top8", [P, TILES, FFN3_TOP])
        total = st.sb("total", [P, TILES])
        spread = st.sb("spread", [FFN3_PIECES * SIDE, SIDE * FFN3_HID], FFN3_BF16)
        ident = st.sb("ident_bf16", [P, P], FFN3_BF16)
        pieces = st.sb("pieces", [P, TILES, 2, FFN3_PIECES, SIDE], FFN3_BF16)
        dve = st.sem("dve")
        grouped = lambda t: t[:, :, :].rearrange("p t (g e) -> p (t g) e", g=ROUTE_GROUPS)
        flat = lambda t: t[:, :, :].rearrange("p t g -> p (t g)")
        with nc.Block() as block:
            @block.gpsimd
            def _(pool):
                nc.gpsimd.tensor_copy(spread[:, :], w["spread"][0:FFN3_PIECES * SIDE, :])
                nc.gpsimd.tensor_copy(ident[:, :], core.ident[:, :])

            @block.vector
            def _(v):
                c = Chain(v, dve)
                c.link(nc.vector.tensor_tensor(sfc[:, :, :], score[:, :, :], bc(w["correction"], 1, TILES), ALU.add))
                c.link(nc.vector.tensor_reduce(flat(first), grouped(sfc), AX.X, ALU.max))
                c.link(nc.vector.tensor_tensor(grouped(work), grouped(sfc), bc(flat(first), 2, IN_GROUP), ALU.is_equal))
                c.link(nc.vector.tensor_reduce(flat(ties), grouped(work), AX.X, ALU.add))
                c.link(nc.vector.scalar_tensor_tensor(work[:, :, :], work[:, :, :], NEG, sfc[:, :, :], ALU.mult, ALU.add))
                c.link(nc.vector.tensor_reduce(flat(second), grouped(work), AX.X, ALU.max))
                c.link(nc.vector.tensor_scalar(ties[:, :, :], ties[:, :, :], 2.0, None, ALU.is_ge))
                c.link(nc.vector.tensor_tensor(gscore[:, :, :], first[:, :, :], ties[:, :, :], ALU.mult))
                c.link(nc.vector.tensor_scalar(ties[:, :, :], ties[:, :, :], -1.0, 1.0, ALU.mult, ALU.add))
                c.link(nc.vector.tensor_tensor(second[:, :, :], second[:, :, :], ties[:, :, :], ALU.mult))
                c.link(nc.vector.tensor_tensor(second[:, :, :], second[:, :, :], gscore[:, :, :], ALU.add))
                c.link(nc.vector.tensor_tensor(gscore[:, :, :], second[:, :, :], first[:, :, :], ALU.add))
                link_ranks(nc, c, gsel[:, :, :], gscore[:, :, :], above[:, :, :, :], same[:, :, :, :], w["earlier"], ROUTE_GROUPS)
                c.link(nc.vector.tensor_scalar(gsel[:, :, :], gsel[:, :, :], float(TOP_GROUPS), None, ALU.is_lt))
                c.link(nc.vector.tensor_tensor(grouped(work), grouped(sfc), bc(flat(gsel), 2, IN_GROUP), ALU.mult))
                for t in range(TILES):
                    ins = nc.vector.max(top8[:, t, :], work[:, t, :])
                c.link(ins)
                for t in range(TILES):
                    ins = nc.vector.match_replace(repl[:, t, :], top8[:, t, :], work[:, t, :], NEG)
                c.link(ins)
                c.link(nc.vector.tensor_tensor(work[:, :, :], work[:, :, :], repl[:, :, :], ALU.not_equal))
                c.link(nc.vector.tensor_tensor(comb[:, :, :], score[:, :, :], work[:, :, :], ALU.mult))
                c.link(nc.vector.tensor_reduce(total[:, :], comb[:, :, :], AX.X, ALU.add))
                c.link(nc.vector.tensor_scalar(total[:, :], total[:, :], 1e-20, None, ALU.add))
                c.link(nc.vector.reciprocal(total[:, :], total[:, :]))
                c.link(nc.vector.tensor_scalar(total[:, :], total[:, :], SCALE, None, ALU.mult))
                c.link(nc.vector.tensor_tensor(comb[:, :, :], comb[:, :, :], bc(total[:, :], 2, FFN3_EXPERTS), ALU.mult))
                by_side = comb[:, :, :].rearrange("p t (s e) -> p t s e", s=2)
                for i in range(FFN3_PIECES):
                    c.link(nc.vector.tensor_copy(pieces[:, :, :, i, :], by_side))
                    if i + 1 < FFN3_PIECES:
                        c.link(nc.vector.tensor_tensor(by_side, by_side, pieces[:, :, :, i, :], ALU.subtract))

        CHUNKS = PAIRS + FFN3_SHARED // P
        combT = st.sb("combT", [FFN3_PIECES * SIDE, 2, BANK], FFN3_BF16)
        relu = st.sb("relu", [P, 2, BANK])
        part = st.sb("part", [P, 2, BANK])
        hid = st.sb("hid", [P, 2, BANK])
        yT = st.sb("yT", [P, BANK])
        names = ("combT_psum", "combT_ready", "up_ready", "relu_ready", "part_ready", "hid_ready", "yT_psum", "yT_ready", "y_ready", "added")
        (combT_psum, combT_ready, up_ready, relu_ready, part_ready, hid_ready, yT_psum, yT_ready, y_ready, added) = (st.sem(n) for n in names)
        with nc.Block() as block:
            @block.tensor
            def _(pe):
                with pe.Fori(0, GROUPS) as g:
                    x = core.xnT[:, bass.ds(g * BANK, BANK)]
                    n0 = g * CHUNKS

                    def up(k):
                        if k < PAIRS:
                            side, at = k // (PAIRS // 2), k % (PAIRS // 2) * P
                            nc.tensor.matmul(bank[2 + k % 2][:, :], spread[:, at:at + P], combT[:, side, :],
                                             start=True, stop=True)
                            lhs = w["up"][:, k * P:(k + 1) * P]
                        else:
                            lhs = w["shared_up"][:, (k - PAIRS) * P:(k - PAIRS + 1) * P]
                        nc.tensor.matmul(bank[k % 2][:, :], lhs, x, start=True, stop=True).then_inc(up_ready, 1)

                    def down(k):
                        pe.wait_ge(hid_ready, n0 + k + 1)
                        lhs = w["down"][:, k * D:(k + 1) * D] if k < PAIRS else w["shared_down"][:, (k - PAIRS) * D:(k - PAIRS + 1) * D]
                        return nc.tensor.matmul(bank[4][:, :], lhs, hid[:, k % 2, :], start=(k == 0), stop=(k == CHUNKS - 1))

                    for t in range(4):
                        for side in range(2):
                            ins = nc.tensor.matmul(bank[5 + 2 * side][0:FFN3_PIECES * SIDE, t * P:(t + 1) * P],
                                                   pieces[:, bass.ds(g * 4 + t, 1), side, :, :].rearrange("p t i e -> p (t i e)"), ident[:, :], start=True, stop=True)
                    ins.then_inc(combT_psum, 1)
                    pe.wait_ge(combT_ready, g + 1)
                    up(0)
                    up(1)
                    for k in range(CHUNKS):
                        ins = down(k)
                        if k + 2 < CHUNKS:
                            up(k + 2)
                    ins.then_inc(yT_psum, 1)
                    pe.wait_ge(yT_ready, g + 1)
                    for t in range(4):
                        ins = nc.tensor.transpose(bank[6][:, t * P:(t + 1) * P], yT[:, t * P:(t + 1) * P], core.ident[:, :])
                    ins.then_inc(y_ready, 1)

            @block.scalar
            def _(a):
                with a.Fori(0, GROUPS) as g:
                    a.wait_ge(combT_psum, g + 1)
                    for side in range(2):
                        ins = nc.scalar.copy(combT[:, side, :], bank[5 + 2 * side][0:FFN3_PIECES * SIDE, :])
                    ins.then_inc(combT_ready, 1)
                    for k in range(CHUNKS):
                        a.wait_ge(up_ready, g * CHUNKS + k + 1)
                        nc.scalar.activation(relu[:, k % 2, :], bank[k % 2][:, :], ACT.Relu).then_inc(relu_ready, 1)

            @block.vector
            def _(v):
                with v.Fori(0, GROUPS) as g:
                    for k in range(CHUNKS):
                        v.wait_ge(relu_ready, g * CHUNKS + k + 1)
                        last = relu if k >= PAIRS else part
                        if k < PAIRS:
                            nc.vector.tensor_tensor(part[:, k % 2, :], relu[:, k % 2, :], bank[2 + k % 2][:, :], ALU.mult).then_inc(part_ready, 1)
                            v.wait_ge(part_ready, g * PAIRS + k + 1)
                        nc.vector.tensor_tensor(hid[:, k % 2, :], last[:, k % 2, :], relu[:, k % 2, :], ALU.mult).then_inc(hid_ready, 1)
                    v.wait_ge(yT_psum, g + 1)
                    nc.vector.tensor_copy(yT[:, :], bank[4][:, :]).then_inc(yT_ready, 1)
                    v.wait_ge(y_ready, g + 1)
                    xr = core.x_res[:, bass.ds(g * 4, 4), :]
                    nc.vector.tensor_tensor(xr, xr, bank[6][:, :].rearrange("p (t d) -> p t d", t=4), ALU.add).then_inc(added, 1)


def build_program(nc, x, ident, blobs, out):
    with ExitStack() as ctx:
        core = Core(nc, ctx)
        load_constants(core, ident, x)
        attn_a(core, *blobs["L0_attn_a"])
        ffn0(core, *blobs["L0_ffn"])
        attn_b0(core, *blobs["L0_attn_b"])
        ffn0(core, *blobs["L0_ffn"])
        attn_a(core, *blobs["L1_attn_a"])
        ffn1(core, *blobs["L1_ffn"])
        scan1(core, *blobs["L1_attn_b"])
        ffn1(core, *blobs["L1_ffn"])
        attn_a2(core, *blobs["L2_attn_a"])
        ffn2(core, *blobs["L2_ffn"])
        attn_b2(core, *blobs["L2_attn_b"])
        ffn2(core, *blobs["L2_ffn"])
        attn_a3(core, *blobs["L3_attn_a"])
        ffn3(core, *blobs["L3_ffn"])
        scan3(core, *blobs["L3_attn_b"])
        ffn3(core, *blobs["L3_ffn"])
        store_output(core, out)


_LAYOUTS = {"L0_attn_a": attn_a_weights, "L0_ffn": ffn0_weights, "L0_attn_b": attn_b0_weights, "L1_attn_a": attn_a_weights,
            "L1_ffn": ffn1_weights, "L1_attn_b": scan1_weights, "L2_attn_a": attn_a2_weights, "L2_ffn": ffn2_weights,
            "L2_attn_b": attn_b2_weights, "L3_attn_a": attn_a3_weights, "L3_ffn": ffn3_weights, "L3_attn_b": scan3_weights}


def kernel(**inputs):
    import concourse.bacc as bacc
    from concourse.bass_utils import run_bass_kernel_spmd

    arrays = {"x": np.ascontiguousarray(np.asarray(inputs["L0_attn_a_x"]).reshape(TOK, D)), "ident": np.eye(P, dtype=np.float32)}
    offsets = {}
    for stage, layout in _LAYOUTS.items():
        own = {k[len(stage) + 1:]: np.asarray(v) for k, v in inputs.items() if k.startswith(stage + "_")}
        arrays[stage], offsets[stage] = layout(own)
    nc = bacc.Bacc("TRN2", target_bir_lowering=False, num_devices=1)
    dram = {k: nc.dram_tensor(f"in_{k}", a.shape, mybir.dt.from_np(a.dtype), kind="ExternalInput").ap() for k, a in arrays.items()}
    out = nc.dram_tensor("out", (TOK, D), F32, kind="ExternalOutput").ap()
    build_program(nc, dram["x"], dram["ident"], {k: (dram[k], offsets[k]) for k in _LAYOUTS}, out)
    r = run_bass_kernel_spmd(nc, [{f"in_{k}": a for k, a in arrays.items()}], core_ids=[0])
    return r.results[0]["out"].reshape(BATCH, SEQ, D)
```

```python
from contextlib import ExitStack

import numpy as np
import concourse.bass as bass
from concourse import mybir

F32 = mybir.dt.float32
I32 = mybir.dt.int32
U8 = mybir.dt.uint8
ALU = mybir.AluOpType
ACT = mybir.ActivationFunctionType
AX = mybir.AxisListType

P = 128
D = 128
BATCH = 16
SEQ = 256
TOK = BATCH * SEQ
TILES = TOK // P
HEADS = 16
LN_EPS = 1e-5
BANK = 512
NEG = -1.0e30


def bc(ap, at, n):
    x = ap.unsqueeze(at)
    return x.broadcast_to([*x.shape[:at], n, *x.shape[at + 1:]])


def known(b, below):
    return isinstance(b, int) and b < below


def sequences(eng, step):
    step(0, 0, True, False)
    step(1, 1, False, False)
    with eng.Fori(1, BATCH // 2 - 1) as pair:
        step(pair * 2, 0, False, False)
        step(pair * 2 + 1, 1, False, False)
    step(BATCH - 2, 0, False, False)
    step(BATCH - 1, 1, False, True)


def in_pairs(eng, *stages):
    with eng.Fori(0, BATCH // 2) as pair:
        for stage in stages:
            for s in range(2):
                stage(pair, s)


class Chain:

    def __init__(self, eng, sem, start=0):
        self.eng, self.sem, self.start, self.n = eng, sem, start, 0

    def link(self, ins):
        self.n += 1
        ins.then_inc(self.sem, 1)
        self.eng.wait_ge(self.sem, self.start + self.n)


class Core:

    def __init__(self, nc, ctx):
        self.nc = nc
        sb = lambda name, shape, dt=F32: ctx.enter_context(nc.sbuf_tensor(name, shape, dt))
        self.x_res = sb("x_res", [P, TILES, D])
        self.xn = sb("xn", [P, TILES, D])
        self.xnT = sb("xnT", [P, TOK])
        self.rstd = sb("rstd", [P, TILES])
        self.ident = sb("ident", [P, P])
        self.ones = sb("ones", [P, P])
        self.n = 0


class Stage:

    def __init__(self, core, name):
        self.core, self.nc = core, core.nc
        core.n += 1
        self.name = f"{name}{core.n}"
        self.ctx = ExitStack()
        self.sems = []

    def __enter__(self):
        self.ctx.__enter__()
        return self

    def __exit__(self, *e):
        self.nc.clear_and_free_semaphores(self.sems)
        self.nc.all_engine_barrier()
        return self.ctx.__exit__(*e)

    def sb(self, name, shape, dt=F32):
        return self.ctx.enter_context(self.nc.sbuf_tensor(f"{self.name}_{name}", shape, dt))

    def ps(self, name, shape, dt=F32):
        return self.ctx.enter_context(self.nc.psum_tensor(f"{self.name}_{name}", shape, dt))

    def sem(self, name):
        s = self.nc.alloc_semaphore(name=f"{self.name}_{name}")
        self.sems.append(s)
        return s

    def weights(self, blob, offsets):
        self.blob = blob
        self.w_sb = self.sb("w", [P, blob.shape[1]])
        return {k: self.w_sb[:, a:b] for k, (a, b) in offsets.items()}


def load_constants(core, ident_dram, x_dram):
    nc = core.nc
    with Stage(core, "init") as st:
        loaded = st.sem("loaded")
        with nc.Block() as block:
            @block.sync
            def _(sp):
                sp.dma_start(core.x_res[:, :, :], x_dram.rearrange("(t p) d -> p t d", p=P)).then_inc(loaded, 16)
                sp.dma_start(core.ident[:, :], ident_dram).then_inc(loaded, 16)
                sp.wait_ge(loaded, 32)

            @block.gpsimd
            def _(pool):
                nc.gpsimd.memset(core.ones[:, :], 1.0)


def store_output(core, out_dram):
    nc = core.nc
    with Stage(core, "store") as st:
        stored = st.sem("stored")
        with nc.Block() as block:
            @block.sync
            def _(sp):
                sp.dma_start(out_dram.rearrange("(t p) d -> p t d", p=P), core.x_res[:, :, :]).then_inc(stored, 16)
                sp.wait_ge(stored, 16)


def layer_norm(core, weights_stage=None):
    nc = core.nc
    GROUPS = TILES // 4
    PARTS = 2
    IN_PART = GROUPS // PARTS
    with Stage(core, "ln") as st:
        sq = st.sb("sq", [P, TILES, D])
        mean = st.sb("mean", [P, TILES])
        var = st.sb("var", [P, TILES])
        rstd = core.rstd
        staged = st.sb("staged", [P, 2, 4, D])
        pT = [st.ps(f"pT{i}", [P, BANK]) for i in range(2)]
        names = ("w_loaded", "summed", "mean_ready", "first_centred", "second_centred", "squared", "squares_summed", "var_ready", "std_ready", "rstd_ready", "norm_ready", "turned", "xnT_ready")
        (w_loaded, summed, mean_ready, first_centred, second_centred, squared, squares_summed, var_ready, std_ready, rstd_ready, norm_ready, turned, xnT_ready) = (st.sem(n) for n in names)
        tiles = lambda part: slice(part * TILES // PARTS, (part + 1) * TILES // PARTS)
        with nc.Block() as block:
            if weights_stage is not None:
                @block.sync
                def _(sp):
                    sp.dma_start(weights_stage.w_sb[:, :], weights_stage.blob).then_inc(w_loaded, 16)
                    sp.wait_ge(w_loaded, 16)

            @block.vector
            def _(v):
                def mean_of(part):
                    ts = tiles(part)
                    nc.vector.tensor_reduce(mean[:, ts], core.x_res[:, ts, :], AX.X, ALU.add).then_inc(summed, 1)
                    v.wait_ge(summed, part + 1)
                    nc.vector.tensor_scalar(mean[:, ts], mean[:, ts], 1.0 / D, None, ALU.mult).then_inc(mean_ready, 1)

                def centre_first():
                    ts = tiles(0)
                    v.wait_ge(mean_ready, 1)
                    nc.vector.tensor_tensor(core.xn[:, ts, :], core.x_res[:, ts, :], bc(mean[:, ts], 2, D), ALU.subtract).then_inc(first_centred, 1)

                def variance(part):
                    ts = tiles(part)
                    v.wait_ge(squared, part + 1)
                    nc.vector.tensor_reduce(var[:, ts], sq[:, ts, :], AX.X, ALU.add).then_inc(squares_summed, 1)
                    v.wait_ge(squares_summed, part + 1)
                    nc.vector.tensor_scalar(var[:, ts], var[:, ts], 1.0 / D, LN_EPS, ALU.mult, ALU.add).then_inc(var_ready, 1)

                def normalise(part):
                    ts = tiles(part)
                    v.wait_ge(std_ready, part + 1)
                    nc.vector.reciprocal(rstd[:, ts], rstd[:, ts]).then_inc(rstd_ready, 1)
                    v.wait_ge(rstd_ready, part + 1)
                    with v.Fori(part * IN_PART // 2, (part + 1) * IN_PART // 2) as g:
                        for i in range(2):
                            four = bass.ds(g * 8 + 4 * i, 4)
                            v.wait_ge(turned, 2 * g + i + 1)
                            nc.vector.tensor_tensor(staged[:, i, :, :], core.xn[:, four, :], bc(rstd[:, four], 2, D),
                                                    ALU.mult).then_inc(norm_ready, 1)

                v.sem_inc(turned, 2)
                mean_of(0)
                centre_first()
                mean_of(1)
                variance(0)
                normalise(0)
                variance(1)
                normalise(1)

            @block.gpsimd
            def _(pool):
                ts = tiles(1)
                pool.wait_ge(mean_ready, 2)
                nc.gpsimd.tensor_tensor(core.xn[:, ts, :], core.x_res[:, ts, :], bc(mean[:, ts], 2, D), ALU.subtract).then_inc(second_centred, 1)

            @block.scalar
            def _(a):
                def square(part):
                    ts = tiles(part)
                    a.wait_ge((first_centred, second_centred)[part], 1)
                    nc.scalar.activation(sq[:, ts, :], core.xn[:, ts, :], ACT.Square).then_inc(squared, 1)

                def root(part):
                    ts = tiles(part)
                    a.wait_ge(var_ready, part + 1)
                    nc.scalar.activation(rstd[:, ts], var[:, ts], ACT.Sqrt).then_inc(std_ready, 1)

                def take(part):
                    with a.Fori(part * IN_PART // 2, (part + 1) * IN_PART // 2) as g:
                        for i in range(2):
                            a.wait_ge(turned, 2 * g + i + 3)
                            nc.scalar.copy(core.xnT[:, bass.ds(g * 2 * BANK + i * BANK, BANK)], pT[i][:, :]).then_inc(xnT_ready, 1)

                square(0)
                root(0)
                square(1)
                take(0)
                root(1)
                take(1)

            @block.tensor
            def _(pe):
                pe.sem_inc(xnT_ready, 2)
                with pe.Fori(0, GROUPS // 2) as g:
                    for i in range(2):
                        pe.wait_ge(norm_ready, 2 * g + i + 1)
                        pe.wait_ge(xnT_ready, 2 * g + i + 1)
                        for k in range(4):
                            ins = nc.tensor.transpose(pT[i][:, k * P:(k + 1) * P],
                                                      staged[:, i, k, :], core.ident[:, :])
                        ins.then_inc(turned, 1)


ROPE_BASE = 10000.0
ATTN_A_HD = D // HEADS
LOW = 64
PER = 32 // ATTN_A_HD
QUADS = HEADS // PER
LEAD = 3


def pack(parts):
    offsets, cols, at = {}, [], 0
    for name, a in parts:
        a = np.asarray(a)
        if a.ndim == 1:
            a = a[:, None]
        full = np.zeros((P, a.shape[1]), a.dtype)
        full[:a.shape[0]] = a
        cols.append(full)
        offsets[name] = (at, at + a.shape[1])
        at += a.shape[1]
    return np.concatenate(cols, axis=1), offsets


def rope_tables():
    ids = np.arange(D // 2, dtype=np.float32)
    theta = (np.float32(ROPE_BASE) ** (np.float32(-2.0) * ids) / np.float32(D // 2)).astype(np.float32)
    r = np.arange(SEQ, dtype=np.float32)[:, None] * theta[None, :]
    cos = np.repeat(np.cos(r), 2, axis=1).T
    sin = np.repeat(np.sin(r), 2, axis=1).T.copy()
    sin[0::2] *= -1
    return cos.astype(np.float32), sin.astype(np.float32)


def attn_a_weights(w):
    swap = np.arange(D) ^ 1
    cos, sin = rope_tables()
    low = lambda a: np.concatenate([np.zeros((LOW, a.shape[1]), a.dtype), a], axis=0)
    scale = np.float32(1.0 / np.sqrt(HEADS + LOW + LOW))
    head_of = np.arange(P) // ATTN_A_HD
    quad_in_32 = np.arange(32) // ATTN_A_HD
    own = (quad_in_32[None, :] == np.arange(QUADS)[:, None]).astype(np.float32)
    wo = w["Wo_w"].reshape(QUADS, PER, ATTN_A_HD, D).transpose(1, 0, 2, 3).reshape(D, D)
    return pack([
        ("down", np.concatenate([w["Wd_q_w"], w["Wd_kv_w"]], axis=1)),
        ("down_b", np.concatenate([w["Wd_q_b"], w["Wd_kv_b"]])),
        ("uq", w["Wu_q_w"]), ("qr", w["Wq_r_w"]), ("qr_swap", w["Wq_r_w"][:, swap]),
        ("uk", low(w["Wu_k_w"])), ("uv", low(w["Wu_v_w"])),
        ("kr", w["Wk_r_w"]), ("kr_swap", w["Wk_r_w"][:, swap]),
        ("uq_b", w["Wu_q_b"]), ("qr_b", w["Wq_r_b"]), ("qr_swap_b", w["Wq_r_b"][swap]),
        ("uk_b", w["Wu_k_b"]), ("kr_b", w["Wk_r_b"]), ("kr_swap_b", w["Wk_r_b"][swap]),
        ("uv_b", np.broadcast_to(w["Wu_v_b"], (P, D))),
        ("wo", wo), ("wo_b", w["Wo_b"][None, :]),
        ("cos_q", cos * scale), ("sin_q", sin * scale), ("cos_k", cos), ("sin_k", sin),
        ("head_mask", (head_of[:, None] == np.arange(HEADS)[None, :]).astype(np.float32)),
        ("own", np.broadcast_to(own.reshape(1, -1), (P, QUADS * 32))),
    ])


def attn_a(core, blob, offsets):
    nc = core.nc
    scale = float(np.float32(1.0 / np.sqrt(HEADS + LOW + LOW)))
    with Stage(core, "attn_a") as st:
        w = st.weights(blob, offsets)
        layer_norm(core, st)
        qT = st.sb("qT", [P, TOK])
        kT = st.sb("kT", [P, TOK])
        val = st.sb("val", [P, TILES, D])
        bank = [st.ps(f"bank{i}", [P, BANK]) for i in range(8)]

        ct = st.sb("ct", [P, BANK])
        plain = st.sb("plain", [P, BANK])
        rot = [st.sb(f"rot{i}", [P, BANK]) for i in range(4)]
        down_ready, ct_ready = st.sem("down_ready"), st.sem("ct_ready")
        q_ready, k_ready, v_ready = st.sem("q_ready"), st.sem("k_ready"), st.sem("v_ready")
        plain_ready, plain_used = st.sem("plain_ready"), st.sem("plain_used")
        group_done, dve1 = st.sem("group_done"), st.sem("dve1")
        pd, pq, pqr, pqs, pk, pkr, pks, pv = bank
        GROUPS = TOK // BANK
        with nc.Block() as block:
            @block.tensor
            def _(pe):
                pe.sem_inc(v_ready, 1)
                with pe.Fori(0, GROUPS) as g:
                    x = core.xnT[:, bass.ds(g * BANK, BANK)]
                    nc.tensor.matmul(pd[:, :], w["down"], x, start=True, stop=True).then_inc(down_ready, 1)
                    pe.wait_ge(group_done, g + 1)
                    nc.tensor.matmul(pkr[:, :], w["kr"], x, start=True, stop=True)
                    nc.tensor.matmul(pks[:, :], w["kr_swap"], x, start=True, stop=True)
                    pe.wait_ge(ct_ready, g + 1)
                    nc.tensor.matmul(pq[:, :], w["uq"][0:LOW, :], ct[0:LOW, :], start=True, stop=True)
                    nc.tensor.matmul(pqr[:, :], w["qr"][0:LOW, :], ct[0:LOW, :], start=True, stop=True)
                    nc.tensor.matmul(pqs[:, :], w["qr_swap"][0:LOW, :], ct[0:LOW, :], start=True, stop=True).then_inc(q_ready, 1)
                    nc.tensor.matmul(pk[:, :], w["uk"][LOW:P, :], ct[LOW:P, :], start=True, stop=True).then_inc(k_ready, 1)
                    for t in range(4):
                        ins = nc.tensor.matmul(pv[:, t * P:(t + 1) * P], ct[LOW:P, t * P:(t + 1) * P], w["uv"][LOW:P, :],
                                               start=True, stop=True)
                    ins.then_inc(v_ready, 1)

            @block.scalar
            def _(a):
                with a.Fori(0, GROUPS) as g:
                    a.wait_ge(down_ready, g + 1)
                    a.wait_ge(v_ready, g + 1)
                    nc.scalar.activation(ct[:, :], pd[:, :], ACT.Identity, bias=w["down_b"]).then_inc(ct_ready, 1)
                    a.wait_ge(q_ready, g + 1)
                    a.wait_ge(plain_used, 2 * g + 1)
                    nc.scalar.activation(plain[:, :], pq[:, :], ACT.Identity, bias=w["uq_b"]).then_inc(plain_ready, 1)
                    a.wait_ge(k_ready, g + 1)
                    a.wait_ge(plain_used, 2 * g + 2)
                    nc.scalar.activation(plain[:, :], pk[:, :], ACT.Identity, bias=w["uk_b"]).then_inc(plain_ready, 1)

            @block.vector
            def _(v):
                v.sem_inc(group_done, 1)
                v.sem_inc(plain_used, 1)
                with v.Fori(0, GROUPS) as g:
                    c = Chain(v, dve1, 4 * g)
                    cols = bass.ds(g * BANK, BANK)
                    two = lambda t: t.rearrange("p (b s) -> p b s", b=2)
                    for i, (side, out, direct, swapped, s) in enumerate((("q", qT, pqr, pqs, scale), ("k", kT, pkr, pks, 1.0))):
                        v.wait_ge((q_ready, k_ready)[i], g + 1)
                        rot_a, rot_b = rot[2 * i], rot[2 * i + 1]
                        nc.vector.scalar_tensor_tensor(two(rot_a[:, :]), two(direct[:, :]), w[f"{side}r_b"],
                                                       bc(w[f"cos_{side}"], 1, 2), ALU.add, ALU.mult)
                        c.link(nc.vector.scalar_tensor_tensor(two(rot_b[:, :]), two(swapped[:, :]), w[f"{side}r_swap_b"],
                                                              bc(w[f"sin_{side}"], 1, 2), ALU.add, ALU.mult))
                        c.link(nc.vector.tensor_tensor(rot_a[:, :], rot_a[:, :], rot_b[:, :], ALU.add))
                        v.wait_ge(plain_ready, 2 * g + i + 1)
                        nc.vector.scalar_tensor_tensor(out[:, cols], plain[:, :], s, rot_a[:, :],
                                                       ALU.mult, ALU.add).then_inc(plain_used, 1)
                    v.wait_ge(v_ready, g + 2)
                    nc.vector.tensor_tensor(val[:, bass.ds(g * 4, 4), :], pv[:, :].rearrange("p (t d) -> p t d", t=4),
                                            bc(w["uv_b"], 1, 4), ALU.add).then_inc(group_done, 1)

        q_heads = st.sb("q_heads", [P, 2, HEADS, SEQ])
        k_now = st.sb("k_now", [P, 2, SEQ])
        v_heads = st.sb("v_heads", [P, 2, 2, QUADS, PER, QUADS, ATTN_A_HD])
        prob = st.sb("prob", [P, 4, 2, SEQ])
        probT = st.sb("probT", [P, 2 * PER, 2, SEQ])
        neg_max = st.sb("neg_max", [P, 4, 2])
        row_sum = st.sb("row_sum", [P, 2, 2, HEADS])
        inv_sum = st.sb("inv_sum", [P, 2, HEADS])
        inv_wide = st.sb("inv_wide", [P, 2, PER, QUADS, ATTN_A_HD])
        inv_T = st.sb("inv_T", [P, SEQ])
        outT = st.sb("outT", [P, SEQ])
        pS, pT, pO, pInv, pY = bank[0:4], bank[4:6], bank[6], bank[7][:, 0:SEQ], bank[7][:, SEQ:2 * SEQ]
        names = ("q_heads_ready", "v_heads_ready", "scores_ready", "max_ready", "prob_ready", "probT_psum", "probT_ready", "quad_done",
                 "sums_inverted", "inv_wide_ready", "inv_psum", "inv_T_ready", "outT_ready", "y_ready", "y_added")
        (q_heads_ready, v_heads_ready, scores_ready, max_ready, prob_ready, probT_psum, probT_ready, quad_done,
         sums_inverted, inv_wide_ready, inv_psum, inv_T_ready, outT_ready, y_ready, y_added) = (st.sem(n) for n in names)

        with nc.Block() as block:
            @block.gpsimd
            def _(pool):
                def prepare(b, s, first, last):
                    if not known(b, 2):
                        pool.wait_ge(scores_ready, (b - 1) * HEADS)
                    nc.gpsimd.tensor_copy(k_now[:, s, :], kT[:, bass.ds(b * SEQ, SEQ)]).then_inc(q_heads_ready, 1)
                    nc.gpsimd.tensor_tensor(q_heads[:, s, :, :], bc(qT[:, bass.ds(b * SEQ, SEQ)], 1, HEADS),
                                            bc(w["head_mask"], 2, SEQ), ALU.mult).then_inc(q_heads_ready, 1)
                    if not known(b, 2):
                        pool.wait_ge(quad_done, (b - 1) * QUADS)
                    for kt in range(2):
                        for quad in range(QUADS):
                            v = val[:, bass.ds(b * 2 + kt, 1), quad * 32:(quad + 1) * 32].squeeze(1).rearrange("p (j d) -> p j d", j=PER)
                            nc.gpsimd.tensor_tensor(v_heads[:, s, kt, quad, :, :, :], bc(v, 2, QUADS),
                                                    bc(w["own"][:, quad * 32:(quad + 1) * 32].rearrange("p (i d) -> p i d", i=QUADS), 1, PER),
                                                    ALU.mult).then_inc(v_heads_ready, 1)

                sequences(pool, prepare)

            @block.tensor
            def _(pe):
                def scores(b, s, h):
                    if h == 0:
                        pe.wait_ge(q_heads_ready, 2 * b + 2)
                    for qt in range(2):
                        ins = nc.tensor.matmul(pS[h % 4][:, qt * SEQ:(qt + 1) * SEQ], q_heads[:, s, h, qt * P:(qt + 1) * P],
                                               k_now[:, s, :], start=True, stop=True)
                    ins.then_inc(scores_ready, 1)

                def turn(b, h):
                    pe.wait_ge(prob_ready, b * HEADS + h + 1)
                    if not (known(b, 1) and h < 2):
                        pe.wait_ge(probT_ready, b * HEADS + h - 1)
                    for kt in range(2):
                        for qt in range(2):
                            ins = nc.tensor.transpose(pT[h % 2][:, kt * SEQ + qt * P:kt * SEQ + (qt + 1) * P],
                                                      prob[:, h % 4, qt, kt * P:(kt + 1) * P], core.ident[:, :])
                    ins.then_inc(probT_psum, 1)

                def weighted(b, s, quad):
                    if quad == 0:
                        pe.wait_ge(v_heads_ready, 2 * QUADS * (b + 1))
                        if not known(b, 1):
                            pe.wait_ge(outT_ready, b)
                    pe.wait_ge(probT_ready, b * HEADS + (quad + 1) * PER)
                    for kt in range(2):
                        for j in range(PER):
                            ins = nc.tensor.matmul(pO[32 * j:32 * (j + 1), 0:SEQ], v_heads[:, s, kt, quad, j, :, :].rearrange("p i d -> p (i d)"),
                                                   probT[:, (quad * PER + j) % (2 * PER), kt, :], start=(quad == 0 and kt == 0),
                                                   stop=(quad == QUADS - 1 and kt == 1), tile_position=(0, 32 * j))
                    ins.then_inc(quad_done, 1)

                def turn_inverses(b):
                    pe.wait_ge(inv_wide_ready, b + 1)
                    for qt in range(2):
                        ins = nc.tensor.transpose(pInv[:, qt * P:(qt + 1) * P], inv_wide[:, qt, :, :, :].rearrange("p j i d -> p (j i d)"), core.ident[:, :])
                    ins.then_inc(inv_psum, 1)

                def project(b):
                    pe.wait_ge(outT_ready, b + 1)
                    for qt in range(2):
                        y = pY[:, qt * P:(qt + 1) * P]
                        nc.tensor.matmul(y, core.ones[0:1, :], w["wo_b"][0:1, :], start=True, stop=False)
                        ins = nc.tensor.matmul(y, outT[:, qt * P:(qt + 1) * P], w["wo"], start=False, stop=True)
                    ins.then_inc(y_ready, 1)

                def step(b, s, first, last):
                    if first:
                        for h in range(LEAD):
                            scores(b, s, h)
                    for h in range(HEADS):
                        turn(b, h)
                        if h + LEAD < HEADS:
                            scores(b, s, h + LEAD)
                        elif not last:
                            scores(b + 1, 1 - s, h + LEAD - HEADS)
                        if h == 1 and not first:
                            weighted(b - 1, 1 - s, QUADS - 1)
                            turn_inverses(b - 1)
                        if h % PER == 1 and h > PER:
                            weighted(b, s, h // PER - 1)
                        if h == 6 and not first:
                            project(b - 1)
                    if last:
                        weighted(b, s, QUADS - 1)
                        turn_inverses(b)
                        project(b)

                sequences(pe, step)

            @block.scalar
            def _(a):
                def invT(b):
                    a.wait_ge(inv_psum, b + 1)
                    nc.scalar.copy(inv_T[:, :], pInv).then_inc(inv_T_ready, 1)

                def step(b, s, first, last):
                    for h in range(HEADS):
                        if h == 5 and not first:
                            invT(b - 1)
                        a.wait_ge(max_ready, b * HEADS + h + 1)
                        for qt in range(2):
                            ins = nc.scalar.activation(prob[:, h % 4, qt, :], pS[h % 4][:, qt * SEQ:(qt + 1) * SEQ], ACT.Exp,
                                                       bias=neg_max[:, h % 4, qt:qt + 1], accum_out=row_sum[:, s, qt, h:h + 1])
                        ins.then_inc(prob_ready, 1)
                    if last:
                        invT(b)

                sequences(a, step)

            @block.vector
            def _(v):
                def row_max(b, h):
                    v.wait_ge(scores_ready, b * HEADS + h + 1)
                    nc.vector.tensor_reduce(neg_max[:, h % 4, :], pS[h % 4][:, :].rearrange("p (q k) -> p q k", q=2),
                                            AX.X, ALU.max, negate=True).then_inc(max_ready, 1)

                def copy(b, h):
                    v.wait_ge(probT_psum, b * HEADS + h + 1)
                    if h % PER == 0 and not (known(b, 1) and h < 2 * PER):
                        v.wait_ge(quad_done, b * QUADS + h // PER - 1)
                    nc.vector.tensor_copy(probT[:, h % (2 * PER), :, :], pT[h % 2][:, :].rearrange("p (k q) -> p k q", k=2)).then_inc(probT_ready, 1)

                def invert(b, s):
                    v.wait_ge(prob_ready, (b + 1) * HEADS)
                    nc.vector.reciprocal(inv_sum[:, :, :], row_sum[:, s, :, :]).then_inc(sums_inverted, 1)
                    v.wait_ge(sums_inverted, b + 1)
                    for qt in range(2):
                        ins = nc.vector.tensor_copy(inv_wide[:, qt, :, :, :], bc(inv_sum[:, qt, :].rearrange("p (i j) -> p j i", i=QUADS), 3, ATTN_A_HD))
                    ins.then_inc(inv_wide_ready, 1)

                def normalise(b):
                    v.wait_ge(quad_done, (b + 1) * QUADS)
                    v.wait_ge(inv_T_ready, b + 1)
                    nc.vector.tensor_tensor(outT[:, :], pO[:, 0:SEQ], inv_T[:, :], ALU.mult).then_inc(outT_ready, 1)

                def add(b):
                    v.wait_ge(y_ready, b + 1)
                    x = core.x_res[:, bass.ds(b * 2, 2), :]
                    nc.vector.tensor_tensor(x, x, pY.rearrange("p (q d) -> p q d", q=2), ALU.add).then_inc(y_added, 1)

                def step(b, s, first, last):
                    if first:
                        for h in range(LEAD):
                            row_max(b, h)
                    for h in range(HEADS):
                        copy(b, h)
                        if h + LEAD < HEADS:
                            row_max(b, h + LEAD)
                        elif not last:
                            row_max(b + 1, h + LEAD - HEADS)
                        if not first:
                            if h == 0:
                                invert(b - 1, 1 - s)
                            if h == 3:
                                normalise(b - 1)
                            if h == 8:
                                add(b - 1)
                    if last:
                        invert(b, s)
                        normalise(b)
                        add(b)

                sequences(v, step)


def earlier_table(n):
    return np.broadcast_to(np.tril(np.ones((n, n), np.float32), -1).reshape(1, n * n), (P, n * n))


def link_ranks(nc, c, rank, val, above, same, earlier, n):
    vj, vi = bc(val, 2, n), bc(val, 3, n)
    nc.vector.tensor_tensor(above, vj, vi, ALU.is_gt)
    c.link(nc.vector.tensor_tensor(same, vj, vi, ALU.is_equal))
    c.link(nc.vector.tensor_tensor(same, same, bc(earlier.rearrange("p (i j) -> p i j", i=n), 1, val.shape[1]), ALU.mult))
    c.link(nc.vector.tensor_tensor(above, above, same, ALU.add))
    c.link(nc.vector.tensor_reduce(rank, above, AX.X, ALU.add))


def router_logits(core, router, out_bank, experts, st):
    nc = core.nc
    x_now = st.sb("router_x", [P, 2, BANK])
    copied, used = st.sem("router_copied"), st.sem("router_used")
    GROUPS = TOK // BANK
    with nc.Block() as block:
        @block.gpsimd
        def _(pool):
            pool.sem_inc(used, 2)
            with pool.Fori(0, GROUPS // 2) as g:
                for s in range(2):
                    pool.wait_ge(used, 2 * g + s + 1)
                    nc.gpsimd.tensor_copy(x_now[:, s, :], core.xnT[:, bass.ds((2 * g + s) * BANK, BANK)]).then_inc(copied, 1)

        @block.tensor
        def _(pe):
            with pe.Fori(0, GROUPS // 2) as g:
                for s in range(2):
                    pe.wait_ge(copied, 2 * g + s + 1)
                    for t in range(4):
                        ins = nc.tensor.matmul(out_bank(g * 8 + s * 4 + t), x_now[:, s, t * P:(t + 1) * P], router, start=True, stop=True)
                    ins.then_inc(used, 1)


CYCLES = 3
QUARTER = D // 4


def ffn0_weights(w):
    twist = np.zeros((D, D), np.float32)
    for to, (frm, sign) in enumerate(((2, 1.0), (3, -1.0), (0, -1.0), (1, 1.0))):
        for k in range(QUARTER):
            twist[frm * QUARTER + k, to * QUARTER + k] = sign
    wide = lambda a: np.broadcast_to(a.reshape(-1, 1), (a.size, P))
    tall = lambda a: np.broadcast_to(a.reshape(1, 1), (P, 1))
    full = lambda a: np.concatenate([a, np.zeros((a.shape[0], P - a.shape[1]), a.dtype)], axis=1)
    return pack([
        ("cn1", w["cn_w1"]), ("cn2", full(w["cn_w2"])), ("cn3", full(w["cn_w3"])), ("cn4", wide(w["cn_w4"])),
        ("cn1_b", w["cn_b1"]), ("cn2_b", w["cn_b2"]), ("cn3_b", w["cn_b3"]), ("cn4_b", tall(w["cn_b4"])),
        ("gc1", full(w["gc_w1"])), ("gc2", full(w["gc_w2"])), ("gc3", wide(w["gc_w3"])),
        ("gc1_b", w["gc_b1"]), ("gc2_b", w["gc_b2"]), ("gc3_b", tall(w["gc_b3"])),
        ("range", tall(w["adaptive_range"])), ("twist", twist),
    ])


def ffn0(core, blob, offsets):
    nc = core.nc
    base, share_gf, share_tf = 0.1, 0.7, 0.3
    with Stage(core, "ffn0") as st:
        w = st.weights(blob, offsets)
        layer_norm(core, st)
        bank = [st.ps(f"bank{i}", [P, BANK]) for i in range(8)]
        mean = st.sb("mean", [P, BATCH])
        g1, g2 = st.sb("g1", [P, BATCH]), st.sb("g2", [P, BATCH])
        gf = st.sb("gf", [P, BATCH])
        offset = st.sb("offset", [P, BATCH])
        half_b = st.sb("half_b", [P, 2])
        slope = st.sb("slope", [P, 1])
        dve, glob, glob_act, h_ready = st.sem("dve"), st.sem("glob"), st.sem("glob_act"), st.sem("h_ready")
        with nc.Block() as block:
            @block.vector
            def _(v):
                c = Chain(v, dve)
                c.link(nc.vector.tensor_reduce(mean[:, :], core.xnT[:, :].rearrange("p (b s) -> p b s", s=SEQ), AX.X, ALU.add))
                nc.vector.tensor_scalar(half_b[:, 0:1], w["gc3_b"], 0.5, None, ALU.mult)
                nc.vector.tensor_scalar(half_b[:, 1:2], w["cn4_b"], 0.5, None, ALU.mult)
                nc.vector.tensor_scalar(slope[:, :], w["range"], share_tf, None, ALU.mult)
                c.link(nc.vector.tensor_scalar(mean[:, :], mean[:, :], 1.0 / SEQ, None, ALU.mult))
                v.wait_ge(glob_act, 3)
                c.link(nc.vector.tensor_scalar(gf[:, :], gf[:, :], share_gf, share_gf + share_tf - 1.0, ALU.mult, ALU.add))
                c.link(nc.vector.tensor_scalar(offset[:, :], gf[:, :], w["range"], base, ALU.mult, ALU.add))

            @block.tensor
            def _(pe):
                pe.wait_ge(dve, 2)
                nc.tensor.matmul(bank[0][:, 0:BATCH], w["gc1"], mean[:, :], start=True, stop=True).then_inc(glob, 1)
                pe.wait_ge(glob_act, 1)
                nc.tensor.matmul(bank[1][:, 0:BATCH], w["gc2"], g1[:, :], start=True, stop=True).then_inc(glob, 1)
                pe.wait_ge(glob_act, 2)
                nc.tensor.matmul(bank[2][:, 0:BATCH], w["gc3"], g2[:, :], start=True, stop=True).then_inc(glob, 1)

            @block.scalar
            def _(a):
                a.wait_ge(glob, 1)
                nc.scalar.activation(g1[:, :], bank[0][:, 0:BATCH], ACT.Gelu, bias=w["gc1_b"]).then_inc(glob_act, 1)
                a.wait_ge(glob, 2)
                nc.scalar.activation(g2[:, :], bank[1][:, 0:BATCH], ACT.Gelu, bias=w["gc2_b"]).then_inc(glob_act, 1)
                a.wait_ge(glob, 3)
                nc.scalar.activation(gf[:, :], bank[2][:, 0:BATCH], ACT.Tanh, bias=half_b[:, 0:1], scale=0.5).then_inc(glob_act, 1)

        SLOTS = 4
        cur = st.sb("cur", [P, SLOTS, 2, SEQ])
        h1, h2, h3 = (st.sb(f"h{i}", [P, SLOTS, SEQ]) for i in (1, 2, 3))
        tf = st.sb("tf", [P, SLOTS, SEQ])
        names = ("psum_ready", "hidden_ready", "twisted", "coupled", "times_twist", "cycled", "turned", "added", "copied")
        psum_ready, hidden_ready, twisted, coupled, times_twist, cycled, turned, added, copied = ([st.sem(f"{n}{s}") for s in range(SLOTS)] for n in names)
        LAYERS = 4
        T = SEQ // P
        p_layer = lambda s, layer: bank[2 * s][:, layer % 2 * SEQ:(layer % 2 + 1) * SEQ]
        p_twist = lambda s: bank[2 * s + 1][:, 0:SEQ]
        p_out = lambda s: bank[2 * s + 1][:, SEQ:2 * SEQ]
        with nc.Block() as block:
            @block.tensor
            def _(pe):
                with pe.Fori(0, BATCH // SLOTS) as g:
                    for cyc in range(CYCLES):
                        for layer, name in enumerate(("cn1", "cn2", "cn3", "cn4")):
                            for s in range(SLOTS):
                                if layer == 0:
                                    if cyc == 0:
                                        pe.wait_ge(copied[s], g + 1)
                                        pe.wait_ge(added[s], g + 1)
                                    else:
                                        pe.wait_ge(cycled[s], g * CYCLES + cyc)
                                    rhs = cur[:, s, cyc % 2, :]
                                    nc.tensor.matmul(p_twist(s), w["twist"], rhs, start=True, stop=True).then_inc(twisted[s], 1)
                                else:
                                    pe.wait_ge(hidden_ready[s], (g * CYCLES + cyc) * LAYERS + layer)
                                    rhs = (h1, h2, h3)[layer - 1][:, s, :]
                                nc.tensor.matmul(p_layer(s, layer), w[name], rhs, start=True, stop=True).then_inc(psum_ready[s], 1)
                    for s in range(SLOTS):
                        pe.wait_ge(cycled[s], (g + 1) * CYCLES)
                        for t in range(T):
                            ins = nc.tensor.transpose(p_out(s)[:, t * P:(t + 1) * P], cur[:, s, CYCLES % 2, t * P:(t + 1) * P], core.ident[:, :])
                        ins.then_inc(turned[s], 1)

            @block.scalar
            def _(a):
                with a.Fori(0, BATCH // SLOTS) as g:
                    for cyc in range(CYCLES):
                        for layer, name in enumerate(("cn1", "cn2", "cn3", "cn4")):
                            for s in range(SLOTS):
                                a.wait_ge(psum_ready[s], (g * CYCLES + cyc) * LAYERS + layer + 1)
                                if layer < 3:
                                    nc.scalar.activation((h1, h2, h3)[layer][:, s, :], p_layer(s, layer), ACT.Gelu,
                                                         bias=w[f"{name}_b"]).then_inc(hidden_ready[s], 1)
                                else:
                                    nc.scalar.activation(tf[:, s, :], p_layer(s, layer), ACT.Tanh, bias=half_b[:, 1:2],
                                                         scale=0.5).then_inc(hidden_ready[s], 1)

            @block.vector
            def _(v):
                for s in range(SLOTS):
                    v.sem_inc(added[s], 1)
                with v.Fori(0, BATCH // SLOTS) as g:
                    for s in range(SLOTS):
                        nc.vector.tensor_copy(cur[:, s, 0, :], core.xnT[:, bass.ds((SLOTS * g + s) * SEQ, SEQ)]).then_inc(copied[s], 1)
                    for cyc in range(CYCLES):
                        n = g * CYCLES + cyc
                        for s in range(SLOTS):
                            v.wait_ge(hidden_ready[s], (n + 1) * LAYERS)
                            nc.vector.tensor_scalar(tf[:, s, :], tf[:, s, :], slope[:, :], offset[:, bass.ds(SLOTS * g + s, 1)], ALU.mult,
                                                    ALU.add).then_inc(coupled[s], 1)
                            v.wait_ge(coupled[s], n + 1)
                            v.wait_ge(twisted[s], n + 1)
                            nc.vector.tensor_tensor(tf[:, s, :], tf[:, s, :], p_twist(s), ALU.mult).then_inc(times_twist[s], 1)
                            v.wait_ge(times_twist[s], n + 1)
                            nc.vector.tensor_tensor(cur[:, s, 1 - cyc % 2, :], cur[:, s, cyc % 2, :], tf[:, s, :], ALU.add).then_inc(cycled[s], 1)
                    for s in range(SLOTS):
                        v.wait_ge(turned[s], g + 1)
                        x = core.x_res[:, bass.ds((SLOTS * g + s) * T, T), :]
                        nc.vector.tensor_tensor(x, x, p_out(s).rearrange("p (t d) -> p t d", t=T), ALU.add).then_inc(added[s], 1)


ATTN_B0_HD = D // HEADS


def attn_b0_weights(w):
    head = np.arange(D) // ATTN_B0_HD
    return pack([
        ("wq", w["Wqkv"][:, 0:D]), ("wk", w["Wqkv"][:, D:2 * D]), ("wv", w["Wqkv"][:, 2 * D:3 * D]),
        ("wg", w["Wg"]), ("bg", w["bg"]), ("wp", w["Wp"]), ("bp", w["bp"][None, :]),
        ("same_head", (head[:, None] == head[None, :]).astype(np.float32)),
        ("of_head", (head[:, None] == np.arange(HEADS)[None, :]).astype(np.float32)),
    ])


def attn_b0(core, blob, offsets):
    nc = core.nc
    KV = D + 1
    OUT = D + HEADS
    with Stage(core, "attn_b0") as st:
        w = st.weights(blob, offsets)
        layer_norm(core, st)
        bank = [st.ps(f"bank{i}", [P, BANK]) for i in range(8)]
        T = SEQ // P
        half_bg = st.sb("half_bg", [P, 1])
        x_now = st.sb("x_now", [P, 2, SEQ])
        gate = st.sb("gate", [P, 2, SEQ])
        z = st.sb("z", [P, 2, 2, SEQ])
        neg_exp = st.sb("neg_exp", [P, 2, 2, SEQ])
        feat = st.sb("feat", [P, 2, 2, SEQ])
        k_tok = st.sb("k_tok", [P, 2, T, D])
        v_tok = st.sb("v_tok", [P, 2, T, KV])
        kv = st.sb("kv", [P, 2, OUT])
        inv = st.sb("inv", [P, 2, T, HEADS])
        o_tok = st.sb("o_tok", [P, 2, T, D])
        oT = st.sb("oT", [P, 2, SEQ])
        p_gate = lambda s: bank[4 * s][:, 0:SEQ]
        p_q = lambda s: bank[4 * s][:, SEQ:2 * SEQ]
        p_k = lambda s: bank[4 * s + 1][:, 0:SEQ]
        p_v = p_y = lambda s: bank[4 * s + 1][:, SEQ:2 * SEQ]
        p_kT = p_oT = lambda s: bank[4 * s + 2][:, 0:SEQ]
        p_kv = lambda s: bank[4 * s + 2][:, SEQ:SEQ + KV]
        p_o = lambda s: bank[4 * s + 3][:, 0:T * OUT].rearrange("p (t o) -> p t o", t=T)
        names = ("x_copied", "qkg_ready", "v_psum", "tanh_ready", "gate_ready", "z_ready", "min_ready", "exp_ready", "feat_ready", "v_ready", "k_psum",
                 "k_ready", "kv_psum", "kv_ready", "o_psum", "sums_ready", "inv_ready", "o_ready", "oT_psum", "oT_ready", "y_ready", "y_added")
        (x_copied, qkg_ready, v_psum, tanh_ready, gate_ready, z_ready, min_ready, exp_ready, feat_ready, v_ready, k_psum,
         k_ready, kv_psum, kv_ready, o_psum, sums_ready, inv_ready, o_ready, oT_psum, oT_ready, y_ready, y_added) = ([st.sem(f"{n}{s}") for s in range(2)] for n in names)
        set_up = st.sem("set_up")
        by_tile = lambda ap: ap.rearrange("p (t d) -> p t d", t=T)
        by_head = lambda ap: ap.rearrange("p t (h d) -> p t h d", h=HEADS)
        with nc.Block() as block:
            @block.gpsimd
            def _(pool):
                nc.gpsimd.memset(v_tok[:, :, :, D:KV], 1.0).then_inc(set_up, 1)

                def x_copy(n, s):
                    pool.wait_ge(v_psum[s], n + 1)
                    nc.gpsimd.tensor_copy(x_now[:, s, :], core.xnT[:, bass.ds((2 * n + s) * SEQ, SEQ)]).then_inc(x_copied[s], 1)

                in_pairs(pool, x_copy)

            @block.tensor
            def _(pe):
                for s in range(2):
                    pe.sem_inc(v_psum[s], 1)

                def project(n, s):
                    pe.wait_ge(x_copied[s], n + 1)
                    pe.wait_ge(y_added[s], n + 1)
                    nc.tensor.matmul(p_gate(s), w["wg"], x_now[:, s, :], start=True, stop=True)
                    nc.tensor.matmul(p_q(s), w["wq"], x_now[:, s, :], start=True, stop=True)
                    nc.tensor.matmul(p_k(s), w["wk"], x_now[:, s, :], start=True, stop=True)
                    for t in range(T):
                        ins = nc.tensor.matmul(p_v(s)[:, t * P:(t + 1) * P], x_now[:, s, t * P:(t + 1) * P], w["wv"], start=True, stop=True)
                    ins.then_inc(v_psum[s], 1)

                def turn_keys(n, s):
                    pe.wait_ge(feat_ready[s], n + 1)
                    for t in range(T):
                        ins = nc.tensor.transpose(p_kT(s)[:, t * P:(t + 1) * P], feat[:, s, 1, t * P:(t + 1) * P], core.ident[:, :])
                    ins.then_inc(k_psum[s], 1)

                def keys_values(n, s):
                    pe.wait_ge(k_ready[s], n + 1)
                    pe.wait_ge(v_ready[s], n + 1)
                    for t in range(T):
                        ins = nc.tensor.matmul(p_kv(s), k_tok[:, s, t, :], v_tok[:, s, t, :], start=(t == 0), stop=(t == T - 1))
                    ins.then_inc(kv_psum[s], 1)

                def query(n, s):
                    pe.wait_ge(kv_ready[s], n + 1)
                    for t in range(T):
                        ins = nc.tensor.matmul(p_o(s)[:, t, :], feat[:, s, 0, t * P:(t + 1) * P], kv[:, s, :], start=True, stop=True)
                    ins.then_inc(o_psum[s], 1)

                def turn_out(n, s):
                    pe.wait_ge(o_ready[s], n + 1)
                    for t in range(T):
                        ins = nc.tensor.transpose(p_oT(s)[:, t * P:(t + 1) * P], o_tok[:, s, t, :], core.ident[:, :])
                    ins.then_inc(oT_psum[s], 1)

                def put_out(n, s):
                    pe.wait_ge(oT_ready[s], n + 1)
                    for t in range(T):
                        y = p_y(s)[:, t * P:(t + 1) * P]
                        nc.tensor.matmul(y, core.ones[0:1, :], w["bp"][0:1, :], start=True, stop=False)
                        ins = nc.tensor.matmul(y, oT[:, s, t * P:(t + 1) * P], w["wp"], start=False, stop=True)
                    ins.then_inc(y_ready[s], 1)

                in_pairs(pe, project, turn_keys, keys_values, query, turn_out, put_out)

            @block.scalar
            def _(a):
                a.wait_ge(set_up, 2)

                def squash(n, s):
                    a.wait_ge(v_psum[s], n + 2)
                    nc.scalar.activation(gate[:, s, :], p_gate(s), ACT.Tanh, bias=half_bg[:, :], scale=0.5).then_inc(tanh_ready[s], 1)

                def exponential(n, s):
                    a.wait_ge(min_ready[s], n + 1)
                    nc.scalar.activation(neg_exp[:, s, :, :], neg_exp[:, s, :, :], ACT.Exp).then_inc(exp_ready[s], 1)

                def take_keys(n, s):
                    a.wait_ge(k_psum[s], n + 1)
                    nc.scalar.copy(k_tok[:, s, :, :], by_tile(p_kT(s))).then_inc(k_ready[s], 1)

                def take_out(n, s):
                    a.wait_ge(oT_psum[s], n + 1)
                    nc.scalar.copy(oT[:, s, :], p_oT(s)).then_inc(oT_ready[s], 1)

                in_pairs(a, squash, exponential, take_keys, take_out)

            @block.vector
            def _(v):
                for s in range(2):
                    v.sem_inc(y_added[s], 1)
                nc.vector.tensor_scalar(half_bg[:, :], w["bg"], 0.5, None, ALU.mult).then_inc(set_up, 1)

                def gated(n, s):
                    v.wait_ge(tanh_ready[s], n + 1)
                    nc.vector.tensor_scalar(gate[:, s, :], gate[:, s, :], 0.5, 0.5, ALU.mult, ALU.add).then_inc(gate_ready[s], 1)
                    v.wait_ge(gate_ready[s], n + 1)
                    nc.vector.tensor_tensor(z[:, s, 0, :], gate[:, s, :], p_q(s), ALU.mult)
                    nc.vector.tensor_tensor(z[:, s, 1, :], gate[:, s, :], p_k(s), ALU.mult).then_inc(z_ready[s], 1)
                    v.wait_ge(z_ready[s], n + 1)
                    nc.vector.tensor_scalar(neg_exp[:, s, :, :], z[:, s, :, :], 0.0, None, ALU.min).then_inc(min_ready[s], 1)
                    nc.vector.tensor_copy(v_tok[:, s, :, 0:D], by_tile(p_v(s))).then_inc(v_ready[s], 1)

                def features(n, s):
                    v.wait_ge(exp_ready[s], n + 1)
                    nc.vector.scalar_tensor_tensor(feat[:, s, :, :], z[:, s, :, :], 0.0, neg_exp[:, s, :, :], ALU.max,
                                                   ALU.add).then_inc(feat_ready[s], 1)

                def mask_heads(n, s):
                    v.wait_ge(kv_psum[s], n + 1)
                    nc.vector.tensor_tensor(kv[:, s, 0:D], p_kv(s)[:, 0:D], w["same_head"], ALU.mult)
                    nc.vector.tensor_tensor(kv[:, s, D:OUT], w["of_head"], p_kv(s)[:, D:KV].broadcast_to([P, HEADS]), ALU.mult).then_inc(kv_ready[s], 1)

                def normalise(n, s):
                    v.wait_ge(o_psum[s], n + 1)
                    nc.vector.tensor_scalar(inv[:, s, :, :], p_o(s)[:, :, D:OUT], 1e-8, None, ALU.add).then_inc(sums_ready[s], 1)
                    v.wait_ge(sums_ready[s], n + 1)
                    nc.vector.reciprocal(inv[:, s, :, :], inv[:, s, :, :]).then_inc(inv_ready[s], 1)
                    v.wait_ge(inv_ready[s], n + 1)
                    nc.vector.tensor_tensor(by_head(o_tok[:, s, :, :]), by_head(p_o(s)[:, :, 0:D]), bc(inv[:, s, :, :], 3, ATTN_B0_HD), ALU.mult).then_inc(o_ready[s], 1)

                def add(n, s):
                    v.wait_ge(y_ready[s], n + 1)
                    x = core.x_res[:, bass.ds((2 * n + s) * T, T), :]
                    nc.vector.tensor_tensor(x, x, by_tile(p_y(s)), ALU.add).then_inc(y_added[s], 1)

                in_pairs(v, gated, features, mask_heads, normalise, add)


FFN1_EXPERTS = 16
FFN1_HID = 4 * D
FFN1_SHARED = 2 * D
CAPACITY = 2 * TOK // FFN1_EXPERTS
SLICES = P // FFN1_EXPERTS
RUNS = TILES // SLICES
RANKS = CAPACITY // P
LO = 32
HI = CAPACITY // LO
ROW = D + FFN1_EXPERTS
BITS = 30
DIGITS = BITS // 2
STEPS = 2 * (TOK // BANK)
TRIALS = 3


def ffn1_weights(w):
    p = np.arange(P)
    same = (p[:, None] % FFN1_EXPERTS) == (p[None, :] % FFN1_EXPERTS)
    before = same & (p[:, None] < p[None, :])
    chunked = lambda a: a.reshape(-1, P, D).transpose(1, 0, 2).reshape(P, -1)
    in_half = p // HI
    return pack([
        ("router", w["gate_w"].T),
        ("token", (np.arange(TILES)[None, :] * P + p[:, None]).astype(np.float32)),
        ("iota", np.broadcast_to(np.arange(LO, dtype=np.float32), (P, LO))),
        ("own", (in_half[:, None] == np.arange(FFN1_EXPERTS // 2)[None, :]).astype(np.float32)),
        ("wg", w["Wg"].reshape(FFN1_EXPERTS * FFN1_HID, D).T), ("wu", w["Wu"].reshape(FFN1_EXPERTS * FFN1_HID, D).T),
        ("wd", chunked(w["Wd"].transpose(0, 2, 1).reshape(FFN1_EXPERTS * FFN1_HID, D))),
        ("sg", w["Sg"].T), ("su", w["Su"].T), ("sd", chunked(w["Sd"].T)),
        ("same", same.astype(np.float32)), ("before", before.astype(np.float32)),
        ("powers", np.broadcast_to(np.concatenate([[0.0], 4.0 ** np.arange(DIGITS - 1, -1, -1)]).astype(np.float32), (P, STEPS))),
    ])


def ffn1(core, blob, offsets):
    nc = core.nc
    GROUPS = TOK // BANK
    with Stage(core, "ffn1") as st:
        w = st.weights(blob, offsets)
        layer_norm(core, st)
        bank = [st.ps(f"bank{i}", [P, BANK]) for i in range(8)]
        tok_major = bank[0][:, :].rearrange("p (t e) -> p t e", t=TILES)
        router_logits(core, w["router"], lambda t: tok_major[:, bass.ds(t, 1), :].squeeze(1), FFN1_EXPERTS, st)

        score = st.sb("score", [P, TILES, FFN1_EXPERTS])
        best, total = st.sb("best", [P, TILES]), st.sb("total", [P, TILES])
        score_e, above, ties, rank, restart = (st.sb(n, [P, BANK]) for n in ("score_e", "above", "ties", "rank", "restart"))
        trial_bits, threshold, trial, kept = st.sb("trial_bits", [P, STEPS, TRIALS], I32), st.sb("threshold", [P, 1], I32), st.sb("trial", [P, TRIALS], I32), st.sb("kept", [P, 1], I32)
        count = st.sb("count", [P, TRIALS])
        reached, digit = st.sb("reached", [P, TRIALS]), st.sb("digit", [P, 1])
        wanted = st.sb("wanted", [P, 1])
        tie_count, base, run_total = (st.sb(n, [P, RUNS]) for n in ("tie_count", "base", "run_total"))
        names = ("dve", "centred", "exp_ready", "score_ready", "score_psum", "counted", "summed", "bit_chain", "tie_chain", "place_e_ready", "place_psum", "consts", "normed", "table_stored")
        (dve, centred, exp_ready, score_ready, score_psum, counted, summed, bit_chain, tie_chain, place_e_ready, place_psum, consts, normed, table_stored) = (st.sem(n) for n in names)
        gelu = st.sb("gelu", [P, 2, BANK])
        hid = st.sb("hid", [P, 2, FFN1_HID // P, BANK])
        N = FFN1_SHARED // P
        names = ("up_psum", "up_copied", "hid_ready", "y_psum", "y_copied", "added")
        s_up_psum, s_up_copied, s_hid_ready, s_y_psum, s_y_copied, s_added = (st.sem("shared_" + n) for n in names)
        table = nc.dram_tensor(f"{st.name}_table", (TOK, ROW), F32, kind="Internal").ap()
        with nc.Block() as block:
            @block.sync
            def _(sp):
                by_tile = table.rearrange("(t p) d -> p t d", p=P)
                sp.wait_ge(normed, 1)
                sp.dma_start(by_tile[:, :, 0:D], core.xn[:, :, :]).then_inc(table_stored, 16)
                sp.wait_ge(score_ready, 1)
                sp.dma_start(by_tile[:, :, D:ROW], score[:, :, :]).then_inc(table_stored, 16)
                sp.wait_ge(table_stored, 32)

            @block.gpsimd
            def _(pool):
                nc.gpsimd.memset(restart[:, :], 1.0).then_inc(consts, 1)
                nc.gpsimd.memset(threshold[:, :], 0).then_inc(consts, 1)
                for j in range(TRIALS):
                    src = w["powers"] if j == 0 else trial_bits[:, :, 0]
                    if j == 0:
                        nc.gpsimd.tensor_copy(trial_bits[:, :, 0], src).then_inc(consts, 1)
                    else:
                        pool.wait_ge(consts, 2 + j)
                        nc.gpsimd.tensor_tensor(trial_bits[:, :, j], trial_bits[:, :, j - 1], trial_bits[:, :, 0], ALU.add).then_inc(consts, 1)
                pool.wait_ge(consts, 2 + TRIALS)
                nc.gpsimd.memset(restart[:, 0:BANK:P], 0.0).then_inc(consts, 1)
                nc.gpsimd.tensor_tensor(core.xn[:, :, :], core.xn[:, :, :], bc(core.rstd[:, :], 2, D), ALU.mult).then_inc(normed, 1)

                pool.sem_inc(s_added, 1)
                with pool.Fori(0, GROUPS) as g:
                    for k in range(N):
                        pool.wait_ge(s_up_copied, g * N + k + 2)
                        nc.gpsimd.tensor_tensor(hid[:, 0, k, :], gelu[:, k, :], hid[:, 1, k, :], ALU.mult).then_inc(s_hid_ready, 1)
                    pool.wait_ge(s_y_copied, g + 2)
                    x = core.x_res[:, bass.ds(g * 4, 4), :]
                    nc.gpsimd.tensor_tensor(x, x, hid[:, 1, 2, :].rearrange("p (t d) -> p t d", t=4), ALU.add).then_inc(s_added, 1)

            @block.tensor
            def _(pe):
                pe.wait_ge(score_ready, 1)
                for r in range(RUNS):
                    ins = nc.tensor.transpose(bank[1][:, r * P:(r + 1) * P], score[:, r * SLICES:(r + 1) * SLICES, :].rearrange("p t e -> p (t e)"), core.ident[:, :])
                ins.then_inc(score_psum, 1)
                pe.sem_inc(s_y_psum, 1)
                with pe.Fori(0, GROUPS) as g:
                    x = core.xnT[:, bass.ds(g * BANK, BANK)]

                    def count_all(i):
                        pe.wait_ge(counted, 2 * g + i + 1)
                        nc.tensor.matmul(bank[2][:, 0:TRIALS], w["same"], count[:, :], start=True, stop=True).then_inc(summed, 1)

                    for k in range(N):
                        pe.wait_ge(s_up_copied, g * N + 1 + k)
                        nc.tensor.matmul(bank[4 + k][:, :], w["sg"][:, k * P:(k + 1) * P], x, start=True, stop=True)
                        nc.tensor.matmul(bank[6 + k][:, :], w["su"][:, k * P:(k + 1) * P], x, start=True, stop=True).then_inc(s_up_psum, 1)
                        count_all(k)
                    pe.wait_ge(s_hid_ready, (g + 1) * N)
                    pe.wait_ge(s_y_copied, g + 1)
                    for t in range(4):
                        for k in range(N):
                            ins = nc.tensor.matmul(bank[1][:, t * P:(t + 1) * P], hid[:, 0, k, t * P:(t + 1) * P], w["sd"][:, k * D:(k + 1) * D],
                                                   start=(k == 0), stop=(k == N - 1))
                    ins.then_inc(s_y_psum, 1)
                pe.wait_ge(counted, STEPS + 1)
                nc.tensor.matmul(bank[2][:, 3:4], w["same"], count[:, 0:1], start=True, stop=True)
                nc.tensor.matmul(bank[2][:, 4:4 + RUNS], w["same"], tie_count[:, :], start=True, stop=True)
                nc.tensor.matmul(bank[2][:, 8:8 + RUNS], w["before"], tie_count[:, :], start=True, stop=True).then_inc(summed, 1)
                pe.wait_ge(counted, STEPS + 2)
                nc.tensor.matmul(bank[2][:, 16:16 + RUNS], w["same"], tie_count[:, :], start=True, stop=True)
                nc.tensor.matmul(bank[2][:, 20:20 + RUNS], w["before"], tie_count[:, :], start=True, stop=True).then_inc(summed, 1)
                pe.wait_ge(place_e_ready, 1)
                for r in range(RUNS):
                    ins = nc.tensor.transpose(bank[3][:, r * P:(r + 1) * P], rank[:, r * P:(r + 1) * P], core.ident[:, :])
                ins.then_inc(place_psum, 1)

            @block.scalar
            def _(a):
                a.wait_ge(centred, 1)
                nc.scalar.activation(score[:, :, :], score[:, :, :], ACT.Exp).then_inc(exp_ready, 1)
                a.sem_inc(s_up_copied, 1)
                with a.Fori(0, GROUPS) as g:
                    for k in range(N):
                        a.wait_ge(s_up_psum, g * N + k + 1)
                        a.wait_ge(s_y_psum, g + 1)
                        nc.scalar.activation(gelu[:, k, :], bank[4 + k][:, :], ACT.Gelu)
                        nc.scalar.copy(hid[:, 1, k, :], bank[6 + k][:, :]).then_inc(s_up_copied, 1)
                    a.wait_ge(s_y_psum, g + 2)
                    a.wait_ge(s_added, g + 1)
                    nc.scalar.copy(hid[:, 1, 2, :], bank[1][:, :]).then_inc(s_y_copied, 1)

            @block.vector
            def _(v):
                c = Chain(v, dve)
                c.link(nc.vector.tensor_reduce(best[:, :], tok_major, AX.X, ALU.max))
                nc.vector.tensor_tensor(score[:, :, :], tok_major, bc(best[:, :], 2, FFN1_EXPERTS), ALU.subtract).then_inc(centred, 1)
                v.wait_ge(exp_ready, 1)
                c.link(nc.vector.tensor_reduce(total[:, :], score[:, :, :], AX.X, ALU.add))
                c.link(nc.vector.reciprocal(total[:, :], total[:, :]))
                nc.vector.tensor_tensor(score[:, :, :], score[:, :, :], bc(total[:, :], 2, FFN1_EXPERTS), ALU.mult).then_inc(score_ready, 1)
                v.wait_ge(score_psum, 1)
                c.link(nc.vector.tensor_copy(score_e[:, :], bank[1][:, :]))
                v.wait_ge(consts, 3 + TRIALS)
                v.sem_inc(s_y_copied, 1)
                with v.Fori(0, STEPS) as i:
                    b = Chain(v, bit_chain, i * 5)
                    b.link(nc.vector.tensor_tensor(trial[:, :], trial_bits[:, bass.ds(i, 1), :].squeeze(1), threshold[:, :].broadcast_to([P, TRIALS]), ALU.bitwise_or))
                    for j in range(TRIALS):
                        ins = nc.vector.tensor_scalar((above, ties, rank)[j][:, :], score_e[:, :], trial[:, j:j + 1].bitcast(F32), 0.0, ALU.is_ge, ALU.add,
                                                      accum_out=count[:, j:j + 1])
                    ins.then_inc(counted, 1)
                    v.wait_ge(summed, i + 1)
                    b.link(nc.vector.tensor_scalar(reached[:, :], bank[2][:, 0:TRIALS], float(CAPACITY), None, ALU.is_ge))
                    b.link(nc.vector.tensor_reduce(digit[:, :], reached[:, :], AX.X, ALU.add))
                    b.link(nc.vector.tensor_scalar(kept[:, :], digit[:, :], w["powers"][:, bass.ds(i, 1)], None, ALU.mult))
                    b.link(nc.vector.tensor_tensor(threshold[:, :], threshold[:, :], kept[:, :], ALU.bitwise_or))
                e = Chain(v, tie_chain)
                limit = threshold[:, :].bitcast(F32)
                e.link(nc.vector.tensor_scalar(above[:, :], score_e[:, :], limit, 0.0, ALU.is_gt, ALU.add, accum_out=count[:, 0:1]))
                e.link(nc.vector.tensor_scalar(ties[:, :], score_e[:, :], limit, None, ALU.is_equal))
                by_run = lambda t: t[:, :].rearrange("p (r s) -> p r s", r=RUNS)

                def places(marks, at, nth):
                    e.link(nc.vector.tensor_tensor_scan(rank[:, :], restart[:, :], marks[:, :], 0.0, ALU.mult, ALU.add))
                    nc.vector.tensor_copy(tie_count[:, :], rank[:, P - 1:BANK:P]).then_inc(counted, 1)
                    v.wait_ge(summed, STEPS + nth)
                    e.link(nc.vector.tensor_copy(run_total[:, :], bank[2][:, at:at + RUNS]))
                    e.link(nc.vector.tensor_copy(base[:, :], bank[2][:, at + RUNS:at + 2 * RUNS]))
                    for r in range(1, RUNS):
                        e.link(nc.vector.tensor_scalar(base[:, r:RUNS], base[:, r:RUNS], run_total[:, r - 1:r], None, ALU.add))
                    e.link(nc.vector.tensor_tensor(rank[:, :], rank[:, :], marks[:, :], ALU.subtract))
                    e.link(nc.vector.tensor_tensor(by_run(rank), by_run(rank), bc(base[:, :], 2, P), ALU.add))

                places(ties, 4, 1)
                e.link(nc.vector.tensor_scalar(wanted[:, :], bank[2][:, 3:4], -1.0, float(CAPACITY), ALU.mult, ALU.add))
                e.link(nc.vector.tensor_scalar(rank[:, :], rank[:, :], wanted[:, :], None, ALU.is_lt))
                e.link(nc.vector.tensor_tensor(ties[:, :], ties[:, :], rank[:, :], ALU.mult))
                e.link(nc.vector.tensor_tensor(above[:, :], above[:, :], ties[:, :], ALU.add))
                places(above, 16, 2)
                e.link(nc.vector.scalar_tensor_tensor(rank[:, :], rank[:, :], 1.0, above[:, :], ALU.add, ALU.mult))
                e.link(nc.vector.tensor_scalar(rank[:, :], rank[:, :], -1.0, None, ALU.add))
                e.eng.sem_inc(place_e_ready, 1)
                v.wait_ge(place_psum, 1)
                place = ties[:, :].bitcast(I32)
                e.link(nc.vector.tensor_copy(place, bank[3][:, :]))
                split = above[:, :].bitcast(I32), restart[:, :].bitcast(I32)
                e.link(nc.vector.tensor_scalar(split[0], place, LO.bit_length() - 1, None, ALU.arith_shift_right))
                e.link(nc.vector.tensor_scalar(split[1], place, LO - 1, None, ALU.bitwise_and))
                e.link(nc.vector.tensor_copy(score_e[:, :], split[0]))
                e.link(nc.vector.tensor_copy(rank[:, :], split[1]))

        index = st.sb("index", [P, FFN1_EXPERTS * RANKS], I32)
        lists = nc.dram_tensor(f"{st.name}_lists", (FFN1_EXPERTS * CAPACITY,), F32, kind="Internal").ap()
        hi = score_e[:, :].rearrange("p (t e) -> p t e", t=TILES)
        lo = rank[:, :].rearrange("p (t e) -> p t e", t=TILES)
        STEP = 2
        hid_flat = hid[:, :, :, :].rearrange("p i k s -> p i (k s)")
        is_hi = [hid_flat[:, i, 0:STEP * FFN1_EXPERTS * HI].rearrange("p (t e h) -> p t e h", t=STEP, e=FFN1_EXPERTS) for i in range(2)]
        is_lo = [hid_flat[:, i, STEP * FFN1_EXPERTS * HI:STEP * FFN1_EXPERTS * (HI + LO)].rearrange("p (t e l) -> p t e l", t=STEP, e=FFN1_EXPERTS) for i in range(2)]
        own_idx, rows_64 = gelu[:, 0, 0:2 * LO], gelu[0:FFN1_EXPERTS * RANKS, 1, 0:P]
        hot_chain, hot_ready, hot_used, list_psum, list_chain, list_ready, list_moved, index_psum = (st.sem(n) for n in (
            "hot_chain", "hot_ready", "hot_used", "list_psum", "list_chain", "list_ready", "list_moved", "index_psum"))
        with nc.Block() as block:
            @block.vector
            def _(v):
                for n in range(TILES // STEP):
                    tiles = slice(n * STEP, (n + 1) * STEP)
                    i = n % 2
                    if n >= 2:
                        v.wait_ge(hot_used, n - 1)
                    nc.vector.tensor_tensor(is_hi[i], bc(hi[:, tiles, :], 3, HI), bc(bc(w["iota"][:, 0:HI], 1, FFN1_EXPERTS), 1, STEP), ALU.is_equal).then_inc(hot_chain, 1)
                    nc.vector.tensor_tensor(is_lo[i], bc(lo[:, tiles, :], 3, LO), bc(bc(w["iota"], 1, FFN1_EXPERTS), 1, STEP), ALU.is_equal).then_inc(hot_ready, 1)
                    v.wait_ge(hot_chain, n + 1)
                    nc.vector.tensor_tensor(is_hi[i].rearrange("p t e h -> p t (e h)"), is_hi[i].rearrange("p t e h -> p t (e h)"),
                                            bc(w["token"][:, tiles], 2, FFN1_EXPERTS * HI), ALU.mult).then_inc(hot_ready, 1)
                v.wait_ge(list_psum, 1)
                c = Chain(v, list_chain)
                own = hid_flat[:, 0, 0:BANK].rearrange("p (h e l) -> p h e l", h=2, e=FFN1_EXPERTS // 2)
                for half in range(2):
                    found = bank[4 + half][:, 0:FFN1_EXPERTS // 2 * LO].rearrange("p (e l) -> p e l", e=FFN1_EXPERTS // 2)
                    c.link(nc.vector.tensor_tensor(own[:, half], found, bc(w["own"], 2, LO), ALU.mult))
                nc.vector.tensor_reduce(own_idx.rearrange("p (h l) -> p h l", h=2), own.rearrange("p h e l -> p h l e"), AX.X, ALU.add).then_inc(list_ready, 1)
                v.wait_ge(index_psum, 1)
                nc.vector.tensor_copy(index[:, :], bank[6][:, 0:FFN1_EXPERTS * RANKS])

            @block.sync
            def _(sp):
                sp.wait_ge(list_ready, 1)
                sp.dma_start(lists.rearrange("(h p l) -> p h l", h=2, p=P), own_idx.rearrange("p (h l) -> p h l", h=2)).then_inc(list_moved, 16)
                sp.wait_ge(list_moved, 16)
                sp.dma_start(rows_64, lists.rearrange("(r p) -> r p", p=P)).then_inc(list_moved, 16)

            @block.tensor
            def _(pe):
                E2 = FFN1_EXPERTS // 2
                for n in range(TILES // STEP):
                    pe.wait_ge(hot_ready, 2 * (n + 1))
                    for t in range(STEP):
                        for half in range(2):
                            es = slice(half * E2, (half + 1) * E2)
                            ins = nc.tensor.matmul(bank[4 + half][:, 0:E2 * LO], is_hi[n % 2][:, t, es, :].rearrange("p e h -> p (e h)"),
                                                   is_lo[n % 2][:, t, es, :].rearrange("p e l -> p (e l)"),
                                                   start=(n == 0 and t == 0), stop=(n == TILES // STEP - 1 and t == STEP - 1))
                    ins.then_inc(hot_used, 1)
                pe.wait_ge(hot_used, TILES // STEP)
                pe.sem_inc(list_psum, 1)
                pe.wait_ge(list_moved, 32)
                nc.tensor.transpose(bank[6][:, 0:FFN1_EXPERTS * RANKS], rows_64, core.ident[0:FFN1_EXPERTS * RANKS, 0:FFN1_EXPERTS * RANKS]).then_inc(index_psum, 1)

        stream = nc.dram_tensor(f"{st.name}_stream", (TOK, D), F32, kind="Internal").ap()
        XS = 3
        rows = st.sb("rows", [P, XS, RANKS, ROW])
        rowsT = st.sb("rowsT", [P, 2, BANK])
        y = st.sb("y", [P, 2, RANKS, D])
        gathered = [st.sem(f"gathered{i}") for i in range(XS)]
        names = ("turned", "rowsT_ready", "up_ready", "gelu_ready", "hid_ready", "y_psum", "y_ready", "scattered", "stream_stored", "stream_loaded")
        (turned, rowsT_ready, up_ready, gelu_ready, hid_ready, y_psum, y_ready, scattered, stream_stored, stream_loaded) = (st.sem(n) for n in names)
        KS = FFN1_HID // P
        with nc.Block() as block:
            @block.sync
            def _(sp):
                sp.dma_start(stream.rearrange("(t p) d -> p t d", p=P), core.x_res[:, :, :]).then_inc(stream_stored, 16)
                sp.wait_ge(stream_stored, 16)
                sp.wait_ge(scattered, FFN1_EXPERTS * RANKS * 16)
                sp.dma_start(core.x_res[:, :, :], stream.rearrange("(t p) d -> p t d", p=P)).then_inc(stream_loaded, 16)
                sp.wait_ge(stream_loaded, 16)

            @block.gpsimd
            def _(pool):
                def gather(e):
                    for r in range(RANKS):
                        at = e * RANKS + r
                        nc.gpsimd.indirect_dma_start(rows[:, e % XS, r, :], None, table, bass.IndirectOffsetOnAxis(index[:, at:at + 1], 0)).then_inc(gathered[e % XS], 16)

                def scatter(e):
                    if e == 0:
                        pool.wait_ge(stream_stored, 16)
                    else:
                        pool.wait_ge(scattered, e * RANKS * 16)
                    for r in range(RANKS):
                        at = e * RANKS + r
                        nc.gpsimd.indirect_dma_start(stream, bass.IndirectOffsetOnAxis(index[:, at:at + 1], 0), y[:, e % 2, r, :], None,
                                                     compute_op=ALU.add).then_inc(scattered, 16)

                gather(0)
                gather(1)
                for e in range(FFN1_EXPERTS):
                    if e > 0:
                        pool.wait_ge(y_ready, e)
                    if e + 2 < FFN1_EXPERTS:
                        gather(e + 2)
                    if e > 0:
                        scatter(e - 1)
                pool.wait_ge(y_ready, FFN1_EXPERTS)
                scatter(FFN1_EXPERTS - 1)

            @block.tensor
            def _(pe):
                def turn(e):
                    pe.wait_ge(gathered[e % XS], (e // XS + 1) * RANKS * 16)
                    if e >= 2:
                        pe.wait_ge(rowsT_ready, e - 1)
                    for r in range(RANKS):
                        ins = nc.tensor.transpose(bank[6 + e % 2][:, r * P:(r + 1) * P], rows[:, e % XS, r, 0:D], core.ident[:, :])
                    ins.then_inc(turned, 1)

                def down(e):
                    pe.wait_ge(hid_ready, (e + 1) * KS)
                    if e >= 2:
                        pe.wait_ge(y_ready, e - 1)
                    for r in range(RANKS):
                        for k in range(KS):
                            at = e * KS + k
                            ins = nc.tensor.matmul(bank[4 + e % 2][:, r * P:(r + 1) * P], hid[:, e % 2, k, r * P:(r + 1) * P], w["wd"][:, at * D:(at + 1) * D],
                                                   start=(k == 0), stop=(k == KS - 1))
                    ins.then_inc(y_psum, 1)

                turn(0)
                for e in range(FFN1_EXPERTS):
                    pe.wait_ge(rowsT_ready, e + 1)
                    for k in range(KS):
                        i = e * KS + k
                        if i >= 2:
                            pe.wait_ge(hid_ready, i - 1)
                        nc.tensor.matmul(bank[2 * (i % 2)][:, :], w["wg"][:, i * P:(i + 1) * P], rowsT[:, e % 2, :], start=True, stop=True)
                        nc.tensor.matmul(bank[2 * (i % 2) + 1][:, :], w["wu"][:, i * P:(i + 1) * P], rowsT[:, e % 2, :], start=True, stop=True).then_inc(up_ready, 1)
                        if k == 1 and e > 0:
                            down(e - 1)
                        if k == 2 and e + 1 < FFN1_EXPERTS:
                            turn(e + 1)
                down(FFN1_EXPERTS - 1)

            @block.scalar
            def _(a):
                def rows_turned(e):
                    a.wait_ge(turned, e + 1)
                    if e >= 2:
                        a.wait_ge(up_ready, (e - 1) * KS)
                    nc.scalar.copy(rowsT[:, e % 2, :], bank[6 + e % 2][:, :]).then_inc(rowsT_ready, 1)

                rows_turned(0)
                for e in range(FFN1_EXPERTS):
                    for k in range(KS):
                        i = e * KS + k
                        a.wait_ge(up_ready, i + 1)
                        if i >= 2:
                            a.wait_ge(hid_ready, i - 1)
                        nc.scalar.activation(gelu[:, i % 2, :], bank[2 * (i % 2)][:, :], ACT.Gelu).then_inc(gelu_ready, 1)
                        if k == 3 and e + 1 < FFN1_EXPERTS:
                            rows_turned(e + 1)

            @block.vector
            def _(v):
                def weigh(e):
                    v.wait_ge(y_psum, e + 1)
                    if e >= 2:
                        v.wait_ge(scattered, (e - 1) * RANKS * 16)
                    nc.vector.tensor_tensor(y[:, e % 2, :, :], bank[4 + e % 2][:, :].rearrange("p (r d) -> p r d", r=RANKS),
                                            bc(rows[:, e % XS, :, D + e:D + e + 1].squeeze(2), 2, D), ALU.mult).then_inc(y_ready, 1)

                for e in range(FFN1_EXPERTS):
                    for k in range(KS):
                        i = e * KS + k
                        v.wait_ge(gelu_ready, i + 1)
                        if e >= 2:
                            v.wait_ge(y_psum, e - 1)
                        nc.vector.tensor_tensor(hid[:, e % 2, k, :], gelu[:, i % 2, :], bank[2 * (i % 2) + 1][:, :], ALU.mult).then_inc(hid_ready, 1)
                        if k == 2 and e > 0:
                            weigh(e - 1)
                weigh(FFN1_EXPERTS - 1)


STATES = 16
RANK = 64
CHN = 4
SCAN_CHUNKS = STATES // CHN


SCAN_PIECES = 3
SCAN_BF16 = mybir.dt.bfloat16


def full(a):
    return np.concatenate([a, np.zeros((a.shape[0], P - a.shape[1]), a.dtype)], axis=1)


def pick(n):
    return np.tile(np.eye(n, dtype=np.float32), (SCAN_PIECES, 1))


def scan1_weights(w):
    xp = w["x_proj_w"].T
    return pack([
        ("low", full(xp[:, 0:RANK])), ("states", np.tile(xp[:, RANK:], (1, SCAN_PIECES))), ("pick", pick(2 * STATES)),
        ("dt", w["dt_proj_w"].T), ("dt_b", w["dt_proj_b"]), ("a_log", w["A_log"]), ("skip", w["D_skip"]),
    ])


def scan3_weights(w):
    wp = w["W_params"].T
    return pack([
        ("low", full(wp[:, 0:RANK])), ("states", np.tile(full(wp[:, RANK + STATES:])[:, 0:2 * STATES], (1, SCAN_PIECES))), ("pick", pick(2 * STATES)),
        ("dt", w["W_dt"].T), ("dt_b", w["b_dt"]), ("a_log", w["A_log"]), ("skip", w["D"]),
        ("conv", w["conv_w"][:, 0, :]), ("wz", w["W_z"].T), ("wo", w["W_out"].T),
    ])


def step_sizes(core, st, w, bank, delta):
    nc = core.nc
    GROUPS = TOK // BANK
    ROWS = 2 * STATES
    KP = SCAN_PIECES * ROWS
    low = st.sb("dt_low", [P, 2, BANK])
    e = core.xn[:, :, :].rearrange("p t d -> p (t d)")
    pieces = st.sb("pieces", [KP, TOK], SCAN_BF16)
    pick_bf = st.sb("pick_bf", [KP, ROWS], SCAN_BF16)
    rounded = st.sb("rounded", [KP, 2, BANK], SCAN_BF16)
    rest = st.sb("rest", [KP, 2, BANK])
    names = ("low_psum", "low_ready", "y_psum", "y_ready", "ln_ready", "delta_done", "act_chain", "picks_ready", "rows_psum", "rounded_1", "rest_1", "rounded_2",
             "rest_2", "pieces_ready")
    (low_psum, low_ready, y_psum, y_ready, ln_ready, delta_done, act_chain, picks_ready, rows_psum, rounded_1, rest_1, rounded_2,
     rest_2, pieces_ready) = (st.sem("dt_" + n) for n in names)
    HALVES = 2
    with nc.Block() as block:
        @block.tensor
        def _(pe):
            pe.sem_inc(y_ready, 2)
            pe.sem_inc(pieces_ready, 2)
            with pe.Fori(0, GROUPS // 2) as g2:
                for i in range(2):
                    g = g2 * 2 + i
                    x = core.xnT[:, bass.ds(g * BANK, BANK)]
                    pe.wait_ge(y_ready, g + 1)
                    nc.tensor.matmul(bank[i][:, :], w["low"], x, start=True, stop=True).then_inc(low_psum, 1)
                    pe.wait_ge(pieces_ready, g + 1)
                    nc.tensor.matmul(bank[4 + i][0:KP, :], w["states"], x, start=True, stop=True).then_inc(rows_psum, 1)
                    pe.wait_ge(low_ready, g + 1)
                    nc.tensor.matmul(bank[2 + i][:, :], w["dt"], low[:, i, :], start=True, stop=True).then_inc(y_psum, 1)

        @block.scalar
        def _(a):
            with a.Fori(0, GROUPS // 2) as g2:
                for i in range(2):
                    g = g2 * 2 + i
                    a.wait_ge(low_psum, g + 1)
                    nc.scalar.copy(low[:, i, :], bank[i][:, :]).then_inc(low_ready, 1)
            a.wait_ge(y_ready, GROUPS + 2)
            c = Chain(a, act_chain)
            for half in range(HALVES):
                part = slice(half * TOK // HALVES, (half + 1) * TOK // HALVES)
                c.link(nc.scalar.activation(e[:, part], delta[:, part], ACT.Abs))
                c.link(nc.scalar.activation(e[:, part], e[:, part], ACT.Exp, scale=-1.0))
                nc.scalar.activation(e[:, part], e[:, part], ACT.Ln, bias=1.0).then_inc(ln_ready, 1)

        @block.vector
        def _(v):
            with v.Fori(0, GROUPS // 2) as g2:
                for i in range(2):
                    g = g2 * 2 + i
                    cols = bass.ds(g * BANK, BANK)
                    rows, src = rounded[:, i, :], bank[4 + i][0:KP, :]
                    v.wait_ge(y_psum, g + 1)
                    nc.vector.tensor_scalar(delta[:, cols], bank[2 + i][:, :], w["dt_b"], None, ALU.add).then_inc(y_ready, 1)
                    v.wait_ge(rows_psum, g + 1)
                    nc.vector.tensor_copy(pieces[0:ROWS, cols], src[0:ROWS])
                    nc.vector.tensor_copy(rows, src).then_inc(rounded_1, 1)
                    v.wait_ge(rounded_1, g + 1)
                    nc.vector.tensor_tensor(rest[:, i, :], src, rows, ALU.subtract).then_inc(rest_1, 1)
                    v.wait_ge(rest_1, g + 1)
                    nc.vector.tensor_copy(pieces[ROWS:2 * ROWS, cols], rest[ROWS:2 * ROWS, i, :])
                    nc.vector.tensor_copy(rounded[2 * ROWS:KP, i, :], rest[2 * ROWS:KP, i, :]).then_inc(rounded_2, 1)
                    v.wait_ge(rounded_2, g + 1)
                    nc.vector.tensor_tensor(rest[2 * ROWS:KP, i, :], rest[2 * ROWS:KP, i, :], rounded[2 * ROWS:KP, i, :], ALU.subtract).then_inc(rest_2, 1)
                    v.wait_ge(rest_2, g + 1)
                    nc.vector.tensor_copy(pieces[2 * ROWS:KP, cols], rest[2 * ROWS:KP, i, :]).then_inc(pieces_ready, 1)
            for half in range(HALVES):
                part = slice(half * TOK // HALVES, (half + 1) * TOK // HALVES)
                v.wait_ge(ln_ready, half + 1)
                nc.vector.scalar_tensor_tensor(delta[:, part], delta[:, part], 0.0, e[:, part], ALU.max, ALU.add).then_inc(delta_done, 1)

        @block.gpsimd
        def _(pool):
            nc.gpsimd.tensor_copy(pick_bf[:, :], w["pick"][0:KP, :]).then_inc(picks_ready, 1)
    return pieces, pick_bf


def scan1(core, blob, offsets):
    nc = core.nc
    with Stage(core, "scan1") as st:
        w = st.weights(blob, offsets)
        layer_norm(core, st)
        bank = [st.ps(f"bank{i}", [P, BANK]) for i in range(8)]
        delta = st.sb("delta", [P, TOK])
        pieces, pick_bf = step_sizes(core, st, w, bank, delta)
        spread = lambda n: pick_bf[:, n:n + 1].broadcast_to([SCAN_PIECES * 2 * STATES, P])
        pB = lambda j: [bank[2 * (j % 2) + i] for i in range(2)]
        pC, pSum = bank[4:6], bank[6:8]
        decay = [st.sb(f"decay{i}", [P, STATES, SEQ]) for i in range(2)]
        h = [st.sb(f"h{i}", [P, STATES, SEQ]) for i in range(2)]
        c_all = st.sb("c_all", [P, STATES, SEQ])
        du = st.sb("du", [P, 2, SEQ])
        y = st.sb("y", [P, 2, SEQ])
        pos_a, neg_a = st.sb("pos_a", [P, STATES]), st.sb("neg_a", [P, STATES])
        names = ("set_up", "du_ready", "b_psum", "b_used", "c_psum", "c_ready", "decay_ready", "scanned", "times_c", "sum_psum", "y_ready", "yT_ready", "added")
        (set_up, du_ready, b_psum, b_used, c_psum, c_ready, decay_ready, scanned, times_c, sum_psum, y_ready, yT_ready, added) = (st.sem(n) for n in names)
        with nc.Block() as block:
            @block.gpsimd
            def _(pool):
                for s in range(2):
                    nc.gpsimd.memset(decay[s][:, :, 0:1], 0.0).then_inc(set_up, 1)

                def enter(b, s):
                    cols = bass.ds(b * SEQ, SEQ)
                    if not known(b, 2):
                        pool.wait_ge(b_used, (b - 1) * SCAN_CHUNKS + 2)
                    nc.gpsimd.tensor_tensor(du[:, s, :], delta[:, cols], core.xnT[:, cols], ALU.mult).then_inc(du_ready, 1)

                def step(b, s, first, last):
                    if first:
                        enter(b, s)
                    if not last:
                        enter(b + 1, 1 - s)
                    for j in range(SCAN_CHUNKS):
                        part = slice(j * CHN, (j + 1) * CHN)
                        pool.wait_ge(scanned, b * SCAN_CHUNKS + j + 1)
                        pool.wait_ge(c_ready, (b * SCAN_CHUNKS + j) * 2 + 4)
                        nc.gpsimd.tensor_tensor(h[s][:, part, :], h[s][:, part, :], c_all[:, part, :], ALU.mult).then_inc(times_c, 1)

                sequences(pool, step)

            @block.tensor
            def _(pe):
                pe.sem_inc(b_used, 2)
                pe.sem_inc(c_ready, 2)
                at = lambda b: pieces[:, bass.ds(b * SEQ, SEQ)]

                def b_rows(b, j):
                    pe.wait_ge(b_used, b * SCAN_CHUNKS + j + 1)
                    for n in range(CHN):
                        ins = nc.tensor.matmul(pB(j)[n // 2][:, n % 2 * SEQ:(n % 2 + 1) * SEQ], spread(j * CHN + n), at(b), start=True, stop=True)
                    ins.then_inc(b_psum, 1)

                def c_rows(b, j):
                    for i in range(2 * j, 2 * j + 2):
                        pe.wait_ge(c_ready, b * 2 * SCAN_CHUNKS + i + 1)
                        for n in range(2):
                            ins = nc.tensor.matmul(pC[i % 2][:, n * SEQ:(n + 1) * SEQ], spread(STATES + i * 2 + n), at(b), start=True, stop=True)
                        ins.then_inc(c_psum, 1)

                def add_up(b, s, j):
                    pe.wait_ge(times_c, b * SCAN_CHUNKS + j + 1)
                    for n in range(j * CHN, (j + 1) * CHN):
                        ins = nc.tensor.matmul(pSum[s][:, 0:SEQ], core.ident[:, :], h[s][:, n, :], start=(n == 0), stop=(n == STATES - 1))
                    if j == SCAN_CHUNKS - 1:
                        ins.then_inc(sum_psum, 1)

                def put_out(b, s):
                    pe.wait_ge(y_ready, b + 1)
                    for t in range(2):
                        ins = nc.tensor.transpose(pSum[s][:, SEQ + t * P:SEQ + (t + 1) * P], y[:, s, t * P:(t + 1) * P], core.ident[:, :])
                    ins.then_inc(yT_ready, 1)

                def step(b, s, first, last):
                    if first:
                        b_rows(b, 0)
                    for j in range(SCAN_CHUNKS):
                        if j + 1 < SCAN_CHUNKS:
                            b_rows(b, j + 1)
                        elif not last:
                            b_rows(b + 1, 0)
                        c_rows(b, j)
                        if j >= 2:
                            if j == 2 and not known(b, 2):
                                pe.wait_ge(added, b - 1)
                            add_up(b, s, j - 2)
                        elif not first:
                            add_up(b - 1, 1 - s, SCAN_CHUNKS - 2 + j)
                        if j == 3 and not first:
                            put_out(b - 1, 1 - s)
                    if last:
                        add_up(b, s, SCAN_CHUNKS - 2)
                        add_up(b, s, SCAN_CHUNKS - 1)
                        put_out(b, s)

                sequences(pe, step)

            @block.scalar
            def _(a):
                nc.scalar.activation(pos_a[:, :], w["a_log"], ACT.Exp).then_inc(set_up, 1)
                a.wait_ge(set_up, 4)

                def decays(b, s, j):
                    for n in range(j * CHN, (j + 1) * CHN):
                        ins = nc.scalar.activation(decay[s][:, n, 1:SEQ], delta[:, bass.ds(b * SEQ + 1, SEQ - 1)], ACT.Exp, scale=neg_a[:, n:n + 1])
                    ins.then_inc(decay_ready, 1)

                def step(b, s, first, last):
                    if first:
                        for j in range(SCAN_CHUNKS):
                            decays(b, s, j)
                    for j in range(SCAN_CHUNKS):
                        for i in range(2 * j, 2 * j + 2):
                            a.wait_ge(c_psum, b * 2 * SCAN_CHUNKS + i + 1)
                            if i % 2 == 0 and not first:
                                a.wait_ge(times_c, (b - 1) * SCAN_CHUNKS + j + 1)
                            nc.scalar.copy(c_all[:, 2 * i:2 * i + 2, :], pC[i % 2][:, :].rearrange("p (n s) -> p n s", n=2)).then_inc(c_ready, 1)
                        if not last:
                            decays(b + 1, 1 - s, j)

                sequences(a, step)

            @block.vector
            def _(v):
                v.wait_ge(set_up, 3)
                nc.vector.tensor_scalar(neg_a[:, :], pos_a[:, :], -1.0, None, ALU.mult).then_inc(set_up, 1)

                def enter(b, s, j):
                    v.wait_ge(b_psum, b * SCAN_CHUNKS + j + 1)
                    for i in range(2):
                        rows = slice(j * CHN + 2 * i, j * CHN + 2 * i + 2)
                        ins = nc.vector.tensor_tensor(h[s][:, rows, :], pB(j)[i][:, :].rearrange("p (n s) -> p n s", n=2), bc(du[:, s, :], 1, 2), ALU.mult)
                    ins.then_inc(b_used, 1)

                def skip(b, s):
                    v.wait_ge(sum_psum, b + 1)
                    nc.vector.scalar_tensor_tensor(y[:, s, :], core.xnT[:, bass.ds(b * SEQ, SEQ)], w["skip"], pSum[s][:, 0:SEQ], ALU.mult, ALU.add).then_inc(y_ready, 1)

                def add(b, s):
                    v.wait_ge(yT_ready, b + 1)
                    x = core.x_res[:, bass.ds(b * 2, 2), :]
                    nc.vector.tensor_tensor(x, x, pSum[s][:, SEQ:2 * SEQ].rearrange("p (t d) -> p t d", t=2), ALU.add).then_inc(added, 1)

                def step(b, s, first, last):
                    v.wait_ge(du_ready, b + 1)
                    enter(b, s, 0)
                    if not known(b, 2):
                        add(b - 2, s)
                    for j in range(SCAN_CHUNKS):
                        if j + 1 < SCAN_CHUNKS:
                            enter(b, s, j + 1)
                        v.wait_ge(b_used, b * SCAN_CHUNKS + j + 3)
                        v.wait_ge(decay_ready, b * SCAN_CHUNKS + j + 1)
                        flat = lambda t: t[:, j * CHN:(j + 1) * CHN, :].rearrange("p n s -> p (n s)")
                        nc.vector.tensor_tensor_scan(flat(h[s]), flat(decay[s]), flat(h[s]), 0.0, ALU.mult, ALU.add).then_inc(scanned, 1)
                        if j == 2 and not first:
                            skip(b - 1, 1 - s)
                    if last:
                        add(b - 1, 1 - s)
                        skip(b, s)
                        add(b, s)

                sequences(v, step)


def scan3(core, blob, offsets):
    nc = core.nc
    TAPS = 4
    GROUPS = TOK // BANK
    with Stage(core, "scan3") as st:
        w = st.weights(blob, offsets)
        layer_norm(core, st)
        bank = [st.ps(f"bank{i}", [P, BANK]) for i in range(8)]
        delta = st.sb("delta", [P, TOK])
        u = st.sb("u", [P, TOK])
        gate = st.sb("gate", [P, TOK])

        conv = st.sb("conv", [P, 2, 2, SEQ])
        z_psum, gate_ready, conv_chain, conv_ready, u_ready = (st.sem(n) for n in ("z_psum", "gate_ready", "conv_chain", "conv_ready", "u_ready"))
        with nc.Block() as block:
            @block.tensor
            def _(pe):
                pe.sem_inc(gate_ready, 2)
                with pe.Fori(0, GROUPS // 2) as g:
                    for s in range(2):
                        pe.wait_ge(gate_ready, 2 * g + s + 1)
                        nc.tensor.matmul(bank[s][:, :], w["wz"], core.xnT[:, bass.ds((2 * g + s) * BANK, BANK)], start=True, stop=True).then_inc(z_psum, 1)

            @block.scalar
            def _(a):
                with a.Fori(0, GROUPS // 2) as g:
                    for s in range(2):
                        cols = bass.ds((2 * g + s) * BANK, BANK)
                        a.wait_ge(z_psum, 2 * g + s + 1)
                        nc.scalar.activation(gate[:, cols], bank[s][:, :], ACT.Silu).then_inc(gate_ready, 1)
                        a.wait_ge(conv_ready, 2 * g + s + 1)
                        nc.scalar.activation(u[:, cols], conv[:, s, :, :].rearrange("p b s -> p (b s)"), ACT.Silu).then_inc(u_ready, 1)

            @block.vector
            def _(v):
                v.sem_inc(u_ready, 2)
                with v.Fori(0, GROUPS // 2) as g:
                    c = Chain(v, conv_chain, g * 2 * (TAPS - 1))
                    for s in range(2):
                        x = core.xnT[:, bass.ds((2 * g + s) * BANK, BANK)].rearrange("p (b s) -> p b s", b=2)
                        out = conv[:, s, :, :]
                        v.wait_ge(u_ready, 2 * g + s + 1)
                        ins = nc.vector.tensor_scalar(out, x, w["conv"][:, TAPS - 1:TAPS], None, ALU.mult)
                        for back in range(1, TAPS):
                            c.link(ins)
                            ins = nc.vector.scalar_tensor_tensor(out[:, :, back:SEQ], x[:, :, 0:SEQ - back], w["conv"][:, TAPS - 1 - back:TAPS - back],
                                                                 out[:, :, back:SEQ], ALU.mult, ALU.add)
                        ins.then_inc(conv_ready, 1)

        pieces, pick_bf = step_sizes(core, st, w, bank, delta)
        spread = lambda n: pick_bf[:, n:n + 1].broadcast_to([SCAN_PIECES * 2 * STATES, P])

        pC, pSum = bank[4:6], bank[6:8]
        decay = st.sb("decay", [P, STATES, SEQ])
        h = [st.sb(f"h{i}", [P, STATES, SEQ]) for i in range(2)]
        c_all = core.xn[:, :, :].rearrange("p t d -> p (t d)").rearrange("p (n s) -> p n s", n=STATES)
        prev = st.sb("prev", [P, 2, 2, SEQ])
        du = st.sb("du", [P, 2, SEQ])
        du_small = st.sb("du_small", [P, STATES, SEQ])
        yT = st.sb("yT", [P, SEQ])
        pos_a, neg_a, small, inv_a, den = (st.sb(n, [P, STATES]) for n in ("pos_a", "neg_a", "small", "inv_a", "den"))
        names = ("set_up", "setup_chain", "du_made", "prev_ready", "small_by_pool", "small_by_act", "decay_ready", "entered", "shrunk", "scanned", "zeroed", "c_psum",
                 "c_ready", "times_c", "sum_psum", "skip_added", "y_ready", "out_psum", "added")
        (set_up, setup_chain, du_made, prev_ready, small_by_pool, small_by_act, decay_ready, entered, shrunk, scanned, zeroed, c_psum,
         c_ready, times_c, sum_psum, skip_added, y_ready, out_psum, added) = (st.sem(n) for n in names)
        BY_POOL = 1
        BY_ACT = SCAN_CHUNKS - BY_POOL
        with nc.Block() as block:
            @block.gpsimd
            def _(pool):
                pool.wait_ge(set_up, 2)

                def before(b, s):
                    for i, src in enumerate((delta, u)):
                        nc.gpsimd.tensor_copy(prev[:, s, i, 1:SEQ], src[:, bass.ds(b * SEQ, SEQ - 1)])
                        ins = nc.gpsimd.tensor_copy(prev[:, s, i, 0:1], src[:, bass.ds(b * SEQ, 1)])
                    ins.then_inc(prev_ready, 1)
                    pool.wait_ge(prev_ready, b + 1)
                    nc.gpsimd.tensor_tensor(du[:, s, :], prev[:, s, 0, :], prev[:, s, 1, :], ALU.mult).then_inc(du_made, 1)

                def small_part(b, s):
                    pool.wait_ge(du_made, b + 1)
                    if not known(b, 1):
                        pool.wait_ge(shrunk, b * SCAN_CHUNKS)
                    part = slice(BY_ACT * CHN, STATES)
                    nc.gpsimd.tensor_tensor(du_small[:, part, :], bc(du[:, s, :], 1, BY_POOL * CHN), bc(small[:, part], 2, SEQ), ALU.mult).then_inc(small_by_pool, 1)

                def step(b, s, first, last):
                    if first:
                        before(b, s)
                        small_part(b, s)
                    if not last:
                        before(b + 1, 1 - s)
                    for j in range(SCAN_CHUNKS):
                        part = slice(j * CHN, (j + 1) * CHN)
                        pool.wait_ge(scanned, b * SCAN_CHUNKS + j + 1)
                        pool.wait_ge(c_ready, (b * SCAN_CHUNKS + j) * 2 + 4)
                        nc.gpsimd.tensor_tensor(h[s][:, part, :], h[s][:, part, :], c_all[:, part, :], ALU.mult).then_inc(times_c, 1)
                    if not last:
                        small_part(b + 1, 1 - s)

                sequences(pool, step)

            @block.tensor
            def _(pe):
                pe.sem_inc(c_ready, 2)

                def c_rows(b, j):
                    for i in range(2 * j, 2 * j + 2):
                        pe.wait_ge(c_ready, b * 2 * SCAN_CHUNKS + i + 1)
                        for n in range(2):
                            ins = nc.tensor.matmul(pC[i % 2][:, n * SEQ:(n + 1) * SEQ], spread(i * 2 + n), pieces[:, bass.ds(b * SEQ, SEQ)], start=True, stop=True)
                        ins.then_inc(c_psum, 1)

                def add_up(b, s, j):
                    pe.wait_ge(times_c, b * SCAN_CHUNKS + j + 1)
                    for n in range(j * CHN, (j + 1) * CHN):
                        ins = nc.tensor.matmul(pSum[s][:, 0:SEQ], core.ident[:, :], h[s][:, n, :], start=(n == 0), stop=(n == STATES - 1))
                    if j == SCAN_CHUNKS - 1:
                        ins.then_inc(sum_psum, 1)

                def put_out(b, s):
                    pe.wait_ge(y_ready, b + 1)
                    for t in range(2):
                        ins = nc.tensor.matmul(pSum[s][:, SEQ + t * P:SEQ + (t + 1) * P], yT[:, t * P:(t + 1) * P], w["wo"], start=True, stop=True)
                    ins.then_inc(out_psum, 1)

                def step(b, s, first, last):
                    for j in range(SCAN_CHUNKS):
                        c_rows(b, j)
                        if j >= 2:
                            if j == 2 and not known(b, 2):
                                pe.wait_ge(added, b - 1)
                            add_up(b, s, j - 2)
                        elif not first:
                            add_up(b - 1, 1 - s, SCAN_CHUNKS - 2 + j)
                        if j == 3 and not first:
                            put_out(b - 1, 1 - s)
                    if last:
                        add_up(b, s, SCAN_CHUNKS - 2)
                        add_up(b, s, SCAN_CHUNKS - 1)
                        put_out(b, s)

                sequences(pe, step)

            @block.scalar
            def _(a):
                nc.scalar.activation(pos_a[:, :], w["a_log"], ACT.Exp).then_inc(set_up, 1)
                a.wait_ge(set_up, 2)

                def decays(b, s, j):
                    a.wait_ge(prev_ready, b + 1)
                    if not known(b, 1):
                        a.wait_ge(scanned, (b - 1) * SCAN_CHUNKS + j + 1)
                    for n in range(j * CHN, (j + 1) * CHN):
                        ins = nc.scalar.activation(decay[:, n, :], prev[:, s, 0, :], ACT.Exp, scale=neg_a[:, n:n + 1])
                    ins.then_inc(decay_ready, 1)
                    if j < BY_ACT:
                        a.wait_ge(du_made, b + 1)
                        for n in range(j * CHN, (j + 1) * CHN):
                            ins = nc.scalar.activation(du_small[:, n, :], du[:, s, :], ACT.Copy, scale=small[:, n:n + 1])
                        ins.then_inc(small_by_act, 1)

                def step(b, s, first, last):
                    if first:
                        for j in range(SCAN_CHUNKS):
                            decays(b, s, j)
                    for j in range(SCAN_CHUNKS):
                        for i in range(2 * j, 2 * j + 2):
                            a.wait_ge(c_psum, b * 2 * SCAN_CHUNKS + i + 1)
                            if i % 2 == 0 and not first:
                                a.wait_ge(times_c, (b - 1) * SCAN_CHUNKS + j + 1)
                            nc.scalar.copy(c_all[:, 2 * i:2 * i + 2, :], pC[i % 2][:, :].rearrange("p (n s) -> p n s", n=2)).then_inc(c_ready, 1)
                        if not last:
                            decays(b + 1, 1 - s, j)

                sequences(a, step)

            @block.vector
            def _(v):
                c = Chain(v, setup_chain)
                v.wait_ge(set_up, 1)
                c.link(nc.vector.tensor_scalar(neg_a[:, :], pos_a[:, :], -1.0, None, ALU.mult))
                c.link(nc.vector.tensor_scalar(small[:, :], pos_a[:, :], 1e-5, None, ALU.is_lt))
                c.link(nc.vector.tensor_scalar(den[:, :], neg_a[:, :], 1e-10, None, ALU.add))
                c.link(nc.vector.tensor_tensor(den[:, :], den[:, :], small[:, :], ALU.add))
                c.link(nc.vector.reciprocal(den[:, :], den[:, :]))
                c.link(nc.vector.tensor_scalar(inv_a[:, :], small[:, :], -1.0, 1.0, ALU.mult, ALU.add))
                nc.vector.tensor_tensor(inv_a[:, :], inv_a[:, :], den[:, :], ALU.mult).then_inc(set_up, 1)
                v.wait_ge(set_up, 2)

                def enter(b, s, j):
                    part = slice(j * CHN, (j + 1) * CHN)
                    v.wait_ge(decay_ready, b * SCAN_CHUNKS + j + 1)
                    nc.vector.scalar_tensor_tensor(h[s][:, part, :], decay[:, part, :], -1.0, bc(prev[:, s, 1, :], 1, CHN), ALU.add,
                                                   ALU.mult).then_inc(entered, 1)
                    v.wait_ge(entered, b * SCAN_CHUNKS + j + 1)
                    nc.vector.memset(decay[:, part, 0:1], 0.0).then_inc(zeroed, 1)
                    if j < BY_ACT:
                        v.wait_ge(small_by_act, b * BY_ACT + j + 1)
                    else:
                        v.wait_ge(small_by_pool, b + 1)
                    for n in range(j * CHN, (j + 1) * CHN):
                        ins = nc.vector.scalar_tensor_tensor(h[s][:, n, :], h[s][:, n, :], inv_a[:, n:n + 1], du_small[:, n, :], ALU.mult, ALU.add)
                    ins.then_inc(shrunk, 1)

                def scan(b, s, j):
                    v.wait_ge(shrunk, b * SCAN_CHUNKS + j + 1)
                    v.wait_ge(zeroed, b * SCAN_CHUNKS + j + 1)
                    flat = lambda t: t[:, j * CHN:(j + 1) * CHN, :].rearrange("p n s -> p (n s)")
                    nc.vector.tensor_tensor_scan(flat(h[s]), flat(decay), flat(h[s]), 0.0, ALU.mult, ALU.add).then_inc(scanned, 1)

                def gated(b, s):
                    cols = bass.ds(b * SEQ, SEQ)
                    v.wait_ge(sum_psum, b + 1)
                    nc.vector.scalar_tensor_tensor(yT[:, :], u[:, cols], w["skip"], pSum[s][:, 0:SEQ], ALU.mult, ALU.add).then_inc(skip_added, 1)
                    v.wait_ge(skip_added, b + 1)
                    nc.vector.tensor_tensor(yT[:, :], yT[:, :], gate[:, cols], ALU.mult).then_inc(y_ready, 1)

                def add(b, s):
                    v.wait_ge(out_psum, b + 1)
                    x = core.x_res[:, bass.ds(b * 2, 2), :]
                    nc.vector.tensor_tensor(x, x, pSum[s][:, SEQ:2 * SEQ].rearrange("p (t d) -> p t d", t=2), ALU.add).then_inc(added, 1)

                def step(b, s, first, last):
                    for j in range(SCAN_CHUNKS):
                        enter(b, s, j)
                        scan(b, s, j)
                        if j == 0 and not known(b, 2):
                            add(b - 2, s)
                        if j == 2 and not first:
                            gated(b - 1, 1 - s)
                    if last:
                        add(b - 1, 1 - s)
                        gated(b, s)
                        add(b, s)

                sequences(v, step)


ATTN_A2_HD = D // HEADS
BD = 16
WINDOW = 64
PAD = WINDOW - 1
HALF = P // BD
SLOTS = P // HEADS
ROWS = WINDOW // SLOTS
KINDS = 2


def attn_a2_weights(w):
    def place(out_w):
        a = np.zeros((HALF, BD, 2, 2, 2, HEADS), np.float32)
        for slot in range(2):
            for half in range(2):
                for h in range(HALF):
                    a[h, :, slot, half, slot, half * HALF + h] = out_w.reshape(BD)
        return a.reshape(P, -1)

    def diag(m):
        a = np.zeros((HALF, BD, HALF, BD), np.float32)
        for h in range(HALF):
            a[h, :, h, :] = m
        return a.reshape(P, P)

    slot, head = np.arange(P) // HEADS, np.arange(P) % HEADS
    to_head = np.arange(D) // ATTN_A2_HD
    spread = [((slot[:, None] == s) & (head[:, None] == to_head[None, :])).astype(np.float32) for s in range(SLOTS)]
    seen = np.where(np.arange(SLOTS)[None, :] >= slot[:, None], np.float32(0.0), np.float32(NEG))
    strain, b = w["strain_fused_w"], w["strain_fused_b"]
    tall = lambda a: np.broadcast_to(a.reshape(1, 1), (P, 1))
    return pack([
        ("disp", w["W_disp"].T), ("val", w["W_val"].T), ("out", w["c_proj_w"].T),
        ("strain", np.concatenate([diag(strain[0:BD].T), diag(strain[BD:].T)], axis=1)),
        ("bond_b", np.tile(b[0:BD], HALF)), ("damage_b", np.tile(b[BD:], HALF)), ("damage_out_b", tall(w["damage_out_b"])),
        ("pos_proj", np.tile(w["pos_proj_w"].T, (1, HALF))), ("pos_emb", w["rel_pos_emb"][::-1].T),
        ("place", np.concatenate([place(w["bond_out_w"]), place(w["damage_out_w"])], axis=1)),
        ("spread", np.concatenate(spread + [sum(spread)], axis=1)),
        ("seen", seen),
    ])


def attn_a2(core, blob, offsets):
    nc = core.nc
    GROUPS = TOK // BANK
    with Stage(core, "attn_a2") as st:
        w = st.weights(blob, offsets)
        layer_norm(core, st)
        bank = [st.ps(f"bank{i}", [P, BANK]) for i in range(8)]
        feat = st.sb("feat", [P, KINDS, 2, BATCH, SEQ])
        val = st.sb("val", [P, BATCH, SEQ])
        lag_b = st.sb("lag_b", [P, WINDOW])
        half_out_b = st.sb("half_out_b", [P, 1])
        two = lambda ap: ap.rearrange("p (b s) -> p b s", b=2)

        disp = st.sb("disp", [P, 2, BANK])
        names = ("disp_psum", "disp_ready", "feat_psum", "feat_ready", "val_psum", "val_ready", "pos_psum", "misc")
        disp_psum, disp_ready, feat_psum, feat_ready, val_psum, val_ready, pos_psum, misc = (st.sem(n) for n in names)
        with nc.Block() as block:
            @block.tensor
            def _(pe):
                nc.tensor.matmul(bank[7][:, 0:WINDOW], w["pos_proj"], w["pos_emb"], start=True, stop=True).then_inc(pos_psum, 1)
                pe.sem_inc(feat_psum, 1)
                with pe.Fori(0, GROUPS) as g:
                    x = core.xnT[:, bass.ds(g * BANK, BANK)]
                    for half in range(2):
                        nc.tensor.matmul(bank[half][:, :], w["disp"][:, half * P:(half + 1) * P], x, start=True, stop=True).then_inc(disp_psum, 1)
                    pe.wait_ge(val_ready, g + 1)
                    nc.tensor.matmul(bank[2][:, :], w["val"], x, start=True, stop=True).then_inc(val_psum, 1)
                    for half in range(2):
                        pe.wait_ge(disp_ready, 2 * g + half + 1)
                        pe.wait_ge(feat_ready, 2 * g + 1)
                        for kind in range(KINDS):
                            ins = nc.tensor.matmul(bank[3 + 2 * half + kind][:, :], w["strain"][:, kind * P:(kind + 1) * P], disp[:, half, :], start=True, stop=True)
                        ins.then_inc(feat_psum, 1)

            @block.scalar
            def _(a):
                a.sem_inc(val_ready, 1)
                with a.Fori(0, GROUPS) as g:
                    for half in range(2):
                        a.wait_ge(disp_psum, 2 * g + half + 1)
                        a.wait_ge(feat_psum, 2 * g + 1)
                        nc.scalar.copy(disp[:, half, :], bank[half][:, :]).then_inc(disp_ready, 1)
                    a.wait_ge(val_psum, g + 1)
                    nc.scalar.copy(val[:, bass.ds(2 * g, 2), :], two(bank[2][:, :])).then_inc(val_ready, 1)

            @block.vector
            def _(v):
                nc.vector.tensor_scalar(half_out_b[:, :], w["damage_out_b"], 0.5, None, ALU.mult)
                v.wait_ge(pos_psum, 1)
                nc.vector.tensor_scalar(lag_b[:, :], bank[7][:, 0:WINDOW], w["bond_b"], None, ALU.add)
                v.sem_inc(feat_ready, 1)
                with v.Fori(0, GROUPS) as g:
                    for half in range(2):
                        v.wait_ge(feat_psum, 2 * g + half + 2)
                        for kind in range(KINDS):
                            ins = nc.vector.tensor_copy(feat[:, kind, half, bass.ds(2 * g, 2), :], two(bank[3 + 2 * half + kind][:, :]))
                        ins.then_inc(feat_ready, 1)

        logit = core.xn[:, :, :].rearrange("p t d -> p (t d)").rearrange("p (r s) -> p r s", r=ROWS)
        RING = 8
        more = st.sb("more", [P, 4, 2, 2, SEQ])
        first_half = core.xnT[:, :].rearrange("p (i h b s) -> p i h b s", i=4, h=2, b=2)
        ring = lambda i, n=1: (first_half if i % RING < 4 else more)[:, i % 4:i % 4 + n]
        tanh_out = disp
        feat_now = st.sb("feat_now", [P, KINDS, 2, 2, PAD + SEQ])
        val_now = st.sb("val_now", [P, 2, PAD + SEQ])
        prob = st.sb("prob", [P, ROWS, BANK])
        product = st.sb("product", [P, 4, BANK])
        slot_max, acc, inv, oT = (st.sb(n, [P, BANK]) for n in ("slot_max", "acc", "inv", "oT"))
        neg_max = st.sb("neg_max", [P, 4, HEADS])
        neg_max_wide = st.sb("neg_max_wide", [P, 4, SLOTS, HEADS])
        p_bond, p_damage, p_wide, p_max, p_x = bank[0:2], bank[2:4], bank[4:6], bank[6], bank[7]
        names = ("padded", "feat_by_act", "feat_by_dve", "val_copied", "diff_v", "diff_p", "gelu_ready", "placed", "tanh_ready", "combined", "masked",
                 "slot_max_ready", "max_psum", "neg_max_done", "neg_max_ready", "neg_max_psum", "shifted", "prob_ready", "den_psum", "wide_even", "wide_odd",
                 "weighted_even", "weighted_odd", "summed", "inv_ready", "oT_ready", "y_ready", "added")
        (padded, feat_by_act, feat_by_dve, val_copied, diff_v, diff_p, gelu_ready, placed, tanh_ready, combined, masked,
         slot_max_ready, max_psum, neg_max_done, neg_max_ready, neg_max_psum, shifted, prob_ready, den_psum, wide_even, wide_odd,
         weighted_even, weighted_odd, summed, inv_ready, oT_ready, y_ready, added) = (st.sem(n) for n in names)
        pairs = [(row, slot, slot + 2) for row in range(ROWS) for slot in range(SLOTS) if slot % 4 < 2]
        units = [(row, slots, kind) for row, *slots in pairs for kind in range(KINDS)]
        UNITS = len(units)
        PER_ROW = UNITS // ROWS
        RING_UNITS = RING // 2
        reach = lambda row: slice(row * SLOTS, SEQ)
        N_DIFF_V, N_DIFF_P = 3 * len(pairs), len(pairs)
        wide_psum, weighted = (wide_even, wide_odd), (weighted_even, weighted_odd)
        LAGS = WINDOW // 2
        PARTS = 4
        BEHIND = 3
        BESIDE = 48
        beside = lambda u: range(u * BESIDE // UNITS, (u + 1) * BESIDE // UNITS)
        MIDDLE = (BESIDE + WINDOW) // 2

        def difference(eng, u, n, row, slot, kind):
            both = feat_now[:, kind].rearrange("p h b s -> p (h b) s")
            lag, at = row * SLOTS + slot, PAD + row * SLOTS
            return eng.tensor_tensor(ring(2 * u + n)[:, 0].rearrange("p h b s -> p (h b) s")[:, :, reach(row)],
                                     both[:, :, at - lag:PAD - lag + SEQ], both[:, :, at:PAD + SEQ], ALU.subtract)

        def groups(eng, logits, lag, finish, before_last=lambda: None):
            logits(0, lambda l: None, lambda *part: None)
            with eng.Fori(1, GROUPS) as g:
                logits(g, lambda l: lag(g - 1, l), lambda *part: finish(g - 1, *part))
            before_last()
            for l in range(WINDOW):
                lag(GROUPS - 1, l)
            finish(GROUPS - 1)

        def later(g):
            return not isinstance(g, int) or g > 0

        with nc.Block() as block:
            @block.tensor
            def _(pe):
                pe.sem_inc(placed, RING_UNITS)

                def logits(g, lag, finish):
                    for u, (row, slots, kind) in enumerate(units):
                        if u % PER_ROW == 0:
                            pe.wait_ge(combined, g * ROWS + row + 1)
                        pe.wait_ge(gelu_ready, g * UNITS + u + 1)
                        for half in range(2):
                            for n, slot in enumerate(slots):
                                at = ((kind * 2 + slot % 2) * 2 + half) * 32
                                part = slice(slot // 2 * 32, (slot // 2 + 1) * 32)
                                ins = nc.tensor.matmul(two((p_bond, p_damage)[kind][row % 2][part, :])[:, :, reach(row)], w["place"][:, at:at + 32],
                                                       ring(2 * u + n)[:, 0, half, :, reach(row)],
                                                       start=(slot % 2 == 0 and half == 0), stop=(slot % 2 == 1 and half == 1),
                                                       tile_position=(0, part.start))
                        ins.then_inc(placed, 1)
                        for l in beside(u):
                            lag(l)
                    pe.wait_ge(slot_max_ready, g + 1)
                    if later(g):
                        pe.wait_ge(inv_ready, g)
                    for t in range(4):
                        ins = nc.tensor.transpose(p_max[:, t * P:(t + 1) * P], slot_max[:, t * P:(t + 1) * P], core.ident[:, :])
                    ins.then_inc(max_psum, 1)
                    for l in range(BESIDE, MIDDLE):
                        lag(l)
                    pe.wait_ge(neg_max_ready, g + 1)
                    for t in range(4):
                        ins = nc.tensor.matmul(p_x[:, t * P:(t + 1) * P], neg_max_wide[:, t, :, :].rearrange("p s h -> p (s h)"), core.ident[:, :],
                                               start=True, stop=True)
                    ins.then_inc(neg_max_psum, 1)
                    for l in range(MIDDLE, WINDOW):
                        lag(l)
                    for row in range(ROWS):
                        pe.wait_ge(prob_ready, g * PARTS + row * PARTS // ROWS + 1)
                        ins = nc.tensor.matmul(two(p_max[:, :])[:, :, reach(row)], w["spread"][:, SLOTS * D:(SLOTS + 1) * D], two(prob[:, row, :])[:, :, reach(row)],
                                               start=(row == 0), stop=(row == ROWS - 1))
                    ins.then_inc(den_psum, 1)
                    finish()

                def lag(g, l):
                    slot, row = l % SLOTS, l // SLOTS
                    pe.wait_ge(weighted[l % 2], g * LAGS + l // 2 + 1)
                    nc.tensor.matmul(two(p_wide[l % 2][:, :])[:, :, reach(row)], w["spread"][:, slot * D:(slot + 1) * D], two(prob[:, row, :])[:, :, reach(row)],
                                     start=True, stop=True).then_inc(wide_psum[l % 2], 1)

                def finish(g):
                    pe.wait_ge(oT_ready, g + 2)
                    for t in range(4):
                        ins = nc.tensor.matmul(p_x[:, t * P:(t + 1) * P], oT[:, t * P:(t + 1) * P], w["out"], start=True, stop=True)
                    ins.then_inc(y_ready, 1)

                groups(pe, logits, lag, finish)

            @block.scalar
            def _(a):
                def logits(g, lag, finish):
                    if later(g):
                        a.wait_ge(diff_v, g * N_DIFF_V)
                        a.wait_ge(diff_p, g * N_DIFF_P)
                    a.wait_ge(padded, 2)
                    nc.scalar.copy(feat_now[:, 1, :, :, PAD:].rearrange("p h b s -> p (h b) s"),
                                   feat[:, 1, :, bass.ds(2 * g, 2), :]).then_inc(feat_by_act, 1)

                    def tanh(row):
                        a.wait_ge(placed, g * UNITS + (row + 1) * PER_ROW + RING_UNITS)
                        a.wait_ge(combined, g * ROWS + row + 1)
                        nc.scalar.activation(two(tanh_out[:, row % 2, :])[:, :, reach(row)], two(p_damage[row % 2][:, :])[:, :, reach(row)],
                                             ACT.Tanh, bias=half_out_b[:, :], scale=0.5).then_inc(tanh_ready, 1)

                    for u, (row, slots, kind) in enumerate(units):
                        pair = u // 2
                        a.wait_ge(diff_v, g * N_DIFF_V + 3 * pair + (2, 3)[kind])
                        if kind == 0:
                            for n, slot in enumerate(slots):
                                x = ring(2 * u + n)[:, 0].rearrange("p h b s -> p (h b) s")[:, :, reach(row)]
                                shift = row * SLOTS + slot
                                ins = nc.scalar.activation(x, x, ACT.Gelu, bias=lag_b[:, shift:shift + 1])
                        else:
                            a.wait_ge(diff_p, g * N_DIFF_P + pair + 1)
                            x = ring(2 * u, 2).rearrange("p i h b s -> p (i h b) s")[:, :, reach(row)]
                            ins = nc.scalar.activation(x, x, ACT.Gelu, bias=w["damage_b"])
                        ins.then_inc(gelu_ready, 1)
                        if row > 0 and u % PER_ROW == 1:
                            tanh(row - 1)
                    tanh(ROWS - 1)
                    if later(g):
                        for parity in range(2):
                            a.wait_ge(wide_psum[parity], g * LAGS)
                    for j in range(PARTS):
                        rows = slice(j * ROWS // PARTS, (j + 1) * ROWS // PARTS)
                        a.wait_ge(shifted, g * PARTS + j + 1)
                        nc.scalar.activation(prob[:, rows, :], logit[:, rows, :], ACT.Exp).then_inc(prob_ready, 1)

                groups(a, logits, lambda g, l: None, lambda g: None)

            @block.gpsimd
            def _(pool):
                nc.gpsimd.memset(feat_now[:, :, :, :, 0:PAD].rearrange("p k h b s -> p (k h b) s"), 0.0).then_inc(padded, 1)
                nc.gpsimd.memset(val_now[:, :, 0:PAD], 0.0).then_inc(padded, 1)
                for row in range(1, ROWS):
                    ins = nc.gpsimd.memset(two(logit[:, row, :])[:, :, 0:row * SLOTS], NEG)
                ins.then_inc(masked, 1)

                def logits(g, lag, finish):
                    def mask(row):
                        pool.wait_ge(combined, g * ROWS + row + 3)
                        x = two(logit[:, row, :])[:, :, row * SLOTS:(row + 1) * SLOTS]
                        nc.gpsimd.tensor_tensor(x, x, bc(w["seen"], 1, 2), ALU.add).then_inc(masked, 1)

                    pool.wait_ge(feat_by_act, g + 1)
                    for u, (row, slots, kind) in enumerate(units):
                        if kind == 1:
                            pool.wait_ge(placed, g * UNITS + u + 1)
                            difference(nc.gpsimd, u, 1, row, slots[1], kind).then_inc(diff_p, 1)
                        if row > 0 and u % PER_ROW == 5:
                            mask(row - 1)
                        if u >= BEHIND + 2:
                            for l in beside(u - BEHIND - 2):
                                lag(l)
                    for l in range(beside(UNITS - BEHIND - 2).start, BESIDE):
                        lag(l)
                    mask(ROWS - 1)
                    for l in range(BESIDE, WINDOW):
                        lag(l)

                def lag(g, l):
                    part = lambda x: two(x)[:, :, reach(l // SLOTS)]
                    pool.wait_ge(weighted[l % 2], g * LAGS + l // 2 + 2)
                    if l == 0:
                        pool.wait_ge(oT_ready, g + 1)
                        by_p = lambda x: x.rearrange("p (t q) -> p t q", q=P)
                        nc.gpsimd.tensor_tensor(by_p(acc[:, :]), by_p(product[:, 0, :]), bc(core.ones[:, :], 1, BANK // P), ALU.mult).then_inc(summed, 1)
                        return
                    pool.wait_ge(summed, g * WINDOW + l)
                    nc.gpsimd.tensor_tensor(part(acc[:, :]), part(acc[:, :]), part(product[:, l % 4, :]), ALU.add).then_inc(summed, 1)

                groups(pool, logits, lag, lambda g: None)

            @block.vector
            def _(v):
                v.sem_inc(combined, 2)
                v.sem_inc(oT_ready, 1)
                v.sem_inc(weighted_even, 1)
                v.sem_inc(weighted_odd, 1)
                v.wait_ge(padded, 2)

                def logits(g, lag, finish):
                    if later(g):
                        v.wait_ge(diff_p, g * N_DIFF_P)
                        v.wait_ge(diff_v, g * N_DIFF_V)
                    nc.vector.tensor_copy(feat_now[:, 0, :, :, PAD:].rearrange("p h b s -> p (h b) s"),
                                          feat[:, 0, :, bass.ds(2 * g, 2), :]).then_inc(feat_by_dve, 1)
                    if later(g):
                        nc.vector.tensor_copy(val_now[:, :, PAD:], val[:, bass.ds(2 * g - 2, 2), :]).then_inc(val_copied, 1)
                    v.wait_ge(feat_by_dve, g + 1)
                    v.wait_ge(feat_by_act, g + 1)
                    if later(g):
                        v.wait_ge(val_copied, g)

                    def combine(row):
                        v.wait_ge(tanh_ready, g * ROWS + row + 1)
                        part = lambda x: two(x)[:, :, reach(row)]
                        nc.vector.scalar_tensor_tensor(part(logit[:, row, :]), part(tanh_out[:, row % 2, :]), -5.0, part(p_bond[row % 2][:, :]), ALU.mult, ALU.add).then_inc(combined, 1)

                    for u, (row, slots, kind) in enumerate(units):
                        v.wait_ge(placed, g * UNITS + u + 1)
                        for n, slot in enumerate(slots):
                            if kind == 0 or n == 0:
                                difference(nc.vector, u, n, row, slot, kind).then_inc(diff_v, 1)
                        if row > 0 and u % PER_ROW == 3:
                            combine(row - 1)
                        if u >= BEHIND:
                            for l in beside(u - BEHIND):
                                lag(l)
                    for l in range(beside(UNITS - BEHIND).start, BESIDE):
                        lag(l)
                    combine(ROWS - 1)
                    v.wait_ge(masked, (g + 1) * ROWS + 1)
                    nc.vector.tensor_reduce(slot_max[:, :], logit.rearrange("p r s -> p s r"), AX.X, ALU.max).then_inc(slot_max_ready, 1)
                    for l in range(BESIDE, MIDDLE):
                        lag(l)
                    v.wait_ge(max_psum, g + 1)
                    by_head = p_max[:, :].rearrange("p (t s h) -> p t h s", t=4, s=SLOTS)
                    nc.vector.tensor_reduce(neg_max[:, :, :], by_head, AX.X, ALU.max, negate=True).then_inc(neg_max_done, 1)
                    v.wait_ge(neg_max_done, g + 1)
                    nc.vector.tensor_copy(neg_max_wide[:, :, :, :], bc(neg_max[:, :, :], 2, SLOTS)).then_inc(neg_max_ready, 1)
                    for l in range(MIDDLE, WINDOW):
                        lag(l)
                    v.wait_ge(neg_max_psum, g + 1)
                    for j in range(PARTS):
                        rows = slice(j * ROWS // PARTS, (j + 1) * ROWS // PARTS)
                        nc.vector.tensor_tensor(logit[:, rows, :], logit[:, rows, :], bc(p_x[:, :], 1, ROWS // PARTS), ALU.add).then_inc(shifted, 1)
                    finish(0)
                    v.wait_ge(den_psum, g + 1)
                    if later(g):
                        v.wait_ge(oT_ready, g + 1)
                    nc.vector.reciprocal(inv[:, :], p_max[:, :]).then_inc(inv_ready, 1)
                    finish(1)

                def lag(g, l):
                    v.wait_ge(wide_psum[l % 2], g * LAGS + l // 2 + 1)
                    if l >= 4:
                        v.wait_ge(summed, g * WINDOW + l - 3)
                    start = l // SLOTS * SLOTS
                    part = lambda x: two(x)[:, :, start:]
                    nc.vector.tensor_tensor(part(product[:, l % 4, :]), part(p_wide[l % 2][:, :]), val_now[:, :, PAD - l + start:PAD - l + SEQ],
                                            ALU.mult).then_inc(weighted[l % 2], 1)

                def finish(g, *parts):
                    if 0 in (parts or (0,)):
                        v.wait_ge(summed, (g + 1) * WINDOW)
                        v.wait_ge(inv_ready, g + 1)
                        nc.vector.tensor_tensor(oT[:, :], acc[:, :], inv[:, :], ALU.mult).then_inc(oT_ready, 1)
                    if 1 in (parts or (1,)):
                        v.wait_ge(y_ready, g + 1)
                        x = core.x_res[:, bass.ds(4 * g, 4), :]
                        nc.vector.tensor_tensor(x, x, p_x[:, :].rearrange("p (t d) -> p t d", t=4), ALU.add).then_inc(added, 1)

                def last_values():
                    for parity in range(2):
                        v.wait_ge(weighted[parity], (GROUPS - 1) * LAGS + 1)
                    nc.vector.tensor_copy(val_now[:, :, PAD:], val[:, BATCH - 2:BATCH, :]).then_inc(val_copied, 1)
                    v.wait_ge(val_copied, GROUPS)

                groups(v, logits, lag, finish, last_values)


FFN2_EXPERTS = 8
FFN2_TOP = 2
FFN2_HID = 2 * D
CH = FFN2_HID // P


def ffn2_weights(w):
    return pack([
        ("router", w["router_w"].T), ("earlier", earlier_table(FFN2_EXPERTS)),
        ("w1", w["w1"].transpose(2, 0, 1).reshape(D, FFN2_EXPERTS * FFN2_HID)),
        ("w2", w["w2"].transpose(2, 0, 1).reshape(CH, P, FFN2_EXPERTS, D).transpose(1, 2, 0, 3).reshape(P, FFN2_EXPERTS * FFN2_HID)),
    ])


def ffn2(core, blob, offsets):
    nc = core.nc
    GROUPS = TOK // BANK
    with Stage(core, "ffn2") as st:
        w = st.weights(blob, offsets)
        layer_norm(core, st)
        w1 = w["w1"].rearrange("p (e c h) -> p e c h", e=FFN2_EXPERTS, c=CH)
        w2 = w["w2"].rearrange("p (e c d) -> p e c d", e=FFN2_EXPERTS, c=CH)
        bank = [st.ps(f"bank{i}", [P, BANK]) for i in range(8)]
        logit_psum = bank[0][:, 0:TILES * FFN2_EXPERTS].rearrange("p (t e) -> p t e", t=TILES)
        router_logits(core, w["router"], lambda t: logit_psum[:, bass.ds(t, 1), :].squeeze(1), FFN2_EXPERTS, st)

        gate = st.sb("gate", [P, TILES, FFN2_EXPERTS])
        logit, sel, rank = (st.sb(n, [P, TILES, FFN2_EXPERTS]) for n in ("logit", "sel", "rank"))
        above, same = (st.sb(n, [P, TILES, FFN2_EXPERTS, FFN2_EXPERTS]) for n in ("above", "same"))
        best, total = st.sb("best", [P, TILES]), st.sb("total", [P, TILES])
        dve, centred, exp_ready = st.sem("dve"), st.sem("centred"), st.sem("exp_ready")
        with nc.Block() as block:
            @block.vector
            def _(v):
                c = Chain(v, dve)
                c.link(nc.vector.tensor_copy(logit[:, :, :], logit_psum))
                c.link(nc.vector.tensor_reduce(best[:, :], logit[:, :, :], AX.X, ALU.max))
                nc.vector.tensor_tensor(gate[:, :, :], logit[:, :, :], bc(best[:, :], 2, FFN2_EXPERTS), ALU.subtract).then_inc(centred, 1)
                link_ranks(nc, c, rank[:, :, :], logit[:, :, :], above[:, :, :, :], same[:, :, :, :], w["earlier"], FFN2_EXPERTS)
                c.link(nc.vector.tensor_scalar(sel[:, :, :], rank[:, :, :], float(FFN2_TOP), None, ALU.is_lt))
                v.wait_ge(exp_ready, 1)
                c.link(nc.vector.tensor_tensor(gate[:, :, :], gate[:, :, :], sel[:, :, :], ALU.mult))
                c.link(nc.vector.tensor_reduce(total[:, :], gate[:, :, :], AX.X, ALU.add))
                c.link(nc.vector.reciprocal(total[:, :], total[:, :]))
                nc.vector.tensor_tensor(gate[:, :, :], gate[:, :, :], bc(total[:, :], 2, FFN2_EXPERTS), ALU.mult)

            @block.scalar
            def _(a):
                a.wait_ge(centred, 1)
                nc.scalar.activation(gate[:, :, :], gate[:, :, :], ACT.Exp).then_inc(exp_ready, 1)

        hid = st.sb("hid", [P, 2, CH, BANK])
        up_ready, hid_ready, y_ready, added, up_free, y_free = (st.sem(n) for n in ("up_ready", "hid_ready", "y_ready", "added", "up_free", "y_free"))
        with nc.Block() as block:
            @block.tensor
            def _(pe):
                with pe.Fori(0, GROUPS) as g:
                    n0 = g * FFN2_EXPERTS
                    x = core.xnT[:, bass.ds(g * BANK, BANK)]

                    def up(e):
                        for k in range(CH):
                            ins = nc.tensor.matmul(bank[2 * (e % 2) + k][:, :], w1[:, e, k, :], x, start=True, stop=True)
                        ins.then_inc(up_ready, 1)

                    def down(e):
                        pe.wait_ge(hid_ready, n0 + e + 1)
                        pe.wait_ge(y_free, n0 + e + 1)
                        for t in range(4):
                            for k in range(CH):
                                ins = nc.tensor.matmul(bank[4 + e % 2][:, t * P:(t + 1) * P], hid[:, e % 2, k, t * P:(t + 1) * P], w2[:, e, k, :],
                                                       start=(k == 0), stop=(k == CH - 1))
                        ins.then_inc(y_ready, 1)

                    up(0)
                    up(1)
                    for e in range(FFN2_EXPERTS):
                        down(e)
                        if e + 2 < FFN2_EXPERTS:
                            up(e + 2)

            @block.scalar
            def _(a):
                with a.Fori(0, GROUPS) as g:
                    for e in range(FFN2_EXPERTS):
                        a.wait_ge(up_ready, g * FFN2_EXPERTS + e + 1)
                        for k in range(CH):
                            ins = nc.scalar.activation(hid[:, e % 2, k, :], bank[2 * (e % 2) + k][:, :], ACT.Gelu)
                        ins.then_inc(hid_ready, 1)

            @block.vector
            def _(v):
                v.sem_inc(y_free, 2)
                with v.Fori(0, GROUPS) as g:
                    for e in range(FFN2_EXPERTS):
                        v.wait_ge(y_ready, g * FFN2_EXPERTS + e + 1)
                        if e > 0:
                            v.wait_ge(y_free, g * FFN2_EXPERTS + e + 2)
                        for t in range(4):
                            x = core.x_res[:, bass.ds(g * 4 + t, 1), :].squeeze(1)
                            ins = nc.vector.scalar_tensor_tensor(x, bank[4 + e % 2][:, t * P:(t + 1) * P],
                                                                 gate[:, bass.ds(g * 4 + t, 1), e:e + 1].squeeze(1), x, ALU.mult, ALU.add)
                        ins.then_inc(y_free, 1)


def attn_b2_weights(w):
    return pack([
        ("wq", w["Wq"]), ("wk", w["Wk"]), ("wv", w["Wv"]), ("wo", w["Wo"]),
        ("bq", w["bq"]), ("bk", w["bk"]), ("bv", np.broadcast_to(w["bv"], (P, D))), ("bo", w["bo"][None, :]),
    ])


def attn_b2(core, blob, offsets):
    nc = core.nc
    T = SEQ // P
    with Stage(core, "attn_b2") as st:
        w = st.weights(blob, offsets)
        layer_norm(core, st)
        bank = [st.ps(f"bank{i}", [P, BANK]) for i in range(8)]
        x_now = st.sb("x_now", [P, 2, SEQ])
        q, k2 = st.sb("q", [P, 2, SEQ]), st.sb("k2", [P, 2, SEQ])
        qk_sq = st.sb("qk_sq", [P, 2, 2, SEQ])
        val = st.sb("val", [P, 2, T, D])
        neg_ones = st.sb("neg_ones", [P, P])
        score = st.sb("score", [P, 2, T, SEQ])
        neg_max = st.sb("neg_max", [P, 2, T])
        prob = st.sb("prob", [P, 2, T, SEQ])
        row_sum, inv = st.sb("row_sum", [P, 2, T]), st.sb("inv", [P, 2, T])
        probT = st.sb("probT", [P, 2, T, SEQ])
        o_tok = st.sb("o_tok", [P, 2, T, D])
        oT = st.sb("oT", [P, 2, SEQ])
        p_qk, p_dist, p_probT, p_mixed = bank[0:2], bank[2:4], bank[4:6], bank[6:8]
        p_v = p_oT = lambda s: p_mixed[s][:, 0:T * D]
        p_o = p_y = lambda s: p_mixed[s][:, T * D:2 * T * D]
        names = ("x_copied", "qk_psum", "v_psum", "qk_ready", "sq_ready", "v_ready", "dist_ready", "score_ready", "max_ready", "prob_ready",
                 "probT_psum", "probT_ready", "o_psum", "inv_ready", "o_ready", "oT_psum", "oT_ready", "y_ready", "y_added")
        (x_copied, qk_psum, v_psum, qk_ready, sq_ready, v_ready, dist_ready, score_ready, max_ready, prob_ready,
         probT_psum, probT_ready, o_psum, inv_ready, o_ready, oT_psum, oT_ready, y_ready, y_added) = ([st.sem(f"{n}{s}") for s in range(2)] for n in names)
        set_up = st.sem("set_up")
        tiled = lambda ap: ap.rearrange("p (t d) -> p t d", t=T)

        with nc.Block() as block:
            @block.gpsimd
            def _(pool):
                nc.gpsimd.memset(neg_ones[:, :], -1.0).then_inc(set_up, 1)

                def x_copy(n, s):
                    pool.wait_ge(v_psum[s], n + 1)
                    nc.gpsimd.tensor_copy(x_now[:, s, :], core.xnT[:, bass.ds((2 * n + s) * SEQ, SEQ)]).then_inc(x_copied[s], 1)

                in_pairs(pool, x_copy)

            @block.tensor
            def _(pe):
                for s in range(2):
                    pe.sem_inc(v_psum[s], 1)
                pe.wait_ge(set_up, 1)

                def project(n, s):
                    pe.wait_ge(x_copied[s], n + 1)
                    nc.tensor.matmul(p_qk[s][:, 0:SEQ], w["wq"], x_now[:, s, :], start=True, stop=True)
                    nc.tensor.matmul(p_qk[s][:, SEQ:2 * SEQ], w["wk"], x_now[:, s, :], start=True, stop=True).then_inc(qk_psum[s], 1)
                    pe.wait_ge(y_added[s], n + 1)
                    for t in range(T):
                        ins = nc.tensor.matmul(p_v(s)[:, t * D:(t + 1) * D], x_now[:, s, t * P:(t + 1) * P], w["wv"], start=True, stop=True)
                    ins.then_inc(v_psum[s], 1)

                def distance(n, s):
                    pe.wait_ge(sq_ready[s], n + 1)
                    for t in range(T):
                        out = p_dist[s][:, t * SEQ:(t + 1) * SEQ]
                        nc.tensor.matmul(out, q[:, s, t * P:(t + 1) * P], k2[:, s, :], start=True, stop=False)
                        nc.tensor.matmul(out, qk_sq[:, s, 0, t * P:(t + 1) * P], neg_ones[:, 0:1].broadcast_to([P, SEQ]), start=False, stop=False)
                        ins = nc.tensor.matmul(out, neg_ones[:, :], qk_sq[:, s, 1, :], start=False, stop=True)
                    ins.then_inc(dist_ready[s], 1)

                def turn(n, s):
                    pe.wait_ge(prob_ready[s], n + 1)
                    for kt in range(T):
                        for qt in range(T):
                            ins = nc.tensor.transpose(p_probT[s][:, kt * SEQ + qt * P:kt * SEQ + (qt + 1) * P],
                                                      prob[:, s, qt, kt * P:(kt + 1) * P], core.ident[:, :])
                    ins.then_inc(probT_psum[s], 1)

                def weigh(n, s):
                    pe.wait_ge(probT_ready[s], n + 1)
                    for qt in range(T):
                        for kt in range(T):
                            ins = nc.tensor.matmul(p_o(s)[:, qt * D:(qt + 1) * D], probT[:, s, kt, qt * P:(qt + 1) * P], val[:, s, kt, :],
                                                   start=(kt == 0), stop=(kt == T - 1))
                    ins.then_inc(o_psum[s], 1)

                def turn_out(n, s):
                    pe.wait_ge(o_ready[s], n + 1)
                    for t in range(T):
                        ins = nc.tensor.transpose(p_oT(s)[:, t * P:(t + 1) * P], o_tok[:, s, t, :], core.ident[:, :])
                    ins.then_inc(oT_psum[s], 1)

                def put_out(n, s):
                    pe.wait_ge(oT_ready[s], n + 1)
                    for t in range(T):
                        y = p_y(s)[:, t * P:(t + 1) * P]
                        nc.tensor.matmul(y, core.ones[0:1, :], w["bo"][0:1, :], start=True, stop=False)
                        ins = nc.tensor.matmul(y, oT[:, s, t * P:(t + 1) * P], w["wo"], start=False, stop=True)
                    ins.then_inc(y_ready[s], 1)

                in_pairs(pe, project, distance, turn, weigh, turn_out, put_out)

            @block.scalar
            def _(a):
                def square(n, s):
                    a.wait_ge(qk_ready[s], n + 1)
                    nc.scalar.activation(qk_sq[:, s, 0, :], q[:, s, :], ACT.Square)
                    nc.scalar.activation(qk_sq[:, s, 1, :], k2[:, s, :], ACT.Square, scale=0.5).then_inc(sq_ready[s], 1)

                def kernel_of(n, s):
                    a.wait_ge(dist_ready[s], n + 1)
                    nc.scalar.activation(score[:, s, :, :], tiled(p_dist[s][:, :]), ACT.Exp).then_inc(score_ready[s], 1)

                def softmax(n, s):
                    a.wait_ge(max_ready[s], n + 1)
                    for t in range(T):
                        ins = nc.scalar.activation(prob[:, s, t, :], score[:, s, t, :], ACT.Exp, bias=neg_max[:, s, t:t + 1],
                                                   accum_out=row_sum[:, s, t:t + 1])
                    ins.then_inc(prob_ready[s], 1)

                def take_out(n, s):
                    a.wait_ge(oT_psum[s], n + 1)
                    nc.scalar.copy(oT[:, s, :], p_oT(s)).then_inc(oT_ready[s], 1)

                in_pairs(a, square, kernel_of, softmax, take_out)

            @block.vector
            def _(v):
                for s in range(2):
                    v.sem_inc(y_added[s], 1)

                def biases(n, s):
                    v.wait_ge(qk_psum[s], n + 1)
                    nc.vector.tensor_scalar(q[:, s, :], p_qk[s][:, 0:SEQ], w["bq"], None, ALU.add)
                    nc.vector.tensor_scalar(k2[:, s, :], p_qk[s][:, SEQ:2 * SEQ], w["bk"], 2.0, ALU.add, ALU.mult).then_inc(qk_ready[s], 1)
                    v.wait_ge(v_psum[s], n + 2)
                    nc.vector.tensor_tensor(val[:, s, :, :], tiled(p_v(s)), bc(w["bv"], 1, T), ALU.add).then_inc(v_ready[s], 1)

                def maximum(n, s):
                    v.wait_ge(score_ready[s], n + 1)
                    nc.vector.tensor_reduce(neg_max[:, s, :], score[:, s, :, :], AX.X, ALU.max, negate=True).then_inc(max_ready[s], 1)

                def take_turned(n, s):
                    v.wait_ge(probT_psum[s], n + 1)
                    nc.vector.tensor_copy(probT[:, s, :, :], tiled(p_probT[s][:, :])).then_inc(probT_ready[s], 1)
                    nc.vector.reciprocal(inv[:, s, :], row_sum[:, s, :]).then_inc(inv_ready[s], 1)

                def normalise(n, s):
                    v.wait_ge(inv_ready[s], n + 1)
                    v.wait_ge(o_psum[s], n + 1)
                    nc.vector.tensor_tensor(o_tok[:, s, :, :], tiled(p_o(s)), bc(inv[:, s, :], 2, D), ALU.mult).then_inc(o_ready[s], 1)

                def add(n, s):
                    v.wait_ge(y_ready[s], n + 1)
                    x = core.x_res[:, bass.ds((2 * n + s) * T, T), :]
                    nc.vector.tensor_tensor(x, x, tiled(p_y(s)), ALU.add).then_inc(y_added[s], 1)

                in_pairs(v, biases, maximum, take_turned, normalise, add)


ATTN_A3_HD = 64
ATTN_A3_CHUNKS = HEADS * ATTN_A3_HD // P
PER_OUT = 4


def attn_a3_weights(w):
    flat = lambda a: a.reshape(HEADS * ATTN_A3_HD, D).T
    col = lambda a: a.reshape(ATTN_A3_CHUNKS, P).T
    query, key = np.arange(P)[:, None], np.arange(P)[None, :]
    return pack([
        ("wq", flat(w["Wq"])), ("wk", flat(w["Wk"])), ("wv", flat(w["Wv"])),
        ("bq", col(w["bq"])), ("bk", col(w["bk"])), ("bv", np.broadcast_to(w["bv"].reshape(1, HEADS * ATTN_A3_HD), (P, HEADS * ATTN_A3_HD))),
        ("proj", w["proj"].reshape(ATTN_A3_CHUNKS, P, D).transpose(1, 0, 2).reshape(P, ATTN_A3_CHUNKS * D)),
        ("causal", np.where(key > query, np.float32(NEG), np.float32(0))),
    ])


def attn_a3(core, blob, offsets):
    nc = core.nc
    T = SEQ // P
    inv_scale = 1.0 / np.sqrt(float(ATTN_A3_HD))
    with Stage(core, "attn_a3") as st:
        w = st.weights(blob, offsets)
        layer_norm(core, st)
        bank = [st.ps(f"bank{i}", [P, BANK]) for i in range(8)]
        pS, pT, pO, pP, pY = bank[0:2], bank[2:4], bank[4], bank[5:7], bank[7]
        x_now = st.sb("x_now", [P, SEQ])
        q = st.sb("q", [P, 2, ATTN_A3_CHUNKS, 2, SEQ])
        k = st.sb("k", [P, 2, ATTN_A3_CHUNKS, SEQ])
        val = st.sb("val", [P, 2, T, HEADS * ATTN_A3_HD])
        small_b = st.sb("small_b", [P, ATTN_A3_CHUNKS])
        prob = st.sb("prob", [P, 2, 3, P])
        probT = st.sb("probT", [P, 4, 3, P])
        neg_max, row_sum, inv = (st.sb(n, [P, 2, T]) for n in ("neg_max", "row_sum", "inv"))
        oT = st.sb("oT", [P, HEADS, SEQ // 2])
        names = ("set_up", "zeroed", "x_copied", "proj_psum", "proj_by_act", "proj_by_dve", "scores_ready", "masked", "max_ready", "exp_ready",
                 "inverted", "prob_ready", "probT_psum", "probT_ready", "pair_done", "oT_ready", "y_ready", "y_added")
        (set_up, zeroed, x_copied, proj_psum, proj_by_act, proj_by_dve, scores_ready, masked, max_ready, exp_ready,
         inverted, prob_ready, probT_psum, probT_ready, pair_done, oT_ready, y_ready, y_added) = (st.sem(n) for n in names)
        by_act = lambda i: i < 8 and i % 2 == 0
        reader = lambda i: (proj_by_act, i // 2 + 1) if by_act(i) else (proj_by_dve, i // 2 + 1 if i < 8 else i - 3)
        ACT_FILLS, DVE_FILLS = 4, 8
        FILLS = 12
        GROUPS = HEADS // PER_OUT
        PAIRS = HEADS // 2
        HALF = HEADS // T * SEQ // 2
        oT_flat = oT[:, :, :].rearrange("p h s -> p (h s)")

        with nc.Block() as block:
            @block.gpsimd
            def _(pool):
                def x_copy(b):
                    if not known(b, 1):
                        pool.wait_ge(proj_psum, b * FILLS)
                    nc.gpsimd.tensor_copy(x_now[:, :], core.xnT[:, bass.ds(b * SEQ, SEQ)]).then_inc(x_copied, 1)

                def step(b, s, first, last):
                    if first:
                        x_copy(b)
                        pool.wait_ge(x_copied, 1)
                        for s_zero in range(2):
                            for head in range(2):
                                other = slice(ATTN_A3_HD * (1 - head), ATTN_A3_HD * (2 - head))
                                nc.gpsimd.memset(q[other, s_zero, :, head, :], 0.0).then_inc(zeroed, 1)
                                pool.wait_ge(zeroed, 2 * s_zero + head + 1)
                        x_copy(b + 1)
                    for h in range(HEADS):
                        pool.wait_ge(inverted, b * HEADS + h + 1)
                        for t, blocks in enumerate((slice(0, 1), slice(1, 3))):
                            x = prob[:, h % 2, blocks, :]
                            ins = nc.gpsimd.tensor_tensor(x, x, bc(bc(inv[:, h % 2, t:t + 1].squeeze(1), 1, P), 1, blocks.stop - blocks.start), ALU.mult)
                        ins.then_inc(prob_ready, 1)
                        if h == 13 and not last:
                            if not known(b, BATCH) or b + 2 < BATCH:
                                x_copy(b + 2)

                sequences(pool, step)

            @block.tensor
            def _(pe):
                def fill(b, i):
                    if i == 0:
                        pe.wait_ge(x_copied, b + 1)
                    if i >= 2 or not known(b, 1):
                        j, c = (i - 2, b) if i >= 2 else (i - 2 + FILLS, b - 1)
                        done, count = reader(j)
                        pe.wait_ge(done, c * (ACT_FILLS if by_act(j) else DVE_FILLS) + count)
                    if i < 8:
                        for c in range(2):
                            ch = 2 * (i % 4) + c
                            ins = nc.tensor.matmul(pP[i % 2][:, c * SEQ:(c + 1) * SEQ], w["wq" if i < 4 else "wk"][:, ch * P:(ch + 1) * P],
                                                   x_now[:, :], start=True, stop=True)
                    else:
                        t, half = (i - 8) // 2, (i - 8) % 2
                        ins = nc.tensor.matmul(pP[i % 2][:, :], x_now[:, t * P:(t + 1) * P], w["wv"][:, half * BANK:(half + 1) * BANK],
                                               start=True, stop=True)
                    ins.then_inc(proj_psum, 1)

                def scores(b, s, h):
                    if h == 0:
                        pe.wait_ge(zeroed, 4)
                        pe.wait_ge(proj_by_act, (b + 1) * ACT_FILLS)
                        pe.wait_ge(proj_by_dve, (b + 1) * DVE_FILLS)
                    qh = q[:, s, h // 2, h % 2, :]
                    nc.tensor.matmul(pS[h % 2][:, 0:P], qh[:, 0:P], k[:, s, h // 2, 0:P], start=True, stop=True)
                    nc.tensor.matmul(pS[h % 2][:, SEQ:2 * SEQ], qh[:, P:2 * P], k[:, s, h // 2, :], start=True, stop=True).then_inc(scores_ready, 1)

                def turn(b, h):
                    pe.wait_ge(prob_ready, b * HEADS + h + 1)
                    if not (known(b, 1) and h < 2):
                        pe.wait_ge(probT_ready, b * HEADS + h - 1)
                    for j in range(3):
                        ins = nc.tensor.transpose(pT[h % 2][:, j * P:(j + 1) * P], prob[:, h % 2, j, :], core.ident[:, :])
                    ins.then_inc(probT_psum, 1)

                def weighted(b, s, pair):
                    pe.wait_ge(probT_ready, b * HEADS + 2 * pair + 2)
                    if pair % 2 == 0 and not (known(b, 1) and pair == 0):
                        pe.wait_ge(oT_ready, b * GROUPS + pair // 2)
                    at = pair % 2 * SEQ
                    for t in range(T):
                        for odd in range(2):
                            h = 2 * pair + odd
                            rows = slice(odd * ATTN_A3_HD, (odd + 1) * ATTN_A3_HD)
                            moving = probT[:, h % 4, 0:2, :] if t == 0 else probT[:, h % 4, 2, :]
                            out = pO[rows, at:at + SEQ].rearrange("p (j q) -> p j q", j=2) if t == 0 else pO[rows, at + P:at + SEQ]
                            ins = nc.tensor.matmul(out, val[:, s, t, h * ATTN_A3_HD:(h + 1) * ATTN_A3_HD], moving, start=(t == 0), stop=(t == 1),
                                                   tile_position=(0, rows.start))
                    ins.then_inc(pair_done, 1)

                def project(b):
                    pe.wait_ge(oT_ready, (b + 1) * GROUPS)
                    if not known(b, 1):
                        pe.wait_ge(y_added, b)
                    for t in range(T):
                        for c in range(ATTN_A3_CHUNKS):
                            ins = nc.tensor.matmul(pY[:, t * P:(t + 1) * P], oT_flat[:, t * HALF + c:(t + 1) * HALF:ATTN_A3_CHUNKS], w["proj"][:, c * D:(c + 1) * D],
                                                   start=(c == 0), stop=(c == ATTN_A3_CHUNKS - 1))
                    ins.then_inc(y_ready, 1)

                def step(b, s, first, last):
                    if first:
                        for i in range(FILLS):
                            fill(b, i)
                        scores(b, s, 0)
                        scores(b, s, 1)
                    for h in range(HEADS):
                        turn(b, h)
                        if h + 2 < HEADS:
                            scores(b, s, h + 2)
                        elif not last:
                            scores(b + 1, 1 - s, h + 2 - HEADS)
                        if h < FILLS and not last:
                            fill(b + 1, h)
                        if h == 0 and not first:
                            weighted(b - 1, 1 - s, PAIRS - 1)
                        if h == 3 and not first:
                            project(b - 1)
                        if h >= 2 and h % 2 == 0:
                            weighted(b, s, h // 2 - 1)
                    if last:
                        weighted(b, s, PAIRS - 1)
                        project(b)

                sequences(pe, step)

            def evacuate(eng, act, b, s, i):
                done = proj_by_act if act else proj_by_dve
                src = pP[i % 2]
                eng.wait_ge(proj_psum, b * FILLS + i + 1)
                if i >= 8:
                    t, half = (i - 8) // 2, (i - 8) % 2
                    if i == 8 and not known(b, 2):
                        eng.wait_ge(pair_done, (b - 1) * PAIRS)
                    nc.vector.tensor_tensor(val[:, s, t, half * BANK:(half + 1) * BANK], src[:, :], w["bv"][:, half * BANK:(half + 1) * BANK],
                                            ALU.add).then_inc(done, 1)
                    return
                for c in range(2):
                    ch, part = 2 * (i % 4) + c, src[:, c * SEQ:(c + 1) * SEQ]
                    if i >= 4:
                        if act:
                            ins = nc.scalar.activation(k[:, s, ch, :], part, ACT.Identity, bias=w["bk"][:, ch:ch + 1])
                        else:
                            ins = nc.vector.tensor_scalar(k[:, s, ch, :], part, w["bk"][:, ch:ch + 1], None, ALU.add)
                        continue
                    for head in range(2):
                        rows = slice(head * ATTN_A3_HD, (head + 1) * ATTN_A3_HD)
                        if act:
                            ins = nc.scalar.activation(q[rows, s, ch, head, :], part[rows], ACT.Identity, bias=small_b[rows, ch:ch + 1], scale=inv_scale)
                        else:
                            ins = nc.vector.tensor_scalar(q[rows, s, ch, head, :], part[rows], w["bq"][rows, ch:ch + 1], inv_scale, ALU.add, ALU.mult)
                ins.then_inc(done, 1)

            @block.scalar
            def _(a):
                a.wait_ge(set_up, 1)

                def out_copy(b, g):
                    a.wait_ge(pair_done, b * PAIRS + 2 * g + 2)
                    if g == 0 and not known(b, 1):
                        a.wait_ge(y_ready, b)
                    for odd_head in range(2):
                        for odd_u in range(2):
                            src = pO[odd_head * ATTN_A3_HD:(odd_head + 1) * ATTN_A3_HD, :].rearrange("p (c s u) -> p c s u", c=2, u=2)[:, :, :, odd_u]
                            dst = oT[odd_u * ATTN_A3_HD:(odd_u + 1) * ATTN_A3_HD, 4 * g + odd_head:4 * g + odd_head + 3:2, :]
                            ins = nc.scalar.activation(dst, src, ACT.Copy, scale=inv_scale)
                    ins.then_inc(oT_ready, 1)

                def step(b, s, first, last):
                    if first:
                        for i in filter(by_act, range(FILLS)):
                            evacuate(a, True, b, s, i)
                    for h in range(HEADS):
                        a.wait_ge(max_ready, b * HEADS + h + 1)
                        nc.scalar.activation(prob[:, h % 2, 0, :], pS[h % 2][:, 0:P], ACT.Exp, bias=neg_max[:, h % 2, 0:1],
                                             accum_out=row_sum[:, h % 2, 0:1])
                        nc.scalar.activation(prob[:, h % 2, 1:3, :], pS[h % 2][:, SEQ:2 * SEQ].rearrange("p (j k) -> p j k", j=2), ACT.Exp,
                                             bias=neg_max[:, h % 2, 1:2], accum_out=row_sum[:, h % 2, 1:2]).then_inc(exp_ready, 1)
                        if h == 2 and not first:
                            out_copy(b - 1, GROUPS - 1)
                        if h >= 2 and by_act(h - 2) and not last:
                            evacuate(a, True, b + 1, 1 - s, h - 2)
                        if h % PER_OUT == 2 and h > 2:
                            out_copy(b, h // PER_OUT - 1)
                    if last:
                        out_copy(b, GROUPS - 1)

                sequences(a, step)

            @block.vector
            def _(v):
                nc.vector.tensor_scalar(small_b[:, :], w["bq"], inv_scale, None, ALU.mult).then_inc(set_up, 1)

                def row_max(b, h):
                    n = b * HEADS + h + 1
                    v.wait_ge(scores_ready, n)
                    blocks = pS[h % 2][:, :].rearrange("p (j k) -> p j k", k=P)[:, 0:4:3, :]
                    nc.vector.tensor_tensor(blocks, blocks, bc(w["causal"], 1, 2), ALU.add).then_inc(masked, 1)
                    v.wait_ge(masked, n)
                    nc.vector.tensor_reduce(neg_max[:, h % 2, 0:1], pS[h % 2][:, 0:P], AX.X, ALU.max, negate=True)
                    nc.vector.tensor_reduce(neg_max[:, h % 2, 1:2], pS[h % 2][:, SEQ:2 * SEQ], AX.X, ALU.max, negate=True).then_inc(max_ready, 1)

                def invert(b, h):
                    v.wait_ge(exp_ready, b * HEADS + h + 1)
                    nc.vector.reciprocal(inv[:, h % 2, :], row_sum[:, h % 2, :]).then_inc(inverted, 1)

                def step(b, s, first, last):
                    if first:
                        for i in (i for i in range(FILLS) if not by_act(i)):
                            evacuate(v, False, b, s, i)
                        row_max(b, 0)
                        invert(b, 0)
                        row_max(b, 1)
                    for h in range(HEADS):
                        v.wait_ge(probT_psum, b * HEADS + h + 1)
                        if h % 2 == 0 and not (known(b, 1) and h < 4):
                            v.wait_ge(pair_done, b * PAIRS + h // 2 - 1)
                        nc.vector.tensor_copy(probT[:, h % 4, :, :], pT[h % 2][:, 0:3 * P].rearrange("p (j q) -> p j q", j=3)).then_inc(probT_ready, 1)
                        if h + 1 < HEADS:
                            invert(b, h + 1)
                        elif not last:
                            invert(b + 1, 0)
                        if h + 2 < HEADS:
                            row_max(b, h + 2)
                        elif not last:
                            row_max(b + 1, h + 2 - HEADS)
                        if 1 <= h <= FILLS and not by_act(h - 1) and not last:
                            evacuate(v, False, b + 1, 1 - s, h - 1)
                        if h == 5 and not first:
                            add(b - 1)
                    if last:
                        add(b)

                def add(b):
                    v.wait_ge(y_ready, b + 1)
                    x = core.x_res[:, bass.ds(b * T, T), :]
                    nc.vector.tensor_tensor(x, x, pY[:, 0:T * D].rearrange("p (t d) -> p t d", t=T), ALU.add).then_inc(y_added, 1)

                sequences(v, step)


FFN3_EXPERTS = 64
FFN3_TOP = 8
ROUTE_GROUPS = 8
TOP_GROUPS = 4
IN_GROUP = FFN3_EXPERTS // ROUTE_GROUPS
FFN3_HID = 64
FFN3_SHARED = 256
PAIRS = FFN3_EXPERTS // 2
SCALE = 2.5
FFN3_PIECES = 3
SIDE = FFN3_EXPERTS // 2
FFN3_BF16 = mybir.dt.bfloat16


def ffn3_weights(w):
    expert_of_row = np.tile(np.arange(SIDE), FFN3_PIECES)
    spread = np.repeat(expert_of_row[:, None] == np.arange(SIDE)[None, :], FFN3_HID, axis=1).astype(np.float32)
    return pack([
        ("spread", spread),
        ("router", w["router_w"].T), ("earlier", earlier_table(ROUTE_GROUPS)),
        ("correction", np.broadcast_to(w["correction_bias"], (P, FFN3_EXPERTS))),
        ("up", w["up_w"].transpose(1, 0, 2).reshape(D, FFN3_EXPERTS * FFN3_HID)),
        ("down", w["down_w"].reshape(PAIRS, P, D).transpose(1, 0, 2).reshape(P, PAIRS * D)),
        ("shared_up", w["shared_up_w"]),
        ("shared_down", w["shared_down_w"].reshape(FFN3_SHARED // P, P, D).transpose(1, 0, 2).reshape(P, FFN3_SHARED // P * D)),
    ])


def ffn3(core, blob, offsets):
    nc = core.nc
    GROUPS = TOK // BANK
    with Stage(core, "ffn3") as st:
        w = st.weights(blob, offsets)
        layer_norm(core, st)
        bank = [st.ps(f"bank{i}", [P, BANK]) for i in range(8)]
        per_bank = BANK // FFN3_EXPERTS
        sfc = st.sb("sfc", [P, TILES, FFN3_EXPERTS])
        score = st.sb("score", [P, TILES, FFN3_EXPERTS])
        x_now = st.sb("x_now", [P, 2, BANK])
        copied, logits_ready, scores_ready = st.sem("copied"), st.sem("logits_ready"), st.sem("scores_ready")
        with nc.Block() as block:
            @block.gpsimd
            def _(pool):
                pool.sem_inc(scores_ready, 2)
                with pool.Fori(0, GROUPS // 2) as g:
                    for s in range(2):
                        pool.wait_ge(scores_ready, 2 * g + s + 1)
                        nc.gpsimd.tensor_copy(x_now[:, s, :], core.xnT[:, bass.ds((2 * g + s) * BANK, BANK)]).then_inc(copied, 1)

            @block.tensor
            def _(pe):
                with pe.Fori(0, GROUPS // 2) as g:
                    for s in range(2):
                        pe.wait_ge(copied, 2 * g + s + 1)
                        for t in range(4):
                            ins = nc.tensor.matmul(bank[s][:, t * FFN3_EXPERTS:(t + 1) * FFN3_EXPERTS], x_now[:, s, t * P:(t + 1) * P], w["router"],
                                                   start=True, stop=True)
                        ins.then_inc(logits_ready, 1)

            @block.scalar
            def _(a):
                with a.Fori(0, GROUPS // 2) as g:
                    for s in range(2):
                        a.wait_ge(logits_ready, 2 * g + s + 1)
                        nc.scalar.activation(score[:, bass.ds(8 * g + 4 * s, 4), :], bank[s][:, 0:4 * FFN3_EXPERTS].rearrange("p (t e) -> p t e", t=4),
                                             ACT.Sigmoid).then_inc(scores_ready, 1)

        comb = st.sb("comb", [P, TILES, FFN3_EXPERTS])
        work = st.sb("work", [P, TILES, FFN3_EXPERTS])
        repl = st.sb("repl", [P, TILES, FFN3_EXPERTS])
        first, second, ties, gscore, gsel = (st.sb(n, [P, TILES, ROUTE_GROUPS]) for n in ("first", "second", "ties", "gscore", "gsel"))
        above, same = (st.sb(n, [P, TILES, ROUTE_GROUPS, ROUTE_GROUPS]) for n in ("above", "same"))
        top8 = st.sb("top8", [P, TILES, FFN3_TOP])
        total = st.sb("total", [P, TILES])
        spread = st.sb("spread", [FFN3_PIECES * SIDE, SIDE * FFN3_HID], FFN3_BF16)
        ident = st.sb("ident_bf16", [P, P], FFN3_BF16)
        pieces = st.sb("pieces", [P, TILES, 2, FFN3_PIECES, SIDE], FFN3_BF16)
        dve = st.sem("dve")
        grouped = lambda t: t[:, :, :].rearrange("p t (g e) -> p (t g) e", g=ROUTE_GROUPS)
        flat = lambda t: t[:, :, :].rearrange("p t g -> p (t g)")
        BLOCKS = FFN3_SHARED // P
        relu = st.sb("relu", [P, 2, BANK])
        part = st.sb("part", [P, 2, BANK])
        hid = st.sb("hid", [P, 2, BANK])
        s_hid = (st.sb("s_hid", [P, BLOCKS, BANK]), hid)
        s_up_ready, s_relu_ready, s_hid_ready, s_y_ready, s_copied, s_added = (
            st.sem(n) for n in ("s_up_ready", "s_relu_ready", "s_hid_ready", "s_y_ready", "s_copied", "s_added"))

        def with_lead(eng, front, back):
            front(0, 0)
            with eng.Fori(0, GROUPS // 2 - 1) as pair:
                front(pair * 2 + 1, 1)
                back(pair * 2, 0)
                front(pair * 2 + 2, 0)
                back(pair * 2 + 1, 1)
            front(GROUPS - 1, 1)
            back(GROUPS - 2, 0)
            back(GROUPS - 1, 1)

        with nc.Block() as block:
            @block.tensor
            def _(pe):
                def up(g, s):
                    for b in range(BLOCKS):
                        pe.wait_ge(s_relu_ready, g * BLOCKS + b + 1)
                        nc.tensor.matmul(bank[b][:, :], w["shared_up"][:, b * P:(b + 1) * P], core.xnT[:, bass.ds(g * BANK, BANK)],
                                         start=True, stop=True).then_inc(s_up_ready, 1)

                def down(g, s):
                    pe.wait_ge(s_copied, g + 1)
                    pe.wait_ge(s_hid_ready, (g + 2) * BLOCKS)
                    for t in range(4):
                        for b in range(BLOCKS):
                            ins = nc.tensor.matmul(bank[4 + s][:, t * P:(t + 1) * P], s_hid[s][:, b, t * P:(t + 1) * P],
                                                   w["shared_down"][:, b * D:(b + 1) * D], start=(b == 0), stop=(b == BLOCKS - 1))
                    ins.then_inc(s_y_ready, 1)

                pe.sem_inc(s_relu_ready, BLOCKS)
                pe.sem_inc(s_copied, 2)
                with_lead(pe, up, down)

            @block.scalar
            def _(a):
                def activate(g, s):
                    for b in range(BLOCKS):
                        a.wait_ge(s_hid_ready, g * BLOCKS + b + 1)
                        a.wait_ge(s_up_ready, g * BLOCKS + b + 1)
                        nc.scalar.activation(relu[:, b, :], bank[b][:, :], ACT.Relu).then_inc(s_relu_ready, 1)

                def copy(g, s):
                    a.wait_ge(s_added, g + 1)
                    a.wait_ge(s_y_ready, g + 3)
                    nc.scalar.copy(part[:, s, :], bank[4 + s][:, :]).then_inc(s_copied, 1)

                a.sem_inc(s_hid_ready, BLOCKS)
                a.sem_inc(s_added, 2)
                with_lead(a, activate, copy)

            @block.gpsimd
            def _(pool):
                def square(g, s):
                    pool.wait_ge(s_y_ready, g + 1)
                    for b in range(BLOCKS):
                        pool.wait_ge(s_relu_ready, (g + 1) * BLOCKS + b + 1)
                        nc.gpsimd.tensor_tensor(s_hid[s][:, b, :], relu[:, b, :], relu[:, b, :], ALU.mult).then_inc(s_hid_ready, 1)

                def add(g, s):
                    pool.wait_ge(s_copied, g + 3)
                    x = core.x_res[:, bass.ds(g * 4, 4), :]
                    nc.gpsimd.tensor_tensor(x, x, part[:, s, :].rearrange("p (t d) -> p t d", t=4), ALU.add).then_inc(s_added, 1)

                nc.gpsimd.tensor_copy(spread[:, :], w["spread"][0:FFN3_PIECES * SIDE, :])
                nc.gpsimd.tensor_copy(ident[:, :], core.ident[:, :])
                pool.sem_inc(s_y_ready, 2)
                with_lead(pool, square, add)

            @block.vector
            def _(v):
                c = Chain(v, dve)
                c.link(nc.vector.tensor_tensor(sfc[:, :, :], score[:, :, :], bc(w["correction"], 1, TILES), ALU.add))
                c.link(nc.vector.tensor_reduce(flat(first), grouped(sfc), AX.X, ALU.max))
                c.link(nc.vector.tensor_tensor(grouped(work), grouped(sfc), bc(flat(first), 2, IN_GROUP), ALU.is_equal))
                c.link(nc.vector.tensor_reduce(flat(ties), grouped(work), AX.X, ALU.add))
                c.link(nc.vector.scalar_tensor_tensor(work[:, :, :], work[:, :, :], NEG, sfc[:, :, :], ALU.mult, ALU.add))
                c.link(nc.vector.tensor_reduce(flat(second), grouped(work), AX.X, ALU.max))
                c.link(nc.vector.tensor_scalar(ties[:, :, :], ties[:, :, :], 2.0, None, ALU.is_ge))
                c.link(nc.vector.tensor_tensor(gscore[:, :, :], first[:, :, :], ties[:, :, :], ALU.mult))
                c.link(nc.vector.tensor_scalar(ties[:, :, :], ties[:, :, :], -1.0, 1.0, ALU.mult, ALU.add))
                c.link(nc.vector.tensor_tensor(second[:, :, :], second[:, :, :], ties[:, :, :], ALU.mult))
                c.link(nc.vector.tensor_tensor(second[:, :, :], second[:, :, :], gscore[:, :, :], ALU.add))
                c.link(nc.vector.tensor_tensor(gscore[:, :, :], second[:, :, :], first[:, :, :], ALU.add))
                link_ranks(nc, c, gsel[:, :, :], gscore[:, :, :], above[:, :, :, :], same[:, :, :, :], w["earlier"], ROUTE_GROUPS)
                c.link(nc.vector.tensor_scalar(gsel[:, :, :], gsel[:, :, :], float(TOP_GROUPS), None, ALU.is_lt))
                c.link(nc.vector.tensor_tensor(grouped(work), grouped(sfc), bc(flat(gsel), 2, IN_GROUP), ALU.mult))
                for t in range(TILES):
                    ins = nc.vector.max(top8[:, t, :], work[:, t, :])
                c.link(ins)
                for t in range(TILES):
                    ins = nc.vector.match_replace(repl[:, t, :], top8[:, t, :], work[:, t, :], NEG)
                c.link(ins)
                c.link(nc.vector.tensor_tensor(work[:, :, :], work[:, :, :], repl[:, :, :], ALU.not_equal))
                c.link(nc.vector.tensor_tensor(comb[:, :, :], score[:, :, :], work[:, :, :], ALU.mult))
                c.link(nc.vector.tensor_reduce(total[:, :], comb[:, :, :], AX.X, ALU.add))
                c.link(nc.vector.tensor_scalar(total[:, :], total[:, :], 1e-20, None, ALU.add))
                c.link(nc.vector.reciprocal(total[:, :], total[:, :]))
                c.link(nc.vector.tensor_scalar(total[:, :], total[:, :], SCALE, None, ALU.mult))
                c.link(nc.vector.tensor_tensor(comb[:, :, :], comb[:, :, :], bc(total[:, :], 2, FFN3_EXPERTS), ALU.mult))
                by_side = comb[:, :, :].rearrange("p t (s e) -> p t s e", s=2)
                for i in range(FFN3_PIECES):
                    c.link(nc.vector.tensor_copy(pieces[:, :, :, i, :], by_side))
                    if i + 1 < FFN3_PIECES:
                        c.link(nc.vector.tensor_tensor(by_side, by_side, pieces[:, :, :, i, :], ALU.subtract))

        combT = st.sb("combT", [FFN3_PIECES * SIDE, 2, TOK], FFN3_BF16)
        combT_psum, combT_ready = st.sem("combT_psum"), st.sem("combT_ready")
        with nc.Block() as block:
            @block.tensor
            def _(pe):
                pe.sem_inc(combT_ready, 2)
                with pe.Fori(0, GROUPS // 2) as g:
                    for i in range(2):
                        pe.wait_ge(combT_ready, 2 * g + i + 1)
                        for side in range(2):
                            for t in range(4):
                                tile = pieces[:, bass.ds(8 * g + 4 * i + t, 1), side, :, :].rearrange("p t i e -> p (t i e)")
                                ins = nc.tensor.matmul(bank[2 * i + side][0:FFN3_PIECES * SIDE, t * P:(t + 1) * P], tile, ident[:, :], start=True, stop=True)
                        ins.then_inc(combT_psum, 1)

            @block.scalar
            def _(a):
                with a.Fori(0, GROUPS // 2) as g:
                    for i in range(2):
                        a.wait_ge(combT_psum, 2 * g + i + 1)
                        for side in range(2):
                            ins = nc.scalar.copy(combT[:, side, bass.ds((2 * g + i) * BANK, BANK)], bank[2 * i + side][0:FFN3_PIECES * SIDE, :])
                        ins.then_inc(combT_ready, 1)

        yT = s_hid[0][:, 0, :]
        p_up, p_gate, p_y = bank[0:2], bank[2:4], bank[4:6]
        names = ("up_ready", "relu_ready", "part_ready", "hid_ready", "yT_psum", "yT_ready", "y_ready", "added")
        (up_ready, relu_ready, part_ready, hid_ready, yT_psum, yT_ready, y_ready, added) = (st.sem(n) for n in names)

        def groups(eng, step):
            step(0, 0, True)
            step(1, 1, False)
            with eng.Fori(1, GROUPS // 2) as pair:
                step(pair * 2, 0, False)
                step(pair * 2 + 1, 1, False)

        with nc.Block() as block:
            @block.tensor
            def _(pe):
                def finish(g, s):
                    pe.wait_ge(yT_ready, g + 1)
                    for t in range(4):
                        ins = nc.tensor.transpose(p_y[s][:, t * P:(t + 1) * P], yT[:, t * P:(t + 1) * P], core.ident[:, :])
                    ins.then_inc(y_ready, 1)

                def step(g, s, first):
                    x = core.xnT[:, bass.ds(g * BANK, BANK)]

                    def up(k):
                        side, at = k // (PAIRS // 2), k % (PAIRS // 2) * P
                        nc.tensor.matmul(p_gate[k % 2][:, :], spread[:, at:at + P], combT[:, side, bass.ds(g * BANK, BANK)],
                                         start=True, stop=True)
                        nc.tensor.matmul(p_up[k % 2][:, :], w["up"][:, k * P:(k + 1) * P], x, start=True, stop=True).then_inc(up_ready, 1)

                    def down(k):
                        pe.wait_ge(hid_ready, g * PAIRS + k + 1)
                        return nc.tensor.matmul(p_y[s][:, :], w["down"][:, k * D:(k + 1) * D], hid[:, k % 2, :], start=(k == 0), stop=(k == PAIRS - 1))

                    up(0)
                    up(1)
                    if not known(g, 2):
                        pe.wait_ge(added, g - 1)
                    for k in range(PAIRS):
                        ins = down(k)
                        if k + 2 < PAIRS:
                            up(k + 2)
                        if k == 1 and not first:
                            finish(g - 1, 1 - s)
                    ins.then_inc(yT_psum, 1)

                groups(pe, step)
                finish(GROUPS - 1, (GROUPS - 1) % 2)

            @block.scalar
            def _(a):
                with a.Fori(0, GROUPS) as g:
                    for k in range(PAIRS):
                        a.wait_ge(up_ready, g * PAIRS + k + 1)
                        nc.scalar.activation(relu[:, k % 2, :], p_up[k % 2][:, :], ACT.Relu).then_inc(relu_ready, 1)

            @block.vector
            def _(v):
                def add(g, s):
                    v.wait_ge(y_ready, g + 1)
                    x = core.x_res[:, bass.ds(g * 4, 4), :]
                    nc.vector.tensor_tensor(x, x, p_y[s][:, :].rearrange("p (t d) -> p t d", t=4), ALU.add).then_inc(added, 1)

                def step(g, s, first):
                    for k in range(PAIRS):
                        v.wait_ge(relu_ready, g * PAIRS + k + 1)
                        nc.vector.tensor_tensor(part[:, k % 2, :], relu[:, k % 2, :], p_gate[k % 2][:, :], ALU.mult).then_inc(part_ready, 1)
                        v.wait_ge(part_ready, g * PAIRS + k + 1)
                        nc.vector.tensor_tensor(hid[:, k % 2, :], part[:, k % 2, :], relu[:, k % 2, :], ALU.mult).then_inc(hid_ready, 1)
                        if k == 5 and not first:
                            add(g - 1, 1 - s)
                    v.wait_ge(yT_psum, g + 1)
                    nc.vector.tensor_copy(yT[:, :], p_y[s][:, :]).then_inc(yT_ready, 1)

                groups(v, step)
                add(GROUPS - 1, (GROUPS - 1) % 2)


def build_program(nc, x, ident, blobs, out):
    with ExitStack() as ctx:
        core = Core(nc, ctx)
        load_constants(core, ident, x)
        attn_a(core, *blobs["L0_attn_a"])
        ffn0(core, *blobs["L0_ffn"])
        attn_b0(core, *blobs["L0_attn_b"])
        ffn0(core, *blobs["L0_ffn"])
        attn_a(core, *blobs["L1_attn_a"])
        ffn1(core, *blobs["L1_ffn"])
        scan1(core, *blobs["L1_attn_b"])
        ffn1(core, *blobs["L1_ffn"])
        attn_a2(core, *blobs["L2_attn_a"])
        ffn2(core, *blobs["L2_ffn"])
        attn_b2(core, *blobs["L2_attn_b"])
        ffn2(core, *blobs["L2_ffn"])
        attn_a3(core, *blobs["L3_attn_a"])
        ffn3(core, *blobs["L3_ffn"])
        scan3(core, *blobs["L3_attn_b"])
        ffn3(core, *blobs["L3_ffn"])
        store_output(core, out)


_LAYOUTS = {"L0_attn_a": attn_a_weights, "L0_ffn": ffn0_weights, "L0_attn_b": attn_b0_weights, "L1_attn_a": attn_a_weights,
            "L1_ffn": ffn1_weights, "L1_attn_b": scan1_weights, "L2_attn_a": attn_a2_weights, "L2_ffn": ffn2_weights,
            "L2_attn_b": attn_b2_weights, "L3_attn_a": attn_a3_weights, "L3_ffn": ffn3_weights, "L3_attn_b": scan3_weights}


def kernel(**inputs):
    import concourse.bacc as bacc
    from concourse.bass_utils import run_bass_kernel_spmd

    arrays = {"x": np.ascontiguousarray(np.asarray(inputs["L0_attn_a_x"]).reshape(TOK, D)), "ident": np.eye(P, dtype=np.float32)}
    offsets = {}
    for stage, layout in _LAYOUTS.items():
        own = {k[len(stage) + 1:]: np.asarray(v) for k, v in inputs.items() if k.startswith(stage + "_")}
        arrays[stage], offsets[stage] = layout(own)
    nc = bacc.Bacc("TRN2", target_bir_lowering=False, num_devices=1)
    dram = {k: nc.dram_tensor(f"in_{k}", a.shape, mybir.dt.from_np(a.dtype), kind="ExternalInput").ap() for k, a in arrays.items()}
    out = nc.dram_tensor("out", (TOK, D), F32, kind="ExternalOutput").ap()
    build_program(nc, dram["x"], dram["ident"], {k: (dram[k], offsets[k]) for k in _LAYOUTS}, out)
    r = run_bass_kernel_spmd(nc, [{f"in_{k}": a for k, a in arrays.items()}], core_ids=[0])
    return r.results[0]["out"].reshape(BATCH, SEQ, D)
```
